# Optimizing a Trainium2 kernel written in Bass

```python
import numpy as np
import jax
import jax.numpy as jnp

def _softmax(x, axis=-1):
    return jax.nn.softmax(x, axis=axis)

def _gelu(x):
    return jax.nn.gelu(x, approximate=True)

def _silu(x):
    return jax.nn.silu(x)

def _sigmoid(x):
    return jax.nn.sigmoid(x)

def _layernorm(x, axis=-1, eps=1e-05):
    m = jnp.mean(x, axis=axis, keepdims=True)
    v = jnp.var(x, axis=axis, keepdims=True)
    return (x - m) / jnp.sqrt(v + eps)

def _scatter_add(tgt, idx, src, axis=0):
    return tgt.at[idx].add(src)

def _segment_sum(src, seg, n):
    return jax.ops.segment_sum(src, seg, n)
kernel_name = 'mk_decoder_postln_d2_seqx_r4_6df7cc'

def setup_inputs(seed: int=0):
    np.random.seed(seed)
    _w = jnp.asarray

    def _rec_inputs():
        import jax
        import jax.numpy as jnp
        _rk = jax.random.key(seed)
        x = 7.22e-05 + 1 * jax.random.normal(jax.random.fold_in(_rk, 1), (8, 256, 256), jnp.float32)
        _lenS = 256 - jax.random.randint(jax.random.fold_in(_rk, 7), (8,), 0, max(1, 256 // 4) + 1, jnp.int32)
        _lenS2 = 77 - jax.random.randint(jax.random.fold_in(_rk, 8), (8,), 0, max(1, 77 // 4) + 1, jnp.int32)
        _ctx_1024P = jax.random.normal(jax.random.fold_in(_rk, 11), (8, 16, 256), jnp.float32)
        _ctx_1024c = jax.random.dirichlet(jax.random.fold_in(_rk, 511), 0.3 * jnp.ones((16,), jnp.float32), (8, 77))
        _ctx_1024t = jnp.einsum('bsk,bkd->bsd', _ctx_1024c, _ctx_1024P)
        _ctx_1024t = _ctx_1024t * jax.lax.rsqrt(jnp.mean(jnp.square(_ctx_1024t)) + 1e-12) * 0.953939
        ctx_1024 = 4.13588e-05 + 0.999923 * (_ctx_1024t + 0.3 * jax.random.normal(jax.random.fold_in(_rk, 611), (8, 77, 256), jnp.float32))
        _validS = jnp.arange(256)[None, :] < _lenS[:, None]
        _validS2 = jnp.arange(77)[None, :] < _lenS2[:, None]
        _causal = jnp.tril(jnp.ones((256, 256), dtype=bool))
        mask_BxS2_if1 = jnp.where(jnp.ones((8, 77), dtype=bool), 1, 0).astype(jnp.int32)
        return (x, ctx_1024, mask_BxS2_if1)
    x, ctx_1024, mask_BxS2_if1 = _rec_inputs()

    def _L0_attn_setup():
        import jax, jax.numpy as jnp
        import numpy as np
        B, S, E = (2, 1024, 256)
        H, DQK, DV = (16, 64, 64)
        ROPE_BASE = 10000.0

        def _rope(t):
            D = t.shape[-1]
            inv_freq = 1.0 / ROPE_BASE ** (jnp.arange(0, D, 2, dtype=jnp.float32) / D)
            pos = jnp.arange(t.shape[2], dtype=jnp.float32)
            ang = pos[:, None] * inv_freq[None, :]
            cos = jnp.cos(ang)[None, None]
            sin = jnp.sin(ang)[None, None]
            t1, t2 = (t[..., :D // 2], t[..., D // 2:])
            return jnp.concatenate([t1 * cos - t2 * sin, t1 * sin + t2 * cos], axis=-1)
        key = jax.random.key(seed)
        ks = jax.random.split(key, 4)
        sE = 1.0 / np.sqrt(E)
        sV = 1.0 / np.sqrt(H * DV)
        return {'x': jax.random.normal(ks[0], (B, S, E), jnp.float32), 'Wq': jax.random.normal(ks[1], (E, H * DQK), jnp.float32) * sE, 'bq': jnp.zeros((H * DQK,), jnp.float32), 'Wkv': jax.random.normal(ks[2], (E, H * (DQK + DV)), jnp.float32) * sE, 'bkv': jnp.zeros((H * (DQK + DV),), jnp.float32), 'Wo': jax.random.normal(ks[3], (H * DV, E), jnp.float32) * sV, 'bo': jnp.zeros((E,), jnp.float32)}
    _L0_attn_all = _L0_attn_setup()
    _L0_attn_in = {k: v for k, v in _L0_attn_all.items() if k in ('Wq', 'bq', 'Wkv', 'bkv', 'Wo', 'bo')}
    del _L0_attn_all

    def _L0_xattn_setup():
        import jax, jax.numpy as jnp
        import numpy as np
        D_MODEL = 256
        NUM_HEADS = 16
        HEAD_DIM = D_MODEL // NUM_HEADS
        key = jax.random.key(seed)
        ks = jax.random.split(key, 10)
        B, SQ, SKV = (4, 512, 512)
        s = 1.0 / np.sqrt(D_MODEL)
        return {'query': jax.random.normal(ks[0], (B, SQ, D_MODEL), jnp.float32), 'key_value': jax.random.normal(ks[1], (B, SKV, D_MODEL), jnp.float32), 'Wq': jax.random.normal(ks[2], (D_MODEL, D_MODEL), jnp.float32) * s, 'bq': jnp.zeros((D_MODEL,), jnp.float32), 'Wk': jax.random.normal(ks[3], (D_MODEL, D_MODEL), jnp.float32) * s, 'bk': jnp.zeros((D_MODEL,), jnp.float32), 'Wv': jax.random.normal(ks[4], (D_MODEL, D_MODEL), jnp.float32) * s, 'bv': jnp.zeros((D_MODEL,), jnp.float32), 'Wo': jax.random.normal(ks[5], (D_MODEL, D_MODEL), jnp.float32) * s, 'bo': jnp.zeros((D_MODEL,), jnp.float32)}
    _L0_xattn_all = _L0_xattn_setup()
    _L0_xattn_in = {k: v for k, v in _L0_xattn_all.items() if k in ('Wq', 'bq', 'Wk', 'bk', 'Wv', 'bv', 'Wo', 'bo')}
    del _L0_xattn_all

    def _L0_ffn_setup():
        import jax, jax.numpy as jnp
        import numpy as np
        BS, SLEN, DIM = (1, 512, 256)
        NUM_EXPERTS, TOP_K = (8, 2)
        HID = 352

        def _masked_grouped_mm(x, w, onehot):
            g = jnp.einsum('tk,gnk->tgn', x, w, preferred_element_type=jnp.float32)
            return jnp.einsum('tgn,tg->tn', g, onehot)

        def moe_forward(x, gate_w, expert_bias, w_up, w_down, shared_w_up, shared_w_down):
            bs, slen, dim = x.shape
            xf = x.reshape(-1, dim)
            scores = jax.nn.sigmoid((xf @ gate_w.T).astype(jnp.float32))
            biased = scores + expert_bias
            _, sel = jax.lax.top_k(biased, TOP_K)
            top_scores = jnp.take_along_axis(scores, sel, axis=-1)
            flat_sel = sel.reshape(-1)
            counts = jnp.bincount(flat_sel, length=NUM_EXPERTS)
            order = jnp.argsort(flat_sel, stable=True)
            scores_sorted = top_scores.reshape(-1)[order]
            token_ids = order // TOP_K
            routed_in = (xf[token_ids] * scores_sorted[:, None]).astype(x.dtype)
            seg = jnp.repeat(jnp.arange(NUM_EXPERTS), counts, total_repeat_length=flat_sel.shape[0])
            onehot = jax.nn.one_hot(seg, NUM_EXPERTS, dtype=jnp.float32)
            h = _masked_grouped_mm(routed_in.astype(jnp.bfloat16), w_up.astype(jnp.bfloat16), onehot)
            h = jnp.square(jax.nn.relu(h.astype(jnp.bfloat16)))
            routed_out = _masked_grouped_mm(h.astype(jnp.bfloat16), w_down.astype(jnp.bfloat16), onehot)
            routed_out = routed_out.astype(jnp.bfloat16).astype(x.dtype)
            hs = jnp.square(jax.nn.relu(xf @ shared_w_up.T))
            shared_out = hs @ shared_w_down.T
            combined = jnp.zeros((flat_sel.shape[0], dim), routed_out.dtype).at[order].set(routed_out)
            out = combined.reshape(-1, TOP_K, dim).sum(axis=1) + shared_out
            return out.reshape(bs, slen, dim)
        key = jax.random.key(seed)
        k = jax.random.split(key, 6)
        s = 0.02
        return {'x': jax.random.normal(k[0], (BS, SLEN, DIM), jnp.float32), 'gate_w': jax.random.normal(k[1], (NUM_EXPERTS, DIM), jnp.float32) * s, 'expert_bias': jnp.zeros((NUM_EXPERTS,), jnp.float32), 'w_up': jax.random.normal(k[2], (NUM_EXPERTS, HID, DIM), jnp.float32) * s, 'w_down': jax.random.normal(k[3], (NUM_EXPERTS, DIM, HID), jnp.float32) * s, 'shared_w_up': jax.random.normal(k[4], (HID, DIM), jnp.float32) * s, 'shared_w_down': jax.random.normal(k[5], (DIM, HID), jnp.float32) * s}
    _L0_ffn_all = _L0_ffn_setup()
    _L0_ffn_in = {k: v for k, v in _L0_ffn_all.items() if k in ('gate_w', 'expert_bias', 'w_up', 'w_down', 'shared_w_up', 'shared_w_down')}
    del _L0_ffn_all

    def _L1_attn_setup():
        import jax, jax.numpy as jnp
        import numpy as np
        CHUNK = 32
        FLOOR = 0.01
        EPS_MIX = 1e-05
        EPS_NORM = 1e-05

        def l2norm(x):
            return x / jnp.sqrt(jnp.sum(x * x, -1, keepdims=True) + 1e-12)

        def dw_causal_conv(x, w):
            K = w.shape[-1]
            L = x.shape[1]
            xp = jnp.pad(x, ((0, 0), (K - 1, 0), (0, 0)))
            y = jnp.zeros_like(x)
            for t in range(K):
                y = y + xp[:, t:t + L, :] * w[:, t]
            return y

        def delta_rule_chunkwise(q, k, v, beta):
            b, h, L, dk = q.shape
            dv = v.shape[-1]
            c = CHUNK
            n = L // c
            q = l2norm(q)
            k = l2norm(k)
            v = v * beta[..., None]
            kb = k * beta[..., None]
            rs = lambda x: x.reshape(b, h, n, c, -1)
            qc, kc, vc, kbc = (rs(q), rs(k), rs(v), rs(kb))
            T = -jnp.einsum('bhnid,bhnjd->bhnij', kbc, kc)
            tri_strict = jnp.tril(jnp.ones((c, c), bool), -1)
            T = jnp.where(tri_strict, T, 0.0)
            for i in range(1, c):
                T = T.at[..., i, :i].add(jnp.einsum('bhnj,bhnji->bhni', T[..., i, :], T[..., :, :i]))
            T = T + jnp.eye(c, dtype=T.dtype)
            u = jnp.einsum('bhnij,bhnjd->bhnid', T, vc)
            w = jnp.einsum('bhnij,bhnjd->bhnid', T, kbc)
            mask_incl = jnp.tril(jnp.ones((c, c), bool), 0)

            def step(S, inp):
                qi, ki, ui, wi = inp
                attn = jnp.einsum('bhid,bhjd->bhij', qi, ki)
                attn = jnp.where(mask_incl, attn, 0.0)
                u_i = ui - jnp.einsum('bhik,bhkd->bhid', wi, S)
                o_i = jnp.einsum('bhik,bhkd->bhid', qi, S) + jnp.einsum('bhij,bhjd->bhid', attn, u_i)
                S = S + jnp.einsum('bhci,bhcd->bhid', ki, u_i)
                return (S, o_i)
            S0 = jnp.zeros((b, h, dk, dv), q.dtype)
            xs = tuple((jnp.moveaxis(a, 2, 0) for a in (qc, kc, u, w)))
            S, o = jax.lax.scan(step, S0, xs)
            o = jnp.moveaxis(o, 0, 2).reshape(b, h, L, dv)
            return (o, S)
        key = jax.random.key(seed)
        B, L, D, H = (4, 1024, 256, 4)
        dh = D // H
        ks = jax.random.split(key, 20)
        s = 1.0 / np.sqrt(D)
        inp = {'hidden_states': jax.random.normal(ks[0], (B, L, D), jnp.float32), 'Wq': jax.random.normal(ks[1], (D, D), jnp.float32) * s, 'Wk': jax.random.normal(ks[2], (D, D), jnp.float32) * s, 'Wv': jax.random.normal(ks[3], (D, D), jnp.float32) * s, 'Wb': jax.random.normal(ks[4], (D, H), jnp.float32) * s, 'conv_q_w': jax.random.normal(ks[5], (D, 4), jnp.float32) * 0.5, 'conv_k_w': jax.random.normal(ks[6], (D, 4), jnp.float32) * 0.5, 'conv_v_w': jax.random.normal(ks[7], (D, 4), jnp.float32) * 0.5, 'local_w': (jax.random.normal(ks[8], (H * dh, 7), jnp.float32) / np.sqrt(7.0)).at[:, -1].add(1.0), 'mid_w': (jax.random.normal(ks[9], (H * dh, 25), jnp.float32) / np.sqrt(25.0)).at[:, -1].add(1.0), 'r_w1': jax.random.normal(ks[10], (D + 14 * H, 2 * (D + 14 * H)), jnp.float32) / np.sqrt(D + 14 * H), 'r_b1': jnp.zeros((2 * (D + 14 * H),), jnp.float32), 'r_w2': jax.random.normal(ks[11], (2 * (D + 14 * H), H * 4), jnp.float32) / np.sqrt(2.0 * (D + 14 * H)), 'r_b2': jnp.zeros((H, 4), jnp.float32).at[:, 2:].set(0.7).reshape(-1), 'mix_w': jnp.ones((H, dh), jnp.float32), 'onorm_w': jnp.ones((dh,), jnp.float32), 'Wo': jax.random.normal(ks[12], (D, D), jnp.float32) * s}
        return inp
    _L1_attn_all = _L1_attn_setup()
    _L1_attn_in = {k: v for k, v in _L1_attn_all.items() if k in ('Wq', 'Wk', 'Wv', 'Wb', 'conv_q_w', 'conv_k_w', 'conv_v_w', 'local_w', 'mid_w', 'r_w1', 'r_b1', 'r_w2', 'r_b2', 'mix_w', 'onorm_w', 'Wo')}
    del _L1_attn_all

    def _L1_xattn_setup():
        import jax, jax.numpy as jnp
        import numpy as np
        D_MODEL = 256
        N_HEADS = 16
        D_K = D_MODEL // N_HEADS
        B, L = (2, 512)

        def _dense_bf16(x, W, b):
            return jnp.matmul(x.astype(jnp.bfloat16), W.astype(jnp.bfloat16)) + b.astype(jnp.bfloat16)

        def _attention(q, k, v, mask):
            Lq, Ls, dk = (q.shape[2], k.shape[2], q.shape[3])
            scale = 1.0 / np.sqrt(dk)
            scores = jnp.einsum('bhqd,bhkd->bhqk', q, k) * scale
            causal = jnp.tril(jnp.ones((Lq, Ls), bool))
            full_mask = causal[None, None] & (mask[:, None, None, :] > 0)
            scores = jnp.where(full_mask, scores, -jnp.inf)
            p = jax.nn.softmax(scores, axis=-1)
            return jnp.einsum('bhqk,bhkd->bhqd', p, v)
        key = jax.random.key(seed)
        ks = jax.random.split(key, 8)
        inp = {'q': jax.random.normal(ks[0], (B, L, D_MODEL), jnp.float32), 'k': jax.random.normal(ks[1], (B, L, D_MODEL), jnp.float32), 'v': jax.random.normal(ks[2], (B, L, D_MODEL), jnp.float32), 'mask': jnp.ones((B, L), jnp.int32), 'Wq': jax.random.normal(ks[3], (D_MODEL, D_MODEL), jnp.float32) * 0.02, 'bq': jnp.zeros((D_MODEL,), jnp.float32), 'Wk': jax.random.normal(ks[4], (D_MODEL, D_MODEL), jnp.float32) * 0.02, 'bk': jnp.zeros((D_MODEL,), jnp.float32), 'Wv': jax.random.normal(ks[5], (D_MODEL, D_MODEL), jnp.float32) * 0.02, 'bv': jnp.zeros((D_MODEL,), jnp.float32), 'Wo': jax.random.normal(ks[6], (D_MODEL, D_MODEL), jnp.float32) * 0.02, 'bo': jnp.zeros((D_MODEL,), jnp.float32)}
        return inp
    _L1_xattn_all = _L1_xattn_setup()
    _L1_xattn_in = {k: v for k, v in _L1_xattn_all.items() if k in ('Wq', 'bq', 'Wk', 'bk', 'Wv', 'bv', 'Wo', 'bo')}
    del _L1_xattn_all

    def _L1_ffn_setup():
        import jax, jax.numpy as jnp
        import numpy as np
        B, S, D, F, E = (2, 512, 256, 1024, 8)
        LN_EPS = 1e-05

        def _layer_norm(x, gamma, beta):
            mu = jnp.mean(x, axis=-1, keepdims=True)
            var = jnp.mean(jnp.square(x - mu), axis=-1, keepdims=True)
            return (x - mu) * jax.lax.rsqrt(var + LN_EPS) * gamma + beta
        key = jax.random.key(seed)
        ks = jax.random.split(key, 8)

        def xavier(k, shape):
            fan_in, fan_out = (shape[-1], shape[-2])
            a = jnp.sqrt(6.0 / (fan_in + fan_out))
            return jax.random.uniform(k, shape, jnp.float32, -a, a)
        return {'tgt': jax.random.normal(ks[0], (B, S, D), jnp.float32), 'Wr': xavier(ks[1], (E, D)), 'br': jnp.zeros((E,), jnp.float32), 'W1': xavier(ks[2], (E, F, D)), 'b1': jnp.zeros((E, F), jnp.float32), 'W2': xavier(ks[3], (E, D, F)), 'b2': jnp.zeros((E, D), jnp.float32), 'gamma': jnp.ones((D,), jnp.float32), 'beta': jnp.zeros((D,), jnp.float32)}
    _L1_ffn_all = _L1_ffn_setup()
    _L1_ffn_in = {k: v for k, v in _L1_ffn_all.items() if k in ('Wr', 'br', 'W1', 'b1', 'W2', 'b2', 'gamma', 'beta')}
    del _L1_ffn_all
    return {'x': x, 'ctx_1024': ctx_1024, 'mask_BxS2_if1': mask_BxS2_if1, 'L0_attn_Wq': _L0_attn_in['Wq'], 'L0_attn_bq': _L0_attn_in['bq'], 'L0_attn_Wkv': _L0_attn_in['Wkv'], 'L0_attn_bkv': _L0_attn_in['bkv'], 'L0_attn_Wo': _L0_attn_in['Wo'], 'L0_attn_bo': _L0_attn_in['bo'], 'L0_xattn_Wq': _L0_xattn_in['Wq'], 'L0_xattn_bq': _L0_xattn_in['bq'], 'L0_xattn_Wk': _L0_xattn_in['Wk'], 'L0_xattn_bk': _L0_xattn_in['bk'], 'L0_xattn_Wv': _L0_xattn_in['Wv'], 'L0_xattn_bv': _L0_xattn_in['bv'], 'L0_xattn_Wo': _L0_xattn_in['Wo'], 'L0_xattn_bo': _L0_xattn_in['bo'], 'L0_ffn_gate_w': _L0_ffn_in['gate_w'], 'L0_ffn_expert_bias': _L0_ffn_in['expert_bias'], 'L0_ffn_w_up': _L0_ffn_in['w_up'], 'L0_ffn_w_down': _L0_ffn_in['w_down'], 'L0_ffn_shared_w_up': _L0_ffn_in['shared_w_up'], 'L0_ffn_shared_w_down': _L0_ffn_in['shared_w_down'], 'L1_attn_Wq': _L1_attn_in['Wq'], 'L1_attn_Wk': _L1_attn_in['Wk'], 'L1_attn_Wv': _L1_attn_in['Wv'], 'L1_attn_Wb': _L1_attn_in['Wb'], 'L1_attn_conv_q_w': _L1_attn_in['conv_q_w'], 'L1_attn_conv_k_w': _L1_attn_in['conv_k_w'], 'L1_attn_conv_v_w': _L1_attn_in['conv_v_w'], 'L1_attn_local_w': _L1_attn_in['local_w'], 'L1_attn_mid_w': _L1_attn_in['mid_w'], 'L1_attn_r_w1': _L1_attn_in['r_w1'], 'L1_attn_r_b1': _L1_attn_in['r_b1'], 'L1_attn_r_w2': _L1_attn_in['r_w2'], 'L1_attn_r_b2': _L1_attn_in['r_b2'], 'L1_attn_mix_w': _L1_attn_in['mix_w'], 'L1_attn_onorm_w': _L1_attn_in['onorm_w'], 'L1_attn_Wo': _L1_attn_in['Wo'], 'L1_xattn_Wq': _L1_xattn_in['Wq'], 'L1_xattn_bq': _L1_xattn_in['bq'], 'L1_xattn_Wk': _L1_xattn_in['Wk'], 'L1_xattn_bk': _L1_xattn_in['bk'], 'L1_xattn_Wv': _L1_xattn_in['Wv'], 'L1_xattn_bv': _L1_xattn_in['bv'], 'L1_xattn_Wo': _L1_xattn_in['Wo'], 'L1_xattn_bo': _L1_xattn_in['bo'], 'L1_ffn_Wr': _L1_ffn_in['Wr'], 'L1_ffn_br': _L1_ffn_in['br'], 'L1_ffn_W1': _L1_ffn_in['W1'], 'L1_ffn_b1': _L1_ffn_in['b1'], 'L1_ffn_W2': _L1_ffn_in['W2'], 'L1_ffn_b2': _L1_ffn_in['b2'], 'L1_ffn_gamma': _L1_ffn_in['gamma'], 'L1_ffn_beta': _L1_ffn_in['beta']}

def reference(x, ctx_1024, mask_BxS2_if1, L0_attn_Wq, L0_attn_bq, L0_attn_Wkv, L0_attn_bkv, L0_attn_Wo, L0_attn_bo, L0_xattn_Wq, L0_xattn_bq, L0_xattn_Wk, L0_xattn_bk, L0_xattn_Wv, L0_xattn_bv, L0_xattn_Wo, L0_xattn_bo, L0_ffn_gate_w, L0_ffn_expert_bias, L0_ffn_w_up, L0_ffn_w_down, L0_ffn_shared_w_up, L0_ffn_shared_w_down, L1_attn_Wq, L1_attn_Wk, L1_attn_Wv, L1_attn_Wb, L1_attn_conv_q_w, L1_attn_conv_k_w, L1_attn_conv_v_w, L1_attn_local_w, L1_attn_mid_w, L1_attn_r_w1, L1_attn_r_b1, L1_attn_r_w2, L1_attn_r_b2, L1_attn_mix_w, L1_attn_onorm_w, L1_attn_Wo, L1_xattn_Wq, L1_xattn_bq, L1_xattn_Wk, L1_xattn_bk, L1_xattn_Wv, L1_xattn_bv, L1_xattn_Wo, L1_xattn_bo, L1_ffn_Wr, L1_ffn_br, L1_ffn_W1, L1_ffn_b1, L1_ffn_W2, L1_ffn_b2, L1_ffn_gamma, L1_ffn_beta):
    import jax
    import jax.numpy as jnp

    def _L0_attn_ref(x, Wq, bq, Wkv, bkv, Wo, bo):
        import jax, jax.numpy as jnp
        import numpy as np
        B, S, E = (2, 1024, 256)
        H, DQK, DV = (16, 64, 64)
        ROPE_BASE = 10000.0

        def _rope(t):
            D = t.shape[-1]
            inv_freq = 1.0 / ROPE_BASE ** (jnp.arange(0, D, 2, dtype=jnp.float32) / D)
            pos = jnp.arange(t.shape[2], dtype=jnp.float32)
            ang = pos[:, None] * inv_freq[None, :]
            cos = jnp.cos(ang)[None, None]
            sin = jnp.sin(ang)[None, None]
            t1, t2 = (t[..., :D // 2], t[..., D // 2:])
            return jnp.concatenate([t1 * cos - t2 * sin, t1 * sin + t2 * cos], axis=-1)
        b, s, e = x.shape
        q = x @ Wq + bq
        kv = x @ Wkv + bkv
        k, v = jnp.split(kv, [H * DQK], axis=-1)
        q = _rope(q.reshape(b, s, H, DQK).transpose(0, 2, 1, 3))
        k = _rope(k.reshape(b, s, H, DQK).transpose(0, 2, 1, 3))
        v = v.reshape(b, s, H, DV).transpose(0, 2, 1, 3)
        scores = jnp.einsum('bhqd,bhkd->bhqk', q, k) * (1.0 / np.sqrt(DQK))
        causal = jnp.tril(jnp.ones((s, s), dtype=bool))
        scores = jnp.where(causal[None, None], scores, -jnp.inf)
        probs = jax.nn.softmax(scores, axis=-1)
        out = jnp.einsum('bhqk,bhkd->bhqd', probs, v)
        out = out.transpose(0, 2, 1, 3).reshape(b, s, H * DV)
        return out @ Wo + bo

    def _L0_xattn_ref(query, key_value, Wq, bq, Wk, bk, Wv, bv, Wo, bo):
        import jax, jax.numpy as jnp
        import numpy as np
        D_MODEL = 256
        NUM_HEADS = 16
        HEAD_DIM = D_MODEL // NUM_HEADS
        B, SQ, _ = query.shape
        SKV = key_value.shape[1]
        H, Dh = (NUM_HEADS, HEAD_DIM)
        Q = (query @ Wq.T + bq).reshape(B, SQ, H, Dh).transpose(0, 2, 1, 3)
        K = (key_value @ Wk.T + bk).reshape(B, SKV, H, Dh).transpose(0, 2, 1, 3)
        V = (key_value @ Wv.T + bv).reshape(B, SKV, H, Dh).transpose(0, 2, 1, 3)
        scale = jnp.asarray(np.sqrt(Dh), query.dtype)
        scores = jnp.einsum('bhqd,bhkd->bhqk', Q, K) / scale
        weights = jax.nn.softmax(scores, axis=-1)
        attn = jnp.einsum('bhqk,bhkd->bhqd', weights, V)
        attn = attn.transpose(0, 2, 1, 3).reshape(B, SQ, H * Dh)
        return attn @ Wo.T + bo

    def _L0_ffn_ref(x, gate_w, expert_bias, w_up, w_down, shared_w_up, shared_w_down):
        import jax, jax.numpy as jnp
        import numpy as np
        BS, SLEN, DIM = (1, 512, 256)
        NUM_EXPERTS, TOP_K = (8, 2)
        HID = 352

        def _masked_grouped_mm(x, w, onehot):
            g = jnp.einsum('tk,gnk->tgn', x, w, preferred_element_type=jnp.float32)
            return jnp.einsum('tgn,tg->tn', g, onehot)

        def moe_forward(x, gate_w, expert_bias, w_up, w_down, shared_w_up, shared_w_down):
            bs, slen, dim = x.shape
            xf = x.reshape(-1, dim)
            scores = jax.nn.sigmoid((xf @ gate_w.T).astype(jnp.float32))
            biased = scores + expert_bias
            _, sel = jax.lax.top_k(biased, TOP_K)
            top_scores = jnp.take_along_axis(scores, sel, axis=-1)
            flat_sel = sel.reshape(-1)
            counts = jnp.bincount(flat_sel, length=NUM_EXPERTS)
            order = jnp.argsort(flat_sel, stable=True)
            scores_sorted = top_scores.reshape(-1)[order]
            token_ids = order // TOP_K
            routed_in = (xf[token_ids] * scores_sorted[:, None]).astype(x.dtype)
            seg = jnp.repeat(jnp.arange(NUM_EXPERTS), counts, total_repeat_length=flat_sel.shape[0])
            onehot = jax.nn.one_hot(seg, NUM_EXPERTS, dtype=jnp.float32)
            h = _masked_grouped_mm(routed_in.astype(jnp.bfloat16), w_up.astype(jnp.bfloat16), onehot)
            h = jnp.square(jax.nn.relu(h.astype(jnp.bfloat16)))
            routed_out = _masked_grouped_mm(h.astype(jnp.bfloat16), w_down.astype(jnp.bfloat16), onehot)
            routed_out = routed_out.astype(jnp.bfloat16).astype(x.dtype)
            hs = jnp.square(jax.nn.relu(xf @ shared_w_up.T))
            shared_out = hs @ shared_w_down.T
            combined = jnp.zeros((flat_sel.shape[0], dim), routed_out.dtype).at[order].set(routed_out)
            out = combined.reshape(-1, TOP_K, dim).sum(axis=1) + shared_out
            return out.reshape(bs, slen, dim)
        return moe_forward(x, gate_w, expert_bias, w_up, w_down, shared_w_up, shared_w_down)

    def _L1_attn_ref(hidden_states, Wq, Wk, Wv, Wb, conv_q_w, conv_k_w, conv_v_w, local_w, mid_w, r_w1, r_b1, r_w2, r_b2, mix_w, onorm_w, Wo):
        import jax, jax.numpy as jnp
        import numpy as np
        CHUNK = 32
        FLOOR = 0.01
        EPS_MIX = 1e-05
        EPS_NORM = 1e-05

        def l2norm(x):
            return x / jnp.sqrt(jnp.sum(x * x, -1, keepdims=True) + 1e-12)

        def dw_causal_conv(x, w):
            K = w.shape[-1]
            L = x.shape[1]
            xp = jnp.pad(x, ((0, 0), (K - 1, 0), (0, 0)))
            y = jnp.zeros_like(x)
            for t in range(K):
                y = y + xp[:, t:t + L, :] * w[:, t]
            return y

        def delta_rule_chunkwise(q, k, v, beta):
            b, h, L, dk = q.shape
            dv = v.shape[-1]
            c = CHUNK
            n = L // c
            q = l2norm(q)
            k = l2norm(k)
            v = v * beta[..., None]
            kb = k * beta[..., None]
            rs = lambda x: x.reshape(b, h, n, c, -1)
            qc, kc, vc, kbc = (rs(q), rs(k), rs(v), rs(kb))
            T = -jnp.einsum('bhnid,bhnjd->bhnij', kbc, kc)
            tri_strict = jnp.tril(jnp.ones((c, c), bool), -1)
            T = jnp.where(tri_strict, T, 0.0)
            for i in range(1, c):
                T = T.at[..., i, :i].add(jnp.einsum('bhnj,bhnji->bhni', T[..., i, :], T[..., :, :i]))
            T = T + jnp.eye(c, dtype=T.dtype)
            u = jnp.einsum('bhnij,bhnjd->bhnid', T, vc)
            w = jnp.einsum('bhnij,bhnjd->bhnid', T, kbc)
            mask_incl = jnp.tril(jnp.ones((c, c), bool), 0)

            def step(S, inp):
                qi, ki, ui, wi = inp
                attn = jnp.einsum('bhid,bhjd->bhij', qi, ki)
                attn = jnp.where(mask_incl, attn, 0.0)
                u_i = ui - jnp.einsum('bhik,bhkd->bhid', wi, S)
                o_i = jnp.einsum('bhik,bhkd->bhid', qi, S) + jnp.einsum('bhij,bhjd->bhid', attn, u_i)
                S = S + jnp.einsum('bhci,bhcd->bhid', ki, u_i)
                return (S, o_i)
            S0 = jnp.zeros((b, h, dk, dv), q.dtype)
            xs = tuple((jnp.moveaxis(a, 2, 0) for a in (qc, kc, u, w)))
            S, o = jax.lax.scan(step, S0, xs)
            o = jnp.moveaxis(o, 0, 2).reshape(b, h, L, dv)
            return (o, S)
        B, L, D = hidden_states.shape
        H = mix_w.shape[0]
        dh = mix_w.shape[1]
        q = jax.nn.silu(dw_causal_conv(hidden_states @ Wq, conv_q_w))
        k = jax.nn.silu(dw_causal_conv(hidden_states @ Wk, conv_k_w))
        v = jax.nn.silu(dw_causal_conv(hidden_states @ Wv, conv_v_w))
        q4 = q.reshape(B, L, H, dh)
        k4 = k.reshape(B, L, H, dh)
        v4 = v.reshape(B, L, H, dh)
        beta = jax.nn.sigmoid(hidden_states @ Wb)
        delta_out, _ = delta_rule_chunkwise(jnp.transpose(q4, (0, 2, 1, 3)), jnp.transpose(k4, (0, 2, 1, 3)), jnp.transpose(v4, (0, 2, 1, 3)), jnp.transpose(beta, (0, 2, 1)))
        delta_out = jnp.transpose(delta_out, (0, 2, 1, 3))
        v_direct = v4
        vflat = v4.reshape(B, L, H * dh)
        local_out = dw_causal_conv(vflat, local_w).reshape(B, L, H, dh)
        mid_out = dw_causal_conv(vflat, mid_w).reshape(B, L, H, dh)
        outs = [local_out, mid_out, delta_out, v_direct]
        feats = []
        for o_ in outs:
            feats.append(o_.mean(-1))
            feats.append(jnp.var(o_, -1, ddof=1))
        for i in range(4):
            for j in range(i + 1, 4):
                feats.append((outs[i] * outs[j]).mean(-1))
        router_feat = jnp.concatenate([hidden_states] + feats, axis=-1)
        h1 = jax.nn.silu(router_feat @ r_w1 + r_b1)
        logits = (h1 @ r_w2 + r_b2).reshape(B, L, H, 4)
        p = jax.nn.softmax(logits, -1)
        p = p * (1.0 - 4.0 * FLOOR) + FLOOR
        mixed = sum((p[..., i:i + 1] * outs[i] for i in range(4)))
        rms = jnp.sqrt(jnp.mean(mixed * mixed, -1, keepdims=True) + EPS_MIX)
        mixed = mixed / rms * mix_w
        rms2 = jnp.sqrt(jnp.mean(mixed * mixed, -1, keepdims=True) + EPS_NORM)
        o_n = mixed / rms2 * onorm_w
        return o_n.reshape(B, L, H * dh) @ Wo

    def _L1_xattn_ref(q, k, v, mask, Wq, bq, Wk, bk, Wv, bv, Wo, bo):
        import jax, jax.numpy as jnp
        import numpy as np
        D_MODEL = 256
        N_HEADS = 16
        D_K = D_MODEL // N_HEADS
        B, L = (2, 512)

        def _dense_bf16(x, W, b):
            return jnp.matmul(x.astype(jnp.bfloat16), W.astype(jnp.bfloat16)) + b.astype(jnp.bfloat16)

        def _attention(q, k, v, mask):
            Lq, Ls, dk = (q.shape[2], k.shape[2], q.shape[3])
            scale = 1.0 / np.sqrt(dk)
            scores = jnp.einsum('bhqd,bhkd->bhqk', q, k) * scale
            causal = jnp.tril(jnp.ones((Lq, Ls), bool))
            full_mask = causal[None, None] & (mask[:, None, None, :] > 0)
            scores = jnp.where(full_mask, scores, -jnp.inf)
            p = jax.nn.softmax(scores, axis=-1)
            return jnp.einsum('bhqk,bhkd->bhqd', p, v)
        query = _dense_bf16(q, Wq, bq).astype(jnp.float32)
        key_p = _dense_bf16(k, Wk, bk).astype(jnp.float32)
        val_p = _dense_bf16(v, Wv, bv).astype(jnp.float32)
        Bb, Lt, _ = query.shape
        Ls = key_p.shape[1]
        query = query.reshape(Bb, Lt, N_HEADS, D_K).transpose(0, 2, 1, 3)
        key_p = key_p.reshape(Bb, Ls, N_HEADS, D_K).transpose(0, 2, 1, 3)
        val_p = val_p.reshape(Bb, Ls, N_HEADS, D_K).transpose(0, 2, 1, 3)
        x = _attention(query, key_p, val_p, mask)
        x = x.transpose(0, 2, 1, 3).reshape(Bb, Lt, D_MODEL)
        out = _dense_bf16(x, Wo, bo)
        return out.astype(jnp.float32)

    def _L1_ffn_ref(tgt, Wr, br, W1, b1, W2, b2, gamma, beta):
        import jax, jax.numpy as jnp
        import numpy as np
        B, S, D, F, E = (2, 512, 256, 1024, 8)
        LN_EPS = 1e-05

        def _layer_norm(x, gamma, beta):
            mu = jnp.mean(x, axis=-1, keepdims=True)
            var = jnp.mean(jnp.square(x - mu), axis=-1, keepdims=True)
            return (x - mu) * jax.lax.rsqrt(var + LN_EPS) * gamma + beta
        logits = jnp.einsum('bsd,ed->bse', tgt, Wr) + br
        top_v, top_i = jax.lax.top_k(logits, 2)
        top_w = jax.nn.softmax(top_v, axis=-1)
        n_exp = logits.shape[-1]
        router_w = jnp.sum(jax.nn.one_hot(top_i, n_exp, dtype=top_w.dtype) * top_w[..., None], axis=-2)
        h = jnp.einsum('bsd,efd->bsef', tgt, W1) + b1
        h = jax.nn.relu(h)
        o = jnp.einsum('bsef,edf->bsed', h, W2) + b2
        tgt2 = jnp.einsum('bsed,bse->bsd', o, router_w)
        return _layer_norm(tgt + tgt2, gamma, beta)
    x = _layernorm(x + _L0_attn_ref(x, L0_attn_Wq, L0_attn_bq, L0_attn_Wkv, L0_attn_bkv, L0_attn_Wo, L0_attn_bo), axis=-1)
    x = _layernorm(x + _L0_xattn_ref(x, ctx_1024, L0_xattn_Wq, L0_xattn_bq, L0_xattn_Wk, L0_xattn_bk, L0_xattn_Wv, L0_xattn_bv, L0_xattn_Wo, L0_xattn_bo), axis=-1)
    x = _layernorm(x + _L0_ffn_ref(x, L0_ffn_gate_w, L0_ffn_expert_bias, L0_ffn_w_up, L0_ffn_w_down, L0_ffn_shared_w_up, L0_ffn_shared_w_down), axis=-1)
    x = _layernorm(x + _L1_attn_ref(x, L1_attn_Wq, L1_attn_Wk, L1_attn_Wv, L1_attn_Wb, L1_attn_conv_q_w, L1_attn_conv_k_w, L1_attn_conv_v_w, L1_attn_local_w, L1_attn_mid_w, L1_attn_r_w1, L1_attn_r_b1, L1_attn_r_w2, L1_attn_r_b2, L1_attn_mix_w, L1_attn_onorm_w, L1_attn_Wo), axis=-1)
    x = _layernorm(x + _L1_xattn_ref(x, ctx_1024, ctx_1024, mask_BxS2_if1, L1_xattn_Wq, L1_xattn_bq, L1_xattn_Wk, L1_xattn_bk, L1_xattn_Wv, L1_xattn_bv, L1_xattn_Wo, L1_xattn_bo), axis=-1)
    x = _layernorm(x + _L1_ffn_ref(x, L1_ffn_Wr, L1_ffn_br, L1_ffn_W1, L1_ffn_b1, L1_ffn_W2, L1_ffn_b2, L1_ffn_gamma, L1_ffn_beta), axis=-1)
    return x

_drawn_inputs = setup_inputs


def setup_inputs(seed=0):
    import zlib

    import numpy as np

    out = dict(_drawn_inputs(seed))
    spreads = {'L0_attn_bq': (0.0, 0.319),
     'L0_attn_bkv': (0.0, 0.1),
     'L0_attn_bo': (0.0, 0.1),
     'L0_xattn_bq': (0.0, 0.1),
     'L0_xattn_bk': (0.0, 0.8),
     'L0_xattn_bv': (0.0, 0.1),
     'L0_xattn_bo': (0.0, 0.1),
     'L0_ffn_expert_bias': (0.0, 0.1),
     'L1_attn_r_b1': (0.0, 0.413),
     'L1_attn_mix_w': (1.0, 0.2),
     'L1_attn_onorm_w': (1.0, 0.2),
     'L1_xattn_bq': (0.0, 0.8),
     'L1_xattn_bk': (0.0, 0.8),
     'L1_xattn_bv': (0.0, 0.1),
     'L1_xattn_bo': (0.0, 0.1),
     'L1_ffn_br': (0.0, 0.1),
     'L1_ffn_b1': (0.0, 0.1),
     'L1_ffn_b2': (0.0, 0.1),
     'L1_ffn_gamma': (1.0, 0.2),
     'L1_ffn_beta': (0.0, 0.1)}
    factors = {'L1_xattn_Wq': 8.0, 'L1_xattn_Wk': 7.334}
    for name, (base, spread) in spreads.items():
        noise = np.random.default_rng([zlib.crc32(name.encode()), seed]).standard_normal(out[name].shape)
        drawn = base * np.exp(spread * noise) if base else spread * noise
        out[name] = jnp.asarray(drawn.astype(out[name].dtype))
    for name, factor in factors.items():
        out[name] = (out[name] * factor).astype(out[name].dtype)
    return out
```

```python
from contextlib import ExitStack

import numpy as np

import concourse.bass as bass
from concourse import mybir

F32 = mybir.dt.float32
BF16 = mybir.dt.bfloat16
I32 = mybir.dt.int32
ALU = mybir.AluOpType
ACT = mybir.ActivationFunctionType
AX = mybir.AxisListType

P = 128
B = 8
SEQ = 256
D = 256
KC = D // P
TB = SEQ // P
LN_EPS = 1e-5
NEG = -1e30


class Signal:

    def __init__(self, core, name, per, unit=1):
        self.sem = core.semaphore(name)
        self.per, self.unit = per, unit

    def start(self, eng):
        eng.sem_inc(self.sem, self.per * self.unit)

    def now(self, i, k):
        return (i + 1) * (self.per * self.unit) + k * self.unit

    def prev(self, i, k):
        return i * (self.per * self.unit) + k * self.unit


def spread(ap, n):
    return ap.unsqueeze(len(ap.shape)).to_broadcast(list(ap.shape) + [n])


class Core:

    def __init__(self, nc, dram, out):
        self.nc, self.dram, self.out = nc, dram, out
        self.block_semaphores = []
        self.PS = nc.alloc_psum_tensor("PS", [P, 8, 512], F32)
        self.ident = nc.alloc_sbuf_tensor("ident", [P, P], F32)
        self.ident16 = nc.alloc_sbuf_tensor("ident16", [P, P], BF16)
        self.minus_half = nc.alloc_sbuf_tensor("minus_half", [P, 16], F32)
        self.eps = nc.alloc_sbuf_tensor("eps", [P, 16], F32)
        self.X = nc.alloc_sbuf_tensor("X", [P, B * TB, D], F32)
        self.XT = nc.alloc_sbuf_tensor("XT", [P, KC, B * SEQ], F32)

        self.norm_signals = {
            name: Signal(self, name, per, unit) for name, per, unit in (
                ("residual_in", 1, 16), ("residual_used", 1, 1), ("var_ready", 1, 1), ("rstd_step", 2, 1),
                ("x_ready", 1, 1), ("transposed", 1, 1), ("xt_ready", 1, 1), ("stored", 2, 16), ("left", 1, 1))}
        self.block_semaphores = []

    def semaphore(self, name):
        self.block_semaphores.append(self.nc.alloc_semaphore(name))
        return self.block_semaphores[-1]

    def end_block(self):
        self.nc.clear_and_free_semaphores(self.block_semaphores)
        self.nc.all_engine_barrier()
        self.block_semaphores = []

    def x_of(self, b):
        return self.X[:, bass.ds(b * TB, TB), :]

    def xt_of(self, b):
        return self.XT[:, :, bass.ds(b * SEQ, SEQ)]


def constants(core):
    nc = core.nc
    loaded = core.semaphore("first_activations_loaded")
    zeroed = core.semaphore("identities_zeroed")
    with nc.Block() as block:
        @block.sync
        def _(sp):
            sp.dma_start(core.X[:], core.dram["x"].rearrange("(n p) d -> p n d", p=P)).then_inc(loaded, 16)
            sp.dma_start(core.XT[:], core.dram["x_t"].rearrange("(c p) n -> p c n", p=P)).then_inc(loaded, 16)
            sp.wait_ge(loaded, 32)

        @block.gpsimd
        def _(pool):
            nc.gpsimd.memset(core.minus_half[:], -0.5)
            nc.gpsimd.memset(core.eps[:], LN_EPS)
            nc.gpsimd.memset(core.ident[:], 0.0).then_inc(zeroed, 1)
            nc.gpsimd.memset(core.ident16[:], 0.0).then_inc(zeroed, 1)
            pool.wait_ge(zeroed, 2)
            for eye in (core.ident, core.ident16):
                nc.gpsimd.affine_select(out=eye[:], in_=eye[:], compare_op=ALU.not_equal, fill=1.0,
                                        base=0, pattern=[[-1, P]], channel_multiplier=1)


class Norm:

    def __init__(self, core, ctx, name, layer, bank, bias=None):
        nc = core.nc
        self.core, self.bank, self.bias = core, bank, bias

        def sb(n, shape, dt=F32):
            return ctx.enter_context(nc.sbuf_tensor(f"{name}_norm_{n}", shape, dt))

        self.x_in = sb("x_in", [P, TB, D])
        self.y = sb("y", [P, TB, D])
        self.x_new = sb("x_new", [P, TB, D])
        self.xt_new = sb("xt_new", [P, KC, SEQ])
        self.stats = sb("stats", [P, TB, 6])
        self.mean_var = sb("mean_var", [P, TB, 2])
        self.rstd = sb("rstd", [P, TB])
        self.layer = layer
        s = core.norm_signals
        self.residual_in, self.residual_used, self.var_ready = s["residual_in"], s["residual_used"], s["var_ready"]
        self.rstd_step, self.x_ready, self.transposed = s["rstd_step"], s["x_ready"], s["transposed"]
        self.xt_ready, self.stored, self.left = s["xt_ready"], s["stored"], s["left"]

    def turn(self, b):
        return b + self.layer * B

    def start(self, eng, *signals):
        if self.layer == 0:
            for s in signals:
                s.start(eng)

    def start_sync(self, sp):
        self.start(sp, self.residual_in, self.stored, self.left)

    def load(self, sp, b):
        sp.wait_ge(self.residual_used.sem, self.residual_used.prev(self.turn(b), 1))
        sp.dma_start(self.x_in[:], self.core.x_of(b)).then_inc(self.residual_in.sem, 16)

    def store(self, sp, b, last=False):
        sp.wait_ge(self.x_ready.sem, self.x_ready.now(self.turn(b), 1))
        if last:
            for t in range(TB):
                sp.dma_start(self.core.out[bass.ds(b * SEQ + t * P, P), :],
                             self.x_new[:, t, :]).then_inc(self.stored.sem, 16)
        else:
            sp.dma_start(self.core.x_of(b), self.x_new[:]).then_inc(self.stored.sem, 16)
            sp.wait_ge(self.xt_ready.sem, self.xt_ready.now(self.turn(b), 1))
            sp.dma_start(self.core.xt_of(b), self.xt_new[:]).then_inc(self.stored.sem, 16)
        sp.wait_ge(self.stored.sem, self.stored.now(self.turn(b), 2))
        sp.sem_inc(self.left.sem, 1)

    def start_vector(self, dve):
        self.start(dve, self.residual_used, self.var_ready, self.x_ready)

    def vector(self, dve, b, out_ready, source=None):
        nc = self.core.nc
        if source is None:
            source = self.core.PS[:, self.bank, :].rearrange("p (t d) -> p t d", t=TB)
        dve.wait_ge(self.residual_in.sem, self.residual_in.now(self.turn(b), 1))
        dve.wait_ge(*out_ready)
        nc.vector.tensor_tensor(self.y[:], source, self.x_in[:], ALU.add).then_inc(self.residual_used.sem, 1)
        dve.drain()
        if self.bias is not None:
            nc.vector.tensor_tensor(self.y[:], self.y[:], self.bias[:, :].unsqueeze(1).to_broadcast([P, TB, D]),
                                    ALU.add)
            dve.drain()
        for t in range(TB):
            nc.vector.bn_stats(self.stats[:, t, :], self.y[:, t, :])
        dve.drain()
        for t in range(TB):
            nc.vector.bn_aggr(self.mean_var[:, t, :], self.stats[:, t, :])
        dve.drain()
        dve.sem_inc(self.var_ready.sem, 1)
        dve.wait_ge(self.rstd_step.sem, self.rstd_step.now(self.turn(b), 2))
        dve.wait_ge(self.left.sem, self.left.prev(self.turn(b), 1))
        for t in range(TB):
            nc.vector.tensor_scalar(self.x_new[:, t, :], self.y[:, t, :], self.mean_var[:, t, 0:1],
                                    self.rstd[:, t:t + 1], ALU.subtract, ALU.mult)
        dve.drain()
        dve.sem_inc(self.x_ready.sem, 1)

    def start_gpsimd(self, pool):
        self.start(pool, self.rstd_step)

    def gpsimd(self, pool, b):
        nc = self.core.nc
        pool.wait_ge(self.var_ready.sem, self.var_ready.now(self.turn(b), 1))
        nc.gpsimd.tensor_tensor(self.rstd[:], self.mean_var[:, :, 1], self.core.eps[:, 0:TB],
                                ALU.add).then_inc(self.rstd_step.sem, 1)
        pool.wait_ge(self.rstd_step.sem, self.rstd_step.now(self.turn(b), 1))
        nc.gpsimd.tensor_tensor(self.rstd[:], self.rstd[:], self.core.minus_half[:, 0:TB],
                                ALU.pow).then_inc(self.rstd_step.sem, 1)

    def start_tensor(self, pe):
        self.start(pe, self.transposed)

    def tensor(self, pe, b):
        nc = self.core.nc
        pe.wait_ge(self.x_ready.sem, self.x_ready.now(self.turn(b), 1))
        for c in range(KC):
            for t in range(TB):
                last = nc.tensor.transpose(self.core.PS[:, self.bank, (c * TB + t) * P:(c * TB + t + 1) * P],
                                           self.x_new[:, t, c * P:(c + 1) * P], self.core.ident[:])
        last.then_inc(self.transposed.sem, 1)

    def start_scalar(self, act):
        self.start(act, self.xt_ready)

    def scalar(self, act, b):
        nc = self.core.nc
        act.wait_ge(self.transposed.sem, self.transposed.now(self.turn(b), 1))
        act.wait_ge(self.left.sem, self.left.prev(self.turn(b), 1))
        nc.scalar.activation(self.xt_new[:].rearrange("p c n -> p (c n)"), self.core.PS[:, self.bank, :],
                             ACT.Copy).then_inc(self.xt_ready.sem, 1)


def block_self_attention(core):
    H, DH, G = 16, 64, 4
    NG = H // G
    HD = H * DH
    nc, PS, dram = core.nc, core.PS, core.dram
    with ExitStack() as ctx:
        def sb(n, shape, dt=F32):
            return ctx.enter_context(nc.sbuf_tensor(f"sa_{n}", shape, dt))

        wqk = sb("wqk", [P, KC, NG, 4, P])
        wv = sb("wv", [P, KC, HD])
        wo = sb("wo", [P, HD // P, D])
        bqk = sb("bqk", [P, NG, 4])
        bv = sb("bv", [P, HD])
        bo = sb("bo", [P, D])
        cos = sb("cos", [P, 2, 2, SEQ])
        sin = sb("sin", [P, 2, 2, SEQ])
        mask_qk = sb("mask_qk", [P, P], BF16)
        mask_kq = sb("mask_kq", [P, P], BF16)
        sel = sb("sel", [P, G, P])
        xt = sb("xt", [P, KC, SEQ])
        v = sb("v", [P, TB, H, DH + 1])
        raw = sb("raw", [P, 2, 2, SEQ])
        rot1 = sb("rot1", [P, 2, 2, SEQ])
        rot2 = sb("rot2", [P, 2, 2, SEQ])
        qk = sb("qk", [P, 2, 4, SEQ])
        neg_max = sb("neg_max", [P, 2, TB, G])
        max_t = sb("max_t", [P, SEQ])
        probs = sb("probs", [P, 2, G, 384])
        rden = sb("rden", [P, TB, G])
        o = sb("o", [P, TB, G * DH])
        ot = sb("ot", [P, HD // P, SEQ])
        norm = Norm(core, ctx, "sa", 0, 4, bias=bo)

        weights_in = core.semaphore("sa_weights_in")
        consts = core.semaphore("sa_constants_ready")
        xt_in = Signal(core, "sa_xt_in", 1, 16)
        v_done = Signal(core, "sa_v_projected", 4)
        v_ready = Signal(core, "sa_v_ready", 4)
        qk_done = Signal(core, "sa_qk_projected", NG)
        raw_ready = Signal(core, "sa_raw_ready", NG)
        raw_used = Signal(core, "sa_raw_used", NG)
        qk_ready = Signal(core, "sa_qk_rotated", NG)
        s_done = Signal(core, "sa_scores_for_max", NG)
        max_ready = Signal(core, "sa_max_ready", NG)
        maxt_done = Signal(core, "sa_max_transposed", NG)
        maxt_ready = Signal(core, "sa_max_row_ready", NG)
        st_done = Signal(core, "sa_scores_ready", NG)
        probs_ready = Signal(core, "sa_probs_ready", NG)
        o_done = Signal(core, "sa_o_done", NG)
        o_ready = Signal(core, "sa_o_ready", NG)
        ot_done = Signal(core, "sa_o_transposed", NG)
        ot_ready = Signal(core, "sa_ot_ready", NG)
        out_done = Signal(core, "sa_out_done", 1)

        with nc.Block() as block:
            @block.sync
            def _(sp):
                for dst, name in ((wqk, "sa_wqk"), (wv, "sa_wv"), (wo, "sa_wo"), (bqk, "sa_bqk"),
                                  (cos, "cos"), (sin, "sin")):
                    sp.dma_start(dst[:], dram[name]).then_inc(weights_in, 16)
                sp.dma_start(bv[:], dram["sa_bv"].partition_broadcast(P)).then_inc(weights_in, 16)
                sp.dma_start(bo[:], dram["sa_bo"].partition_broadcast(P)).then_inc(weights_in, 16)
                xt_in.start(sp)
                norm.start_sync(sp)
                with sp.Fori(0, B) as b:
                    sp.wait_ge(v_done.sem, v_done.prev(b, 4))
                    sp.wait_ge(qk_done.sem, qk_done.prev(b, NG))
                    sp.dma_start(xt[:], core.xt_of(b)).then_inc(xt_in.sem, 16)
                    norm.load(sp, b)
                    norm.store(sp, b)

            @block.gpsimd
            def _(pool):
                nc.gpsimd.memset(mask_qk[:], 0.0).then_inc(consts, 1)
                nc.gpsimd.memset(mask_kq[:], 0.0).then_inc(consts, 1)
                nc.gpsimd.memset(sel[:], 0.0).then_inc(consts, 1)
                nc.gpsimd.memset(max_t[:], 0.0).then_inc(consts, 1)
                nc.gpsimd.memset(v[:, :, :, DH:DH + 1], 1.0).then_inc(consts, 1)
                pool.wait_ge(consts, 5)
                nc.gpsimd.affine_select(out=mask_qk[:], in_=mask_qk[:], compare_op=ALU.is_ge, fill=NEG,
                                        base=0, pattern=[[-1, P]], channel_multiplier=1).then_inc(consts, 1)
                nc.gpsimd.affine_select(out=mask_kq[:], in_=mask_kq[:], compare_op=ALU.is_ge, fill=NEG,
                                        base=0, pattern=[[1, P]], channel_multiplier=-1).then_inc(consts, 1)
                nc.gpsimd.affine_select(out=sel[:], in_=sel[:], compare_op=ALU.not_equal, fill=1.0,
                                        base=0, pattern=[[-1, G], [0, P]], channel_multiplier=1).then_inc(consts, 1)
                norm.start_gpsimd(pool)
                with pool.Fori(0, B) as b:
                    norm.gpsimd(pool, b)

            @block.scalar
            def _(act):
                act.wait_ge(weights_in, 128)
                act.wait_ge(consts, 8)
                for s in (raw_ready, maxt_ready, probs_ready, ot_ready):
                    s.start(act)
                norm.start_scalar(act)
                with act.Fori(0, B) as b:
                    def evacuate_qk(g):
                        act.wait_ge(qk_done.sem, qk_done.now(b, g + 1))
                        act.wait_ge(raw_used.sem, raw_used.prev(b, NG) if g == 0 else raw_used.now(b, g))
                        for n in range(4):
                            last = nc.scalar.activation(raw[:, n // 2, n % 2, :],
                                                        PS[:, 4 + n // 2, (n % 2) * SEQ:(n % 2 + 1) * SEQ],
                                                        ACT.Identity, bias=bqk[:, g, n:n + 1])
                        act.drain()
                        act.sem_inc(raw_ready.sem, 1)

                    evacuate_qk(0)
                    for g in range(NG):
                        if g + 1 < NG:
                            evacuate_qk(g + 1)
                        act.wait_ge(maxt_done.sem, maxt_done.now(b, g + 1))
                        nc.scalar.activation(max_t[0:G, :], PS[0:G, 7, 0:SEQ], ACT.Copy).then_inc(maxt_ready.sem, 1)
                        act.wait_ge(st_done.sem, st_done.now(b, g + 1))
                        if g >= 2:
                            act.wait_ge(o_done.sem, o_done.now(b, g - 1))
                        else:
                            act.wait_ge(o_done.sem, o_done.prev(b, NG + g - 1))
                        nc.scalar.activation(probs[:, g % 2, :, :], PS[:, 0:G, 0:384], ACT.Exp)\
                            .then_inc(probs_ready.sem, 1)
                        act.wait_ge(ot_done.sem, ot_done.now(b, g + 1))
                        if g == 0:
                            act.wait_ge(out_done.sem, out_done.prev(b, 1))
                        nc.scalar.activation(ot[:, 2 * g:2 * g + 2, :], PS[:, 7, :].rearrange("p (c n) -> p c n", c=2),
                                             ACT.Copy).then_inc(ot_ready.sem, 1)
                    norm.scalar(act, b)

            @block.vector
            def _(dve):
                dve.wait_ge(weights_in, 128)
                dve.wait_ge(consts, 8)
                for s in (v_ready, raw_used, qk_ready, max_ready, o_ready):
                    s.start(dve)
                norm.start_vector(dve)
                with dve.Fori(0, B) as b:
                    dve.wait_ge(o_done.sem, o_done.prev(b, NG))
                    for n in range(4):
                        t, h8 = n // 2, (n % 2) * 8
                        dve.wait_ge(v_done.sem, v_done.now(b, n + 1))
                        nc.vector.tensor_tensor(v[:, t, h8:h8 + 8, 0:DH],
                                                PS[:, 6 + n % 2, :].rearrange("p (h d) -> p h d", d=DH),
                                                bv[:, h8 * DH:(h8 + 8) * DH].rearrange("p (h d) -> p h d", d=DH),
                                                ALU.add).then_inc(v_ready.sem, 1)

                    def rotate(g):
                        dve.wait_ge(raw_ready.sem, raw_ready.now(b, g + 1))
                        nc.vector.tensor_tensor(rot1[:], raw[:], cos[:], ALU.mult)
                        for half in range(2):
                            nc.vector.tensor_tensor(rot2[:, :, half, :], raw[:, :, 1 - half, :],
                                                    sin[:, :, half, :], ALU.mult)
                        dve.drain()
                        dve.sem_inc(raw_used.sem, 1)
                        if g >= 2:
                            dve.wait_ge(st_done.sem, st_done.now(b, g - 1))
                        else:
                            dve.wait_ge(st_done.sem, st_done.prev(b, NG + g - 1))
                        nc.vector.tensor_tensor(qk[:, g % 2, :, :].rearrange("p (a h) n -> p a h n", h=2), rot1[:],
                                                rot2[:], ALU.add).then_inc(qk_ready.sem, 1)

                    rotate(0)
                    for g in range(NG):
                        if g + 1 < NG:
                            rotate(g + 1)
                        dve.wait_ge(s_done.sem, s_done.now(b, g + 1))
                        nc.vector.tensor_reduce(neg_max[:, g % 2, 0, :], PS[:, 0:G, 0:P], AX.X, ALU.max, negate=True)
                        nc.vector.tensor_reduce(neg_max[:, g % 2, 1, :], PS[:, 0:G, P:384], AX.X, ALU.max, negate=True)
                        dve.drain()
                        dve.sem_inc(max_ready.sem, 1)
                        dve.wait_ge(o_done.sem, o_done.now(b, g + 1))
                        for t in range(TB):
                            nc.vector.reciprocal(rden[:, t, :],
                                                 PS[:, 6 + t, 0:G * 65].rearrange("p (h d) -> p h d", d=65)[:, :, DH])
                        dve.drain()
                        if g:
                            dve.wait_ge(ot_done.sem, ot_done.now(b, g))
                        else:
                            dve.wait_ge(ot_done.sem, ot_done.prev(b, NG))
                        for t in range(TB):
                            nc.vector.tensor_tensor(o[:, t, :].rearrange("p (h d) -> p h d", d=DH),
                                                    PS[:, 6 + t, 0:G * 65].rearrange("p (h d) -> p h d", d=65)[:, :, 0:DH],
                                                    spread(rden[:, t, :], DH), ALU.mult)
                        dve.drain()
                        dve.sem_inc(o_ready.sem, 1)
                    norm.vector(dve, b, (out_done.sem, out_done.now(b, 1)))

            @block.tensor
            def _(pe):
                pe.wait_ge(weights_in, 128)
                pe.wait_ge(consts, 8)
                for s in (v_done, qk_done, s_done, maxt_done, st_done, o_done, ot_done, out_done):
                    s.start(pe)
                norm.start_tensor(pe)
                mm = nc.tensor.matmul
                with pe.Fori(0, B) as b:
                    pe.wait_ge(xt_in.sem, xt_in.now(b, 1))
                    for n in range(4):
                        t, half = n // 2, n % 2
                        if n >= 2:
                            pe.wait_ge(v_ready.sem, v_ready.now(b, n - 1))
                        else:
                            pe.wait_ge(o_ready.sem, o_ready.prev(b, NG))
                            pe.wait_ge(ot_ready.sem, ot_ready.prev(b, NG))
                        for k in range(KC):
                            last = mm(PS[:, 6 + half, :], xt[:, k, t * P:(t + 1) * P],
                                      wv[:, k, half * 512:(half + 1) * 512], start=k == 0, stop=k == KC - 1)
                        last.then_inc(v_done.sem, 1)

                    def project(g):
                        if g:
                            pe.wait_ge(raw_ready.sem, raw_ready.now(b, g))
                        else:
                            pe.wait_ge(norm.xt_ready.sem, norm.xt_ready.prev(norm.turn(b), 1))
                        for n in range(4):
                            for k in range(KC):
                                last = mm(PS[:, 4 + n // 2, (n % 2) * SEQ:(n % 2 + 1) * SEQ], wqk[:, k, g, n, :],
                                          xt[:, k, :], start=k == 0, stop=k == KC - 1)
                        last.then_inc(qk_done.sem, 1)

                    project(0)
                    for g in range(NG):
                        rows = [slice(32 * j, 32 * j + 32) for j in range(G)]
                        q = [qk[:, g % 2, i, :] for i in range(2)]
                        k_ = [qk[:, g % 2, 2 + i, :] for i in range(2)]
                        pe.wait_ge(qk_ready.sem, qk_ready.now(b, g + 1))
                        if g:
                            pe.wait_ge(probs_ready.sem, probs_ready.now(b, g))
                        else:
                            pe.wait_ge(probs_ready.sem, probs_ready.prev(b, NG))
                        for i in range(2):
                            for j, r in enumerate(rows):
                                mm(PS[:, j, 0:P], q[i][r, 0:P], k_[i][r, 0:P], start=i == 0, stop=False,
                                   skip_group_check=True)
                        for i in range(2):
                            for j, r in enumerate(rows):
                                mm(PS[:, j, P:384], q[i][r, P:SEQ], k_[i][r, :], start=False, stop=False,
                                   skip_group_check=True)
                        for j in range(G):
                            mm(PS[:, j, 0:P], core.ident16[:], mask_qk[:], start=False, stop=True,
                               skip_group_check=True)
                            last = mm(PS[:, j, SEQ:384], core.ident16[:], mask_qk[:], start=False, stop=True,
                                      skip_group_check=True)
                        last.then_inc(s_done.sem, 1)
                        if g + 1 < NG:
                            project(g + 1)
                        pe.wait_ge(max_ready.sem, max_ready.now(b, g + 1))
                        if g:
                            pe.wait_ge(ot_ready.sem, ot_ready.now(b, g))
                        else:
                            pe.wait_ge(v_ready.sem, v_ready.now(b, 4))
                        for t in range(TB):
                            last = nc.tensor.transpose(PS[0:G, 7, t * P:(t + 1) * P], neg_max[:, g % 2, t, :],
                                                       core.ident[:])
                        last.then_inc(maxt_done.sem, 1)
                        for i in range(2):
                            for j, r in enumerate(rows):
                                mm(PS[:, j, 0:SEQ], k_[i][r, 0:P], q[i][r, :], start=i == 0, stop=False,
                                   skip_group_check=True)
                        for i in range(2):
                            for j, r in enumerate(rows):
                                mm(PS[:, j, SEQ:384], k_[i][r, P:SEQ], q[i][r, P:SEQ], start=False, stop=False,
                                   skip_group_check=True)
                        pe.wait_ge(maxt_ready.sem, maxt_ready.now(b, g + 1))
                        for j in range(G):
                            mm(PS[:, j, 0:SEQ], sel[:, j, :], max_t[:, :], start=False, stop=False,
                               skip_group_check=True)
                            mm(PS[:, j, SEQ:384], sel[:, j, :], max_t[:, P:SEQ], start=False, stop=False,
                               skip_group_check=True)
                            mm(PS[:, j, 0:P], core.ident16[:], mask_kq[:], start=False, stop=True,
                               skip_group_check=True)
                            last = mm(PS[:, j, SEQ:384], core.ident16[:], mask_kq[:], start=False, stop=True,
                                      skip_group_check=True)
                        last.then_inc(st_done.sem, 1)
                        pe.wait_ge(probs_ready.sem, probs_ready.now(b, g + 1))
                        for t in range(TB):
                            for j in range(G):
                                if t == 0:
                                    parts = [(0, 0)]
                                else:
                                    parts = [(P, 0), (SEQ, 1)]
                                for m, (col, kt) in enumerate(parts):
                                    last = mm(PS[:, 6 + t, j * 65:(j + 1) * 65], probs[:, g % 2, j, col:col + P],
                                              v[:, kt, g * G + j, :], start=m == 0, stop=m == len(parts) - 1)
                        last.then_inc(o_done.sem, 1)
                        pe.wait_ge(o_ready.sem, o_ready.now(b, g + 1))
                        for c in range(2):
                            for t in range(TB):
                                last = nc.tensor.transpose(PS[:, 7, (c * TB + t) * P:(c * TB + t + 1) * P],
                                                           o[:, t, c * P:(c + 1) * P], core.ident[:])
                        last.then_inc(ot_done.sem, 1)
                    pe.wait_ge(ot_ready.sem, ot_ready.now(b, NG))
                    for t in range(TB):
                        for c in range(HD // P):
                            last = mm(PS[:, 4, t * D:(t + 1) * D], ot[:, c, t * P:(t + 1) * P], wo[:, c, :],
                                      start=c == 0, stop=c == HD // P - 1)
                    last.then_inc(out_done.sem, 1)
                    norm.tensor(pe, b)


def cross_attention(core, name, half, dram_name):
    H, DH, G, CTX = 16, 16, 4, 77
    NG = H // G
    WIDE = DH + 1
    nc, PS, dram = core.nc, core.PS, core.dram
    PD = BF16 if half else F32
    with ExitStack() as ctx:
        def sb(n, shape, dt=F32):
            return ctx.enter_context(nc.sbuf_tensor(f"{name}_{n}", shape, dt))

        def sig(n, per, unit=1):
            return Signal(core, f"{name}_{n}", per, unit)

        shapes = {"wq": [P, KC, NG, P], "wk": [P, KC, NG, P], "wv": [P, KC, D], "wo": [P, KC, D]}
        w32 = {n: sb(n, s) for n, s in shapes.items()}
        w = {n: sb(n + "16", s, BF16) for n, s in shapes.items()} if half else w32
        bias_shapes = {"bq": [P, NG], "bk": [P, NG], "bv": [P, D], "bo": [P, D]}
        b32 = {n: sb(n, s) for n, s in bias_shapes.items()}
        b16 = {n: sb(n + "16", s, BF16) for n, s in bias_shapes.items()} if half else None
        sel = sb("sel", [P, H, CTX])
        xt_in_tile = sb("xt", [P, KC, SEQ])
        ct_in_tile = sb("ct", [P, KC, CTX])
        xt = sb("xt16", [P, KC, SEQ], BF16) if half else xt_in_tile
        ct = sb("ct16", [P, KC, CTX], BF16) if half else ct_in_tile
        q = sb("q", [P, NG, SEQ], PD)
        k = sb("k", [P, NG, CTX], PD)
        v = sb("v", [P, H, WIDE])
        neg_max = sb("neg_max", [P, TB, H])
        max_t = sb("max_t", [P, SEQ])
        probs = sb("probs", [P, G, NG, SEQ])
        rden = sb("rden", [P, TB, H])
        o = sb("o", [P, TB, D])
        ot = sb("ot", [P, KC, SEQ], PD)
        if half:
            q_round = sb("q_round", [P, NG, SEQ], BF16)
            k_round = sb("k_round", [P, NG, CTX], BF16)
            v_round = sb("v_round", [P, D], BF16)
            v16 = sb("v16", [P, D], BF16)
            out_round = sb("out_round", [P, TB, D], BF16)
            out16 = sb("out16", [P, TB, D], BF16)
            causal_qk = sb("causal_qk", [P, CTX])
            causal_kq = sb("causal_kq", [P, SEQ])
            keys_row = sb("keys_row", [P, CTX], I32)
            keys_col = sb("keys_col", [P, 1], I32)
            keymask_row = sb("keymask_row", [P, CTX])
            keymask_col = sb("keymask_col", [P, 1])
            mask_qk = sb("mask_qk", [P, TB, CTX], BF16)
            mask_kq = sb("mask_kq", [P, SEQ], BF16)
        norm = Norm(core, ctx, name, 4 if half else 1, 3, bias=None if half else b32["bo"])

        weights_in = core.semaphore(f"{name}_weights_in")
        n_weights = len(w32) + len(b32)
        consts = core.semaphore(f"{name}_constants_ready")
        n_consts = 10 if half else 4
        inputs_in = sig("inputs_in", 4 if half else 2, 16)
        inputs_ready = sig("inputs_ready", 1)
        qkv_done = sig("qkv_projected", 1)
        rounded = sig("projections_rounded", 1)
        qkv_ready = sig("qkv_ready", 1)
        s_done = sig("scores_for_max", TB)
        max_ready = sig("max_ready", 1)
        maxt_done = sig("max_transposed", 1)
        maxt_ready = sig("max_rows_ready", 1)
        st_done = sig("scores_ready", 2)
        probs_ready = sig("probs_ready", 2)
        o_done = sig("o_done", 1)
        o_ready = sig("o_ready", 1)
        ot_done = sig("o_transposed", 1)
        ot_ready = sig("ot_ready", 1)
        out_done = sig("out_done", 1)
        if half:
            out_rounded = sig("out_rounded", 1)

        def q_banks():
            return PS[:, 4:6, :].rearrange("p a (g n) -> p (a g) n", n=SEQ)

        def k_bank():
            return PS[:, 6, 0:NG * CTX].rearrange("p (g n) -> p g n", n=CTX)

        with nc.Block() as block:
            @block.sync
            def _(sp):
                for n in ("wq", "wk", "wv", "wo", "bq", "bk"):
                    sp.dma_start({**w32, **b32}[n][:], dram[f"{dram_name}_{n}"]).then_inc(weights_in, 16)
                for n in ("bv", "bo"):
                    sp.dma_start(b32[n][:], dram[f"{dram_name}_{n}"].partition_broadcast(P)).then_inc(weights_in, 16)
                inputs_in.start(sp)
                norm.start_sync(sp)
                with sp.Fori(0, B) as b:
                    if half:
                        sp.wait_ge(qkv_ready.sem, qkv_ready.prev(b, 1))
                        sp.dma_start(keys_row[:], dram["key_mask"][bass.ds(b, 1), :]
                                     .rearrange("a n -> (a n)").partition_broadcast(P)).then_inc(inputs_in.sem, 16)
                        sp.dma_start(keys_col[0:CTX, :], dram["key_mask"][bass.ds(b, 1), :]
                                     .rearrange("a n -> n a")).then_inc(inputs_in.sem, 16)
                    sp.wait_ge(qkv_done.sem, qkv_done.prev(b, 1))
                    sp.dma_start(xt_in_tile[:], core.xt_of(b)).then_inc(inputs_in.sem, 16)
                    sp.dma_start(ct_in_tile[:], dram["ctx_t"][:, :, bass.ds(b * CTX, CTX)]).then_inc(inputs_in.sem, 16)
                    norm.load(sp, b)
                    norm.store(sp, b)

            @block.gpsimd
            def _(pool):
                nc.gpsimd.memset(sel[:], 0.0).then_inc(consts, 1)
                nc.gpsimd.memset(max_t[:], 0.0).then_inc(consts, 1)
                nc.gpsimd.memset(v[:, :, DH:WIDE], 1.0).then_inc(consts, 1)
                if half:
                    nc.gpsimd.memset(causal_qk[:], 0.0).then_inc(consts, 1)
                    nc.gpsimd.memset(causal_kq[:], 0.0).then_inc(consts, 1)
                    nc.gpsimd.memset(keymask_col[:], 0.0).then_inc(consts, 1)
                    nc.gpsimd.memset(keys_col[:], 1).then_inc(consts, 1)
                pool.wait_ge(consts, 7 if half else 3)
                nc.gpsimd.affine_select(out=sel[:], in_=sel[:], compare_op=ALU.not_equal, fill=1.0,
                                        base=0, pattern=[[-1, H], [0, CTX]], channel_multiplier=1).then_inc(consts, 1)
                if half:
                    nc.gpsimd.affine_select(out=causal_qk[:], in_=causal_qk[:], compare_op=ALU.is_ge, fill=NEG,
                                            base=0, pattern=[[-1, CTX]], channel_multiplier=1).then_inc(consts, 1)
                    nc.gpsimd.affine_select(out=causal_kq[:], in_=causal_kq[:], compare_op=ALU.is_ge, fill=NEG,
                                            base=0, pattern=[[1, SEQ]], channel_multiplier=-1).then_inc(consts, 1)
                norm.start_gpsimd(pool)
                with pool.Fori(0, B) as b:
                    norm.gpsimd(pool, b)

            @block.scalar
            def _(act):
                act.wait_ge(weights_in, 16 * n_weights)
                act.wait_ge(consts, n_consts)
                for s in (rounded, maxt_ready, probs_ready, ot_ready) + ((out_rounded,) if half else ()):
                    s.start(act)
                norm.start_scalar(act)
                with act.Fori(0, B) as b:
                    if half:
                        act.wait_ge(qkv_done.sem, qkv_done.now(b, 1))
                        nc.scalar.activation(q_round[:], q_banks(), ACT.Copy)
                        nc.scalar.activation(k_round[:], k_bank(), ACT.Copy)
                        nc.scalar.activation(v_round[0:CTX, :], PS[0:CTX, 7, 0:D], ACT.Copy)
                        act.drain()
                        act.sem_inc(rounded.sem, 1)
                    act.wait_ge(maxt_done.sem, maxt_done.now(b, 1))
                    nc.scalar.activation(max_t[0:H, :], PS[0:H, 0, 0:SEQ], ACT.Copy).then_inc(maxt_ready.sem, 1)
                    act.wait_ge(o_done.sem, o_done.prev(b, 1))
                    for pair in range(2):
                        act.wait_ge(st_done.sem, st_done.now(b, pair + 1))
                        nc.scalar.activation(probs[0:CTX, :, 2 * pair:2 * pair + 2, :],
                                             PS[0:CTX, 4 * pair:4 * pair + 4, :].rearrange("p a (g n) -> p a g n", g=2),
                                             ACT.Exp).then_inc(probs_ready.sem, 1)
                    act.wait_ge(ot_done.sem, ot_done.now(b, 1))
                    nc.scalar.activation(ot[:].rearrange("p c n -> p (c n)"), PS[:, 2, :],
                                         ACT.Copy).then_inc(ot_ready.sem, 1)
                    if half:
                        act.wait_ge(out_done.sem, out_done.now(b, 1))
                        nc.scalar.activation(out_round[:].rearrange("p t d -> p (t d)"), PS[:, 3, :],
                                             ACT.Copy).then_inc(out_rounded.sem, 1)
                    norm.scalar(act, b)

            @block.vector
            def _(dve):
                dve.wait_ge(weights_in, 16 * n_weights)
                dve.wait_ge(consts, n_consts)
                if half:
                    for n in w32:
                        nc.vector.tensor_copy(w[n][:], w32[n][:])
                    for n in b32:
                        nc.vector.tensor_copy(b16[n][:], b32[n][:])
                    dve.drain()
                    for n in b32:
                        nc.vector.tensor_copy(b32[n][:], b16[n][:])
                    dve.drain()
                for s in (inputs_ready, qkv_ready, max_ready, o_ready):
                    s.start(dve)
                norm.start_vector(dve)
                with dve.Fori(0, B) as b:
                    dve.wait_ge(inputs_in.sem, inputs_in.now(b, inputs_in.per))
                    if half:
                        nc.vector.tensor_copy(xt[:], xt_in_tile[:])
                        nc.vector.tensor_copy(ct[:], ct_in_tile[:])
                        nc.vector.tensor_scalar(keymask_row[:], keys_row[:], 0.0, NEG, ALU.is_le, ALU.mult)
                        nc.vector.tensor_scalar(keymask_col[0:CTX, :], keys_col[0:CTX, :], 0.0, NEG, ALU.is_le,
                                                ALU.mult)
                        dve.drain()
                        nc.vector.tensor_tensor(mask_qk[:, 0, :], causal_qk[:], keymask_row[:], ALU.add)
                        nc.vector.tensor_copy(mask_qk[:, 1, :], keymask_row[:])
                        nc.vector.tensor_scalar(mask_kq[:], causal_kq[:], keymask_col[:, 0:1], None, ALU.add)
                        dve.drain()
                    dve.sem_inc(inputs_ready.sem, 1)
                    if half:
                        dve.wait_ge(rounded.sem, rounded.now(b, 1))
                        q_from, k_from, v_from, v_to = q_round[:], k_round[:], v_round[0:CTX, :], v16[0:CTX, :]
                        bv_part = b16["bv"][0:CTX, :]
                    else:
                        dve.wait_ge(qkv_done.sem, qkv_done.now(b, 1))
                        q_from, k_from, v_from = q_banks(), k_bank(), PS[0:CTX, 7, 0:D]
                        bv_part = b32["bv"][0:CTX, :]
                    for g in range(NG):
                        nc.vector.tensor_scalar(q[:, g, :], q_from[:, g, :], b32["bq"][:, g:g + 1], DH ** -0.5,
                                                ALU.add, ALU.mult)
                        nc.vector.tensor_scalar(k[:, g, :], k_from[:, g, :], b32["bk"][:, g:g + 1], None, ALU.add)
                    def heads(ap):
                        return ap.rearrange("p (h d) -> p h d", d=DH)

                    dve.wait_ge(o_done.sem, o_done.prev(b, 1))
                    if half:
                        nc.vector.tensor_tensor(v_to, v_from, bv_part, ALU.add)
                        dve.drain()
                        nc.vector.tensor_copy(v[0:CTX, :, 0:DH], heads(v_to))
                    else:
                        nc.vector.tensor_tensor(v[0:CTX, :, 0:DH], heads(v_from), heads(bv_part), ALU.add)
                    dve.drain()
                    dve.sem_inc(qkv_ready.sem, 1)
                    for t in range(TB):
                        dve.wait_ge(s_done.sem, s_done.now(b, t + 1))
                        nc.vector.tensor_reduce(
                            neg_max[:, t, :].rearrange("p (j g) -> p j g", g=NG),
                            PS[:, 4 * t:4 * t + 4, 0:NG * CTX].rearrange("p j (g n) -> p j g n", n=CTX),
                            AX.X, ALU.max, negate=True)
                    dve.drain()
                    dve.sem_inc(max_ready.sem, 1)
                    dve.wait_ge(o_done.sem, o_done.now(b, 1))

                    def o_bank(t):
                        return PS[:, t, 0:H * WIDE].rearrange("p (h d) -> p h d", d=WIDE)

                    for t in range(TB):
                        nc.vector.reciprocal(rden[:, t, :], o_bank(t)[:, :, DH])
                    dve.drain()
                    for t in range(TB):
                        nc.vector.tensor_tensor(heads(o[:, t, :]), o_bank(t)[:, :, 0:DH], spread(rden[:, t, :], DH),
                                                ALU.mult)
                    dve.drain()
                    dve.sem_inc(o_ready.sem, 1)
                    if half:
                        dve.wait_ge(out_rounded.sem, out_rounded.now(b, 1))
                        nc.vector.tensor_tensor(out16[:], out_round[:],
                                                b16["bo"][:, :].unsqueeze(1).to_broadcast([P, TB, D]), ALU.add)
                        dve.drain()
                        norm.vector(dve, b, (out_rounded.sem, out_rounded.now(b, 1)), source=out16[:])
                    else:
                        norm.vector(dve, b, (out_done.sem, out_done.now(b, 1)))

            @block.tensor
            def _(pe):
                pe.wait_ge(weights_in, 16 * n_weights)
                pe.wait_ge(consts, n_consts)
                for s in (qkv_done, s_done, maxt_done, st_done, o_done, ot_done, out_done):
                    s.start(pe)
                norm.start_tensor(pe)
                mm = nc.tensor.matmul
                rows = [slice(32 * j, 32 * j + 32) for j in range(G)]
                with pe.Fori(0, B) as b:
                    pe.wait_ge(inputs_ready.sem, inputs_ready.now(b, 1))
                    pe.wait_ge(probs_ready.sem, probs_ready.prev(b, 2))
                    for g in range(NG):
                        for c in range(KC):
                            mm(q_banks()[:, g, :], w["wq"][:, c, g, :], xt[:, c, :], start=c == 0, stop=c == KC - 1)
                    for g in range(NG):
                        for c in range(KC):
                            mm(k_bank()[:, g, :], w["wk"][:, c, g, :], ct[:, c, :], start=c == 0, stop=c == KC - 1)
                    for c in range(KC):
                        last = mm(PS[0:CTX, 7, 0:D], ct[:, c, :], w["wv"][:, c, :], start=c == 0, stop=c == KC - 1)
                    last.then_inc(qkv_done.sem, 1)
                    pe.wait_ge(qkv_ready.sem, qkv_ready.now(b, 1))
                    pe.wait_ge(norm.xt_ready.sem, norm.xt_ready.prev(norm.turn(b), 1))
                    for t in range(TB):
                        for g in range(NG):
                            for j, r in enumerate(rows):
                                last = mm(PS[:, 4 * t + j, g * CTX:(g + 1) * CTX], q[r, g, t * P:(t + 1) * P],
                                          k[r, g, :], start=g == 0, stop=not half, skip_group_check=True)
                        if half:
                            for j in range(G):
                                for g in range(NG):
                                    last = mm(PS[:, 4 * t + j, g * CTX:(g + 1) * CTX], core.ident16[:],
                                              mask_qk[:, t, :], start=False, stop=True, skip_group_check=True)
                        last.then_inc(s_done.sem, 1)
                    pe.wait_ge(max_ready.sem, max_ready.now(b, 1))
                    for t in range(TB):
                        last = nc.tensor.transpose(PS[0:H, 0, t * P:(t + 1) * P], neg_max[:, t, :], core.ident[:])
                    last.then_inc(maxt_done.sem, 1)
                    pe.wait_ge(maxt_ready.sem, maxt_ready.now(b, 1))
                    for pair in range(2):
                        for gg in range(2):
                            for j, r in enumerate(rows):
                                mm(PS[0:CTX, 4 * pair + j, gg * SEQ:(gg + 1) * SEQ], k[r, 2 * pair + gg, :],
                                   q[r, 2 * pair + gg, :], start=gg == 0, stop=False, skip_group_check=True)
                        for gg in range(2):
                            for j in range(G):
                                to = PS[0:CTX, 4 * pair + j, gg * SEQ:(gg + 1) * SEQ]
                                last = mm(to, sel[:, j * NG + 2 * pair + gg, :], max_t[:], start=False,
                                          stop=not half, skip_group_check=True)
                                if half:
                                    last = mm(to, core.ident16[:, 0:CTX], mask_kq[:], start=False, stop=True,
                                              skip_group_check=True)
                        last.then_inc(st_done.sem, 1)
                    pe.wait_ge(probs_ready.sem, probs_ready.now(b, 2))
                    for t in range(TB):
                        for h in range(H):
                            last = mm(PS[:, t, h * WIDE:(h + 1) * WIDE],
                                      probs[0:CTX, h % G, h // G, t * P:(t + 1) * P], v[0:CTX, h, :],
                                      start=True, stop=True)
                    last.then_inc(o_done.sem, 1)
                    pe.wait_ge(o_ready.sem, o_ready.now(b, 1))
                    for c in range(KC):
                        for t in range(TB):
                            last = nc.tensor.transpose(PS[:, 2, (c * TB + t) * P:(c * TB + t + 1) * P],
                                                       o[:, t, c * P:(c + 1) * P], core.ident[:])
                    last.then_inc(ot_done.sem, 1)
                    pe.wait_ge(ot_ready.sem, ot_ready.now(b, 1))
                    for t in range(TB):
                        for c in range(KC):
                            last = mm(PS[:, 3, t * D:(t + 1) * D], ot[:, c, t * P:(t + 1) * P], w["wo"][:, c, :],
                                      start=c == 0, stop=c == KC - 1)
                    last.then_inc(out_done.sem, 1)
                    norm.tensor(pe, b)


def block_cross_attention_0(core):
    cross_attention(core, "ca", False, "ca")


def block_cross_attention_1(core):
    cross_attention(core, "cb", True, "cb")


def top2(nc, dve, t, scores, iota8, best, index, index_f, chosen):
    nc.vector.max(best[:, t, :], scores[:, t, :])
    dve.drain()
    nc.vector.max_index(index[:, t, :], best[:, t, :], scores[:, t, :])
    dve.drain()
    nc.vector.tensor_copy(index_f[:, t, :], index[:, t, :])
    dve.drain()
    for r in range(2):
        nc.vector.tensor_scalar(chosen[:, t, r, :], iota8[:], index_f[:, t, r:r + 1], None, ALU.is_equal)
    dve.drain()


def block_experts_0(core):
    E, HB = 8, 3
    nc, PS, dram = core.nc, core.PS, core.dram
    with ExitStack() as ctx:
        def sb(n, shape, dt=F32):
            return ctx.enter_context(nc.sbuf_tensor(f"ea_{n}", shape, dt))

        def sig(n, per, unit=1):
            return Signal(core, f"ea_{n}", per, unit)

        up32 = sb("up32", [P, KC, E, HB, P])
        down32 = sb("down32", [P, E, HB, D])
        up = sb("up", [P, KC, E, HB, P], BF16)
        down = sb("down", [P, E, HB, D], BF16)
        shared_up = sb("shared_up", [P, KC, HB, P])
        shared_down = sb("shared_down", [P, HB, D])
        gate = sb("gate", [P, KC, E])
        gate_bias = sb("gate_bias", [P, E])
        iota8 = sb("iota8", [P, E])
        sel = sb("sel", [P, E, P])
        xt = sb("xt", [P, KC, SEQ])
        tanh = sb("tanh", [P, TB, E])
        scores = sb("scores", [P, TB, E])
        biased = sb("biased", [P, TB, E])
        best = sb("best", [P, TB, 8])
        index = sb("index", [P, TB, 8], mybir.dt.uint32)
        index_f = sb("index_f", [P, TB, 8])
        chosen = sb("chosen", [P, TB, 2, E])
        both = sb("both", [P, TB, E])
        weight = sb("weight", [P, TB, E])
        weight_t = sb("weight_t", [P, SEQ])
        scaled = sb("scaled", [P, 2, KC, SEQ], BF16)
        relu = sb("relu", [P, 2, HB, SEQ], BF16)
        hidden = sb("hidden", [P, 2, HB, SEQ], BF16)
        shared_relu = sb("shared_relu", [P, HB, SEQ])
        shared_hidden = sb("shared_hidden", [P, HB, SEQ])
        routed = sb("routed", [P, 2, TB, D], BF16)
        total = sb("total", [P, TB, D])
        summed = sb("summed", [P, TB, D])
        norm = Norm(core, ctx, "ea", 2, 7)

        weights_in = core.semaphore("ea_weights_in")
        consts = core.semaphore("ea_constants_ready")
        xt_in = sig("xt_in", 1, 16)
        gate_done = sig("gate_done", 1)
        tanh_ready = sig("tanh_ready", 1)
        weight_ready = sig("weight_ready", 1)
        weight_turned = sig("weight_turned", 1)
        weight_t_ready = sig("weight_t_ready", 1)
        spread_done = sig("scores_spread", E)
        scaled_ready = sig("scaled_ready", E)
        up_done = sig("up_done", E + 1)
        relu_ready = sig("relu_ready", E + 1)
        hidden_ready = sig("hidden_ready", E + 1)
        down_done = sig("down_done", E)
        routed_ready = sig("routed_ready", E)
        summed_step = sig("summed_step", E - 1)
        shared_done = sig("shared_done", 1)
        total_ready = sig("total_ready", 1)

        def up_banks(e):
            return PS[:, 2 + 2 * (e % 2):4 + 2 * (e % 2), :].rearrange("p a n -> p (a n)")[:, 0:HB * SEQ]\
                .rearrange("p (h n) -> p h n", n=SEQ)

        def tiles(ap):
            return ap.rearrange("p (t d) -> p t d", t=TB)

        with nc.Block() as block:
            @block.sync
            def _(sp):
                for dst, n in ((up32, "ea_up"), (down32, "ea_down"), (shared_up, "ea_shared_up"),
                               (shared_down, "ea_shared_down"), (gate, "ea_gate")):
                    sp.dma_start(dst[:], dram[n]).then_inc(weights_in, 16)
                sp.dma_start(gate_bias[:], dram["ea_gate_bias"].partition_broadcast(P)).then_inc(weights_in, 16)
                xt_in.start(sp)
                norm.start_sync(sp)
                with sp.Fori(0, B) as b:
                    sp.wait_ge(up_done.sem, up_done.prev(b, E + 1))
                    sp.wait_ge(scaled_ready.sem, scaled_ready.prev(b, E))
                    sp.dma_start(xt[:], core.xt_of(b)).then_inc(xt_in.sem, 16)
                    norm.load(sp, b)
                    norm.store(sp, b)

            @block.gpsimd
            def _(pool):
                nc.gpsimd.iota(iota8[:], pattern=[[1, E]], base=0, channel_multiplier=0,
                               allow_small_or_imprecise_dtypes=True).then_inc(consts, 1)
                nc.gpsimd.memset(sel[:], 0.0).then_inc(consts, 1)
                nc.gpsimd.memset(weight_t[:], 0.0).then_inc(consts, 1)
                pool.wait_ge(consts, 3)
                nc.gpsimd.affine_select(out=sel[:], in_=sel[:], compare_op=ALU.not_equal, fill=1.0,
                                        base=0, pattern=[[-1, E], [0, P]], channel_multiplier=1).then_inc(consts, 1)
                summed_step.start(pool)
                norm.start_gpsimd(pool)
                with pool.Fori(0, B) as b:
                    pool.wait_ge(total_ready.sem, total_ready.prev(b, 1))
                    for e in range(1, E):
                        pool.wait_ge(routed_ready.sem, routed_ready.now(b, e + 1))
                        if e > 1:
                            pool.wait_ge(summed_step.sem, summed_step.now(b, e - 1))
                        nc.gpsimd.tensor_tensor(summed[:], summed[:] if e > 1 else routed[:, 0, :, :],
                                                routed[:, e % 2, :, :], ALU.add).then_inc(summed_step.sem, 1)
                    norm.gpsimd(pool, b)

            @block.scalar
            def _(act):
                for s in (tanh_ready, weight_t_ready, relu_ready, routed_ready):
                    s.start(act)
                norm.start_scalar(act)
                with act.Fori(0, B) as b:
                    act.wait_ge(gate_done.sem, gate_done.now(b, 1))
                    act.wait_ge(weight_ready.sem, weight_ready.prev(b, 1))
                    nc.scalar.activation(tanh[:], PS[:, 0, 0:TB * E].rearrange("p (t e) -> p t e", t=TB), ACT.Tanh,
                                         scale=0.5).then_inc(tanh_ready.sem, 1)
                    act.wait_ge(weight_turned.sem, weight_turned.now(b, 1))
                    act.wait_ge(consts, 4)
                    nc.scalar.activation(weight_t[0:E, :], PS[0:E, 0, 0:SEQ], ACT.Copy).then_inc(weight_t_ready.sem, 1)

                    def relu_of(e):
                        act.wait_ge(up_done.sem, up_done.now(b, e + 1))
                        if e == E:
                            act.wait_ge(hidden_ready.sem, hidden_ready.prev(b, E + 1))
                            to = shared_relu[:]
                        else:
                            k = e - 1 if e >= 2 else E - 1 + e
                            act.wait_ge(hidden_ready.sem,
                                        hidden_ready.now(b, k) if e >= 2 else hidden_ready.prev(b, k))
                            to = relu[:, e % 2, :, :]
                        nc.scalar.activation(to, up_banks(e), ACT.Relu).then_inc(relu_ready.sem, 1)

                    relu_of(0)
                    for e in range(E):
                        relu_of(e + 1)
                        act.wait_ge(down_done.sem, down_done.now(b, e + 1))
                        if e >= 2:
                            act.wait_ge(summed_step.sem, summed_step.now(b, max(e - 2, 1)))
                        else:
                            act.wait_ge(summed_step.sem, summed_step.prev(b, E - 2 + e))
                        nc.scalar.activation(routed[:, e % 2, :, :], tiles(PS[:, 6, :]),
                                             ACT.Copy).then_inc(routed_ready.sem, 1)
                    norm.scalar(act, b)

            @block.vector
            def _(dve):
                dve.wait_ge(weights_in, 96)
                dve.wait_ge(consts, 4)
                nc.vector.tensor_copy(up[:], up32[:])
                nc.vector.tensor_copy(down[:], down32[:])
                dve.drain()
                dve.sem_inc(consts, 1)
                for s in (weight_ready, scaled_ready, hidden_ready, total_ready):
                    s.start(dve)
                norm.start_vector(dve)
                with dve.Fori(0, B) as b:
                    dve.wait_ge(tanh_ready.sem, tanh_ready.now(b, 1))
                    nc.vector.tensor_scalar(scores[:], tanh[:], 0.5, 0.5, ALU.mult, ALU.add)
                    dve.drain()
                    nc.vector.tensor_tensor(biased[:], scores[:],
                                            gate_bias[:, :].unsqueeze(1).to_broadcast([P, TB, E]), ALU.add)
                    dve.drain()
                    for t in range(TB):
                        top2(nc, dve, t, biased, iota8, best, index, index_f, chosen)
                    nc.vector.tensor_tensor(both[:], chosen[:, :, 0, :], chosen[:, :, 1, :], ALU.add)
                    dve.drain()
                    nc.vector.tensor_tensor(weight[:], both[:], scores[:], ALU.mult).then_inc(weight_ready.sem, 1)
                    dve.wait_ge(xt_in.sem, xt_in.now(b, 1))

                    def scale(e):
                        dve.wait_ge(spread_done.sem, spread_done.now(b, e + 1))
                        if e >= 2:
                            dve.wait_ge(up_done.sem, up_done.now(b, e - 1))
                        else:
                            dve.wait_ge(up_done.sem, up_done.prev(b, E - 1 + e))
                        nc.vector.tensor_tensor(scaled[:, e % 2, :, :], xt[:],
                                                PS[:, e % 2, 0:SEQ].unsqueeze(1).to_broadcast([P, KC, SEQ]),
                                                ALU.mult).then_inc(scaled_ready.sem, 1)

                    def square(e):
                        dve.wait_ge(relu_ready.sem, relu_ready.now(b, e + 1))
                        if e == E:
                            dve.wait_ge(shared_done.sem, shared_done.prev(b, 1))
                            nc.vector.tensor_tensor(shared_hidden[:], shared_relu[:], shared_relu[:],
                                                    ALU.mult).then_inc(hidden_ready.sem, 1)
                        else:
                            if e >= 2:
                                dve.wait_ge(down_done.sem, down_done.now(b, e - 1))
                            else:
                                dve.wait_ge(down_done.sem, down_done.prev(b, E - 1 + e))
                            nc.vector.tensor_tensor(hidden[:, e % 2, :, :], relu[:, e % 2, :, :],
                                                    relu[:, e % 2, :, :], ALU.mult).then_inc(hidden_ready.sem, 1)

                    scale(0)
                    for e in range(E + 1):
                        if e + 1 < E:
                            scale(e + 1)
                        square(e)
                    dve.wait_ge(summed_step.sem, summed_step.now(b, E - 1))
                    dve.wait_ge(shared_done.sem, shared_done.now(b, 1))
                    nc.vector.tensor_tensor(total[:], tiles(PS[:, 7, :]), summed[:], ALU.add)\
                        .then_inc(total_ready.sem, 1)
                    dve.drain()
                    norm.vector(dve, b, (shared_done.sem, shared_done.now(b, 1)), source=total[:])

            @block.tensor
            def _(pe):
                pe.wait_ge(weights_in, 96)
                pe.wait_ge(consts, 5)
                for s in (gate_done, weight_turned, spread_done, up_done, down_done, shared_done):
                    s.start(pe)
                norm.start_tensor(pe)
                mm = nc.tensor.matmul
                with pe.Fori(0, B) as b:
                    pe.wait_ge(xt_in.sem, xt_in.now(b, 1))
                    pe.wait_ge(scaled_ready.sem, scaled_ready.prev(b, E))
                    for t in range(TB):
                        for c in range(KC):
                            last = mm(PS[:, 0, t * E:(t + 1) * E], xt[:, c, t * P:(t + 1) * P], gate[:, c, :],
                                      start=c == 0, stop=c == KC - 1)
                    last.then_inc(gate_done.sem, 1)

                    def up_of(e):
                        if e >= 2:
                            pe.wait_ge(relu_ready.sem, relu_ready.now(b, e - 1))
                        else:
                            pe.wait_ge(relu_ready.sem, relu_ready.prev(b, E + 1 - e))
                        for h in range(HB):
                            for c in range(KC):
                                if e < E:
                                    last = mm(up_banks(e)[:, h, :], up[:, c, e, h, :], scaled[:, e % 2, c, :],
                                              start=c == 0, stop=c == KC - 1)
                                else:
                                    last = mm(up_banks(e)[:, h, :], shared_up[:, c, h, :], xt[:, c, :],
                                              start=c == 0, stop=c == KC - 1)
                        last.then_inc(up_done.sem, 1)

                    def spread_of(e):
                        if e >= 2:
                            pe.wait_ge(scaled_ready.sem, scaled_ready.now(b, e - 1))
                        mm(PS[:, e % 2, 0:SEQ], sel[:, e, :], weight_t[:], start=True, stop=True)\
                            .then_inc(spread_done.sem, 1)

                    pe.wait_ge(weight_ready.sem, weight_ready.now(b, 1))
                    for t in range(TB):
                        last = nc.tensor.transpose(PS[0:E, 0, t * P:(t + 1) * P], weight[:, t, :], core.ident[:])
                    last.then_inc(weight_turned.sem, 1)
                    pe.wait_ge(weight_t_ready.sem, weight_t_ready.now(b, 1))
                    spread_of(0)
                    spread_of(1)
                    pe.wait_ge(scaled_ready.sem, scaled_ready.now(b, 1))
                    up_of(0)
                    for e in range(E):
                        if e + 2 < E:
                            spread_of(e + 2)
                        if e + 1 < E:
                            pe.wait_ge(scaled_ready.sem, scaled_ready.now(b, e + 2))
                        up_of(e + 1)
                        pe.wait_ge(hidden_ready.sem, hidden_ready.now(b, e + 1))
                        if e:
                            pe.wait_ge(routed_ready.sem, routed_ready.now(b, e))
                        else:
                            pe.wait_ge(routed_ready.sem, routed_ready.prev(b, E))
                        for t in range(TB):
                            for h in range(HB):
                                last = mm(PS[:, 6, t * D:(t + 1) * D], hidden[:, e % 2, h, t * P:(t + 1) * P],
                                          down[:, e, h, :], start=h == 0, stop=h == HB - 1)
                        last.then_inc(down_done.sem, 1)
                    pe.wait_ge(hidden_ready.sem, hidden_ready.now(b, E + 1))
                    pe.wait_ge(norm.xt_ready.sem, norm.xt_ready.prev(norm.turn(b), 1))
                    for t in range(TB):
                        for h in range(HB):
                            last = mm(PS[:, 7, t * D:(t + 1) * D], shared_hidden[:, h, t * P:(t + 1) * P],
                                      shared_down[:, h, :], start=h == 0, stop=h == HB - 1)
                    last.then_inc(shared_done.sem, 1)
                    norm.tensor(pe, b)



MH, MD = 4, 64
CHUNK = 32
NCH = SEQ // CHUNK
LOCAL, MID = 7, 25
CONV = 4
OUTS = ("local", "mid", "delta", "v")


class MixerScratch:

    def __init__(self, nc):
        def dram(name, shape):
            return nc.dram_tensor(name, shape, F32, kind="Internal").ap()

        self.outs = dram("mixer_outs", (len(OUTS), B * SEQ, D))
        self.k = dram("mixer_k", (B, NCH, CHUNK, MH, MD))
        self.qk_t = dram("mixer_qk_t", (2, P, KC, B, NCH, CHUNK))
        self.gram = dram("mixer_gram", (B, TB, P // CHUNK, CHUNK, MH, CHUNK))
        self.beta = dram("mixer_beta", (B, MH, NCH, CHUNK))
        self.solved = dram("mixer_solved", (NCH, MH, CHUNK, B, CHUNK))


def block_mixer_project(core):
    nc, PS, dram = core.nc, core.PS, core.dram
    core.mixer = scratch = MixerScratch(nc)
    PAD = MID - 1
    with ExitStack() as ctx:
        def sb(n, shape, dt=F32):
            return ctx.enter_context(nc.sbuf_tensor(f"mp_{n}", shape, dt))

        def sig(n, per, unit=1):
            return Signal(core, f"mp_{n}", per, unit)

        w = sb("w", [P, KC, 3, KC, P])
        w_beta = sb("w_beta", [P, KC, MH])
        conv_w = sb("conv_w", [P, 3, KC, CONV])
        conv_half = sb("conv_half", [P, 3, KC, CONV])
        local_w = sb("local_w", [P, KC, LOCAL])
        mid_w = sb("mid_w", [P, KC, MID])
        mid_diag = sb("mid_diag", [P, KC, MID, P])
        eps12 = sb("eps12", [P, 16])
        xt = sb("xt", [P, KC, SEQ])
        padded = sb("padded", [P, 3, KC, CONV - 1 + SEQ])
        y = sb("y", [P, 3, KC, SEQ])
        tanh = sb("tanh", [P, 3, KC, SEQ])
        tanh_beta = sb("tanh_beta", [MH, SEQ])
        beta = sb("beta", [MH, SEQ])
        qk = sb("qk", [P, 2, KC, SEQ])
        v_pad = sb("v_pad", [P, KC, PAD + SEQ])
        local_t = sb("local_t", [P, KC, SEQ])
        mid_t = sb("mid_t", [P, KC, SEQ])
        squares = sb("squares", [P, 2 * TB * MH, MD])
        sums = sb("sums", [P, 2 * TB * MH])
        rnorm = sb("rnorm", [P, 2 * TB * MH])
        v_tok = sb("v_tok", [P, TB, D])
        lm_tok = sb("lm_tok", [P, 2, TB, D])
        qk_tok = sb("qk_tok", [P, 2, TB, D])
        qk_t = sb("qk_t", [P, 2, KC, SEQ])
        gram = sb("gram", [P, TB, MH, CHUNK])

        weights_in = core.semaphore("mp_weights_in")
        consts = core.semaphore("mp_constants_ready")
        xt_in = sig("xt_in", 1, 16)
        projected = sig("projected", 1)
        padded_ready = sig("padded_ready", 1)
        conv_ready = sig("conv_ready", 1)
        tanh_ready = sig("tanh_ready", 1)
        silu_ready = sig("silu_ready", 1)
        local_ready = sig("local_ready", 1)
        mid_done = sig("mid_done", 1)
        mid_ready = sig("mid_ready", 1)
        qkv_turned = sig("qkv_turned", 1)
        squares_ready = sig("squares_ready", 1)
        sums_ready = sig("sums_ready", 1)
        rnorm_step = sig("rnorm_step", 2)
        lm_turned = sig("lm_turned", 1)
        lm_ready = sig("lm_ready", 1)
        qk_tok_ready = sig("qk_normed", 1)
        qk_turned = sig("qk_turned", 1)
        qk_t_ready = sig("qk_t_ready", 1)
        gram_done = sig("gram_done", 1)
        gram_ready = sig("gram_ready", 1)
        N_STORES = 3 * TB + TB + 2 + TB + 1
        stored = sig("stored", N_STORES, 16)
        left = sig("results_left", 1)

        with nc.Block() as block:
            @block.sync
            def _(sp):
                for dst, n in ((w, "mp_w"), (w_beta, "mp_w_beta"), (conv_w, "mp_conv_w"), (local_w, "mp_local_w"),
                               (mid_w, "mp_mid_w")):
                    sp.dma_start(dst[:], dram[n]).then_inc(weights_in, 16)
                for s in (xt_in, stored, left):
                    s.start(sp)
                with sp.Fori(0, B) as b:
                    sp.wait_ge(projected.sem, projected.prev(b, 1))
                    sp.dma_start(xt[:], core.xt_of(b)).then_inc(xt_in.sem, 16)
                    sp.wait_ge(squares_ready.sem, squares_ready.now(b, 1))
                    sp.wait_ge(lm_ready.sem, lm_ready.now(b, 1))
                    for t in range(TB):
                        rows = bass.ds(b * SEQ + t * P, P)
                        sp.dma_start(scratch.outs[0, rows, :], lm_tok[:, 0, t, :]).then_inc(stored.sem, 16)
                        sp.dma_start(scratch.outs[1, rows, :], lm_tok[:, 1, t, :]).then_inc(stored.sem, 16)
                        sp.dma_start(scratch.outs[3, rows, :], v_tok[:, t, :]).then_inc(stored.sem, 16)
                    sp.wait_ge(qk_tok_ready.sem, qk_tok_ready.now(b, 1))
                    k_rows = scratch.k.rearrange("b n t h d -> (b n t) (h d)")
                    for t in range(TB):
                        sp.dma_start(k_rows[bass.ds(b * SEQ + t * P, P), :], qk_tok[:, 1, t, :])\
                            .then_inc(stored.sem, 16)
                    sp.dma_start(scratch.beta.rearrange("b h n t -> b h (n t)")[bass.ds(b, 1), :, :]
                                 .rearrange("a h n -> h (a n)"), beta[:]).then_inc(stored.sem, 16)
                    sp.wait_ge(qk_t_ready.sem, qk_t_ready.now(b, 1))
                    for i in range(2):
                        sp.dma_start(scratch.qk_t[i].rearrange("p c b n t -> p c (b n t)")
                                     [:, :, bass.ds(b * SEQ, SEQ)], qk_t[:, i, :, :]).then_inc(stored.sem, 16)
                    sp.wait_ge(gram_ready.sem, gram_ready.now(b, 1))
                    gram_rows = scratch.gram.rearrange("b u c i h j -> (b u c i) (h j)")
                    for t in range(TB):
                        sp.dma_start(gram_rows[bass.ds(b * SEQ + t * P, P), :],
                                     gram[:, t, :, :].rearrange("p h j -> p (h j)")).then_inc(stored.sem, 16)
                    sp.wait_ge(stored.sem, stored.now(b, N_STORES))
                    sp.sem_inc(left.sem, 1)

            @block.gpsimd
            def _(pool):
                nc.gpsimd.memset(eps12[:], 1e-12).then_inc(consts, 1)
                nc.gpsimd.memset(padded[:], 0.0).then_inc(consts, 1)
                nc.gpsimd.memset(v_pad[:], 0.0).then_inc(consts, 1)
                pool.wait_ge(weights_in, 80)
                for c in range(KC):
                    nc.gpsimd.tensor_tensor(mid_diag[:, c, :, :],
                                            core.ident[:, :].unsqueeze(1).to_broadcast([P, MID, P]),
                                            spread(mid_w[:, c, :], P), ALU.mult).then_inc(consts, 1)
                rnorm_step.start(pool)
                with pool.Fori(0, B) as b:
                    pool.wait_ge(sums_ready.sem, sums_ready.now(b, 1))
                    nc.gpsimd.tensor_tensor(rnorm[:], sums[:], eps12[:], ALU.add).then_inc(rnorm_step.sem, 1)
                    pool.wait_ge(rnorm_step.sem, rnorm_step.now(b, 1))
                    nc.gpsimd.tensor_tensor(rnorm[:], rnorm[:], core.minus_half[:], ALU.pow)\
                        .then_inc(rnorm_step.sem, 1)

            @block.scalar
            def _(act):
                act.wait_ge(consts, 5)
                for s in (padded_ready, tanh_ready, mid_ready, squares_ready, lm_ready, qk_t_ready, gram_ready):
                    s.start(act)
                with act.Fori(0, B) as b:
                    act.wait_ge(projected.sem, projected.now(b, 1))
                    act.wait_ge(conv_ready.sem, conv_ready.prev(b, 1))
                    act.wait_ge(silu_ready.sem, silu_ready.prev(b, 1))
                    nc.scalar.activation(padded[:].rearrange("p a c n -> p (a c) n")[:, :, CONV - 1:],
                                         PS[:, 0:3, :].rearrange("p a (c n) -> p (a c) n", c=KC), ACT.Copy)
                    nc.scalar.activation(tanh_beta[:], PS[0:MH, 3, 0:SEQ], ACT.Tanh, scale=0.5)
                    act.drain()
                    act.sem_inc(padded_ready.sem, 1)
                    act.wait_ge(conv_ready.sem, conv_ready.now(b, 1))
                    nc.scalar.activation(tanh[:], y[:], ACT.Tanh).then_inc(tanh_ready.sem, 1)
                    act.wait_ge(left.sem, left.prev(b, 1))
                    act.wait_ge(qkv_turned.sem, qkv_turned.now(b, 1))
                    nc.scalar.activation(squares[:].rearrange("p (a m) d -> p a (m d)", a=2), PS[:, 0:2, :], ACT.Square)
                    nc.scalar.activation(v_tok[:].rearrange("p t d -> p (t d)"), PS[:, 2, :], ACT.Copy)
                    act.drain()
                    act.sem_inc(squares_ready.sem, 1)
                    act.wait_ge(mid_done.sem, mid_done.now(b, 1))
                    nc.scalar.activation(mid_t[:].rearrange("p c n -> p (c n)"), PS[:, 4, :],
                                         ACT.Copy).then_inc(mid_ready.sem, 1)
                    act.wait_ge(lm_turned.sem, lm_turned.now(b, 1))
                    nc.scalar.activation(lm_tok[:].rearrange("p a t d -> p a (t d)"), PS[:, 5:7, :],
                                         ACT.Copy).then_inc(lm_ready.sem, 1)
                    act.wait_ge(qk_turned.sem, qk_turned.now(b, 1))
                    for i, bank in enumerate((3, 7)):
                        nc.scalar.activation(qk_t[:, i, :, :].rearrange("p c n -> p (c n)"), PS[:, bank, :], ACT.Copy)
                    act.drain()
                    act.sem_inc(qk_t_ready.sem, 1)
                    act.wait_ge(gram_done.sem, gram_done.now(b, 1))
                    for i in range(2):
                        for c4 in range(P // CHUNK):
                            at = slice(c4 * CHUNK, (c4 + 1) * CHUNK)
                            nc.scalar.activation(
                                gram[at, :, :, :].rearrange("p t (g i) j -> p t g i j", i=2)[:, :, :, i, :],
                                PS[at, i, :].rearrange("p (t g j) -> p t g j", t=TB, g=2)[:, :, :, at], ACT.Copy)
                    act.drain()
                    act.sem_inc(gram_ready.sem, 1)

            @block.vector
            def _(dve):
                dve.wait_ge(weights_in, 80)
                dve.wait_ge(consts, 5)
                nc.vector.tensor_scalar(conv_half[:], conv_w[:], 0.5, None, ALU.mult)
                dve.drain()
                for s in (conv_ready, silu_ready, local_ready, sums_ready, qk_tok_ready):
                    s.start(dve)

                def convolve(to, source, weight, taps, parts):
                    for tap in range(taps):
                        for part in parts:
                            shifted = source(part, tap)
                            scalar = weight(part, tap)
                            if tap == 0:
                                nc.vector.tensor_scalar(to(part), shifted, scalar, None, ALU.mult)
                            else:
                                nc.vector.scalar_tensor_tensor(to(part), shifted, scalar, to(part), ALU.mult, ALU.add)
                        dve.drain()

                with dve.Fori(0, B) as b:
                    dve.wait_ge(padded_ready.sem, padded_ready.now(b, 1))
                    convolve(lambda p: y[:, p[0], p[1], :],
                             lambda p, tap: padded[:, p[0], p[1], tap:tap + SEQ],
                             lambda p, tap: conv_half[:, p[0], p[1], tap:tap + 1],
                             CONV, [(a, c) for a in range(3) for c in range(KC)])
                    dve.sem_inc(conv_ready.sem, 1)
                    dve.wait_ge(tanh_ready.sem, tanh_ready.now(b, 1))
                    dve.wait_ge(left.sem, left.prev(b, 1))
                    dve.wait_ge(lm_turned.sem, lm_turned.prev(b, 1))
                    nc.vector.scalar_tensor_tensor(qk[:], tanh[:, 0:2, :, :], 1.0, y[:, 0:2, :, :], ALU.add, ALU.mult)
                    nc.vector.scalar_tensor_tensor(v_pad[:, :, PAD:], tanh[:, 2, :, :], 1.0, y[:, 2, :, :], ALU.add,
                                                   ALU.mult)
                    nc.vector.tensor_scalar(beta[:], tanh_beta[:], 0.5, 0.5, ALU.mult, ALU.add)
                    dve.drain()
                    dve.sem_inc(silu_ready.sem, 1)
                    convolve(lambda c: local_t[:, c, :],
                             lambda c, tap: v_pad[:, c, PAD - LOCAL + 1 + tap:PAD - LOCAL + 1 + tap + SEQ],
                             lambda c, tap: local_w[:, c, tap:tap + 1], LOCAL, range(KC))
                    dve.sem_inc(local_ready.sem, 1)
                    dve.wait_ge(squares_ready.sem, squares_ready.now(b, 1))
                    nc.vector.tensor_reduce(sums[:], squares[:], AX.X, ALU.add).then_inc(sums_ready.sem, 1)
                    dve.wait_ge(rnorm_step.sem, rnorm_step.now(b, 2))
                    nc.vector.tensor_tensor(qk_tok[:].rearrange("p a t (h d) -> p (a t h) d", d=MD),
                                            PS[:, 0:2, :].rearrange("p a (m d) -> p (a m) d", d=MD),
                                            spread(rnorm[:], MD), ALU.mult).then_inc(qk_tok_ready.sem, 1)

            @block.tensor
            def _(pe):
                pe.wait_ge(weights_in, 80)
                pe.wait_ge(consts, 5)
                for s in (projected, mid_done, qkv_turned, lm_turned, qk_turned, gram_done):
                    s.start(pe)
                mm = nc.tensor.matmul

                def turn(bank, source):
                    for t in range(TB):
                        for c in range(KC):
                            last = nc.tensor.transpose(PS[:, bank, t * D + c * P:t * D + (c + 1) * P],
                                                       source(c, t), core.ident[:])
                    return last

                with pe.Fori(0, B) as b:
                    pe.wait_ge(xt_in.sem, xt_in.now(b, 1))
                    pe.wait_ge(gram_ready.sem, gram_ready.prev(b, 1))
                    pe.wait_ge(squares_ready.sem, squares_ready.prev(b, 1))
                    pe.wait_ge(qk_t_ready.sem, qk_t_ready.prev(b, 1))
                    for a in range(3):
                        for oc in range(KC):
                            for c in range(KC):
                                mm(PS[:, a, oc * SEQ:(oc + 1) * SEQ], w[:, c, a, oc, :], xt[:, c, :],
                                   start=c == 0, stop=c == KC - 1)
                    for c in range(KC):
                        last = mm(PS[0:MH, 3, 0:SEQ], w_beta[:, c, :], xt[:, c, :], start=c == 0, stop=c == KC - 1)
                    last.then_inc(projected.sem, 1)
                    pe.wait_ge(silu_ready.sem, silu_ready.now(b, 1))
                    turn(0, lambda c, t: qk[:, 0, c, t * P:(t + 1) * P])
                    turn(1, lambda c, t: qk[:, 1, c, t * P:(t + 1) * P])
                    turn(2, lambda c, t: v_pad[:, c, PAD + t * P:PAD + (t + 1) * P]).then_inc(qkv_turned.sem, 1)
                    pe.wait_ge(mid_ready.sem, mid_ready.prev(b, 1))
                    for c in range(KC):
                        for tap in range(MID):
                            last = mm(PS[:, 4, c * SEQ:(c + 1) * SEQ], mid_diag[:, c, tap, :],
                                      v_pad[:, c, tap:tap + SEQ], start=tap == 0, stop=tap == MID - 1)
                    last.then_inc(mid_done.sem, 1)
                    pe.wait_ge(lm_ready.sem, lm_ready.prev(b, 1))
                    pe.wait_ge(local_ready.sem, local_ready.now(b, 1))
                    turn(5, lambda c, t: local_t[:, c, t * P:(t + 1) * P])
                    pe.wait_ge(mid_ready.sem, mid_ready.now(b, 1))
                    turn(6, lambda c, t: mid_t[:, c, t * P:(t + 1) * P]).then_inc(lm_turned.sem, 1)
                    pe.wait_ge(qk_tok_ready.sem, qk_tok_ready.now(b, 1))
                    for i, bank in enumerate((3, 7)):
                        for c in range(KC):
                            for t in range(TB):
                                last = nc.tensor.transpose(PS[:, bank, (c * TB + t) * P:(c * TB + t + 1) * P],
                                                           qk_tok[:, i, t, c * P:(c + 1) * P], core.ident[:])
                    last.then_inc(qk_turned.sem, 1)
                    pe.wait_ge(qk_t_ready.sem, qk_t_ready.now(b, 1))
                    for t in range(TB):
                        for g in range(KC):
                            for i in range(2):
                                keys = qk_t[MD * i:MD * (i + 1), 1, g, t * P:(t + 1) * P]
                                last = mm(PS[:, i, (t * 2 + g) * P:(t * 2 + g + 1) * P], keys, keys,
                                          start=True, stop=True)
                    last.then_inc(gram_done.sem, 1)


def block_mixer_solve(core):
    nc, scratch = core.nc, core.mixer
    NG = B * NCH * MH // P
    BG = B // NG
    C = CHUNK
    with ExitStack() as ctx:
        def sb(n, shape, dt=F32):
            return ctx.enter_context(nc.sbuf_tensor(f"ms_{n}", shape, dt))

        gram = sb("gram", [P, NG, C, C])
        beta = sb("beta", [P, NG, C])
        strict = sb("strict", [P, C, C])
        eye = sb("eye", [P, C, C])
        T = sb("T", [P, NG, C, C])
        product = sb("product", [P, NG * C * C])
        row = sb("row", [P, NG, C])
        out = sb("out", [P, NG, C, C])
        loaded = core.semaphore("ms_loaded")
        consts = core.semaphore("ms_constants_ready")
        solved = core.semaphore("ms_solved")
        stored = core.semaphore("ms_stored")
        with nc.Block() as block:
            @block.sync
            def _(sp):
                for g in range(NG):
                    for h in range(MH):
                        rows = slice(h, P, MH)
                        src = scratch.gram[g * BG:(g + 1) * BG, :, :, :, h, :]
                        sp.dma_start(gram[rows, g, :, :], src.rearrange("b u c i j -> (b u c) i j"))\
                            .then_inc(loaded, 16)
                        sp.dma_start(beta[rows, g, :], scratch.beta[g * BG:(g + 1) * BG, h, :, :])\
                            .then_inc(loaded, 16)
                sp.wait_ge(solved, 1)
                for b in range(B):
                    rows = slice((b % BG) * NCH * MH, (b % BG + 1) * NCH * MH)
                    sp.dma_start(scratch.solved.rearrange("n h j b i -> (n h) j b i")[:, :, b, :],
                                 out[rows, b // BG, :, :]).then_inc(stored, 16)
                sp.wait_ge(stored, 16 * B)

            @block.gpsimd
            def _(pool):
                nc.gpsimd.memset(strict[:], -1.0).then_inc(consts, 1)
                nc.gpsimd.memset(eye[:], 0.0).then_inc(consts, 1)
                pool.wait_ge(consts, 2)
                nc.gpsimd.affine_select(out=strict[:], in_=strict[:], compare_op=ALU.is_gt, fill=0.0, base=0,
                                        pattern=[[1, C], [-1, C]], channel_multiplier=0).then_inc(consts, 1)
                nc.gpsimd.affine_select(out=eye[:], in_=eye[:], compare_op=ALU.not_equal, fill=1.0, base=0,
                                        pattern=[[1, C], [-1, C]], channel_multiplier=0).then_inc(consts, 1)

            @block.vector
            def _(dve):
                dve.wait_ge(loaded, 16 * 2 * NG * MH)
                dve.wait_ge(consts, 4)
                for g in range(NG):
                    nc.vector.tensor_tensor(T[:, g, :, :], gram[:, g, :, :], strict[:], ALU.mult)
                dve.drain()
                nc.vector.tensor_tensor(T[:], T[:], spread(beta[:], C), ALU.mult)
                dve.drain()
                for i in range(1, C):
                    prod = product[:, 0:NG * i * i].rearrange("p (g c j) -> p g c j", g=NG, c=i)
                    nc.vector.tensor_tensor(prod, T[:, :, i, 0:i].unsqueeze(2).to_broadcast([P, NG, i, i]),
                                            T[:, :, 0:i, 0:i].rearrange("p g j c -> p g c j"), ALU.mult)
                    dve.drain()
                    nc.vector.tensor_reduce(row[:, :, 0:i], prod, AX.X, ALU.add)
                    dve.drain()
                    nc.vector.tensor_tensor(T[:, :, i, 0:i], T[:, :, i, 0:i], row[:, :, 0:i], ALU.add)
                    dve.drain()
                for g in range(NG):
                    nc.vector.tensor_tensor(out[:, g, :, :], T[:, g, :, :].rearrange("p i j -> p j i"), eye[:], ALU.add)
                dve.drain()
                nc.vector.tensor_tensor(out[:], out[:], spread(beta[:], C), ALU.mult).then_inc(solved, 1)


def block_mixer_scan(core):
    nc, PS, scratch = core.nc, core.PS, core.mixer
    C = CHUNK
    with ExitStack() as ctx:
        def sb(n, shape, dt=F32):
            return ctx.enter_context(nc.sbuf_tensor(f"mc_{n}", shape, dt))

        qk_bd = sb("qk_bd", [P, 2, 2, KC, B, P])
        k_bd = sb("k_bd", [P, 2, KC, B, P])
        t_bd = sb("t_bd", [P, 2, B, P])
        v = sb("v", [P, 2, B, MD])
        causal = sb("causal", [P, P])
        attn = sb("attn", [P, B, P])
        rest = sb("rest", [P, B, MD])
        u = sb("u", [P, B, MD])
        S = sb("S", [P, KC, B, MD])
        o = sb("o", [P, 2, B, MD])
        zeroed = core.semaphore("mc_zeroed")
        N_LOADS = 4 * MH + MH
        loaded = [core.semaphore(f"mc_loaded_{i}") for i in range(2)]

        def sig(n, per, unit=1):
            return Signal(core, f"mc_{n}", per, unit)

        attn_done = sig("attn_done", 2)
        attn_ready = sig("attn_ready", 2)
        ks_done = sig("ks_done", 2)
        rest_ready = sig("rest_ready", 2)
        u_done = sig("u_done", 2)
        u_ready = sig("u_ready", 2)
        o_done = sig("o_done", 2)
        o_ready = sig("o_ready", 2)
        s_done = sig("state_update_done", 2)
        s_ready = sig("state_ready", 2)
        o_stored = sig("o_stored", 2 * MH, 16)

        def by_head(bank):
            return PS[:, bank, :].rearrange("p (b d) -> p b d", d=MD)

        with nc.Block() as block:
            @block.sync
            def _(sp):
                sp.wait_ge(zeroed, 3)
                o_stored.start(sp)
                with sp.Fori(0, NCH // 2) as m:
                    def load(par):
                        n = bass.ds(2 * m + par, 1)
                        for h in range(MH):
                            c, i = h // 2, h % 2
                            at = slice(h * C, (h + 1) * C)
                            rows = slice(i * MD, (i + 1) * MD)
                            for a in range(2):
                                sp.dma_start(qk_bd[rows, par, a, c, :, at],
                                             scratch.qk_t[a, rows, c, :, n, :].rearrange("p b a t -> p b (a t)"))\
                                    .then_inc(loaded[par], 16)
                            sp.dma_start(k_bd[at, par, c, :, rows],
                                         scratch.k[:, n, :, h, :].rearrange("b a t d -> (a t) b d"))\
                                .then_inc(loaded[par], 16)
                            sp.dma_start(v[at, par, :, :],
                                         scratch.outs[3].rearrange("(b n t) f -> b n t f", n=NCH, t=C)
                                         [:, n, :, h * MD:(h + 1) * MD].rearrange("b a t d -> (a t) b d"))\
                                .then_inc(loaded[par], 16)
                            sp.dma_start(t_bd[at, par, :, at],
                                         scratch.solved[n, h, :, :, :].rearrange("a j b i -> (a j) b i"))\
                                .then_inc(loaded[par], 16)

                    sp.wait_ge(s_done.sem, s_done.prev(m, 1))
                    load(0)
                    sp.wait_ge(s_done.sem, s_done.prev(m, 2))
                    load(1)
                    for par in range(2):
                        n = bass.ds(2 * m + par, 1)
                        sp.wait_ge(o_ready.sem, o_ready.now(m, par + 1))
                        for h in range(MH):
                            sp.dma_start(scratch.outs[2].rearrange("(b n t) f -> b n t f", n=NCH, t=C)
                                         [:, n, :, h * MD:(h + 1) * MD].rearrange("b a t d -> (a t) b d"),
                                         o[h * C:(h + 1) * C, par, :, :]).then_inc(o_stored.sem, 16)
                sp.wait_ge(o_stored.sem, o_stored.now(NCH // 2 - 1, 2 * MH))

            @block.gpsimd
            def _(pool):
                nc.gpsimd.memset(qk_bd[:], 0.0).then_inc(zeroed, 1)
                nc.gpsimd.memset(k_bd[:], 0.0).then_inc(zeroed, 1)
                nc.gpsimd.memset(t_bd[:], 0.0).then_inc(zeroed, 1)
                nc.gpsimd.memset(S[:], 0.0).then_inc(zeroed, 1)
                nc.gpsimd.memset(causal[:], 1.0).then_inc(zeroed, 1)
                pool.wait_ge(zeroed, 5)
                nc.gpsimd.affine_select(out=causal[:], in_=causal[:], compare_op=ALU.is_ge, fill=0.0, base=0,
                                        pattern=[[1, P]], channel_multiplier=-1).then_inc(zeroed, 1)

            @block.scalar
            def _(act):
                for s in (u_ready, o_ready):
                    s.start(act)
                with act.Fori(0, NCH // 2) as m:
                    act.wait_ge(o_stored.sem, o_stored.prev(m, 2 * MH))
                    for par in range(2):
                        act.wait_ge(u_done.sem, u_done.now(m, par + 1))
                        nc.scalar.activation(u[:], by_head(3), ACT.Copy).then_inc(u_ready.sem, 1)
                        act.wait_ge(o_done.sem, o_done.now(m, par + 1))
                        nc.scalar.activation(o[:, par, :, :], by_head(4), ACT.Copy).then_inc(o_ready.sem, 1)

            @block.vector
            def _(dve):
                dve.wait_ge(zeroed, 6)
                for s in (attn_ready, rest_ready, s_ready):
                    s.start(dve)
                with dve.Fori(0, NCH // 2) as m:
                    for par in range(2):
                        dve.wait_ge(attn_done.sem, attn_done.now(m, par + 1))
                        dve.wait_ge(o_done.sem, o_done.now(m, 1) if par else o_done.prev(m, 2))
                        for half in range(2):
                            nc.vector.tensor_tensor(attn[:, 4 * half:4 * half + 4, :],
                                                    PS[:, half, :].rearrange("p (b i) -> p b i", i=P),
                                                    causal[:, :].unsqueeze(1).to_broadcast([P, 4, P]), ALU.mult)
                        dve.drain()
                        dve.sem_inc(attn_ready.sem, 1)
                        dve.wait_ge(ks_done.sem, ks_done.now(m, par + 1))
                        nc.vector.tensor_tensor(rest[:], v[:, par, :, :], by_head(2), ALU.subtract)\
                            .then_inc(rest_ready.sem, 1)
                        dve.wait_ge(s_done.sem, s_done.now(m, par + 1))
                        for c in range(KC):
                            nc.vector.tensor_tensor(S[:, c, :, :], by_head(5 + c), S[:, c, :, :], ALU.add)
                        dve.drain()
                        dve.sem_inc(s_ready.sem, 1)

            @block.tensor
            def _(pe):
                pe.wait_ge(zeroed, 6)
                for s in (attn_done, ks_done, u_done, o_done, s_done):
                    s.start(pe)
                mm = nc.tensor.matmul
                with pe.Fori(0, NCH // 2) as m:
                    for par in range(2):
                        pe.wait_ge(loaded[par], (m + 1) * (16 * N_LOADS))
                        before = (lambda s: s.now(m, 1)) if par else (lambda s: s.prev(m, 2))
                        pe.wait_ge(attn_ready.sem, before(attn_ready))
                        for b in range(B):
                            for c in range(KC):
                                last = mm(PS[:, b // 4, (b % 4) * P:(b % 4 + 1) * P], qk_bd[:, par, 1, c, b, :],
                                          qk_bd[:, par, 0, c, b, :], start=c == 0, stop=c == KC - 1)
                        last.then_inc(attn_done.sem, 1)
                        pe.wait_ge(s_ready.sem, before(s_ready))
                        pe.wait_ge(rest_ready.sem, before(rest_ready))
                        for b in range(B):
                            for c in range(KC):
                                last = mm(by_head(2)[:, b, :], qk_bd[:, par, 1, c, b, :], S[:, c, b, :],
                                          start=c == 0, stop=c == KC - 1)
                        last.then_inc(ks_done.sem, 1)
                        pe.wait_ge(rest_ready.sem, rest_ready.now(m, par + 1))
                        pe.wait_ge(u_ready.sem, before(u_ready))
                        for b in range(B):
                            last = mm(by_head(3)[:, b, :], t_bd[:, par, b, :], rest[:, b, :], start=True, stop=True)
                        last.then_inc(u_done.sem, 1)
                        pe.wait_ge(u_ready.sem, u_ready.now(m, par + 1))
                        pe.wait_ge(attn_ready.sem, attn_ready.now(m, par + 1))
                        pe.wait_ge(o_ready.sem, before(o_ready))
                        for b in range(B):
                            for c in range(KC):
                                mm(by_head(4)[:, b, :], qk_bd[:, par, 0, c, b, :], S[:, c, b, :],
                                   start=c == 0, stop=False)
                            last = mm(by_head(4)[:, b, :], attn[:, b, :], u[:, b, :], start=False, stop=True)
                        last.then_inc(o_done.sem, 1)
                        for b in range(B):
                            for c in range(KC):
                                last = mm(by_head(5 + c)[:, b, :], k_bd[:, par, c, b, :], u[:, b, :],
                                          start=True, stop=True)
                        last.then_inc(s_done.sem, 1)


def block_mixer_mix(core):
    nc, PS, dram, scratch = core.nc, core.PS, core.dram, core.mixer
    O = len(OUTS)
    HB = 5
    NF = 14 * MH
    FLOOR = 0.01
    PAIRS = [(0, 1, 3), (1, 2, 2), (2, 3, 1)]
    with ExitStack() as ctx:
        def sb(n, shape, dt=F32):
            return ctx.enter_context(nc.sbuf_tensor(f"mm_{n}", shape, dt))

        def sig(n, per, unit=1):
            return Signal(core, f"mm_{n}", per, unit)

        w1 = sb("w1", [P, KC + 1, HB, P])
        b1 = sb("b1", [P, HB])
        w2 = sb("w2", [P, HB, O * MH])
        b2 = sb("b2", [P, O * MH])
        mix_w = sb("mix_w", [P, D])
        onorm_w = sb("onorm_w", [P, MD])
        wo = sb("wo", [P, KC, D])
        eps5 = sb("eps5", [P, 16])
        inv_md = sb("inv_md", [P, 16])
        xt = sb("xt", [P, KC, SEQ])
        outs = sb("outs", [P, TB, O, D])
        squares = sb("squares", [P, TB, O, D])
        pairs = sb("pairs", [P, TB, 6, D])
        sums = sb("sums", [P, TB, O, MH])
        sumsq = sb("sumsq", [P, TB, O, MH])
        stats = sb("stats", [P, TB, P])
        stats_t = sb("stats_t", [NF, SEQ])
        hid = sb("hid", [P, HB, SEQ])
        tanh = sb("tanh", [P, HB, SEQ])
        act2 = sb("act2", [P, HB, SEQ])
        logits = sb("logits", [P, TB, MH, O])
        top = sb("top", [P, TB, MH])
        expd = sb("expd", [P, TB, MH, O])
        den = sb("den", [P, TB, MH])
        prob = sb("prob", [P, TB, MH, O])
        weighted = sb("weighted", [P, TB, O, D])
        mixed = sb("mixed", [P, TB, D])
        mixed2 = sb("mixed2", [P, TB, D])
        ms = sb("ms", [P, 2, TB, MH])
        rms = sb("rms", [P, 2, TB, MH])
        mixed_t = sb("mixed_t", [P, KC, SEQ])
        norm = Norm(core, ctx, "mm", 3, 7)

        weights_in = core.semaphore("mm_weights_in")
        consts = core.semaphore("mm_constants_ready")
        w2_halved = core.semaphore("mm_w2_halved")
        N_IN = 1 + TB
        inputs_in = sig("inputs_in", N_IN, 16)
        pairs_ready = sig("pairs_ready", 1)
        squares_ready = sig("squares_ready", 1)
        stats_ready = sig("stats_ready", 1)
        stats_turned = sig("stats_turned", 1)
        stats_t_ready = sig("stats_t_ready", 1)
        hid_done = sig("hid_done", 1)
        tanh_ready = sig("tanh_ready", 1)
        act_ready = sig("hidden_ready", 1)
        logits_done = sig("logits_done", 1)
        shifted_ready = sig("shifted_ready", 1)
        exp_ready = sig("exp_ready", 1)
        ms_ready = sig("ms_ready", 2)
        rms_step = sig("rms_step", 6)
        mixed_ready = sig("mixed_ready", 1)
        mixed_turned = sig("mixed_turned", 1)
        mixed_t_ready = sig("mixed_t_ready", 1)
        out_done = sig("out_done", 1)

        def heads(ap):
            return ap.rearrange("p t (h d) -> p (t h) d", d=MD)

        with nc.Block() as block:
            @block.sync
            def _(sp):
                for dst, n in ((w1, "mm_w1"), (b1, "mm_b1"), (w2, "mm_w2"), (wo, "mm_wo")):
                    sp.dma_start(dst[:], dram[n]).then_inc(weights_in, 16)
                for dst, n in ((b2, "mm_b2"), (mix_w, "mm_mix_w"), (onorm_w, "mm_onorm_w")):
                    sp.dma_start(dst[:], dram[n].partition_broadcast(P)).then_inc(weights_in, 16)
                inputs_in.start(sp)
                norm.start_sync(sp)
                with sp.Fori(0, B) as b:
                    sp.wait_ge(hid_done.sem, hid_done.prev(b, 1))
                    sp.wait_ge(mixed_ready.sem, mixed_ready.prev(b, 1))
                    sp.dma_start(xt[:], core.xt_of(b)).then_inc(inputs_in.sem, 16)
                    for t in range(TB):
                        sp.dma_start(outs[:, t, :, :], scratch.outs[:, bass.ds(b * SEQ + t * P, P), :]
                                     .rearrange("o p f -> p o f")).then_inc(inputs_in.sem, 16)
                    norm.load(sp, b)
                    norm.store(sp, b)

            @block.gpsimd
            def _(pool):
                nc.gpsimd.memset(eps5[:], 1e-5).then_inc(consts, 1)
                nc.gpsimd.memset(inv_md[:], 1.0 / MD).then_inc(consts, 1)
                nc.gpsimd.memset(stats[:], 0.0).then_inc(consts, 1)
                pool.wait_ge(consts, 3)
                pairs_ready.start(pool)
                rms_step.start(pool)
                norm.start_gpsimd(pool)
                with pool.Fori(0, B) as b:
                    pool.wait_ge(inputs_in.sem, inputs_in.now(b, N_IN))
                    pool.wait_ge(stats_ready.sem, stats_ready.prev(b, 1))
                    for t in range(TB):
                        at = 0
                        for first, second, n in PAIRS:
                            nc.gpsimd.tensor_tensor(pairs[:, t, at:at + n, :], outs[:, t, second:second + n, :],
                                                    outs[:, t, first, :].unsqueeze(1).to_broadcast([P, n, D]),
                                                    ALU.mult)
                            at += n
                    pool.drain()
                    pool.sem_inc(pairs_ready.sem, 1)
                    for k in range(2):
                        pool.wait_ge(ms_ready.sem, ms_ready.now(b, k + 1))
                        flat = rms[:, k, :, :].rearrange("p t h -> p (t h)")
                        steps = ((ms[:, k, :, :].rearrange("p t h -> p (t h)"), inv_md, ALU.mult),
                                 (flat, eps5, ALU.add), (flat, core.minus_half, ALU.pow))
                        for i, (src, const, op) in enumerate(steps):
                            if i:
                                pool.wait_ge(rms_step.sem, rms_step.now(b, 3 * k + i))
                            nc.gpsimd.tensor_tensor(flat, src, const[:, 0:TB * MH], op).then_inc(rms_step.sem, 1)
                    norm.gpsimd(pool, b)

            @block.scalar
            def _(act):
                act.wait_ge(weights_in, 112)
                for s in (squares_ready, stats_t_ready, tanh_ready, exp_ready, mixed_t_ready):
                    s.start(act)
                norm.start_scalar(act)
                with act.Fori(0, B) as b:
                    act.wait_ge(inputs_in.sem, inputs_in.now(b, N_IN))
                    act.wait_ge(stats_ready.sem, stats_ready.prev(b, 1))
                    nc.scalar.activation(squares[:], outs[:], ACT.Square).then_inc(squares_ready.sem, 1)
                    act.wait_ge(stats_turned.sem, stats_turned.now(b, 1))
                    nc.scalar.activation(stats_t[:], PS[0:NF, 3, 0:SEQ], ACT.Copy).then_inc(stats_t_ready.sem, 1)
                    act.wait_ge(hid_done.sem, hid_done.now(b, 1))
                    act.wait_ge(act_ready.sem, act_ready.prev(b, 1))
                    for h in range(HB):
                        nc.scalar.activation(hid[:, h, :], PS[:, h // 2, (h % 2) * SEQ:(h % 2 + 1) * SEQ],
                                             ACT.Identity, bias=b1[:, h:h + 1])
                    act.drain()
                    nc.scalar.activation(tanh[:], hid[:], ACT.Tanh, scale=0.5).then_inc(tanh_ready.sem, 1)
                    act.wait_ge(shifted_ready.sem, shifted_ready.now(b, 1))
                    nc.scalar.activation(expd[:], logits[:], ACT.Exp).then_inc(exp_ready.sem, 1)
                    act.wait_ge(mixed_turned.sem, mixed_turned.now(b, 1))
                    nc.scalar.activation(mixed_t[:].rearrange("p c n -> p (c n)"), PS[:, 5, :],
                                         ACT.Copy).then_inc(mixed_t_ready.sem, 1)
                    norm.scalar(act, b)

            @block.vector
            def _(dve):
                dve.wait_ge(weights_in, 112)
                nc.vector.tensor_scalar(w2[:], w2[:], 0.5, None, ALU.mult).then_inc(w2_halved, 1)
                dve.wait_ge(consts, 3)
                for s in (stats_ready, act_ready, shifted_ready, ms_ready, mixed_ready):
                    s.start(dve)
                norm.start_vector(dve)
                with dve.Fori(0, B) as b:
                    dve.wait_ge(inputs_in.sem, inputs_in.now(b, N_IN))
                    dve.wait_ge(stats_turned.sem, stats_turned.prev(b, 1))
                    by_kind = stats[:, :, 0:NF].rearrange("p t (k h) -> p t k h", h=MH)
                    nc.vector.tensor_reduce(sums[:], outs[:].rearrange("p t o (h d) -> p (t o) h d", d=MD), AX.X,
                                            ALU.add)
                    dve.wait_ge(squares_ready.sem, squares_ready.now(b, 1))
                    nc.vector.tensor_reduce(sumsq[:], squares[:].rearrange("p t o (h d) -> p (t o) h d", d=MD), AX.X,
                                            ALU.add)
                    dve.wait_ge(pairs_ready.sem, pairs_ready.now(b, 1))
                    for t in range(TB):
                        nc.vector.tensor_reduce(by_kind[:, t, 8:14, :], pairs[:, t, :, :]
                                                .rearrange("p k (h d) -> p k h d", d=MD), AX.X, ALU.add)
                    dve.drain()
                    nc.vector.tensor_scalar(by_kind[:, :, 8:14, :], by_kind[:, :, 8:14, :], 1.0 / MD, None, ALU.mult)
                    for t in range(TB):
                        nc.vector.tensor_scalar(by_kind[:, t, 0:8:2, :], sums[:, t, :, :], 1.0 / MD, None, ALU.mult)
                    dve.drain()
                    for t in range(TB):
                        nc.vector.tensor_tensor(sums[:, t, :, :], sums[:, t, :, :], by_kind[:, t, 0:8:2, :], ALU.mult)
                    dve.drain()
                    nc.vector.tensor_tensor(sumsq[:], sumsq[:], sums[:], ALU.subtract)
                    dve.drain()
                    for t in range(TB):
                        nc.vector.tensor_scalar(by_kind[:, t, 1:8:2, :], sumsq[:, t, :, :], 1.0 / (MD - 1), None,
                                                ALU.mult)
                    dve.drain()
                    dve.sem_inc(stats_ready.sem, 1)
                    dve.wait_ge(tanh_ready.sem, tanh_ready.now(b, 1))
                    dve.wait_ge(logits_done.sem, logits_done.prev(b, 1))
                    nc.vector.scalar_tensor_tensor(act2[:], tanh[:], 1.0, hid[:], ALU.add, ALU.mult)\
                        .then_inc(act_ready.sem, 1)
                    dve.wait_ge(logits_done.sem, logits_done.now(b, 1))
                    flat = logits[:].rearrange("p t h o -> p t (h o)")
                    nc.vector.tensor_tensor(flat, PS[:, 4, 0:TB * O * MH].rearrange("p (t n) -> p t n", t=TB),
                                            b2[:, :].unsqueeze(1).to_broadcast([P, TB, O * MH]), ALU.add)
                    dve.drain()
                    nc.vector.tensor_reduce(top[:], logits[:], AX.X, ALU.max)
                    dve.drain()
                    nc.vector.tensor_tensor(logits[:], logits[:], spread(top[:], O), ALU.subtract)\
                        .then_inc(shifted_ready.sem, 1)
                    dve.wait_ge(exp_ready.sem, exp_ready.now(b, 1))
                    nc.vector.tensor_reduce(den[:], expd[:], AX.X, ALU.add)
                    dve.drain()
                    nc.vector.reciprocal(den[:], den[:])
                    dve.drain()
                    nc.vector.tensor_tensor(prob[:], expd[:], spread(den[:], O), ALU.mult)
                    dve.drain()
                    nc.vector.tensor_scalar(prob[:], prob[:], 1.0 - 4.0 * FLOOR, FLOOR, ALU.mult, ALU.add)
                    dve.drain()
                    for t in range(TB):
                        nc.vector.tensor_tensor(weighted[:, t, :, :].rearrange("p o (h d) -> p o h d", d=MD),
                                                outs[:, t, :, :].rearrange("p o (h d) -> p o h d", d=MD),
                                                spread(prob[:, t, :, :].rearrange("p h o -> p o h"), MD), ALU.mult)
                    dve.drain()
                    for t in range(TB):
                        nc.vector.tensor_reduce(mixed[:, t, :], weighted[:, t, :, :].rearrange("p o f -> p f o"), AX.X,
                                                ALU.add)
                    dve.drain()

                    def mean_square(k, src):
                        nc.vector.tensor_tensor(weighted[:, :, 0, :], src[:], src[:], ALU.mult)
                        dve.drain()
                        nc.vector.tensor_reduce(ms[:, k, :, :], weighted[:, :, 0, :]
                                                .rearrange("p t (h d) -> p t h d", d=MD), AX.X, ALU.add)\
                            .then_inc(ms_ready.sem, 1)
                        dve.wait_ge(rms_step.sem, rms_step.now(b, 3 * k + 3))
                        nc.vector.tensor_tensor(heads(mixed2[:] if k == 0 else mixed[:]), heads(src[:]),
                                                spread(rms[:, k, :, :].rearrange("p t h -> p (t h)"), MD), ALU.mult)
                        dve.drain()

                    mean_square(0, mixed)
                    nc.vector.tensor_tensor(mixed2[:], mixed2[:], mix_w[:, :].unsqueeze(1).to_broadcast([P, TB, D]),
                                            ALU.mult)
                    dve.drain()
                    dve.wait_ge(mixed_turned.sem, mixed_turned.prev(b, 1))
                    mean_square(1, mixed2)
                    nc.vector.tensor_tensor(heads(mixed[:]), heads(mixed[:]),
                                            onorm_w[:, :].unsqueeze(1).to_broadcast([P, TB * MH, MD]), ALU.mult)\
                        .then_inc(mixed_ready.sem, 1)
                    norm.vector(dve, b, (out_done.sem, out_done.now(b, 1)))

            @block.tensor
            def _(pe):
                pe.wait_ge(weights_in, 112)
                pe.wait_ge(consts, 3)
                pe.wait_ge(w2_halved, 1)
                for s in (stats_turned, hid_done, logits_done, mixed_turned, out_done):
                    s.start(pe)
                norm.start_tensor(pe)
                mm = nc.tensor.matmul
                with pe.Fori(0, B) as b:
                    pe.wait_ge(stats_ready.sem, stats_ready.now(b, 1))
                    pe.wait_ge(stats_t_ready.sem, stats_t_ready.prev(b, 1))
                    for t in range(TB):
                        last = nc.tensor.transpose(PS[:, 3, t * P:(t + 1) * P], stats[:, t, :], core.ident[:])
                    last.then_inc(stats_turned.sem, 1)
                    pe.wait_ge(stats_t_ready.sem, stats_t_ready.now(b, 1))
                    pe.wait_ge(tanh_ready.sem, tanh_ready.prev(b, 1))
                    for h in range(HB):
                        to = PS[:, h // 2, (h % 2) * SEQ:(h % 2 + 1) * SEQ]
                        for c in range(KC):
                            mm(to, w1[:, c, h, :], xt[:, c, :], start=c == 0, stop=False)
                        last = mm(to, w1[0:NF, KC, h, :], stats_t[:], start=False, stop=True)
                    last.then_inc(hid_done.sem, 1)
                    pe.wait_ge(act_ready.sem, act_ready.now(b, 1))
                    pe.wait_ge(shifted_ready.sem, shifted_ready.prev(b, 1))
                    for t in range(TB):
                        for h in range(HB):
                            last = mm(PS[:, 4, t * O * MH:(t + 1) * O * MH], act2[:, h, t * P:(t + 1) * P], w2[:, h, :],
                                      start=h == 0, stop=h == HB - 1)
                    last.then_inc(logits_done.sem, 1)
                    pe.wait_ge(mixed_ready.sem, mixed_ready.now(b, 1))
                    pe.wait_ge(mixed_t_ready.sem, mixed_t_ready.prev(b, 1))
                    for c in range(KC):
                        for t in range(TB):
                            last = nc.tensor.transpose(PS[:, 5, (c * TB + t) * P:(c * TB + t + 1) * P],
                                                       mixed[:, t, c * P:(c + 1) * P], core.ident[:])
                    last.then_inc(mixed_turned.sem, 1)
                    pe.wait_ge(mixed_t_ready.sem, mixed_t_ready.now(b, 1))
                    pe.wait_ge(norm.xt_ready.sem, norm.xt_ready.prev(norm.turn(b), 1))
                    for t in range(TB):
                        for c in range(KC):
                            last = mm(PS[:, 7, t * D:(t + 1) * D], mixed_t[:, c, t * P:(t + 1) * P], wo[:, c, :],
                                      start=c == 0, stop=c == KC - 1)
                    last.then_inc(out_done.sem, 1)
                    norm.tensor(pe, b)


def block_experts_1(core):
    E, HB = 8, 8
    nc, PS, dram = core.nc, core.PS, core.dram
    with ExitStack() as ctx:
        def sb(n, shape, dt=F32):
            return ctx.enter_context(nc.sbuf_tensor(f"eb_{n}", shape, dt))

        def sig(n, per, unit=1):
            return Signal(core, f"eb_{n}", per, unit)

        up = sb("up", [P, KC, E, HB, P])
        down = sb("down", [P, E, HB, D])
        up_bias = sb("up_bias", [P, E, HB])
        down_bias = sb("down_bias", [P, D])
        router = sb("router", [P, KC, E])
        router_bias = sb("router_bias", [P, E])
        gamma = sb("gamma", [P, D])
        beta = sb("beta", [P, D])
        iota8 = sb("iota8", [P, E])
        xt = sb("xt", [P, KC, SEQ])
        logits = sb("logits", [P, TB, E])
        best = sb("best", [P, TB, 8])
        index = sb("index", [P, TB, 8], mybir.dt.uint32)
        index_f = sb("index_f", [P, TB, 8])
        chosen = sb("chosen", [P, TB, 2, E])
        gap = sb("gap", [P, TB])
        mix = sb("mix", [P, TB, 2])
        exp_gap = sb("exp_gap", [P, TB])
        weight = sb("weight", [P, TB, E])
        weight_t = sb("weight_t", [P, SEQ])
        hidden = sb("hidden", [P, 2, HB // 2, SEQ])
        total = sb("total", [P, TB, D])
        inner_stats = sb("inner_stats", [P, TB, 6])
        inner_mv = sb("inner_mean_var", [P, TB, 2])
        inner_rstd = sb("inner_rstd", [P, TB])
        norm = Norm(core, ctx, "eb", 5, 7)

        weights_in = core.semaphore("eb_weights_in")
        consts = core.semaphore("eb_constants_ready")
        xt_in = sig("xt_in", 1, 16)
        router_done = sig("router_done", 1)
        gap_ready = sig("gap_ready", 1)
        exp_ready = sig("exp_ready", 1)
        weight_ready = sig("weight_ready", 1)
        weight_turned = sig("weight_turned", 1)
        weight_t_ready = sig("weight_t_ready", 1)
        bias_done = sig("mixed_bias_done", 1)
        total_started = sig("total_started", 1)
        up_done = sig("up_done", 2 * E)
        hidden_ready = sig("hidden_ready", 2 * E)
        down_half = sig("down_half", 2 * E)
        added = sig("expert_added", E)
        inner_var_ready = sig("inner_variance_ready", 1)
        inner_rstd_step = sig("inner_rstd_step", 2)

        def tiles(ap):
            return ap.rearrange("p (t d) -> p t d", t=TB)

        def half_banks(h):
            return PS[:, 2 * (h % 2):2 * (h % 2) + 2, :].rearrange("p a (m n) -> p (a m) n", n=SEQ)

        with nc.Block() as block:
            @block.sync
            def _(sp):
                for dst, n in ((up_bias, "eb_up_bias"), (router, "eb_router")):
                    sp.dma_start(dst[:], dram[n]).then_inc(weights_in, 16)
                sp.dma_start(down_bias[0:E, :], dram["eb_down_bias"]).then_inc(weights_in, 16)
                for dst, n in ((router_bias, "eb_router_bias"), (gamma, "eb_gamma"), (beta, "eb_beta")):
                    sp.dma_start(dst[:], dram[n].partition_broadcast(P)).then_inc(weights_in, 16)
                sp.dma_start(up[:], dram["eb_up"]).then_inc(weights_in, 16)
                sp.dma_start(down[:], dram["eb_down"]).then_inc(weights_in, 16)
                xt_in.start(sp)
                norm.start_sync(sp)
                with sp.Fori(0, B) as b:
                    sp.wait_ge(up_done.sem, up_done.prev(b, 2 * E))
                    sp.dma_start(xt[:], core.xt_of(b)).then_inc(xt_in.sem, 16)
                    norm.load(sp, b)
                    norm.store(sp, b, last=True)

            @block.gpsimd
            def _(pool):
                nc.gpsimd.iota(iota8[:], pattern=[[1, E]], base=0, channel_multiplier=0,
                               allow_small_or_imprecise_dtypes=True).then_inc(consts, 1)
                inner_rstd_step.start(pool)
                norm.start_gpsimd(pool)
                with pool.Fori(0, B) as b:
                    pool.wait_ge(inner_var_ready.sem, inner_var_ready.now(b, 1))
                    nc.gpsimd.tensor_tensor(inner_rstd[:], inner_mv[:, :, 1], core.eps[:, 0:TB],
                                            ALU.add).then_inc(inner_rstd_step.sem, 1)
                    pool.wait_ge(inner_rstd_step.sem, inner_rstd_step.now(b, 1))
                    nc.gpsimd.tensor_tensor(inner_rstd[:], inner_rstd[:], core.minus_half[:, 0:TB],
                                            ALU.pow).then_inc(inner_rstd_step.sem, 1)
                    norm.gpsimd(pool, b)

            @block.scalar
            def _(act):
                act.wait_ge(weights_in, 128)
                for s in (exp_ready, weight_t_ready, hidden_ready):
                    s.start(act)
                norm.start_scalar(act)
                with act.Fori(0, B) as b:
                    act.wait_ge(gap_ready.sem, gap_ready.now(b, 1))
                    nc.scalar.activation(exp_gap[:], gap[:], ACT.Exp).then_inc(exp_ready.sem, 1)
                    act.wait_ge(weight_turned.sem, weight_turned.now(b, 1))
                    nc.scalar.activation(weight_t[0:E, :], PS[0:E, 6, 0:SEQ], ACT.Copy).then_inc(weight_t_ready.sem, 1)
                    for h in range(2 * E):
                        act.wait_ge(up_done.sem, up_done.now(b, h + 1))
                        if h >= 2:
                            act.wait_ge(down_half.sem, down_half.now(b, h - 1))
                        else:
                            act.wait_ge(down_half.sem, down_half.prev(b, 2 * E - 1 + h))
                        for m in range(HB // 2):
                            n = (h % 2) * (HB // 2) + m
                            last = nc.scalar.activation(hidden[:, h % 2, m, :], half_banks(h)[:, m, :], ACT.Relu,
                                                        bias=up_bias[:, h // 2, n:n + 1])
                        act.drain()
                        act.sem_inc(hidden_ready.sem, 1)

            @block.vector
            def _(dve):
                dve.wait_ge(weights_in, 128)
                dve.wait_ge(consts, 1)
                for s in (gap_ready, weight_ready, total_started, added, inner_var_ready):
                    s.start(dve)
                norm.start_vector(dve)
                with dve.Fori(0, B) as b:
                    dve.wait_ge(router_done.sem, router_done.now(b, 1))
                    nc.vector.tensor_tensor(logits[:], PS[:, 6, 0:TB * E].rearrange("p (t e) -> p t e", t=TB),
                                            router_bias[:, :].unsqueeze(1).to_broadcast([P, TB, E]), ALU.add)
                    dve.drain()
                    for t in range(TB):
                        top2(nc, dve, t, logits, iota8, best, index, index_f, chosen)
                    nc.vector.tensor_tensor(gap[:], best[:, :, 1], best[:, :, 0], ALU.subtract)\
                        .then_inc(gap_ready.sem, 1)
                    dve.wait_ge(exp_ready.sem, exp_ready.now(b, 1))
                    nc.vector.tensor_scalar(mix[:, :, 1], exp_gap[:], 1.0, None, ALU.add)
                    dve.drain()
                    nc.vector.reciprocal(mix[:, :, 0], mix[:, :, 1])
                    dve.drain()
                    nc.vector.tensor_tensor(mix[:, :, 1], mix[:, :, 0], exp_gap[:], ALU.mult)
                    dve.drain()
                    nc.vector.tensor_tensor(chosen[:], chosen[:], spread(mix[:], E), ALU.mult)
                    dve.drain()
                    nc.vector.tensor_tensor(weight[:], chosen[:, :, 0, :], chosen[:, :, 1, :], ALU.add)\
                        .then_inc(weight_ready.sem, 1)
                    dve.wait_ge(bias_done.sem, bias_done.now(b, 1))
                    nc.vector.tensor_copy(total[:], tiles(PS[:, 6, :])).then_inc(total_started.sem, 1)
                    for e in range(E):
                        dve.drain()
                        dve.wait_ge(down_half.sem, down_half.now(b, 2 * e + 2))
                        for t in range(TB):
                            nc.vector.scalar_tensor_tensor(total[:, t, :], tiles(PS[:, 4 + e % 2, :])[:, t, :],
                                                           weight[:, t, e:e + 1], total[:, t, :], ALU.mult, ALU.add)
                        dve.drain()
                        dve.sem_inc(added.sem, 1)
                    dve.wait_ge(norm.residual_in.sem, norm.residual_in.now(norm.turn(b), 1))
                    nc.vector.tensor_tensor(total[:], total[:], norm.x_in[:], ALU.add)
                    dve.drain()
                    for t in range(TB):
                        nc.vector.bn_stats(inner_stats[:, t, :], total[:, t, :])
                    dve.drain()
                    for t in range(TB):
                        nc.vector.bn_aggr(inner_mv[:, t, :], inner_stats[:, t, :])
                    dve.drain()
                    dve.sem_inc(inner_var_ready.sem, 1)
                    dve.wait_ge(inner_rstd_step.sem, inner_rstd_step.now(b, 2))
                    for t in range(TB):
                        nc.vector.tensor_scalar(total[:, t, :], total[:, t, :], inner_mv[:, t, 0:1],
                                                inner_rstd[:, t:t + 1], ALU.subtract, ALU.mult)
                    dve.drain()
                    for w, op in ((gamma, ALU.mult), (beta, ALU.add)):
                        nc.vector.tensor_tensor(total[:], total[:], w[:, :].unsqueeze(1).to_broadcast([P, TB, D]), op)
                        dve.drain()
                    norm.vector(dve, b, (down_half.sem, down_half.now(b, 2 * E)), source=total[:])

            @block.tensor
            def _(pe):
                pe.wait_ge(weights_in, 128)
                for s in (router_done, weight_turned, bias_done, up_done, down_half):
                    s.start(pe)
                norm.start_tensor(pe)
                mm = nc.tensor.matmul
                with pe.Fori(0, B) as b:
                    pe.wait_ge(xt_in.sem, xt_in.now(b, 1))
                    pe.wait_ge(total_started.sem, total_started.prev(b, 1))
                    for t in range(TB):
                        for c in range(KC):
                            last = mm(PS[:, 6, t * E:(t + 1) * E], xt[:, c, t * P:(t + 1) * P], router[:, c, :],
                                      start=c == 0, stop=c == KC - 1)
                    last.then_inc(router_done.sem, 1)

                    def up_half(h):
                        e = h // 2
                        if h >= 2:
                            pe.wait_ge(hidden_ready.sem, hidden_ready.now(b, h - 1))
                        else:
                            pe.wait_ge(hidden_ready.sem, hidden_ready.prev(b, 2 * E - 1 + h))
                        for m in range(HB // 2):
                            for c in range(KC):
                                last = mm(half_banks(h)[:, m, :], up[:, c, e, (h % 2) * (HB // 2) + m, :],
                                          xt[:, c, :], start=c == 0, stop=c == KC - 1)
                        last.then_inc(up_done.sem, 1)

                    up_half(0)
                    pe.wait_ge(weight_ready.sem, weight_ready.now(b, 1))
                    for t in range(TB):
                        last = nc.tensor.transpose(PS[0:E, 6, t * P:(t + 1) * P], weight[:, t, :], core.ident[:])
                    last.then_inc(weight_turned.sem, 1)
                    up_half(1)
                    pe.wait_ge(weight_t_ready.sem, weight_t_ready.now(b, 1))
                    for t in range(TB):
                        last = mm(PS[:, 6, t * D:(t + 1) * D], weight_t[0:E, t * P:(t + 1) * P], down_bias[0:E, :],
                                  start=True, stop=True)
                    last.then_inc(bias_done.sem, 1)
                    for h in range(2 * E):
                        e = h // 2
                        pe.wait_ge(hidden_ready.sem, hidden_ready.now(b, h + 1))
                        if h % 2 == 0:
                            if e >= 2:
                                pe.wait_ge(added.sem, added.now(b, e - 1))
                            else:
                                pe.wait_ge(added.sem, added.prev(b, E - 1 + e))
                        for t in range(TB):
                            for m in range(HB // 2):
                                last = mm(PS[:, 4 + e % 2, t * D:(t + 1) * D], hidden[:, h % 2, m, t * P:(t + 1) * P],
                                          down[:, e, (h % 2) * (HB // 2) + m, :],
                                          start=h % 2 == 0 and m == 0 and t == 0,
                                          stop=h % 2 == 1 and m == HB // 2 - 1, skip_group_check=True)
                        last.then_inc(down_half.sem, 1)
                        if h + 2 < 2 * E:
                            up_half(h + 2)


def program(nc, dram, out):
    core = Core(nc, dram, out)
    constants(core)
    core.end_block()
    for layer in BLOCKS:
        for build in layer:
            build(core)
            core.end_block()


BLOCKS = [
    [block_self_attention], [block_cross_attention_0], [block_experts_0],
    [block_mixer_project, block_mixer_solve, block_mixer_scan, block_mixer_mix],
    [block_cross_attention_1], [block_experts_1],
]


def layouts(a):
    f = {}
    x = a["x"].reshape(B * SEQ, D)
    f["x"], f["x_t"] = x, x.T

    def chunks(w, n=P):
        return w.reshape(w.shape[0] // n, n, -1).transpose(1, 0, 2)

    def halves(w):
        return w.reshape(-1, 4, 4, 2, 32).transpose(0, 1, 3, 2, 4).reshape(-1, 4, 2, P)

    hd = 1024
    wkv, bkv = a["L0_attn_Wkv"], a["L0_attn_bkv"]
    wqk = np.concatenate([halves(a["L0_attn_Wq"]), halves(wkv[:, :hd])], axis=2)
    f["sa_wqk"] = wqk.reshape(KC, P, 4, 4, P).transpose(1, 0, 2, 3, 4)
    bqk = np.concatenate([halves(a["L0_attn_bq"][None]), halves(bkv[None, :hd])], axis=2)[0]
    f["sa_bqk"] = bqk.transpose(2, 0, 1)
    f["sa_wv"] = chunks(wkv[:, hd:])
    f["sa_bv"] = bkv[hd:]
    f["sa_wo"] = chunks(a["L0_attn_Wo"])
    f["sa_bo"] = a["L0_attn_bo"]
    dim = 64
    inv_freq = 1.0 / np.float32(10000.0) ** (np.arange(0, dim, 2, dtype=np.float32) / np.float32(dim))
    angle = np.tile(inv_freq.astype(np.float32), 4)[:, None] * np.arange(SEQ, dtype=np.float32)[None]
    angle = angle.astype(np.float32)
    scale = np.array([dim ** -0.5, 1.0], np.float32)[None, :, None, None]
    sign = np.array([-1.0, 1.0], np.float32)[None, None, :, None]
    one = np.ones((1, 2, 2, 1), np.float32)
    f["cos"] = np.cos(angle)[:, None, None, :] * scale * one
    f["sin"] = np.sin(angle)[:, None, None, :] * scale * sign

    def padded(w):
        w = w.reshape(-1, 4, 4, 16)
        return np.concatenate([w, np.zeros_like(w)], axis=3).reshape(-1, 4, P)

    f["ctx_t"] = chunks(a["ctx_1024"].reshape(-1, D).T)
    f["key_mask"] = a["mask_BxS2_if1"]
    for to, src, turn in (("ca", "L0_xattn", True), ("cb", "L1_xattn", False)):
        w = {n: a[f"{src}_W{n}"].T if turn else a[f"{src}_W{n}"] for n in "qkvo"}
        for n in "qk":
            f[f"{to}_w{n}"] = padded(w[n]).reshape(KC, P, 4, P).transpose(1, 0, 2, 3)
            f[f"{to}_b{n}"] = padded(a[f"{src}_b{n}"][None])[0].T
        for n in "vo":
            f[f"{to}_w{n}"] = chunks(w[n])
            f[f"{to}_b{n}"] = a[f"{src}_b{n}"]

    def pad(w, axis):
        widths = [(0, 0)] * w.ndim
        widths[axis] = (0, -w.shape[axis] % P)
        return np.pad(w, widths)

    f["ea_up"] = pad(a["L0_ffn_w_up"], 1).reshape(8, 3, P, KC, P).transpose(4, 3, 0, 1, 2)
    f["ea_down"] = pad(a["L0_ffn_w_down"], 2).reshape(8, D, 3, P).transpose(3, 0, 2, 1)
    f["ea_shared_up"] = pad(a["L0_ffn_shared_w_up"], 0).reshape(3, P, KC, P).transpose(3, 2, 0, 1)
    f["ea_shared_down"] = pad(a["L0_ffn_shared_w_down"], 1).reshape(D, 3, P).transpose(2, 1, 0)
    f["ea_gate"] = chunks(a["L0_ffn_gate_w"].T)
    f["ea_gate_bias"] = a["L0_ffn_expert_bias"]
    f["eb_up"] = a["L1_ffn_W1"].reshape(8, 8, P, KC, P).transpose(4, 3, 0, 1, 2)
    f["eb_up_bias"] = a["L1_ffn_b1"].reshape(8, 8, P).transpose(2, 0, 1)
    f["eb_down"] = a["L1_ffn_W2"].reshape(8, D, 8, P).transpose(3, 0, 2, 1)
    f["eb_down_bias"] = a["L1_ffn_b2"]
    f["eb_router"] = chunks(a["L1_ffn_Wr"].T)
    f["eb_router_bias"] = a["L1_ffn_br"]
    qkv = np.stack([a[f"L1_attn_W{n}"] for n in "qkv"], axis=1)
    f["mp_w"] = qkv.reshape(KC, P, 3, KC, P).transpose(1, 0, 2, 3, 4)
    f["mp_w_beta"] = chunks(a["L1_attn_Wb"])
    conv = np.stack([a[f"L1_attn_conv_{n}_w"] for n in "qkv"])
    f["mp_conv_w"] = conv.reshape(3, KC, P, CONV).transpose(2, 0, 1, 3)
    f["mp_local_w"], f["mp_mid_w"] = chunks(a["L1_attn_local_w"]), chunks(a["L1_attn_mid_w"])
    f["mm_w1"] = pad(pad(a["L1_attn_r_w1"], 0), 1).reshape(KC + 1, P, 5, P).transpose(1, 0, 2, 3)
    f["mm_b1"] = pad(a["L1_attn_r_b1"], 0).reshape(5, P).T
    f["mm_w2"] = chunks(pad(a["L1_attn_r_w2"], 0))
    f["mm_b2"] = a["L1_attn_r_b2"]
    f["mm_mix_w"], f["mm_onorm_w"] = a["L1_attn_mix_w"].reshape(-1), a["L1_attn_onorm_w"]
    f["mm_wo"] = chunks(a["L1_attn_Wo"])
    f["eb_gamma"], f["eb_beta"] = a["L1_ffn_gamma"], a["L1_ffn_beta"]
    return f


def kernel(**inputs):
    import concourse.bacc as bacc
    from concourse.bass_utils import run_bass_kernel_spmd

    f = layouts({k: np.asarray(v) for k, v in inputs.items()})
    nc = bacc.Bacc("TRN2", target_bir_lowering=False, num_devices=1)
    arrays, dram = {}, {}
    for name, v in f.items():
        v = np.ascontiguousarray(v)
        arrays["in_" + name] = v
        dram[name] = nc.dram_tensor("in_" + name, v.shape, mybir.dt.from_np(v.dtype), kind="ExternalInput").ap()
    out = nc.dram_tensor("out", (B * SEQ, D), F32, kind="ExternalOutput").ap()
    program(nc, dram, out)
    r = run_bass_kernel_spmd(nc, [arrays], core_ids=[0])
    return r.results[0]["out"].reshape(B, SEQ, D)
```

```python
from contextlib import ExitStack

import numpy as np

import concourse.bass as bass
from concourse import mybir

F32 = mybir.dt.float32
BF16 = mybir.dt.bfloat16
I32 = mybir.dt.int32
ALU = mybir.AluOpType
ACT = mybir.ActivationFunctionType
AX = mybir.AxisListType

P = 128
B = 8
SEQ = 256
D = 256
KC = D // P
TB = SEQ // P
LN_EPS = 1e-5
NEG = -1e30


class Signal:

    def __init__(self, core, name, per, unit=1):
        self.sem = core.semaphore(name)
        self.per, self.unit = per, unit

    def start(self, eng):
        eng.sem_inc(self.sem, self.per * self.unit)

    def now(self, i, k):
        return (i + 1) * (self.per * self.unit) + k * self.unit

    def prev(self, i, k):
        return i * (self.per * self.unit) + k * self.unit


def spread(ap, n):
    return ap.unsqueeze(len(ap.shape)).to_broadcast(list(ap.shape) + [n])


class Core:

    def __init__(self, nc, dram, out):
        self.nc, self.dram, self.out = nc, dram, out
        self.block_semaphores = []
        self.PS = nc.alloc_psum_tensor("PS", [P, 8, 512], F32)
        self.ident = nc.alloc_sbuf_tensor("ident", [P, P], F32)
        self.ident16 = nc.alloc_sbuf_tensor("ident16", [P, P], BF16)
        self.minus_half = nc.alloc_sbuf_tensor("minus_half", [P, 16], F32)
        self.eps = nc.alloc_sbuf_tensor("eps", [P, 16], F32)
        self.X = nc.alloc_sbuf_tensor("X", [P, B * TB, D], F32)
        self.XT = nc.alloc_sbuf_tensor("XT", [P, KC, B * SEQ], F32)

        self.norm_signals = {
            name: Signal(self, name, per, unit) for name, per, unit in (
                ("residual_in", 1, 16), ("residual_used", 1, 1), ("var_ready", 1, 1), ("rstd_step", 2, 1),
                ("x_ready", 1, 1), ("transposed", 1, 1), ("xt_ready", 1, 1), ("stored", 2, 16), ("left", 1, 1))}
        self.block_semaphores = []

    def semaphore(self, name):
        self.block_semaphores.append(self.nc.alloc_semaphore(name))
        return self.block_semaphores[-1]

    def end_block(self):
        self.nc.clear_and_free_semaphores(self.block_semaphores)
        self.nc.all_engine_barrier()
        self.block_semaphores = []

    def x_of(self, b):
        return self.X[:, bass.ds(b * TB, TB), :]

    def xt_of(self, b):
        return self.XT[:, :, bass.ds(b * SEQ, SEQ)]


def constants(core):
    nc = core.nc
    loaded = core.semaphore("first_activations_loaded")
    zeroed = core.semaphore("identities_zeroed")
    with nc.Block() as block:
        @block.sync
        def _(sp):
            sp.dma_start(core.X[:], core.dram["x"].rearrange("(n p) d -> p n d", p=P)).then_inc(loaded, 16)
            sp.dma_start(core.XT[:], core.dram["x_t"].rearrange("(c p) n -> p c n", p=P)).then_inc(loaded, 16)
            sp.wait_ge(loaded, 32)

        @block.gpsimd
        def _(pool):
            nc.gpsimd.memset(core.minus_half[:], -0.5)
            nc.gpsimd.memset(core.eps[:], LN_EPS)
            nc.gpsimd.memset(core.ident[:], 0.0).then_inc(zeroed, 1)
            nc.gpsimd.memset(core.ident16[:], 0.0).then_inc(zeroed, 1)
            pool.wait_ge(zeroed, 2)
            for eye in (core.ident, core.ident16):
                nc.gpsimd.affine_select(out=eye[:], in_=eye[:], compare_op=ALU.not_equal, fill=1.0,
                                        base=0, pattern=[[-1, P]], channel_multiplier=1)


class Norm:

    def __init__(self, core, ctx, name, layer, bank, bias=None):
        nc = core.nc
        self.core, self.bank, self.bias = core, bank, bias

        def sb(n, shape, dt=F32):
            return ctx.enter_context(nc.sbuf_tensor(f"{name}_norm_{n}", shape, dt))

        self.x_in = sb("x_in", [P, TB, D])
        self.y = sb("y", [P, TB, D])
        self.x_new = sb("x_new", [P, TB, D])
        self.xt_new = sb("xt_new", [P, KC, SEQ])
        self.stats = sb("stats", [P, TB, 6])
        self.mean_var = sb("mean_var", [P, TB, 2])
        self.rstd = sb("rstd", [P, TB])
        self.layer = layer
        s = core.norm_signals
        self.residual_in, self.residual_used, self.var_ready = s["residual_in"], s["residual_used"], s["var_ready"]
        self.rstd_step, self.x_ready, self.transposed = s["rstd_step"], s["x_ready"], s["transposed"]
        self.xt_ready, self.stored, self.left = s["xt_ready"], s["stored"], s["left"]

    def turn(self, b):
        return b + self.layer * B

    def start(self, eng, *signals):
        if self.layer == 0:
            for s in signals:
                s.start(eng)

    def start_sync(self, sp):
        self.start(sp, self.residual_in, self.stored, self.left)

    def load(self, sp, b):
        sp.wait_ge(self.residual_used.sem, self.residual_used.prev(self.turn(b), 1))
        sp.dma_start(self.x_in[:], self.core.x_of(b)).then_inc(self.residual_in.sem, 16)

    def store(self, sp, b, last=False):
        sp.wait_ge(self.x_ready.sem, self.x_ready.now(self.turn(b), 1))
        if last:
            for t in range(TB):
                sp.dma_start(self.core.out[bass.ds(b * SEQ + t * P, P), :],
                             self.x_new[:, t, :]).then_inc(self.stored.sem, 16)
        else:
            sp.dma_start(self.core.x_of(b), self.x_new[:]).then_inc(self.stored.sem, 16)
            sp.wait_ge(self.xt_ready.sem, self.xt_ready.now(self.turn(b), 1))
            sp.dma_start(self.core.xt_of(b), self.xt_new[:]).then_inc(self.stored.sem, 16)
        sp.wait_ge(self.stored.sem, self.stored.now(self.turn(b), 2))
        sp.sem_inc(self.left.sem, 1)

    def start_vector(self, dve):
        self.start(dve, self.residual_used, self.var_ready, self.x_ready)

    def vector(self, dve, b, out_ready, source=None):
        nc = self.core.nc
        if source is None:
            source = self.core.PS[:, self.bank, :].rearrange("p (t d) -> p t d", t=TB)
        dve.wait_ge(self.residual_in.sem, self.residual_in.now(self.turn(b), 1))
        dve.wait_ge(*out_ready)
        nc.vector.tensor_tensor(self.y[:], source, self.x_in[:], ALU.add).then_inc(self.residual_used.sem, 1)
        dve.drain()
        if self.bias is not None:
            nc.vector.tensor_tensor(self.y[:], self.y[:], self.bias[:, :].unsqueeze(1).to_broadcast([P, TB, D]),
                                    ALU.add)
            dve.drain()
        for t in range(TB):
            nc.vector.bn_stats(self.stats[:, t, :], self.y[:, t, :])
        dve.drain()
        for t in range(TB):
            nc.vector.bn_aggr(self.mean_var[:, t, :], self.stats[:, t, :])
        dve.drain()
        dve.sem_inc(self.var_ready.sem, 1)
        dve.wait_ge(self.rstd_step.sem, self.rstd_step.now(self.turn(b), 2))
        dve.wait_ge(self.left.sem, self.left.prev(self.turn(b), 1))
        for t in range(TB):
            nc.vector.tensor_scalar(self.x_new[:, t, :], self.y[:, t, :], self.mean_var[:, t, 0:1],
                                    self.rstd[:, t:t + 1], ALU.subtract, ALU.mult)
        dve.drain()
        dve.sem_inc(self.x_ready.sem, 1)

    def start_gpsimd(self, pool):
        self.start(pool, self.rstd_step)

    def gpsimd(self, pool, b):
        nc = self.core.nc
        pool.wait_ge(self.var_ready.sem, self.var_ready.now(self.turn(b), 1))
        nc.gpsimd.tensor_tensor(self.rstd[:], self.mean_var[:, :, 1], self.core.eps[:, 0:TB],
                                ALU.add).then_inc(self.rstd_step.sem, 1)
        pool.wait_ge(self.rstd_step.sem, self.rstd_step.now(self.turn(b), 1))
        nc.gpsimd.tensor_tensor(self.rstd[:], self.rstd[:], self.core.minus_half[:, 0:TB],
                                ALU.pow).then_inc(self.rstd_step.sem, 1)

    def start_tensor(self, pe):
        self.start(pe, self.transposed)

    def tensor(self, pe, b):
        nc = self.core.nc
        pe.wait_ge(self.x_ready.sem, self.x_ready.now(self.turn(b), 1))
        for c in range(KC):
            for t in range(TB):
                last = nc.tensor.transpose(self.core.PS[:, self.bank, (c * TB + t) * P:(c * TB + t + 1) * P],
                                           self.x_new[:, t, c * P:(c + 1) * P], self.core.ident[:])
        last.then_inc(self.transposed.sem, 1)

    def start_scalar(self, act):
        self.start(act, self.xt_ready)

    def scalar(self, act, b):
        nc = self.core.nc
        act.wait_ge(self.transposed.sem, self.transposed.now(self.turn(b), 1))
        act.wait_ge(self.left.sem, self.left.prev(self.turn(b), 1))
        nc.scalar.activation(self.xt_new[:].rearrange("p c n -> p (c n)"), self.core.PS[:, self.bank, :],
                             ACT.Copy).then_inc(self.xt_ready.sem, 1)


def block_self_attention(core):
    H, DH = 16, 64
    NP, HD = H // 2, H * DH
    WIDE = DH + 1
    PARTS = 3
    DEEP = 4
    nc, PS, dram = core.nc, core.PS, core.dram
    with ExitStack() as ctx:
        def sb(n, shape, dt=F32):
            return ctx.enter_context(nc.sbuf_tensor(f"sa_{n}", shape, dt))

        wqk = sb("wqk", [P, KC, NP, 2, P])
        wv = sb("wv", [P, KC, HD])
        wo = sb("wo", [P, NP, D])
        bqk = sb("bqk", [P, NP, 2])
        bv = sb("bv", [P, HD])
        bo = sb("bo", [P, D])
        cos = sb("cos", [P, 2, SEQ])
        sin = sb("sin", [P, 2, SEQ])
        mask_qk = sb("mask_qk", [P, P], BF16)
        mask_kq = sb("mask_kq", [P, P], BF16)
        sel32 = sb("sel32", [P, PARTS, 2, P])
        sel = sb("sel", [P, 2, P], BF16)
        xt = sb("xt", [P, KC, SEQ])
        v = sb("v", [P, TB, H, WIDE])
        raw = sb("raw", [P, DEEP, 2, SEQ])
        swapped = sb("swapped", [P, DEEP, 2, SEQ])
        rot1 = sb("rot1", [P, 2, SEQ])
        q = sb("q", [P, DEEP, SEQ])
        k = sb("k", [P, DEEP, 2, SEQ])
        neg_max = sb("neg_max", [P, TB, 2])
        rest = sb("rest", [P, 2, TB, 2])
        max_parts = sb("max_parts", [P, TB, PARTS, 2], BF16)
        max_t = sb("max_t", [P, SEQ], BF16)
        probs = sb("probs", [P, 2, 2, 384])
        rden = sb("rden", [P, TB, 2])
        o = sb("o", [P, TB, 2, DH])
        ot = sb("ot", [P, NP, SEQ])
        norm = Norm(core, ctx, "sa", 0, 6, bias=bo)

        weights_in = core.semaphore("sa_weights_in")
        consts = core.semaphore("sa_constants_ready")
        sel_ready = core.semaphore("sa_selector_ready")
        xt_in = Signal(core, "sa_xt_in", 1, 16)
        v_done = Signal(core, "sa_v_projected", 1)
        v_ready = Signal(core, "sa_v_ready", 1)
        qk_done = Signal(core, "sa_qk_projected", NP)
        raw_ready = Signal(core, "sa_raw_ready", NP)
        swap_ready = Signal(core, "sa_swapped_ready", NP)
        raw_used = Signal(core, "sa_raw_used", NP)
        qk_ready = Signal(core, "sa_qk_rotated", NP)
        s_done = Signal(core, "sa_scores_for_max", NP)
        max_ready = Signal(core, "sa_max_ready", NP)
        maxt_done = Signal(core, "sa_max_transposed", NP)
        maxt_ready = Signal(core, "sa_max_row_ready", NP)
        st_done = Signal(core, "sa_scores_ready", NP)
        probs_ready = Signal(core, "sa_probs_ready", NP)
        o_done = Signal(core, "sa_o_done", NP)
        o_ready = Signal(core, "sa_o_ready", NP)
        ot_done = Signal(core, "sa_o_transposed", NP)
        ot_ready = Signal(core, "sa_ot_ready", NP)
        out_done = Signal(core, "sa_out_done", 1)

        def ago(signal, b, p, n):
            return signal.now(b, p + 1 - n) if p >= n else signal.prev(b, NP + p + 1 - n)

        def turned_max():
            return PS[:, 5, :].bitcast(BF16)

        with nc.Block() as block:
            @block.sync
            def _(sp):
                for dst, name in ((wv, "sa_wv"), (wqk, "sa_wqk"), (bqk, "sa_bqk"), (cos, "cos"), (sin, "sin"),
                                  (wo, "sa_wo")):
                    sp.dma_start(dst[:], dram[name]).then_inc(weights_in, 16)
                sp.dma_start(bv[:], dram["sa_bv"].partition_broadcast(P)).then_inc(weights_in, 16)
                sp.dma_start(bo[:], dram["sa_bo"].partition_broadcast(P)).then_inc(weights_in, 16)
                xt_in.start(sp)
                norm.start_sync(sp)
                with sp.Fori(0, B) as b:
                    sp.wait_ge(v_done.sem, v_done.prev(b, 1))
                    sp.wait_ge(qk_done.sem, qk_done.prev(b, NP))
                    sp.dma_start(xt[:], core.xt_of(b)).then_inc(xt_in.sem, 16)
                    norm.load(sp, b)
                    norm.store(sp, b)

            @block.gpsimd
            def _(pool):
                nc.gpsimd.memset(mask_qk[:], 0.0).then_inc(consts, 1)
                nc.gpsimd.memset(mask_kq[:], 0.0).then_inc(consts, 1)
                nc.gpsimd.memset(sel32[:], 0.0).then_inc(consts, 1)
                nc.gpsimd.memset(max_t[:], 0.0).then_inc(consts, 1)
                nc.gpsimd.memset(k[:], 0.0).then_inc(consts, 1)
                nc.gpsimd.memset(v[:, :, :, DH:WIDE], 1.0).then_inc(consts, 1)
                pool.wait_ge(consts, 6)
                nc.gpsimd.affine_select(out=mask_qk[:], in_=mask_qk[:], compare_op=ALU.is_ge, fill=NEG,
                                        base=0, pattern=[[-1, P]], channel_multiplier=1).then_inc(consts, 1)
                nc.gpsimd.affine_select(out=mask_kq[:], in_=mask_kq[:], compare_op=ALU.is_ge, fill=NEG,
                                        base=0, pattern=[[1, P]], channel_multiplier=-1).then_inc(consts, 1)
                nc.gpsimd.affine_select(out=sel32[:], in_=sel32[:], compare_op=ALU.not_equal, fill=1.0, base=0,
                                        pattern=[[-2, PARTS], [-1, 2], [0, P]], channel_multiplier=1)\
                    .then_inc(consts, 1)
                pool.wait_ge(weights_in, 128)
                swap_ready.start(pool)
                norm.start_gpsimd(pool)
                with pool.Fori(0, B) as b:
                    for p in range(NP):
                        pool.wait_ge(raw_ready.sem, raw_ready.now(b, p + 1))
                        pool.wait_ge(raw_used.sem, ago(raw_used, b, p, DEEP))
                        for to in range(4):
                            source = to ^ 1
                            nc.gpsimd.tensor_tensor(swapped[32 * to:32 * to + 32, p % DEEP, :, :],
                                                    raw[32 * source:32 * source + 32, p % DEEP, :, :],
                                                    sin[32 * source:32 * source + 32, :, :], ALU.mult)
                        pool.drain()
                        pool.sem_inc(swap_ready.sem, 1)
                    norm.gpsimd(pool, b)

            @block.scalar
            def _(act):
                act.wait_ge(weights_in, 128)
                act.wait_ge(consts, 9)
                for s in (raw_ready, maxt_ready, probs_ready, ot_ready):
                    s.start(act)
                norm.start_scalar(act)
                with act.Fori(0, B) as b:
                    def evacuate_qk(p):
                        act.wait_ge(qk_done.sem, qk_done.now(b, p + 1))
                        act.wait_ge(raw_used.sem, ago(raw_used, b, p, DEEP))
                        for n in range(2):
                            nc.scalar.activation(raw[:, p % DEEP, n, :], PS[:, 6 + p % 2, n * SEQ:(n + 1) * SEQ],
                                                 ACT.Identity, bias=bqk[:, p, n:n + 1])
                        act.drain()
                        act.sem_inc(raw_ready.sem, 1)

                    def evacuate_ot(p):
                        act.wait_ge(ot_done.sem, ot_done.now(b, p + 1))
                        if p == 0:
                            act.wait_ge(out_done.sem, out_done.prev(b, 1))
                        nc.scalar.activation(ot[:, p, :], PS[:, 5, 0:SEQ], ACT.Identity).then_inc(ot_ready.sem, 1)

                    for p in range(3):
                        evacuate_qk(p)
                    for p in range(NP):
                        if p >= 2:
                            evacuate_ot(p - 2)
                        if p + 3 < NP:
                            evacuate_qk(p + 3)
                        act.wait_ge(maxt_done.sem, maxt_done.now(b, p + 1))
                        nc.scalar.activation(max_t[0:2 * PARTS, :], turned_max()[0:2 * PARTS, 0:SEQ], ACT.Identity)\
                            .then_inc(maxt_ready.sem, 1)
                        act.wait_ge(st_done.sem, st_done.now(b, p + 1))
                        act.wait_ge(o_done.sem, ago(o_done, b, p, 2))
                        nc.scalar.activation(probs[:, p % 2, :, :], PS[:, 2:4, 0:384], ACT.Exp)\
                            .then_inc(probs_ready.sem, 1)
                    evacuate_ot(NP - 2)
                    evacuate_ot(NP - 1)
                    norm.scalar(act, b)

            @block.vector
            def _(dve):
                dve.wait_ge(weights_in, 128)
                dve.wait_ge(consts, 9)
                nc.vector.tensor_tensor(sel[:], sel32[:, 0, :, :], sel32[:, 1, :, :], ALU.add)
                dve.drain()
                nc.vector.tensor_tensor(sel[:], sel[:], sel32[:, 2, :, :], ALU.add).then_inc(sel_ready, 1)
                for s in (v_ready, raw_used, qk_ready, max_ready, o_ready):
                    s.start(dve)
                norm.start_vector(dve)
                with dve.Fori(0, B) as b:
                    dve.wait_ge(o_done.sem, o_done.prev(b, NP))
                    dve.wait_ge(v_done.sem, v_done.now(b, 1))
                    for t in range(TB):
                        for h8 in (0, 8):
                            nc.vector.tensor_tensor(v[:, t, h8:h8 + 8, 0:DH],
                                                    PS[:, 2 * t + h8 // 8, :].rearrange("p (h d) -> p h d", d=DH),
                                                    bv[:, h8 * DH:(h8 + 8) * DH].rearrange("p (h d) -> p h d", d=DH),
                                                    ALU.add)
                    dve.drain()
                    dve.sem_inc(v_ready.sem, 1)

                    def rotate(p):
                        dve.wait_ge(raw_ready.sem, raw_ready.now(b, p + 1))
                        nc.vector.tensor_tensor(rot1[:], raw[:, p % DEEP, :, :], cos[:], ALU.mult)
                        dve.drain()
                        dve.wait_ge(swap_ready.sem, swap_ready.now(b, p + 1))
                        dve.wait_ge(st_done.sem, ago(st_done, b, p, DEEP))
                        nc.vector.tensor_tensor(q[:, p % DEEP, :], rot1[:, 0, :], swapped[:, p % DEEP, 0, :], ALU.add)
                        for h in range(2):
                            rows = slice(DH * h, DH * h + DH)
                            nc.vector.tensor_tensor(k[rows, p % DEEP, h, :], rot1[rows, 1, :],
                                                    swapped[rows, p % DEEP, 1, :], ALU.add)
                        dve.drain()
                        dve.sem_inc(raw_used.sem, 1)
                        dve.sem_inc(qk_ready.sem, 1)

                    def maxima(p):
                        dve.wait_ge(s_done.sem, s_done.now(b, p + 1))
                        dve.wait_ge(maxt_done.sem, ago(maxt_done, b, p, 1))
                        for t in range(TB):
                            nc.vector.tensor_reduce(neg_max[:, t, :], PS[:, t, 0:(t + 1) * SEQ]
                                                    .rearrange("p (h n) -> p h n", h=2), AX.X, ALU.max, negate=True)
                        dve.drain()
                        nc.vector.tensor_copy(max_parts[:, :, 0, :], neg_max[:])
                        dve.drain()
                        nc.vector.tensor_tensor(rest[:, 0, :, :], neg_max[:], max_parts[:, :, 0, :], ALU.subtract)
                        dve.drain()
                        nc.vector.tensor_copy(max_parts[:, :, 1, :], rest[:, 0, :, :])
                        dve.drain()
                        nc.vector.tensor_tensor(max_parts[:, :, 2, :], rest[:, 0, :, :], max_parts[:, :, 1, :],
                                                ALU.subtract).then_inc(max_ready.sem, 1)

                    def normalize(p):
                        dve.wait_ge(o_done.sem, o_done.now(b, p + 1))
                        wide = PS[:, 4, 0:4 * WIDE].rearrange("p (t h d) -> p t h d", t=TB, h=2)
                        nc.vector.reciprocal(rden[:], wide[:, :, :, DH])
                        dve.drain()
                        dve.wait_ge(ot_done.sem, ago(ot_done, b, p, 1))
                        nc.vector.tensor_tensor(o[:], wide[:, :, :, 0:DH], spread(rden[:], DH), ALU.mult)\
                            .then_inc(o_ready.sem, 1)

                    rotate(0)
                    rotate(1)
                    maxima(0)
                    for p in range(NP):
                        if p + 2 < NP:
                            rotate(p + 2)
                        if p + 1 < NP:
                            maxima(p + 1)
                        if p:
                            normalize(p - 1)
                    normalize(NP - 1)
                    norm.vector(dve, b, (out_done.sem, out_done.now(b, 1)))

            @block.tensor
            def _(pe):
                pe.wait_ge(weights_in, 128)
                pe.wait_ge(consts, 9)
                pe.wait_ge(sel_ready, 1)
                for s in (v_done, qk_done, s_done, maxt_done, st_done, o_done, ot_done, out_done):
                    s.start(pe)
                norm.start_tensor(pe)
                mm = nc.tensor.matmul
                with pe.Fori(0, B) as b:
                    pe.wait_ge(xt_in.sem, xt_in.now(b, 1))
                    pe.wait_ge(max_ready.sem, max_ready.prev(b, NP))
                    pe.wait_ge(probs_ready.sem, probs_ready.prev(b, NP))
                    for t in range(TB):
                        for half in range(2):
                            for c in range(KC):
                                last = mm(PS[:, 2 * t + half, :], xt[:, c, t * P:(t + 1) * P],
                                          wv[:, c, half * 512:(half + 1) * 512], start=c == 0, stop=c == KC - 1)
                    last.then_inc(v_done.sem, 1)

                    def project(p):
                        if p < 2:
                            pe.wait_ge(norm.xt_ready.sem, norm.xt_ready.prev(norm.turn(b), 1))
                        pe.wait_ge(raw_ready.sem, ago(raw_ready, b, p, 2))
                        for n in range(2):
                            for c in range(KC):
                                last = mm(PS[:, 6 + p % 2, n * SEQ:(n + 1) * SEQ], wqk[:, c, p, n, :],
                                          xt[:, c, :], start=c == 0, stop=c == KC - 1)
                        last.then_inc(qk_done.sem, 1)

                    def scores_for_max(p):
                        pe.wait_ge(qk_ready.sem, qk_ready.now(b, p + 1))
                        if p == 0:
                            pe.wait_ge(v_ready.sem, v_ready.now(b, 1))
                        else:
                            pe.wait_ge(max_ready.sem, max_ready.now(b, p))
                        for t in range(TB):
                            keys = (t + 1) * P
                            mm(PS[:, t, 0:2 * keys], q[:, p % DEEP, t * P:(t + 1) * P], k[:, p % DEEP, :, 0:keys],
                               start=True, stop=False, skip_group_check=True)
                            diagonal = PS[:, t, 0:2 * keys].rearrange("p (h n) -> p h n", h=2)[:, :, t * P:keys]
                            last = mm(diagonal, core.ident16[:], mask_qk[:, :].unsqueeze(1).to_broadcast([P, 2, P]),
                                      start=False, stop=True, skip_group_check=True)
                        last.then_inc(s_done.sem, 1)

                    def turn_max(p):
                        pe.wait_ge(max_ready.sem, max_ready.now(b, p + 1))
                        pe.wait_ge(ot_ready.sem, ot_ready.now(b, p - 1) if p >= 2 else ot_ready.prev(b, NP))
                        for t in range(TB):
                            last = nc.tensor.transpose(turned_max()[0:2 * PARTS, t * P:(t + 1) * P],
                                                       max_parts[:, t, :, :].rearrange("p a h -> p (a h)"),
                                                       core.ident16[:])
                        last.then_inc(maxt_done.sem, 1)

                    def scores(p):
                        if p == 0:
                            pe.wait_ge(v_ready.sem, v_ready.now(b, 1))
                        else:
                            pe.wait_ge(probs_ready.sem, probs_ready.now(b, p))
                        for h in range(2):
                            mm(PS[:, 2 + h, 0:SEQ], k[:, p % DEEP, h, 0:P], q[:, p % DEEP, :], start=True, stop=False,
                               skip_group_check=True)
                            mm(PS[:, 2 + h, SEQ:384], k[:, p % DEEP, h, P:SEQ], q[:, p % DEEP, P:SEQ], start=False,
                               stop=False, skip_group_check=True)
                            mm(PS[:, 2 + h, 0:512].rearrange("p (a n) -> p a n", a=2)[:, :, 0:P], core.ident16[:],
                               mask_kq[:, :].unsqueeze(1).to_broadcast([P, 2, P]), start=False, stop=False,
                               skip_group_check=True)
                        pe.wait_ge(maxt_ready.sem, maxt_ready.now(b, p + 1))
                        for h in range(2):
                            mm(PS[:, 2 + h, 0:SEQ], sel[:, h, :], max_t[:, :], start=False, stop=True,
                               skip_group_check=True)
                            last = mm(PS[:, 2 + h, SEQ:384], sel[:, h, :], max_t[:, P:SEQ], start=False, stop=True,
                                      skip_group_check=True)
                        last.then_inc(st_done.sem, 1)

                    def outputs(p):
                        pe.wait_ge(probs_ready.sem, probs_ready.now(b, p + 1))
                        pe.wait_ge(o_ready.sem, ago(o_ready, b, p, 1))
                        for t in range(TB):
                            parts = [(0, 0)] if t == 0 else [(P, 0), (SEQ, 1)]
                            for h in range(2):
                                at = (t * 2 + h) * WIDE
                                for m, (col, kt) in enumerate(parts):
                                    last = mm(PS[:, 4, at:at + WIDE], probs[:, p % 2, h, col:col + P],
                                              v[:, kt, 2 * p + h, :], start=m == 0, stop=m == len(parts) - 1)
                        last.then_inc(o_done.sem, 1)

                    def turn_outputs(p):
                        pe.wait_ge(o_ready.sem, o_ready.now(b, p + 1))
                        pe.wait_ge(maxt_ready.sem, maxt_ready.now(b, min(p + 2, NP)))
                        pe.wait_ge(ot_ready.sem, ago(ot_ready, b, p, 1))
                        for t in range(TB):
                            last = nc.tensor.transpose(PS[:, 5, t * P:(t + 1) * P],
                                                       o[:, t, :, :].rearrange("p h d -> p (h d)"), core.ident[:])
                        last.then_inc(ot_done.sem, 1)

                    for p in range(3):
                        project(p)
                    scores_for_max(0)
                    for p in range(NP):
                        if p + 1 < NP:
                            scores_for_max(p + 1)
                        if p >= 2:
                            turn_outputs(p - 2)
                        if p + 3 < NP:
                            project(p + 3)
                        turn_max(p)
                        scores(p)
                        if p:
                            outputs(p - 1)
                    outputs(NP - 1)
                    turn_outputs(NP - 2)
                    turn_outputs(NP - 1)
                    pe.wait_ge(raw_ready.sem, raw_ready.now(b, NP))
                    pe.wait_ge(ot_ready.sem, ot_ready.now(b, NP))
                    for t in range(TB):
                        for c in range(NP):
                            last = mm(PS[:, 6, t * D:(t + 1) * D], ot[:, c, t * P:(t + 1) * P], wo[:, c, :],
                                      start=c == 0, stop=c == NP - 1)
                    last.then_inc(out_done.sem, 1)
                    norm.tensor(pe, b)


def cross_attention(core, name, half, dram_name):
    H, DH, G, CTX = 16, 16, 4, 77
    NG = H // G
    WIDE = DH + 1
    nc, PS, dram = core.nc, core.PS, core.dram
    PD = BF16 if half else F32
    with ExitStack() as ctx:
        def sb(n, shape, dt=F32):
            return ctx.enter_context(nc.sbuf_tensor(f"{name}_{n}", shape, dt))

        def sig(n, per, unit=1):
            return Signal(core, f"{name}_{n}", per, unit)

        shapes = {"wq": [P, KC, NG, P], "wk": [P, KC, NG, P], "wv": [P, KC, D], "wo": [P, KC, D]}
        w32 = {n: sb(n, s) for n, s in shapes.items()}
        w = {n: sb(n + "16", s, BF16) for n, s in shapes.items()} if half else w32
        bias_shapes = {"bq": [P, NG], "bk": [P, NG], "bv": [P, D], "bo": [P, D]}
        b32 = {n: sb(n, s) for n, s in bias_shapes.items()}
        b16 = {n: sb(n + "16", s, BF16) for n, s in bias_shapes.items()} if half else None
        sel = sb("sel", [P, H, CTX])
        xt_in_tile = sb("xt", [P, KC, SEQ])
        ct_in_tile = sb("ct", [P, KC, CTX])
        xt = sb("xt16", [P, KC, SEQ], BF16) if half else xt_in_tile
        ct = sb("ct16", [P, KC, CTX], BF16) if half else ct_in_tile
        q = sb("q", [P, NG, SEQ], PD)
        k = sb("k", [P, NG, CTX], PD)
        v = sb("v", [P, H, WIDE])
        neg_max = sb("neg_max", [P, TB, H])
        max_t = sb("max_t", [P, SEQ])
        probs = sb("probs", [P, G, NG, SEQ])
        rden = sb("rden", [P, TB, H])
        o = sb("o", [P, TB, D])
        ot = sb("ot", [P, KC, SEQ], PD)
        if half:
            q_round = sb("q_round", [P, NG, SEQ], BF16)
            k_round = sb("k_round", [P, NG, CTX], BF16)
            v_round = sb("v_round", [P, D], BF16)
            v16 = sb("v16", [P, D], BF16)
            out_round = sb("out_round", [P, TB, D], BF16)
            out16 = sb("out16", [P, TB, D], BF16)
            causal_qk = sb("causal_qk", [P, CTX])
            causal_kq = sb("causal_kq", [P, SEQ])
            keys_row = sb("keys_row", [P, CTX], I32)
            keys_col = sb("keys_col", [P, 1], I32)
            keymask_row = sb("keymask_row", [P, CTX])
            keymask_col = sb("keymask_col", [P, 1])
            mask_qk = sb("mask_qk", [P, TB, CTX], BF16)
            mask_kq = sb("mask_kq", [P, SEQ], BF16)
        norm = Norm(core, ctx, name, 4 if half else 1, 3, bias=None if half else b32["bo"])

        weights_in = core.semaphore(f"{name}_weights_in")
        n_weights = len(w32) + len(b32)
        consts = core.semaphore(f"{name}_constants_ready")
        n_consts = 10 if half else 4
        inputs_in = sig("inputs_in", 4 if half else 2, 16)
        inputs_ready = sig("inputs_ready", 1)
        qkv_done = sig("qkv_projected", 1)
        rounded = sig("projections_rounded", 1)
        qkv_ready = sig("qkv_ready", 1)
        s_done = sig("scores_for_max", TB)
        max_ready = sig("max_ready", 1)
        maxt_done = sig("max_transposed", 1)
        maxt_ready = sig("max_rows_ready", 1)
        st_done = sig("scores_ready", 2)
        probs_ready = sig("probs_ready", 2)
        o_done = sig("o_done", 1)
        o_ready = sig("o_ready", 1)
        ot_done = sig("o_transposed", 1)
        ot_ready = sig("ot_ready", 1)
        out_done = sig("out_done", 1)
        if half:
            out_rounded = sig("out_rounded", 1)

        def q_banks():
            return PS[:, 4:6, :].rearrange("p a (g n) -> p (a g) n", n=SEQ)

        def k_bank():
            return PS[:, 6, 0:NG * CTX].rearrange("p (g n) -> p g n", n=CTX)

        with nc.Block() as block:
            @block.sync
            def _(sp):
                for n in ("wq", "wk", "wv", "wo", "bq", "bk"):
                    sp.dma_start({**w32, **b32}[n][:], dram[f"{dram_name}_{n}"]).then_inc(weights_in, 16)
                for n in ("bv", "bo"):
                    sp.dma_start(b32[n][:], dram[f"{dram_name}_{n}"].partition_broadcast(P)).then_inc(weights_in, 16)
                inputs_in.start(sp)
                norm.start_sync(sp)
                with sp.Fori(0, B) as b:
                    if half:
                        sp.wait_ge(qkv_ready.sem, qkv_ready.prev(b, 1))
                        sp.dma_start(keys_row[:], dram["key_mask"][bass.ds(b, 1), :]
                                     .rearrange("a n -> (a n)").partition_broadcast(P)).then_inc(inputs_in.sem, 16)
                        sp.dma_start(keys_col[0:CTX, :], dram["key_mask"][bass.ds(b, 1), :]
                                     .rearrange("a n -> n a")).then_inc(inputs_in.sem, 16)
                    sp.wait_ge(qkv_done.sem, qkv_done.prev(b, 1))
                    sp.dma_start(xt_in_tile[:], core.xt_of(b)).then_inc(inputs_in.sem, 16)
                    sp.dma_start(ct_in_tile[:], dram["ctx_t"][:, :, bass.ds(b * CTX, CTX)]).then_inc(inputs_in.sem, 16)
                    norm.load(sp, b)
                    norm.store(sp, b)

            @block.gpsimd
            def _(pool):
                nc.gpsimd.memset(sel[:], 0.0).then_inc(consts, 1)
                nc.gpsimd.memset(max_t[:], 0.0).then_inc(consts, 1)
                nc.gpsimd.memset(v[:, :, DH:WIDE], 1.0).then_inc(consts, 1)
                if half:
                    nc.gpsimd.memset(causal_qk[:], 0.0).then_inc(consts, 1)
                    nc.gpsimd.memset(causal_kq[:], 0.0).then_inc(consts, 1)
                    nc.gpsimd.memset(keymask_col[:], 0.0).then_inc(consts, 1)
                    nc.gpsimd.memset(keys_col[:], 1).then_inc(consts, 1)
                pool.wait_ge(consts, 7 if half else 3)
                nc.gpsimd.affine_select(out=sel[:], in_=sel[:], compare_op=ALU.not_equal, fill=1.0,
                                        base=0, pattern=[[-1, H], [0, CTX]], channel_multiplier=1).then_inc(consts, 1)
                if half:
                    nc.gpsimd.affine_select(out=causal_qk[:], in_=causal_qk[:], compare_op=ALU.is_ge, fill=NEG,
                                            base=0, pattern=[[-1, CTX]], channel_multiplier=1).then_inc(consts, 1)
                    nc.gpsimd.affine_select(out=causal_kq[:], in_=causal_kq[:], compare_op=ALU.is_ge, fill=NEG,
                                            base=0, pattern=[[1, SEQ]], channel_multiplier=-1).then_inc(consts, 1)
                norm.start_gpsimd(pool)
                with pool.Fori(0, B) as b:
                    norm.gpsimd(pool, b)

            @block.scalar
            def _(act):
                act.wait_ge(weights_in, 16 * n_weights)
                act.wait_ge(consts, n_consts)
                for s in (rounded, maxt_ready, probs_ready, ot_ready) + ((out_rounded,) if half else ()):
                    s.start(act)
                norm.start_scalar(act)
                with act.Fori(0, B) as b:
                    if half:
                        act.wait_ge(qkv_done.sem, qkv_done.now(b, 1))
                        nc.scalar.activation(q_round[:], q_banks(), ACT.Copy)
                        nc.scalar.activation(k_round[:], k_bank(), ACT.Copy)
                        nc.scalar.activation(v_round[0:CTX, :], PS[0:CTX, 7, 0:D], ACT.Copy)
                        act.drain()
                        act.sem_inc(rounded.sem, 1)
                    act.wait_ge(maxt_done.sem, maxt_done.now(b, 1))
                    nc.scalar.activation(max_t[0:H, :], PS[0:H, 0, 0:SEQ], ACT.Copy).then_inc(maxt_ready.sem, 1)
                    act.wait_ge(o_done.sem, o_done.prev(b, 1))
                    for pair in range(2):
                        act.wait_ge(st_done.sem, st_done.now(b, pair + 1))
                        nc.scalar.activation(probs[0:CTX, :, 2 * pair:2 * pair + 2, :],
                                             PS[0:CTX, 4 * pair:4 * pair + 4, :].rearrange("p a (g n) -> p a g n", g=2),
                                             ACT.Exp).then_inc(probs_ready.sem, 1)
                    act.wait_ge(ot_done.sem, ot_done.now(b, 1))
                    nc.scalar.activation(ot[:].rearrange("p c n -> p (c n)"), PS[:, 2, :],
                                         ACT.Copy).then_inc(ot_ready.sem, 1)
                    if half:
                        act.wait_ge(out_done.sem, out_done.now(b, 1))
                        nc.scalar.activation(out_round[:].rearrange("p t d -> p (t d)"), PS[:, 3, :],
                                             ACT.Copy).then_inc(out_rounded.sem, 1)
                    norm.scalar(act, b)

            @block.vector
            def _(dve):
                dve.wait_ge(weights_in, 16 * n_weights)
                dve.wait_ge(consts, n_consts)
                if half:
                    for n in w32:
                        nc.vector.tensor_copy(w[n][:], w32[n][:])
                    for n in b32:
                        nc.vector.tensor_copy(b16[n][:], b32[n][:])
                    dve.drain()
                    for n in b32:
                        nc.vector.tensor_copy(b32[n][:], b16[n][:])
                    dve.drain()
                for s in (inputs_ready, qkv_ready, max_ready, o_ready):
                    s.start(dve)
                norm.start_vector(dve)
                with dve.Fori(0, B) as b:
                    dve.wait_ge(inputs_in.sem, inputs_in.now(b, inputs_in.per))
                    if half:
                        nc.vector.tensor_copy(xt[:], xt_in_tile[:])
                        nc.vector.tensor_copy(ct[:], ct_in_tile[:])
                        nc.vector.tensor_scalar(keymask_row[:], keys_row[:], 0.0, NEG, ALU.is_le, ALU.mult)
                        nc.vector.tensor_scalar(keymask_col[0:CTX, :], keys_col[0:CTX, :], 0.0, NEG, ALU.is_le,
                                                ALU.mult)
                        dve.drain()
                        nc.vector.tensor_tensor(mask_qk[:, 0, :], causal_qk[:], keymask_row[:], ALU.add)
                        nc.vector.tensor_copy(mask_qk[:, 1, :], keymask_row[:])
                        nc.vector.tensor_scalar(mask_kq[:], causal_kq[:], keymask_col[:, 0:1], None, ALU.add)
                        dve.drain()
                    dve.sem_inc(inputs_ready.sem, 1)
                    if half:
                        dve.wait_ge(rounded.sem, rounded.now(b, 1))
                        q_from, k_from, v_from, v_to = q_round[:], k_round[:], v_round[0:CTX, :], v16[0:CTX, :]
                        bv_part = b16["bv"][0:CTX, :]
                    else:
                        dve.wait_ge(qkv_done.sem, qkv_done.now(b, 1))
                        q_from, k_from, v_from = q_banks(), k_bank(), PS[0:CTX, 7, 0:D]
                        bv_part = b32["bv"][0:CTX, :]
                    for g in range(NG):
                        nc.vector.tensor_scalar(q[:, g, :], q_from[:, g, :], b32["bq"][:, g:g + 1], DH ** -0.5,
                                                ALU.add, ALU.mult)
                        nc.vector.tensor_scalar(k[:, g, :], k_from[:, g, :], b32["bk"][:, g:g + 1], None, ALU.add)
                    def heads(ap):
                        return ap.rearrange("p (h d) -> p h d", d=DH)

                    dve.wait_ge(o_done.sem, o_done.prev(b, 1))
                    if half:
                        nc.vector.tensor_tensor(v_to, v_from, bv_part, ALU.add)
                        dve.drain()
                        nc.vector.tensor_copy(v[0:CTX, :, 0:DH], heads(v_to))
                    else:
                        nc.vector.tensor_tensor(v[0:CTX, :, 0:DH], heads(v_from), heads(bv_part), ALU.add)
                    dve.drain()
                    dve.sem_inc(qkv_ready.sem, 1)
                    for t in range(TB):
                        dve.wait_ge(s_done.sem, s_done.now(b, t + 1))
                        nc.vector.tensor_reduce(
                            neg_max[:, t, :].rearrange("p (j g) -> p j g", g=NG),
                            PS[:, 4 * t:4 * t + 4, 0:NG * CTX].rearrange("p j (g n) -> p j g n", n=CTX),
                            AX.X, ALU.max, negate=True)
                    dve.drain()
                    dve.sem_inc(max_ready.sem, 1)
                    dve.wait_ge(o_done.sem, o_done.now(b, 1))

                    def o_bank(t):
                        return PS[:, t, 0:H * WIDE].rearrange("p (h d) -> p h d", d=WIDE)

                    for t in range(TB):
                        nc.vector.reciprocal(rden[:, t, :], o_bank(t)[:, :, DH])
                    dve.drain()
                    for t in range(TB):
                        nc.vector.tensor_tensor(heads(o[:, t, :]), o_bank(t)[:, :, 0:DH], spread(rden[:, t, :], DH),
                                                ALU.mult)
                    dve.drain()
                    dve.sem_inc(o_ready.sem, 1)
                    if half:
                        dve.wait_ge(out_rounded.sem, out_rounded.now(b, 1))
                        nc.vector.tensor_tensor(out16[:], out_round[:],
                                                b16["bo"][:, :].unsqueeze(1).to_broadcast([P, TB, D]), ALU.add)
                        dve.drain()
                        norm.vector(dve, b, (out_rounded.sem, out_rounded.now(b, 1)), source=out16[:])
                    else:
                        norm.vector(dve, b, (out_done.sem, out_done.now(b, 1)))

            @block.tensor
            def _(pe):
                pe.wait_ge(weights_in, 16 * n_weights)
                pe.wait_ge(consts, n_consts)
                for s in (qkv_done, s_done, maxt_done, st_done, o_done, ot_done, out_done):
                    s.start(pe)
                norm.start_tensor(pe)
                mm = nc.tensor.matmul
                rows = [slice(32 * j, 32 * j + 32) for j in range(G)]
                with pe.Fori(0, B) as b:
                    pe.wait_ge(inputs_ready.sem, inputs_ready.now(b, 1))
                    pe.wait_ge(probs_ready.sem, probs_ready.prev(b, 2))
                    for g in range(NG):
                        for c in range(KC):
                            mm(q_banks()[:, g, :], w["wq"][:, c, g, :], xt[:, c, :], start=c == 0, stop=c == KC - 1)
                    for g in range(NG):
                        for c in range(KC):
                            mm(k_bank()[:, g, :], w["wk"][:, c, g, :], ct[:, c, :], start=c == 0, stop=c == KC - 1)
                    for c in range(KC):
                        last = mm(PS[0:CTX, 7, 0:D], ct[:, c, :], w["wv"][:, c, :], start=c == 0, stop=c == KC - 1)
                    last.then_inc(qkv_done.sem, 1)
                    pe.wait_ge(qkv_ready.sem, qkv_ready.now(b, 1))
                    pe.wait_ge(norm.xt_ready.sem, norm.xt_ready.prev(norm.turn(b), 1))
                    for t in range(TB):
                        for g in range(NG):
                            for j, r in enumerate(rows):
                                last = mm(PS[:, 4 * t + j, g * CTX:(g + 1) * CTX], q[r, g, t * P:(t + 1) * P],
                                          k[r, g, :], start=g == 0, stop=not half, skip_group_check=True)
                        if half:
                            for j in range(G):
                                for g in range(NG):
                                    last = mm(PS[:, 4 * t + j, g * CTX:(g + 1) * CTX], core.ident16[:],
                                              mask_qk[:, t, :], start=False, stop=True, skip_group_check=True)
                        last.then_inc(s_done.sem, 1)
                    pe.wait_ge(max_ready.sem, max_ready.now(b, 1))
                    for t in range(TB):
                        last = nc.tensor.transpose(PS[0:H, 0, t * P:(t + 1) * P], neg_max[:, t, :], core.ident[:])
                    last.then_inc(maxt_done.sem, 1)
                    pe.wait_ge(maxt_ready.sem, maxt_ready.now(b, 1))
                    for pair in range(2):
                        for gg in range(2):
                            for j, r in enumerate(rows):
                                mm(PS[0:CTX, 4 * pair + j, gg * SEQ:(gg + 1) * SEQ], k[r, 2 * pair + gg, :],
                                   q[r, 2 * pair + gg, :], start=gg == 0, stop=False, skip_group_check=True)
                        for gg in range(2):
                            for j in range(G):
                                to = PS[0:CTX, 4 * pair + j, gg * SEQ:(gg + 1) * SEQ]
                                last = mm(to, sel[:, j * NG + 2 * pair + gg, :], max_t[:], start=False,
                                          stop=not half, skip_group_check=True)
                                if half:
                                    last = mm(to, core.ident16[:, 0:CTX], mask_kq[:], start=False, stop=True,
                                              skip_group_check=True)
                        last.then_inc(st_done.sem, 1)
                    pe.wait_ge(probs_ready.sem, probs_ready.now(b, 2))
                    for t in range(TB):
                        for h in range(H):
                            last = mm(PS[:, t, h * WIDE:(h + 1) * WIDE],
                                      probs[0:CTX, h % G, h // G, t * P:(t + 1) * P], v[0:CTX, h, :],
                                      start=True, stop=True)
                    last.then_inc(o_done.sem, 1)
                    pe.wait_ge(o_ready.sem, o_ready.now(b, 1))
                    for c in range(KC):
                        for t in range(TB):
                            last = nc.tensor.transpose(PS[:, 2, (c * TB + t) * P:(c * TB + t + 1) * P],
                                                       o[:, t, c * P:(c + 1) * P], core.ident[:])
                    last.then_inc(ot_done.sem, 1)
                    pe.wait_ge(ot_ready.sem, ot_ready.now(b, 1))
                    for t in range(TB):
                        for c in range(KC):
                            last = mm(PS[:, 3, t * D:(t + 1) * D], ot[:, c, t * P:(t + 1) * P], w["wo"][:, c, :],
                                      start=c == 0, stop=c == KC - 1)
                    last.then_inc(out_done.sem, 1)
                    norm.tensor(pe, b)


def block_cross_attention_0(core):
    cross_attention(core, "ca", False, "ca")


def block_cross_attention_1(core):
    cross_attention(core, "cb", True, "cb")


def top2(nc, dve, t, scores, iota8, best, index, index_f, chosen):
    nc.vector.max(best[:, t, :], scores[:, t, :])
    dve.drain()
    nc.vector.max_index(index[:, t, :], best[:, t, :], scores[:, t, :])
    dve.drain()
    nc.vector.tensor_copy(index_f[:, t, :], index[:, t, :])
    dve.drain()
    for r in range(2):
        nc.vector.tensor_scalar(chosen[:, t, r, :], iota8[:], index_f[:, t, r:r + 1], None, ALU.is_equal)
    dve.drain()


def block_experts_0(core):
    E, HB = 8, 3
    nc, PS, dram = core.nc, core.PS, core.dram
    with ExitStack() as ctx:
        def sb(n, shape, dt=F32):
            return ctx.enter_context(nc.sbuf_tensor(f"ea_{n}", shape, dt))

        def sig(n, per, unit=1):
            return Signal(core, f"ea_{n}", per, unit)

        up32 = sb("up32", [P, KC, E, HB, P])
        down32 = sb("down32", [P, E, HB, D])
        up = sb("up", [P, KC, E, HB, P], BF16)
        down = sb("down", [P, E, HB, D], BF16)
        shared_up = sb("shared_up", [P, KC, HB, P])
        shared_down = sb("shared_down", [P, HB, D])
        gate = sb("gate", [P, KC, E])
        gate_bias = sb("gate_bias", [P, E])
        iota8 = sb("iota8", [P, E])
        sel = sb("sel", [P, E, P])
        xt = sb("xt", [P, KC, SEQ])
        tanh = sb("tanh", [P, TB, E])
        scores = sb("scores", [P, TB, E])
        biased = sb("biased", [P, TB, E])
        best = sb("best", [P, TB, 8])
        index = sb("index", [P, TB, 8], mybir.dt.uint32)
        index_f = sb("index_f", [P, TB, 8])
        chosen = sb("chosen", [P, TB, 2, E])
        both = sb("both", [P, TB, E])
        weight = sb("weight", [P, TB, E])
        weight_t = sb("weight_t", [P, SEQ])
        scaled = sb("scaled", [P, 2, KC, SEQ], BF16)
        relu = sb("relu", [P, 2, HB, SEQ], BF16)
        hidden = sb("hidden", [P, 2, HB, SEQ], BF16)
        shared_relu = sb("shared_relu", [P, HB, SEQ])
        shared_hidden = sb("shared_hidden", [P, HB, SEQ])
        routed = sb("routed", [P, 2, TB, D], BF16)
        total = sb("total", [P, TB, D])
        summed = sb("summed", [P, TB, D])
        norm = Norm(core, ctx, "ea", 2, 7)

        weights_in = core.semaphore("ea_weights_in")
        consts = core.semaphore("ea_constants_ready")
        xt_in = sig("xt_in", 1, 16)
        gate_done = sig("gate_done", 1)
        tanh_ready = sig("tanh_ready", 1)
        weight_ready = sig("weight_ready", 1)
        weight_turned = sig("weight_turned", 1)
        weight_t_ready = sig("weight_t_ready", 1)
        spread_done = sig("scores_spread", E)
        scaled_ready = sig("scaled_ready", E)
        up_done = sig("up_done", E + 1)
        relu_ready = sig("relu_ready", E + 1)
        hidden_ready = sig("hidden_ready", E + 1)
        down_done = sig("down_done", E)
        routed_ready = sig("routed_ready", E)
        summed_step = sig("summed_step", E - 1)
        shared_done = sig("shared_done", 1)
        total_ready = sig("total_ready", 1)

        def up_banks(e):
            return PS[:, 2 + 2 * (e % 2):4 + 2 * (e % 2), :].rearrange("p a n -> p (a n)")[:, 0:HB * SEQ]\
                .rearrange("p (h n) -> p h n", n=SEQ)

        def tiles(ap):
            return ap.rearrange("p (t d) -> p t d", t=TB)

        with nc.Block() as block:
            @block.sync
            def _(sp):
                for dst, n in ((up32, "ea_up"), (down32, "ea_down"), (shared_up, "ea_shared_up"),
                               (shared_down, "ea_shared_down"), (gate, "ea_gate")):
                    sp.dma_start(dst[:], dram[n]).then_inc(weights_in, 16)
                sp.dma_start(gate_bias[:], dram["ea_gate_bias"].partition_broadcast(P)).then_inc(weights_in, 16)
                xt_in.start(sp)
                norm.start_sync(sp)
                with sp.Fori(0, B) as b:
                    sp.wait_ge(up_done.sem, up_done.prev(b, E + 1))
                    sp.wait_ge(scaled_ready.sem, scaled_ready.prev(b, E))
                    sp.dma_start(xt[:], core.xt_of(b)).then_inc(xt_in.sem, 16)
                    norm.load(sp, b)
                    norm.store(sp, b)

            @block.gpsimd
            def _(pool):
                nc.gpsimd.iota(iota8[:], pattern=[[1, E]], base=0, channel_multiplier=0,
                               allow_small_or_imprecise_dtypes=True).then_inc(consts, 1)
                nc.gpsimd.memset(sel[:], 0.0).then_inc(consts, 1)
                nc.gpsimd.memset(weight_t[:], 0.0).then_inc(consts, 1)
                pool.wait_ge(consts, 3)
                nc.gpsimd.affine_select(out=sel[:], in_=sel[:], compare_op=ALU.not_equal, fill=1.0,
                                        base=0, pattern=[[-1, E], [0, P]], channel_multiplier=1).then_inc(consts, 1)
                summed_step.start(pool)
                norm.start_gpsimd(pool)
                with pool.Fori(0, B) as b:
                    pool.wait_ge(total_ready.sem, total_ready.prev(b, 1))
                    for e in range(1, E):
                        pool.wait_ge(routed_ready.sem, routed_ready.now(b, e + 1))
                        if e > 1:
                            pool.wait_ge(summed_step.sem, summed_step.now(b, e - 1))
                        nc.gpsimd.tensor_tensor(summed[:], summed[:] if e > 1 else routed[:, 0, :, :],
                                                routed[:, e % 2, :, :], ALU.add).then_inc(summed_step.sem, 1)
                    norm.gpsimd(pool, b)

            @block.scalar
            def _(act):
                for s in (tanh_ready, weight_t_ready, relu_ready, routed_ready):
                    s.start(act)
                norm.start_scalar(act)
                with act.Fori(0, B) as b:
                    act.wait_ge(gate_done.sem, gate_done.now(b, 1))
                    act.wait_ge(weight_ready.sem, weight_ready.prev(b, 1))
                    nc.scalar.activation(tanh[:], PS[:, 0, 0:TB * E].rearrange("p (t e) -> p t e", t=TB), ACT.Tanh,
                                         scale=0.5).then_inc(tanh_ready.sem, 1)
                    act.wait_ge(weight_turned.sem, weight_turned.now(b, 1))
                    act.wait_ge(consts, 4)
                    nc.scalar.activation(weight_t[0:E, :], PS[0:E, 0, 0:SEQ], ACT.Copy).then_inc(weight_t_ready.sem, 1)

                    def relu_of(e):
                        act.wait_ge(up_done.sem, up_done.now(b, e + 1))
                        if e == E:
                            act.wait_ge(hidden_ready.sem, hidden_ready.prev(b, E + 1))
                            to = shared_relu[:]
                        else:
                            k = e - 1 if e >= 2 else E - 1 + e
                            act.wait_ge(hidden_ready.sem,
                                        hidden_ready.now(b, k) if e >= 2 else hidden_ready.prev(b, k))
                            to = relu[:, e % 2, :, :]
                        nc.scalar.activation(to, up_banks(e), ACT.Relu).then_inc(relu_ready.sem, 1)

                    relu_of(0)
                    for e in range(E):
                        relu_of(e + 1)
                        act.wait_ge(down_done.sem, down_done.now(b, e + 1))
                        if e >= 2:
                            act.wait_ge(summed_step.sem, summed_step.now(b, max(e - 2, 1)))
                        else:
                            act.wait_ge(summed_step.sem, summed_step.prev(b, E - 2 + e))
                        nc.scalar.activation(routed[:, e % 2, :, :], tiles(PS[:, 6, :]),
                                             ACT.Copy).then_inc(routed_ready.sem, 1)
                    norm.scalar(act, b)

            @block.vector
            def _(dve):
                dve.wait_ge(weights_in, 96)
                dve.wait_ge(consts, 4)
                nc.vector.tensor_copy(up[:], up32[:])
                nc.vector.tensor_copy(down[:], down32[:])
                dve.drain()
                dve.sem_inc(consts, 1)
                for s in (weight_ready, scaled_ready, hidden_ready, total_ready):
                    s.start(dve)
                norm.start_vector(dve)
                with dve.Fori(0, B) as b:
                    dve.wait_ge(tanh_ready.sem, tanh_ready.now(b, 1))
                    nc.vector.tensor_scalar(scores[:], tanh[:], 0.5, 0.5, ALU.mult, ALU.add)
                    dve.drain()
                    nc.vector.tensor_tensor(biased[:], scores[:],
                                            gate_bias[:, :].unsqueeze(1).to_broadcast([P, TB, E]), ALU.add)
                    dve.drain()
                    for t in range(TB):
                        top2(nc, dve, t, biased, iota8, best, index, index_f, chosen)
                    nc.vector.tensor_tensor(both[:], chosen[:, :, 0, :], chosen[:, :, 1, :], ALU.add)
                    dve.drain()
                    nc.vector.tensor_tensor(weight[:], both[:], scores[:], ALU.mult).then_inc(weight_ready.sem, 1)
                    dve.wait_ge(xt_in.sem, xt_in.now(b, 1))

                    def scale(e):
                        dve.wait_ge(spread_done.sem, spread_done.now(b, e + 1))
                        if e >= 2:
                            dve.wait_ge(up_done.sem, up_done.now(b, e - 1))
                        else:
                            dve.wait_ge(up_done.sem, up_done.prev(b, E - 1 + e))
                        nc.vector.tensor_tensor(scaled[:, e % 2, :, :], xt[:],
                                                PS[:, e % 2, 0:SEQ].unsqueeze(1).to_broadcast([P, KC, SEQ]),
                                                ALU.mult).then_inc(scaled_ready.sem, 1)

                    def square(e):
                        dve.wait_ge(relu_ready.sem, relu_ready.now(b, e + 1))
                        if e == E:
                            dve.wait_ge(shared_done.sem, shared_done.prev(b, 1))
                            nc.vector.tensor_tensor(shared_hidden[:], shared_relu[:], shared_relu[:],
                                                    ALU.mult).then_inc(hidden_ready.sem, 1)
                        else:
                            if e >= 2:
                                dve.wait_ge(down_done.sem, down_done.now(b, e - 1))
                            else:
                                dve.wait_ge(down_done.sem, down_done.prev(b, E - 1 + e))
                            nc.vector.tensor_tensor(hidden[:, e % 2, :, :], relu[:, e % 2, :, :],
                                                    relu[:, e % 2, :, :], ALU.mult).then_inc(hidden_ready.sem, 1)

                    scale(0)
                    for e in range(E + 1):
                        if e + 1 < E:
                            scale(e + 1)
                        square(e)
                    dve.wait_ge(summed_step.sem, summed_step.now(b, E - 1))
                    dve.wait_ge(shared_done.sem, shared_done.now(b, 1))
                    nc.vector.tensor_tensor(total[:], tiles(PS[:, 7, :]), summed[:], ALU.add)\
                        .then_inc(total_ready.sem, 1)
                    dve.drain()
                    norm.vector(dve, b, (shared_done.sem, shared_done.now(b, 1)), source=total[:])

            @block.tensor
            def _(pe):
                pe.wait_ge(weights_in, 96)
                pe.wait_ge(consts, 5)
                for s in (gate_done, weight_turned, spread_done, up_done, down_done, shared_done):
                    s.start(pe)
                norm.start_tensor(pe)
                mm = nc.tensor.matmul
                with pe.Fori(0, B) as b:
                    pe.wait_ge(xt_in.sem, xt_in.now(b, 1))
                    pe.wait_ge(scaled_ready.sem, scaled_ready.prev(b, E))
                    for t in range(TB):
                        for c in range(KC):
                            last = mm(PS[:, 0, t * E:(t + 1) * E], xt[:, c, t * P:(t + 1) * P], gate[:, c, :],
                                      start=c == 0, stop=c == KC - 1)
                    last.then_inc(gate_done.sem, 1)

                    def up_of(e):
                        if e >= 2:
                            pe.wait_ge(relu_ready.sem, relu_ready.now(b, e - 1))
                        else:
                            pe.wait_ge(relu_ready.sem, relu_ready.prev(b, E + 1 - e))
                        for h in range(HB):
                            for c in range(KC):
                                if e < E:
                                    last = mm(up_banks(e)[:, h, :], up[:, c, e, h, :], scaled[:, e % 2, c, :],
                                              start=c == 0, stop=c == KC - 1)
                                else:
                                    last = mm(up_banks(e)[:, h, :], shared_up[:, c, h, :], xt[:, c, :],
                                              start=c == 0, stop=c == KC - 1)
                        last.then_inc(up_done.sem, 1)

                    def spread_of(e):
                        if e >= 2:
                            pe.wait_ge(scaled_ready.sem, scaled_ready.now(b, e - 1))
                        mm(PS[:, e % 2, 0:SEQ], sel[:, e, :], weight_t[:], start=True, stop=True)\
                            .then_inc(spread_done.sem, 1)

                    pe.wait_ge(weight_ready.sem, weight_ready.now(b, 1))
                    for t in range(TB):
                        last = nc.tensor.transpose(PS[0:E, 0, t * P:(t + 1) * P], weight[:, t, :], core.ident[:])
                    last.then_inc(weight_turned.sem, 1)
                    pe.wait_ge(weight_t_ready.sem, weight_t_ready.now(b, 1))
                    spread_of(0)
                    spread_of(1)
                    pe.wait_ge(scaled_ready.sem, scaled_ready.now(b, 1))
                    up_of(0)
                    for e in range(E):
                        if e + 2 < E:
                            spread_of(e + 2)
                        if e + 1 < E:
                            pe.wait_ge(scaled_ready.sem, scaled_ready.now(b, e + 2))
                        up_of(e + 1)
                        pe.wait_ge(hidden_ready.sem, hidden_ready.now(b, e + 1))
                        if e:
                            pe.wait_ge(routed_ready.sem, routed_ready.now(b, e))
                        else:
                            pe.wait_ge(routed_ready.sem, routed_ready.prev(b, E))
                        for t in range(TB):
                            for h in range(HB):
                                last = mm(PS[:, 6, t * D:(t + 1) * D], hidden[:, e % 2, h, t * P:(t + 1) * P],
                                          down[:, e, h, :], start=h == 0, stop=h == HB - 1)
                        last.then_inc(down_done.sem, 1)
                    pe.wait_ge(hidden_ready.sem, hidden_ready.now(b, E + 1))
                    pe.wait_ge(norm.xt_ready.sem, norm.xt_ready.prev(norm.turn(b), 1))
                    for t in range(TB):
                        for h in range(HB):
                            last = mm(PS[:, 7, t * D:(t + 1) * D], shared_hidden[:, h, t * P:(t + 1) * P],
                                      shared_down[:, h, :], start=h == 0, stop=h == HB - 1)
                    last.then_inc(shared_done.sem, 1)
                    norm.tensor(pe, b)



MH, MD = 4, 64
CHUNK = 32
NCH = SEQ // CHUNK
LOCAL, MID = 7, 25
CONV = 4
OUTS = ("local", "mid", "delta", "v")


class MixerScratch:

    def __init__(self, nc):
        def dram(name, shape):
            return nc.dram_tensor(name, shape, F32, kind="Internal").ap()

        self.outs = dram("mixer_outs", (len(OUTS), B * SEQ, D))
        self.k = dram("mixer_k", (B, NCH, CHUNK, MH, MD))
        self.qk_t = dram("mixer_qk_t", (2, P, KC, B, NCH, CHUNK))
        self.gram = dram("mixer_gram", (B, TB, P // CHUNK, CHUNK, MH, CHUNK))
        self.beta = dram("mixer_beta", (B, MH, NCH, CHUNK))
        self.solved = dram("mixer_solved", (NCH, MH, CHUNK, B, CHUNK))


def block_mixer_project(core):
    nc, PS, dram = core.nc, core.PS, core.dram
    core.mixer = scratch = MixerScratch(nc)
    PAD = MID - 1
    with ExitStack() as ctx:
        def sb(n, shape, dt=F32):
            return ctx.enter_context(nc.sbuf_tensor(f"mp_{n}", shape, dt))

        def sig(n, per, unit=1):
            return Signal(core, f"mp_{n}", per, unit)

        w = sb("w", [P, KC, 3, KC, P])
        w_beta = sb("w_beta", [P, KC, MH])
        conv_w = sb("conv_w", [P, 3, KC, CONV])
        conv_half = sb("conv_half", [P, 3, KC, CONV])
        local_w = sb("local_w", [P, KC, LOCAL])
        mid_w = sb("mid_w", [P, KC, MID])
        mid_diag = sb("mid_diag", [P, KC, MID, P])
        eps12 = sb("eps12", [P, 16])
        xt = sb("xt", [P, KC, SEQ])
        padded = sb("padded", [P, 3, KC, CONV - 1 + SEQ])
        y = sb("y", [P, 3, KC, SEQ])
        tanh = sb("tanh", [P, 3, KC, SEQ])
        tanh_beta = sb("tanh_beta", [MH, SEQ])
        beta = sb("beta", [MH, SEQ])
        qk = sb("qk", [P, 2, KC, SEQ])
        v_pad = sb("v_pad", [P, KC, PAD + SEQ])
        local_t = sb("local_t", [P, KC, SEQ])
        mid_t = sb("mid_t", [P, KC, SEQ])
        squares = sb("squares", [P, 2 * TB * MH, MD])
        sums = sb("sums", [P, 2 * TB * MH])
        rnorm = sb("rnorm", [P, 2 * TB * MH])
        v_tok = sb("v_tok", [P, TB, D])
        lm_tok = sb("lm_tok", [P, 2, TB, D])
        qk_tok = sb("qk_tok", [P, 2, TB, D])
        qk_t = sb("qk_t", [P, 2, KC, SEQ])
        gram = sb("gram", [P, TB, MH, CHUNK])

        weights_in = core.semaphore("mp_weights_in")
        consts = core.semaphore("mp_constants_ready")
        xt_in = sig("xt_in", 1, 16)
        projected = sig("projected", 1)
        padded_ready = sig("padded_ready", 1)
        conv_ready = sig("conv_ready", 1)
        tanh_ready = sig("tanh_ready", 1)
        silu_ready = sig("silu_ready", 1)
        local_ready = sig("local_ready", 1)
        mid_done = sig("mid_done", 1)
        mid_ready = sig("mid_ready", 1)
        qkv_turned = sig("qkv_turned", 1)
        squares_ready = sig("squares_ready", 1)
        sums_ready = sig("sums_ready", 1)
        rnorm_step = sig("rnorm_step", 2)
        lm_turned = sig("lm_turned", 1)
        lm_ready = sig("lm_ready", 1)
        qk_tok_ready = sig("qk_normed", 1)
        qk_turned = sig("qk_turned", 1)
        qk_t_ready = sig("qk_t_ready", 1)
        gram_done = sig("gram_done", 1)
        gram_ready = sig("gram_ready", 1)
        N_STORES = 3 * TB + TB + 2 + TB + 1
        stored = sig("stored", N_STORES, 16)
        left = sig("results_left", 1)

        with nc.Block() as block:
            @block.sync
            def _(sp):
                for dst, n in ((w, "mp_w"), (w_beta, "mp_w_beta"), (conv_w, "mp_conv_w"), (local_w, "mp_local_w"),
                               (mid_w, "mp_mid_w")):
                    sp.dma_start(dst[:], dram[n]).then_inc(weights_in, 16)
                for s in (xt_in, stored, left):
                    s.start(sp)
                with sp.Fori(0, B) as b:
                    sp.wait_ge(projected.sem, projected.prev(b, 1))
                    sp.dma_start(xt[:], core.xt_of(b)).then_inc(xt_in.sem, 16)
                    sp.wait_ge(squares_ready.sem, squares_ready.now(b, 1))
                    sp.wait_ge(lm_ready.sem, lm_ready.now(b, 1))
                    for t in range(TB):
                        rows = bass.ds(b * SEQ + t * P, P)
                        sp.dma_start(scratch.outs[0, rows, :], lm_tok[:, 0, t, :]).then_inc(stored.sem, 16)
                        sp.dma_start(scratch.outs[1, rows, :], lm_tok[:, 1, t, :]).then_inc(stored.sem, 16)
                        sp.dma_start(scratch.outs[3, rows, :], v_tok[:, t, :]).then_inc(stored.sem, 16)
                    sp.wait_ge(qk_tok_ready.sem, qk_tok_ready.now(b, 1))
                    k_rows = scratch.k.rearrange("b n t h d -> (b n t) (h d)")
                    for t in range(TB):
                        sp.dma_start(k_rows[bass.ds(b * SEQ + t * P, P), :], qk_tok[:, 1, t, :])\
                            .then_inc(stored.sem, 16)
                    sp.dma_start(scratch.beta.rearrange("b h n t -> b h (n t)")[bass.ds(b, 1), :, :]
                                 .rearrange("a h n -> h (a n)"), beta[:]).then_inc(stored.sem, 16)
                    sp.wait_ge(qk_t_ready.sem, qk_t_ready.now(b, 1))
                    for i in range(2):
                        sp.dma_start(scratch.qk_t[i].rearrange("p c b n t -> p c (b n t)")
                                     [:, :, bass.ds(b * SEQ, SEQ)], qk_t[:, i, :, :]).then_inc(stored.sem, 16)
                    sp.wait_ge(gram_ready.sem, gram_ready.now(b, 1))
                    gram_rows = scratch.gram.rearrange("b u c i h j -> (b u c i) (h j)")
                    for t in range(TB):
                        sp.dma_start(gram_rows[bass.ds(b * SEQ + t * P, P), :],
                                     gram[:, t, :, :].rearrange("p h j -> p (h j)")).then_inc(stored.sem, 16)
                    sp.wait_ge(stored.sem, stored.now(b, N_STORES))
                    sp.sem_inc(left.sem, 1)

            @block.gpsimd
            def _(pool):
                nc.gpsimd.memset(eps12[:], 1e-12).then_inc(consts, 1)
                nc.gpsimd.memset(padded[:], 0.0).then_inc(consts, 1)
                nc.gpsimd.memset(v_pad[:], 0.0).then_inc(consts, 1)
                pool.wait_ge(weights_in, 80)
                for c in range(KC):
                    nc.gpsimd.tensor_tensor(mid_diag[:, c, :, :],
                                            core.ident[:, :].unsqueeze(1).to_broadcast([P, MID, P]),
                                            spread(mid_w[:, c, :], P), ALU.mult).then_inc(consts, 1)
                rnorm_step.start(pool)
                with pool.Fori(0, B) as b:
                    pool.wait_ge(sums_ready.sem, sums_ready.now(b, 1))
                    nc.gpsimd.tensor_tensor(rnorm[:], sums[:], eps12[:], ALU.add).then_inc(rnorm_step.sem, 1)
                    pool.wait_ge(rnorm_step.sem, rnorm_step.now(b, 1))
                    nc.gpsimd.tensor_tensor(rnorm[:], rnorm[:], core.minus_half[:], ALU.pow)\
                        .then_inc(rnorm_step.sem, 1)

            @block.scalar
            def _(act):
                act.wait_ge(consts, 5)
                for s in (padded_ready, tanh_ready, mid_ready, squares_ready, lm_ready, qk_t_ready, gram_ready):
                    s.start(act)
                with act.Fori(0, B) as b:
                    act.wait_ge(projected.sem, projected.now(b, 1))
                    act.wait_ge(conv_ready.sem, conv_ready.prev(b, 1))
                    act.wait_ge(silu_ready.sem, silu_ready.prev(b, 1))
                    nc.scalar.activation(padded[:].rearrange("p a c n -> p (a c) n")[:, :, CONV - 1:],
                                         PS[:, 0:3, :].rearrange("p a (c n) -> p (a c) n", c=KC), ACT.Copy)
                    nc.scalar.activation(tanh_beta[:], PS[0:MH, 3, 0:SEQ], ACT.Tanh, scale=0.5)
                    act.drain()
                    act.sem_inc(padded_ready.sem, 1)
                    act.wait_ge(conv_ready.sem, conv_ready.now(b, 1))
                    nc.scalar.activation(tanh[:], y[:], ACT.Tanh).then_inc(tanh_ready.sem, 1)
                    act.wait_ge(left.sem, left.prev(b, 1))
                    act.wait_ge(qkv_turned.sem, qkv_turned.now(b, 1))
                    nc.scalar.activation(squares[:].rearrange("p (a m) d -> p a (m d)", a=2), PS[:, 0:2, :], ACT.Square)
                    nc.scalar.activation(v_tok[:].rearrange("p t d -> p (t d)"), PS[:, 2, :], ACT.Copy)
                    act.drain()
                    act.sem_inc(squares_ready.sem, 1)
                    act.wait_ge(mid_done.sem, mid_done.now(b, 1))
                    nc.scalar.activation(mid_t[:].rearrange("p c n -> p (c n)"), PS[:, 4, :],
                                         ACT.Copy).then_inc(mid_ready.sem, 1)
                    act.wait_ge(lm_turned.sem, lm_turned.now(b, 1))
                    nc.scalar.activation(lm_tok[:].rearrange("p a t d -> p a (t d)"), PS[:, 5:7, :],
                                         ACT.Copy).then_inc(lm_ready.sem, 1)
                    act.wait_ge(qk_turned.sem, qk_turned.now(b, 1))
                    for i, bank in enumerate((3, 7)):
                        nc.scalar.activation(qk_t[:, i, :, :].rearrange("p c n -> p (c n)"), PS[:, bank, :], ACT.Copy)
                    act.drain()
                    act.sem_inc(qk_t_ready.sem, 1)
                    act.wait_ge(gram_done.sem, gram_done.now(b, 1))
                    for i in range(2):
                        for c4 in range(P // CHUNK):
                            at = slice(c4 * CHUNK, (c4 + 1) * CHUNK)
                            nc.scalar.activation(
                                gram[at, :, :, :].rearrange("p t (g i) j -> p t g i j", i=2)[:, :, :, i, :],
                                PS[at, i, :].rearrange("p (t g j) -> p t g j", t=TB, g=2)[:, :, :, at], ACT.Copy)
                    act.drain()
                    act.sem_inc(gram_ready.sem, 1)

            @block.vector
            def _(dve):
                dve.wait_ge(weights_in, 80)
                dve.wait_ge(consts, 5)
                nc.vector.tensor_scalar(conv_half[:], conv_w[:], 0.5, None, ALU.mult)
                dve.drain()
                for s in (conv_ready, silu_ready, local_ready, sums_ready, qk_tok_ready):
                    s.start(dve)

                def convolve(to, source, weight, taps, parts):
                    for tap in range(taps):
                        for part in parts:
                            shifted = source(part, tap)
                            scalar = weight(part, tap)
                            if tap == 0:
                                nc.vector.tensor_scalar(to(part), shifted, scalar, None, ALU.mult)
                            else:
                                nc.vector.scalar_tensor_tensor(to(part), shifted, scalar, to(part), ALU.mult, ALU.add)
                        dve.drain()

                with dve.Fori(0, B) as b:
                    dve.wait_ge(padded_ready.sem, padded_ready.now(b, 1))
                    convolve(lambda p: y[:, p[0], p[1], :],
                             lambda p, tap: padded[:, p[0], p[1], tap:tap + SEQ],
                             lambda p, tap: conv_half[:, p[0], p[1], tap:tap + 1],
                             CONV, [(a, c) for a in range(3) for c in range(KC)])
                    dve.sem_inc(conv_ready.sem, 1)
                    dve.wait_ge(tanh_ready.sem, tanh_ready.now(b, 1))
                    dve.wait_ge(left.sem, left.prev(b, 1))
                    dve.wait_ge(lm_turned.sem, lm_turned.prev(b, 1))
                    nc.vector.scalar_tensor_tensor(qk[:], tanh[:, 0:2, :, :], 1.0, y[:, 0:2, :, :], ALU.add, ALU.mult)
                    nc.vector.scalar_tensor_tensor(v_pad[:, :, PAD:], tanh[:, 2, :, :], 1.0, y[:, 2, :, :], ALU.add,
                                                   ALU.mult)
                    nc.vector.tensor_scalar(beta[:], tanh_beta[:], 0.5, 0.5, ALU.mult, ALU.add)
                    dve.drain()
                    dve.sem_inc(silu_ready.sem, 1)
                    convolve(lambda c: local_t[:, c, :],
                             lambda c, tap: v_pad[:, c, PAD - LOCAL + 1 + tap:PAD - LOCAL + 1 + tap + SEQ],
                             lambda c, tap: local_w[:, c, tap:tap + 1], LOCAL, range(KC))
                    dve.sem_inc(local_ready.sem, 1)
                    dve.wait_ge(squares_ready.sem, squares_ready.now(b, 1))
                    nc.vector.tensor_reduce(sums[:], squares[:], AX.X, ALU.add).then_inc(sums_ready.sem, 1)
                    dve.wait_ge(rnorm_step.sem, rnorm_step.now(b, 2))
                    nc.vector.tensor_tensor(qk_tok[:].rearrange("p a t (h d) -> p (a t h) d", d=MD),
                                            PS[:, 0:2, :].rearrange("p a (m d) -> p (a m) d", d=MD),
                                            spread(rnorm[:], MD), ALU.mult).then_inc(qk_tok_ready.sem, 1)

            @block.tensor
            def _(pe):
                pe.wait_ge(weights_in, 80)
                pe.wait_ge(consts, 5)
                for s in (projected, mid_done, qkv_turned, lm_turned, qk_turned, gram_done):
                    s.start(pe)
                mm = nc.tensor.matmul

                def turn(bank, source):
                    for t in range(TB):
                        for c in range(KC):
                            last = nc.tensor.transpose(PS[:, bank, t * D + c * P:t * D + (c + 1) * P],
                                                       source(c, t), core.ident[:])
                    return last

                with pe.Fori(0, B) as b:
                    pe.wait_ge(xt_in.sem, xt_in.now(b, 1))
                    pe.wait_ge(gram_ready.sem, gram_ready.prev(b, 1))
                    pe.wait_ge(squares_ready.sem, squares_ready.prev(b, 1))
                    pe.wait_ge(qk_t_ready.sem, qk_t_ready.prev(b, 1))
                    for a in range(3):
                        for oc in range(KC):
                            for c in range(KC):
                                mm(PS[:, a, oc * SEQ:(oc + 1) * SEQ], w[:, c, a, oc, :], xt[:, c, :],
                                   start=c == 0, stop=c == KC - 1)
                    for c in range(KC):
                        last = mm(PS[0:MH, 3, 0:SEQ], w_beta[:, c, :], xt[:, c, :], start=c == 0, stop=c == KC - 1)
                    last.then_inc(projected.sem, 1)
                    pe.wait_ge(silu_ready.sem, silu_ready.now(b, 1))
                    turn(0, lambda c, t: qk[:, 0, c, t * P:(t + 1) * P])
                    turn(1, lambda c, t: qk[:, 1, c, t * P:(t + 1) * P])
                    turn(2, lambda c, t: v_pad[:, c, PAD + t * P:PAD + (t + 1) * P]).then_inc(qkv_turned.sem, 1)
                    pe.wait_ge(mid_ready.sem, mid_ready.prev(b, 1))
                    for c in range(KC):
                        for tap in range(MID):
                            last = mm(PS[:, 4, c * SEQ:(c + 1) * SEQ], mid_diag[:, c, tap, :],
                                      v_pad[:, c, tap:tap + SEQ], start=tap == 0, stop=tap == MID - 1)
                    last.then_inc(mid_done.sem, 1)
                    pe.wait_ge(lm_ready.sem, lm_ready.prev(b, 1))
                    pe.wait_ge(local_ready.sem, local_ready.now(b, 1))
                    turn(5, lambda c, t: local_t[:, c, t * P:(t + 1) * P])
                    pe.wait_ge(mid_ready.sem, mid_ready.now(b, 1))
                    turn(6, lambda c, t: mid_t[:, c, t * P:(t + 1) * P]).then_inc(lm_turned.sem, 1)
                    pe.wait_ge(qk_tok_ready.sem, qk_tok_ready.now(b, 1))
                    for i, bank in enumerate((3, 7)):
                        for c in range(KC):
                            for t in range(TB):
                                last = nc.tensor.transpose(PS[:, bank, (c * TB + t) * P:(c * TB + t + 1) * P],
                                                           qk_tok[:, i, t, c * P:(c + 1) * P], core.ident[:])
                    last.then_inc(qk_turned.sem, 1)
                    pe.wait_ge(qk_t_ready.sem, qk_t_ready.now(b, 1))
                    for t in range(TB):
                        for g in range(KC):
                            for i in range(2):
                                keys = qk_t[MD * i:MD * (i + 1), 1, g, t * P:(t + 1) * P]
                                last = mm(PS[:, i, (t * 2 + g) * P:(t * 2 + g + 1) * P], keys, keys,
                                          start=True, stop=True)
                    last.then_inc(gram_done.sem, 1)


def block_mixer_solve(core):
    nc, scratch = core.nc, core.mixer
    NG = B * NCH * MH // P
    BG = B // NG
    C = CHUNK
    with ExitStack() as ctx:
        def sb(n, shape, dt=F32):
            return ctx.enter_context(nc.sbuf_tensor(f"ms_{n}", shape, dt))

        gram = sb("gram", [P, NG, C, C])
        beta = sb("beta", [P, NG, C])
        strict = sb("strict", [P, C, C])
        eye = sb("eye", [P, C, C])
        T = sb("T", [P, NG, C, C])
        product = sb("product", [P, NG * C * C])
        row = sb("row", [P, NG, C])
        out = sb("out", [P, NG, C, C])
        loaded = core.semaphore("ms_loaded")
        consts = core.semaphore("ms_constants_ready")
        solved = core.semaphore("ms_solved")
        stored = core.semaphore("ms_stored")
        with nc.Block() as block:
            @block.sync
            def _(sp):
                for g in range(NG):
                    for h in range(MH):
                        rows = slice(h, P, MH)
                        src = scratch.gram[g * BG:(g + 1) * BG, :, :, :, h, :]
                        sp.dma_start(gram[rows, g, :, :], src.rearrange("b u c i j -> (b u c) i j"))\
                            .then_inc(loaded, 16)
                        sp.dma_start(beta[rows, g, :], scratch.beta[g * BG:(g + 1) * BG, h, :, :])\
                            .then_inc(loaded, 16)
                sp.wait_ge(solved, 1)
                for b in range(B):
                    rows = slice((b % BG) * NCH * MH, (b % BG + 1) * NCH * MH)
                    sp.dma_start(scratch.solved.rearrange("n h j b i -> (n h) j b i")[:, :, b, :],
                                 out[rows, b // BG, :, :]).then_inc(stored, 16)
                sp.wait_ge(stored, 16 * B)

            @block.gpsimd
            def _(pool):
                nc.gpsimd.memset(strict[:], -1.0).then_inc(consts, 1)
                nc.gpsimd.memset(eye[:], 0.0).then_inc(consts, 1)
                pool.wait_ge(consts, 2)
                nc.gpsimd.affine_select(out=strict[:], in_=strict[:], compare_op=ALU.is_gt, fill=0.0, base=0,
                                        pattern=[[1, C], [-1, C]], channel_multiplier=0).then_inc(consts, 1)
                nc.gpsimd.affine_select(out=eye[:], in_=eye[:], compare_op=ALU.not_equal, fill=1.0, base=0,
                                        pattern=[[1, C], [-1, C]], channel_multiplier=0).then_inc(consts, 1)

            @block.vector
            def _(dve):
                dve.wait_ge(loaded, 16 * 2 * NG * MH)
                dve.wait_ge(consts, 4)
                for g in range(NG):
                    nc.vector.tensor_tensor(T[:, g, :, :], gram[:, g, :, :], strict[:], ALU.mult)
                dve.drain()
                nc.vector.tensor_tensor(T[:], T[:], spread(beta[:], C), ALU.mult)
                dve.drain()
                for i in range(1, C):
                    prod = product[:, 0:NG * i * i].rearrange("p (g c j) -> p g c j", g=NG, c=i)
                    nc.vector.tensor_tensor(prod, T[:, :, i, 0:i].unsqueeze(2).to_broadcast([P, NG, i, i]),
                                            T[:, :, 0:i, 0:i].rearrange("p g j c -> p g c j"), ALU.mult)
                    dve.drain()
                    nc.vector.tensor_reduce(row[:, :, 0:i], prod, AX.X, ALU.add)
                    dve.drain()
                    nc.vector.tensor_tensor(T[:, :, i, 0:i], T[:, :, i, 0:i], row[:, :, 0:i], ALU.add)
                    dve.drain()
                for g in range(NG):
                    nc.vector.tensor_tensor(out[:, g, :, :], T[:, g, :, :].rearrange("p i j -> p j i"), eye[:], ALU.add)
                dve.drain()
                nc.vector.tensor_tensor(out[:], out[:], spread(beta[:], C), ALU.mult).then_inc(solved, 1)


def block_mixer_scan(core):
    nc, PS, scratch = core.nc, core.PS, core.mixer
    C = CHUNK
    with ExitStack() as ctx:
        def sb(n, shape, dt=F32):
            return ctx.enter_context(nc.sbuf_tensor(f"mc_{n}", shape, dt))

        qk_bd = sb("qk_bd", [P, 2, 2, KC, B, P])
        k_bd = sb("k_bd", [P, 2, KC, B, P])
        t_bd = sb("t_bd", [P, 2, B, P])
        v = sb("v", [P, 2, B, MD])
        causal = sb("causal", [P, P])
        attn = sb("attn", [P, B, P])
        rest = sb("rest", [P, B, MD])
        u = sb("u", [P, B, MD])
        S = sb("S", [P, KC, B, MD])
        o = sb("o", [P, 2, B, MD])
        zeroed = core.semaphore("mc_zeroed")
        N_LOADS = 4 * MH + MH
        loaded = [core.semaphore(f"mc_loaded_{i}") for i in range(2)]

        def sig(n, per, unit=1):
            return Signal(core, f"mc_{n}", per, unit)

        attn_done = sig("attn_done", 2)
        attn_ready = sig("attn_ready", 2)
        ks_done = sig("ks_done", 2)
        rest_ready = sig("rest_ready", 2)
        u_done = sig("u_done", 2)
        u_ready = sig("u_ready", 2)
        o_done = sig("o_done", 2)
        o_ready = sig("o_ready", 2)
        s_done = sig("state_update_done", 2)
        s_ready = sig("state_ready", 2)
        o_stored = sig("o_stored", 2 * MH, 16)

        def by_head(bank):
            return PS[:, bank, :].rearrange("p (b d) -> p b d", d=MD)

        with nc.Block() as block:
            @block.sync
            def _(sp):
                sp.wait_ge(zeroed, 3)
                o_stored.start(sp)
                with sp.Fori(0, NCH // 2) as m:
                    def load(par):
                        n = bass.ds(2 * m + par, 1)
                        for h in range(MH):
                            c, i = h // 2, h % 2
                            at = slice(h * C, (h + 1) * C)
                            rows = slice(i * MD, (i + 1) * MD)
                            for a in range(2):
                                sp.dma_start(qk_bd[rows, par, a, c, :, at],
                                             scratch.qk_t[a, rows, c, :, n, :].rearrange("p b a t -> p b (a t)"))\
                                    .then_inc(loaded[par], 16)
                            sp.dma_start(k_bd[at, par, c, :, rows],
                                         scratch.k[:, n, :, h, :].rearrange("b a t d -> (a t) b d"))\
                                .then_inc(loaded[par], 16)
                            sp.dma_start(v[at, par, :, :],
                                         scratch.outs[3].rearrange("(b n t) f -> b n t f", n=NCH, t=C)
                                         [:, n, :, h * MD:(h + 1) * MD].rearrange("b a t d -> (a t) b d"))\
                                .then_inc(loaded[par], 16)
                            sp.dma_start(t_bd[at, par, :, at],
                                         scratch.solved[n, h, :, :, :].rearrange("a j b i -> (a j) b i"))\
                                .then_inc(loaded[par], 16)

                    sp.wait_ge(s_done.sem, s_done.prev(m, 1))
                    load(0)
                    sp.wait_ge(s_done.sem, s_done.prev(m, 2))
                    load(1)
                    for par in range(2):
                        n = bass.ds(2 * m + par, 1)
                        sp.wait_ge(o_ready.sem, o_ready.now(m, par + 1))
                        for h in range(MH):
                            sp.dma_start(scratch.outs[2].rearrange("(b n t) f -> b n t f", n=NCH, t=C)
                                         [:, n, :, h * MD:(h + 1) * MD].rearrange("b a t d -> (a t) b d"),
                                         o[h * C:(h + 1) * C, par, :, :]).then_inc(o_stored.sem, 16)
                sp.wait_ge(o_stored.sem, o_stored.now(NCH // 2 - 1, 2 * MH))

            @block.gpsimd
            def _(pool):
                nc.gpsimd.memset(qk_bd[:], 0.0).then_inc(zeroed, 1)
                nc.gpsimd.memset(k_bd[:], 0.0).then_inc(zeroed, 1)
                nc.gpsimd.memset(t_bd[:], 0.0).then_inc(zeroed, 1)
                nc.gpsimd.memset(S[:], 0.0).then_inc(zeroed, 1)
                nc.gpsimd.memset(causal[:], 1.0).then_inc(zeroed, 1)
                pool.wait_ge(zeroed, 5)
                nc.gpsimd.affine_select(out=causal[:], in_=causal[:], compare_op=ALU.is_ge, fill=0.0, base=0,
                                        pattern=[[1, P]], channel_multiplier=-1).then_inc(zeroed, 1)

            @block.scalar
            def _(act):
                for s in (u_ready, o_ready):
                    s.start(act)
                with act.Fori(0, NCH // 2) as m:
                    act.wait_ge(o_stored.sem, o_stored.prev(m, 2 * MH))
                    for par in range(2):
                        act.wait_ge(u_done.sem, u_done.now(m, par + 1))
                        nc.scalar.activation(u[:], by_head(3), ACT.Copy).then_inc(u_ready.sem, 1)
                        act.wait_ge(o_done.sem, o_done.now(m, par + 1))
                        nc.scalar.activation(o[:, par, :, :], by_head(4), ACT.Copy).then_inc(o_ready.sem, 1)

            @block.vector
            def _(dve):
                dve.wait_ge(zeroed, 6)
                for s in (attn_ready, rest_ready, s_ready):
                    s.start(dve)
                with dve.Fori(0, NCH // 2) as m:
                    for par in range(2):
                        dve.wait_ge(attn_done.sem, attn_done.now(m, par + 1))
                        dve.wait_ge(o_done.sem, o_done.now(m, 1) if par else o_done.prev(m, 2))
                        for half in range(2):
                            nc.vector.tensor_tensor(attn[:, 4 * half:4 * half + 4, :],
                                                    PS[:, half, :].rearrange("p (b i) -> p b i", i=P),
                                                    causal[:, :].unsqueeze(1).to_broadcast([P, 4, P]), ALU.mult)
                        dve.drain()
                        dve.sem_inc(attn_ready.sem, 1)
                        dve.wait_ge(ks_done.sem, ks_done.now(m, par + 1))
                        nc.vector.tensor_tensor(rest[:], v[:, par, :, :], by_head(2), ALU.subtract)\
                            .then_inc(rest_ready.sem, 1)
                        dve.wait_ge(s_done.sem, s_done.now(m, par + 1))
                        for c in range(KC):
                            nc.vector.tensor_tensor(S[:, c, :, :], by_head(5 + c), S[:, c, :, :], ALU.add)
                        dve.drain()
                        dve.sem_inc(s_ready.sem, 1)

            @block.tensor
            def _(pe):
                pe.wait_ge(zeroed, 6)
                for s in (attn_done, ks_done, u_done, o_done, s_done):
                    s.start(pe)
                mm = nc.tensor.matmul
                with pe.Fori(0, NCH // 2) as m:
                    for par in range(2):
                        pe.wait_ge(loaded[par], (m + 1) * (16 * N_LOADS))
                        before = (lambda s: s.now(m, 1)) if par else (lambda s: s.prev(m, 2))
                        pe.wait_ge(attn_ready.sem, before(attn_ready))
                        for b in range(B):
                            for c in range(KC):
                                last = mm(PS[:, b // 4, (b % 4) * P:(b % 4 + 1) * P], qk_bd[:, par, 1, c, b, :],
                                          qk_bd[:, par, 0, c, b, :], start=c == 0, stop=c == KC - 1)
                        last.then_inc(attn_done.sem, 1)
                        pe.wait_ge(s_ready.sem, before(s_ready))
                        pe.wait_ge(rest_ready.sem, before(rest_ready))
                        for b in range(B):
                            for c in range(KC):
                                last = mm(by_head(2)[:, b, :], qk_bd[:, par, 1, c, b, :], S[:, c, b, :],
                                          start=c == 0, stop=c == KC - 1)
                        last.then_inc(ks_done.sem, 1)
                        pe.wait_ge(rest_ready.sem, rest_ready.now(m, par + 1))
                        pe.wait_ge(u_ready.sem, before(u_ready))
                        for b in range(B):
                            last = mm(by_head(3)[:, b, :], t_bd[:, par, b, :], rest[:, b, :], start=True, stop=True)
                        last.then_inc(u_done.sem, 1)
                        pe.wait_ge(u_ready.sem, u_ready.now(m, par + 1))
                        pe.wait_ge(attn_ready.sem, attn_ready.now(m, par + 1))
                        pe.wait_ge(o_ready.sem, before(o_ready))
                        for b in range(B):
                            for c in range(KC):
                                mm(by_head(4)[:, b, :], qk_bd[:, par, 0, c, b, :], S[:, c, b, :],
                                   start=c == 0, stop=False)
                            last = mm(by_head(4)[:, b, :], attn[:, b, :], u[:, b, :], start=False, stop=True)
                        last.then_inc(o_done.sem, 1)
                        for b in range(B):
                            for c in range(KC):
                                last = mm(by_head(5 + c)[:, b, :], k_bd[:, par, c, b, :], u[:, b, :],
                                          start=True, stop=True)
                        last.then_inc(s_done.sem, 1)


def block_mixer_mix(core):
    nc, PS, dram, scratch = core.nc, core.PS, core.dram, core.mixer
    O = len(OUTS)
    HB = 5
    NF = 14 * MH
    FLOOR = 0.01
    PAIRS = [(0, 1, 3), (1, 2, 2), (2, 3, 1)]
    with ExitStack() as ctx:
        def sb(n, shape, dt=F32):
            return ctx.enter_context(nc.sbuf_tensor(f"mm_{n}", shape, dt))

        def sig(n, per, unit=1):
            return Signal(core, f"mm_{n}", per, unit)

        w1 = sb("w1", [P, KC + 1, HB, P])
        b1 = sb("b1", [P, HB])
        w2 = sb("w2", [P, HB, O * MH])
        b2 = sb("b2", [P, O * MH])
        mix_w = sb("mix_w", [P, D])
        onorm_w = sb("onorm_w", [P, MD])
        wo = sb("wo", [P, KC, D])
        eps5 = sb("eps5", [P, 16])
        inv_md = sb("inv_md", [P, 16])
        xt = sb("xt", [P, KC, SEQ])
        outs = sb("outs", [P, TB, O, D])
        squares = sb("squares", [P, TB, O, D])
        pairs = sb("pairs", [P, TB, 6, D])
        sums = sb("sums", [P, TB, O, MH])
        sumsq = sb("sumsq", [P, TB, O, MH])
        stats = sb("stats", [P, TB, P])
        stats_t = sb("stats_t", [NF, SEQ])
        hid = sb("hid", [P, HB, SEQ])
        tanh = sb("tanh", [P, HB, SEQ])
        act2 = sb("act2", [P, HB, SEQ])
        logits = sb("logits", [P, TB, MH, O])
        top = sb("top", [P, TB, MH])
        expd = sb("expd", [P, TB, MH, O])
        den = sb("den", [P, TB, MH])
        prob = sb("prob", [P, TB, MH, O])
        weighted = sb("weighted", [P, TB, O, D])
        mixed = sb("mixed", [P, TB, D])
        mixed2 = sb("mixed2", [P, TB, D])
        ms = sb("ms", [P, 2, TB, MH])
        rms = sb("rms", [P, 2, TB, MH])
        mixed_t = sb("mixed_t", [P, KC, SEQ])
        norm = Norm(core, ctx, "mm", 3, 7)

        weights_in = core.semaphore("mm_weights_in")
        consts = core.semaphore("mm_constants_ready")
        w2_halved = core.semaphore("mm_w2_halved")
        N_IN = 1 + TB
        inputs_in = sig("inputs_in", N_IN, 16)
        pairs_ready = sig("pairs_ready", 1)
        squares_ready = sig("squares_ready", 1)
        stats_ready = sig("stats_ready", 1)
        stats_turned = sig("stats_turned", 1)
        stats_t_ready = sig("stats_t_ready", 1)
        hid_done = sig("hid_done", 1)
        tanh_ready = sig("tanh_ready", 1)
        act_ready = sig("hidden_ready", 1)
        logits_done = sig("logits_done", 1)
        shifted_ready = sig("shifted_ready", 1)
        exp_ready = sig("exp_ready", 1)
        ms_ready = sig("ms_ready", 2)
        rms_step = sig("rms_step", 6)
        mixed_ready = sig("mixed_ready", 1)
        mixed_turned = sig("mixed_turned", 1)
        mixed_t_ready = sig("mixed_t_ready", 1)
        out_done = sig("out_done", 1)

        def heads(ap):
            return ap.rearrange("p t (h d) -> p (t h) d", d=MD)

        with nc.Block() as block:
            @block.sync
            def _(sp):
                for dst, n in ((w1, "mm_w1"), (b1, "mm_b1"), (w2, "mm_w2"), (wo, "mm_wo")):
                    sp.dma_start(dst[:], dram[n]).then_inc(weights_in, 16)
                for dst, n in ((b2, "mm_b2"), (mix_w, "mm_mix_w"), (onorm_w, "mm_onorm_w")):
                    sp.dma_start(dst[:], dram[n].partition_broadcast(P)).then_inc(weights_in, 16)
                inputs_in.start(sp)
                norm.start_sync(sp)
                with sp.Fori(0, B) as b:
                    sp.wait_ge(hid_done.sem, hid_done.prev(b, 1))
                    sp.wait_ge(mixed_ready.sem, mixed_ready.prev(b, 1))
                    sp.dma_start(xt[:], core.xt_of(b)).then_inc(inputs_in.sem, 16)
                    for t in range(TB):
                        sp.dma_start(outs[:, t, :, :], scratch.outs[:, bass.ds(b * SEQ + t * P, P), :]
                                     .rearrange("o p f -> p o f")).then_inc(inputs_in.sem, 16)
                    norm.load(sp, b)
                    norm.store(sp, b)

            @block.gpsimd
            def _(pool):
                nc.gpsimd.memset(eps5[:], 1e-5).then_inc(consts, 1)
                nc.gpsimd.memset(inv_md[:], 1.0 / MD).then_inc(consts, 1)
                nc.gpsimd.memset(stats[:], 0.0).then_inc(consts, 1)
                pool.wait_ge(consts, 3)
                pairs_ready.start(pool)
                rms_step.start(pool)
                norm.start_gpsimd(pool)
                with pool.Fori(0, B) as b:
                    pool.wait_ge(inputs_in.sem, inputs_in.now(b, N_IN))
                    pool.wait_ge(stats_ready.sem, stats_ready.prev(b, 1))
                    for t in range(TB):
                        at = 0
                        for first, second, n in PAIRS:
                            nc.gpsimd.tensor_tensor(pairs[:, t, at:at + n, :], outs[:, t, second:second + n, :],
                                                    outs[:, t, first, :].unsqueeze(1).to_broadcast([P, n, D]),
                                                    ALU.mult)
                            at += n
                    pool.drain()
                    pool.sem_inc(pairs_ready.sem, 1)
                    for k in range(2):
                        pool.wait_ge(ms_ready.sem, ms_ready.now(b, k + 1))
                        flat = rms[:, k, :, :].rearrange("p t h -> p (t h)")
                        steps = ((ms[:, k, :, :].rearrange("p t h -> p (t h)"), inv_md, ALU.mult),
                                 (flat, eps5, ALU.add), (flat, core.minus_half, ALU.pow))
                        for i, (src, const, op) in enumerate(steps):
                            if i:
                                pool.wait_ge(rms_step.sem, rms_step.now(b, 3 * k + i))
                            nc.gpsimd.tensor_tensor(flat, src, const[:, 0:TB * MH], op).then_inc(rms_step.sem, 1)
                    norm.gpsimd(pool, b)

            @block.scalar
            def _(act):
                act.wait_ge(weights_in, 112)
                for s in (squares_ready, stats_t_ready, tanh_ready, exp_ready, mixed_t_ready):
                    s.start(act)
                norm.start_scalar(act)
                with act.Fori(0, B) as b:
                    act.wait_ge(inputs_in.sem, inputs_in.now(b, N_IN))
                    act.wait_ge(stats_ready.sem, stats_ready.prev(b, 1))
                    nc.scalar.activation(squares[:], outs[:], ACT.Square).then_inc(squares_ready.sem, 1)
                    act.wait_ge(stats_turned.sem, stats_turned.now(b, 1))
                    nc.scalar.activation(stats_t[:], PS[0:NF, 3, 0:SEQ], ACT.Copy).then_inc(stats_t_ready.sem, 1)
                    act.wait_ge(hid_done.sem, hid_done.now(b, 1))
                    act.wait_ge(act_ready.sem, act_ready.prev(b, 1))
                    for h in range(HB):
                        nc.scalar.activation(hid[:, h, :], PS[:, h // 2, (h % 2) * SEQ:(h % 2 + 1) * SEQ],
                                             ACT.Identity, bias=b1[:, h:h + 1])
                    act.drain()
                    nc.scalar.activation(tanh[:], hid[:], ACT.Tanh, scale=0.5).then_inc(tanh_ready.sem, 1)
                    act.wait_ge(shifted_ready.sem, shifted_ready.now(b, 1))
                    nc.scalar.activation(expd[:], logits[:], ACT.Exp).then_inc(exp_ready.sem, 1)
                    act.wait_ge(mixed_turned.sem, mixed_turned.now(b, 1))
                    nc.scalar.activation(mixed_t[:].rearrange("p c n -> p (c n)"), PS[:, 5, :],
                                         ACT.Copy).then_inc(mixed_t_ready.sem, 1)
                    norm.scalar(act, b)

            @block.vector
            def _(dve):
                dve.wait_ge(weights_in, 112)
                nc.vector.tensor_scalar(w2[:], w2[:], 0.5, None, ALU.mult).then_inc(w2_halved, 1)
                dve.wait_ge(consts, 3)
                for s in (stats_ready, act_ready, shifted_ready, ms_ready, mixed_ready):
                    s.start(dve)
                norm.start_vector(dve)
                with dve.Fori(0, B) as b:
                    dve.wait_ge(inputs_in.sem, inputs_in.now(b, N_IN))
                    dve.wait_ge(stats_turned.sem, stats_turned.prev(b, 1))
                    by_kind = stats[:, :, 0:NF].rearrange("p t (k h) -> p t k h", h=MH)
                    nc.vector.tensor_reduce(sums[:], outs[:].rearrange("p t o (h d) -> p (t o) h d", d=MD), AX.X,
                                            ALU.add)
                    dve.wait_ge(squares_ready.sem, squares_ready.now(b, 1))
                    nc.vector.tensor_reduce(sumsq[:], squares[:].rearrange("p t o (h d) -> p (t o) h d", d=MD), AX.X,
                                            ALU.add)
                    dve.wait_ge(pairs_ready.sem, pairs_ready.now(b, 1))
                    for t in range(TB):
                        nc.vector.tensor_reduce(by_kind[:, t, 8:14, :], pairs[:, t, :, :]
                                                .rearrange("p k (h d) -> p k h d", d=MD), AX.X, ALU.add)
                    dve.drain()
                    nc.vector.tensor_scalar(by_kind[:, :, 8:14, :], by_kind[:, :, 8:14, :], 1.0 / MD, None, ALU.mult)
                    for t in range(TB):
                        nc.vector.tensor_scalar(by_kind[:, t, 0:8:2, :], sums[:, t, :, :], 1.0 / MD, None, ALU.mult)
                    dve.drain()
                    for t in range(TB):
                        nc.vector.tensor_tensor(sums[:, t, :, :], sums[:, t, :, :], by_kind[:, t, 0:8:2, :], ALU.mult)
                    dve.drain()
                    nc.vector.tensor_tensor(sumsq[:], sumsq[:], sums[:], ALU.subtract)
                    dve.drain()
                    for t in range(TB):
                        nc.vector.tensor_scalar(by_kind[:, t, 1:8:2, :], sumsq[:, t, :, :], 1.0 / (MD - 1), None,
                                                ALU.mult)
                    dve.drain()
                    dve.sem_inc(stats_ready.sem, 1)
                    dve.wait_ge(tanh_ready.sem, tanh_ready.now(b, 1))
                    dve.wait_ge(logits_done.sem, logits_done.prev(b, 1))
                    nc.vector.scalar_tensor_tensor(act2[:], tanh[:], 1.0, hid[:], ALU.add, ALU.mult)\
                        .then_inc(act_ready.sem, 1)
                    dve.wait_ge(logits_done.sem, logits_done.now(b, 1))
                    flat = logits[:].rearrange("p t h o -> p t (h o)")
                    nc.vector.tensor_tensor(flat, PS[:, 4, 0:TB * O * MH].rearrange("p (t n) -> p t n", t=TB),
                                            b2[:, :].unsqueeze(1).to_broadcast([P, TB, O * MH]), ALU.add)
                    dve.drain()
                    nc.vector.tensor_reduce(top[:], logits[:], AX.X, ALU.max)
                    dve.drain()
                    nc.vector.tensor_tensor(logits[:], logits[:], spread(top[:], O), ALU.subtract)\
                        .then_inc(shifted_ready.sem, 1)
                    dve.wait_ge(exp_ready.sem, exp_ready.now(b, 1))
                    nc.vector.tensor_reduce(den[:], expd[:], AX.X, ALU.add)
                    dve.drain()
                    nc.vector.reciprocal(den[:], den[:])
                    dve.drain()
                    nc.vector.tensor_tensor(prob[:], expd[:], spread(den[:], O), ALU.mult)
                    dve.drain()
                    nc.vector.tensor_scalar(prob[:], prob[:], 1.0 - 4.0 * FLOOR, FLOOR, ALU.mult, ALU.add)
                    dve.drain()
                    for t in range(TB):
                        nc.vector.tensor_tensor(weighted[:, t, :, :].rearrange("p o (h d) -> p o h d", d=MD),
                                                outs[:, t, :, :].rearrange("p o (h d) -> p o h d", d=MD),
                                                spread(prob[:, t, :, :].rearrange("p h o -> p o h"), MD), ALU.mult)
                    dve.drain()
                    for t in range(TB):
                        nc.vector.tensor_reduce(mixed[:, t, :], weighted[:, t, :, :].rearrange("p o f -> p f o"), AX.X,
                                                ALU.add)
                    dve.drain()

                    def mean_square(k, src):
                        nc.vector.tensor_tensor(weighted[:, :, 0, :], src[:], src[:], ALU.mult)
                        dve.drain()
                        nc.vector.tensor_reduce(ms[:, k, :, :], weighted[:, :, 0, :]
                                                .rearrange("p t (h d) -> p t h d", d=MD), AX.X, ALU.add)\
                            .then_inc(ms_ready.sem, 1)
                        dve.wait_ge(rms_step.sem, rms_step.now(b, 3 * k + 3))
                        nc.vector.tensor_tensor(heads(mixed2[:] if k == 0 else mixed[:]), heads(src[:]),
                                                spread(rms[:, k, :, :].rearrange("p t h -> p (t h)"), MD), ALU.mult)
                        dve.drain()

                    mean_square(0, mixed)
                    nc.vector.tensor_tensor(mixed2[:], mixed2[:], mix_w[:, :].unsqueeze(1).to_broadcast([P, TB, D]),
                                            ALU.mult)
                    dve.drain()
                    dve.wait_ge(mixed_turned.sem, mixed_turned.prev(b, 1))
                    mean_square(1, mixed2)
                    nc.vector.tensor_tensor(heads(mixed[:]), heads(mixed[:]),
                                            onorm_w[:, :].unsqueeze(1).to_broadcast([P, TB * MH, MD]), ALU.mult)\
                        .then_inc(mixed_ready.sem, 1)
                    norm.vector(dve, b, (out_done.sem, out_done.now(b, 1)))

            @block.tensor
            def _(pe):
                pe.wait_ge(weights_in, 112)
                pe.wait_ge(consts, 3)
                pe.wait_ge(w2_halved, 1)
                for s in (stats_turned, hid_done, logits_done, mixed_turned, out_done):
                    s.start(pe)
                norm.start_tensor(pe)
                mm = nc.tensor.matmul
                with pe.Fori(0, B) as b:
                    pe.wait_ge(stats_ready.sem, stats_ready.now(b, 1))
                    pe.wait_ge(stats_t_ready.sem, stats_t_ready.prev(b, 1))
                    for t in range(TB):
                        last = nc.tensor.transpose(PS[:, 3, t * P:(t + 1) * P], stats[:, t, :], core.ident[:])
                    last.then_inc(stats_turned.sem, 1)
                    pe.wait_ge(stats_t_ready.sem, stats_t_ready.now(b, 1))
                    pe.wait_ge(tanh_ready.sem, tanh_ready.prev(b, 1))
                    for h in range(HB):
                        to = PS[:, h // 2, (h % 2) * SEQ:(h % 2 + 1) * SEQ]
                        for c in range(KC):
                            mm(to, w1[:, c, h, :], xt[:, c, :], start=c == 0, stop=False)
                        last = mm(to, w1[0:NF, KC, h, :], stats_t[:], start=False, stop=True)
                    last.then_inc(hid_done.sem, 1)
                    pe.wait_ge(act_ready.sem, act_ready.now(b, 1))
                    pe.wait_ge(shifted_ready.sem, shifted_ready.prev(b, 1))
                    for t in range(TB):
                        for h in range(HB):
                            last = mm(PS[:, 4, t * O * MH:(t + 1) * O * MH], act2[:, h, t * P:(t + 1) * P], w2[:, h, :],
                                      start=h == 0, stop=h == HB - 1)
                    last.then_inc(logits_done.sem, 1)
                    pe.wait_ge(mixed_ready.sem, mixed_ready.now(b, 1))
                    pe.wait_ge(mixed_t_ready.sem, mixed_t_ready.prev(b, 1))
                    for c in range(KC):
                        for t in range(TB):
                            last = nc.tensor.transpose(PS[:, 5, (c * TB + t) * P:(c * TB + t + 1) * P],
                                                       mixed[:, t, c * P:(c + 1) * P], core.ident[:])
                    last.then_inc(mixed_turned.sem, 1)
                    pe.wait_ge(mixed_t_ready.sem, mixed_t_ready.now(b, 1))
                    pe.wait_ge(norm.xt_ready.sem, norm.xt_ready.prev(norm.turn(b), 1))
                    for t in range(TB):
                        for c in range(KC):
                            last = mm(PS[:, 7, t * D:(t + 1) * D], mixed_t[:, c, t * P:(t + 1) * P], wo[:, c, :],
                                      start=c == 0, stop=c == KC - 1)
                    last.then_inc(out_done.sem, 1)
                    norm.tensor(pe, b)


def block_experts_1(core):
    E, HB = 8, 8
    nc, PS, dram = core.nc, core.PS, core.dram
    with ExitStack() as ctx:
        def sb(n, shape, dt=F32):
            return ctx.enter_context(nc.sbuf_tensor(f"eb_{n}", shape, dt))

        def sig(n, per, unit=1):
            return Signal(core, f"eb_{n}", per, unit)

        up = sb("up", [P, KC, E, HB, P])
        down = sb("down", [P, E, HB, D])
        up_bias = sb("up_bias", [P, E, HB])
        down_bias = sb("down_bias", [P, D])
        router = sb("router", [P, KC, E])
        router_bias = sb("router_bias", [P, E])
        gamma = sb("gamma", [P, D])
        beta = sb("beta", [P, D])
        iota8 = sb("iota8", [P, E])
        xt = sb("xt", [P, KC, SEQ])
        logits = sb("logits", [P, TB, E])
        best = sb("best", [P, TB, 8])
        index = sb("index", [P, TB, 8], mybir.dt.uint32)
        index_f = sb("index_f", [P, TB, 8])
        chosen = sb("chosen", [P, TB, 2, E])
        gap = sb("gap", [P, TB])
        mix = sb("mix", [P, TB, 2])
        exp_gap = sb("exp_gap", [P, TB])
        weight = sb("weight", [P, TB, E])
        weight_t = sb("weight_t", [P, SEQ])
        hidden = sb("hidden", [P, 2, HB // 2, SEQ])
        total = sb("total", [P, TB, D])
        inner_stats = sb("inner_stats", [P, TB, 6])
        inner_mv = sb("inner_mean_var", [P, TB, 2])
        inner_rstd = sb("inner_rstd", [P, TB])
        norm = Norm(core, ctx, "eb", 5, 7)

        weights_in = core.semaphore("eb_weights_in")
        consts = core.semaphore("eb_constants_ready")
        xt_in = sig("xt_in", 1, 16)
        router_done = sig("router_done", 1)
        gap_ready = sig("gap_ready", 1)
        exp_ready = sig("exp_ready", 1)
        weight_ready = sig("weight_ready", 1)
        weight_turned = sig("weight_turned", 1)
        weight_t_ready = sig("weight_t_ready", 1)
        bias_done = sig("mixed_bias_done", 1)
        total_started = sig("total_started", 1)
        up_done = sig("up_done", 2 * E)
        hidden_ready = sig("hidden_ready", 2 * E)
        down_half = sig("down_half", 2 * E)
        added = sig("expert_added", E)
        inner_var_ready = sig("inner_variance_ready", 1)
        inner_rstd_step = sig("inner_rstd_step", 2)

        def tiles(ap):
            return ap.rearrange("p (t d) -> p t d", t=TB)

        def half_banks(h):
            return PS[:, 2 * (h % 2):2 * (h % 2) + 2, :].rearrange("p a (m n) -> p (a m) n", n=SEQ)

        with nc.Block() as block:
            @block.sync
            def _(sp):
                for dst, n in ((up_bias, "eb_up_bias"), (router, "eb_router")):
                    sp.dma_start(dst[:], dram[n]).then_inc(weights_in, 16)
                sp.dma_start(down_bias[0:E, :], dram["eb_down_bias"]).then_inc(weights_in, 16)
                for dst, n in ((router_bias, "eb_router_bias"), (gamma, "eb_gamma"), (beta, "eb_beta")):
                    sp.dma_start(dst[:], dram[n].partition_broadcast(P)).then_inc(weights_in, 16)
                sp.dma_start(up[:], dram["eb_up"]).then_inc(weights_in, 16)
                sp.dma_start(down[:], dram["eb_down"]).then_inc(weights_in, 16)
                xt_in.start(sp)
                norm.start_sync(sp)
                with sp.Fori(0, B) as b:
                    sp.wait_ge(up_done.sem, up_done.prev(b, 2 * E))
                    sp.dma_start(xt[:], core.xt_of(b)).then_inc(xt_in.sem, 16)
                    norm.load(sp, b)
                    norm.store(sp, b, last=True)

            @block.gpsimd
            def _(pool):
                nc.gpsimd.iota(iota8[:], pattern=[[1, E]], base=0, channel_multiplier=0,
                               allow_small_or_imprecise_dtypes=True).then_inc(consts, 1)
                inner_rstd_step.start(pool)
                norm.start_gpsimd(pool)
                with pool.Fori(0, B) as b:
                    pool.wait_ge(inner_var_ready.sem, inner_var_ready.now(b, 1))
                    nc.gpsimd.tensor_tensor(inner_rstd[:], inner_mv[:, :, 1], core.eps[:, 0:TB],
                                            ALU.add).then_inc(inner_rstd_step.sem, 1)
                    pool.wait_ge(inner_rstd_step.sem, inner_rstd_step.now(b, 1))
                    nc.gpsimd.tensor_tensor(inner_rstd[:], inner_rstd[:], core.minus_half[:, 0:TB],
                                            ALU.pow).then_inc(inner_rstd_step.sem, 1)
                    norm.gpsimd(pool, b)

            @block.scalar
            def _(act):
                act.wait_ge(weights_in, 128)
                for s in (exp_ready, weight_t_ready, hidden_ready):
                    s.start(act)
                norm.start_scalar(act)
                with act.Fori(0, B) as b:
                    act.wait_ge(gap_ready.sem, gap_ready.now(b, 1))
                    nc.scalar.activation(exp_gap[:], gap[:], ACT.Exp).then_inc(exp_ready.sem, 1)
                    act.wait_ge(weight_turned.sem, weight_turned.now(b, 1))
                    nc.scalar.activation(weight_t[0:E, :], PS[0:E, 6, 0:SEQ], ACT.Copy).then_inc(weight_t_ready.sem, 1)
                    for h in range(2 * E):
                        act.wait_ge(up_done.sem, up_done.now(b, h + 1))
                        if h >= 2:
                            act.wait_ge(down_half.sem, down_half.now(b, h - 1))
                        else:
                            act.wait_ge(down_half.sem, down_half.prev(b, 2 * E - 1 + h))
                        for m in range(HB // 2):
                            n = (h % 2) * (HB // 2) + m
                            last = nc.scalar.activation(hidden[:, h % 2, m, :], half_banks(h)[:, m, :], ACT.Relu,
                                                        bias=up_bias[:, h // 2, n:n + 1])
                        act.drain()
                        act.sem_inc(hidden_ready.sem, 1)

            @block.vector
            def _(dve):
                dve.wait_ge(weights_in, 128)
                dve.wait_ge(consts, 1)
                for s in (gap_ready, weight_ready, total_started, added, inner_var_ready):
                    s.start(dve)
                norm.start_vector(dve)
                with dve.Fori(0, B) as b:
                    dve.wait_ge(router_done.sem, router_done.now(b, 1))
                    nc.vector.tensor_tensor(logits[:], PS[:, 6, 0:TB * E].rearrange("p (t e) -> p t e", t=TB),
                                            router_bias[:, :].unsqueeze(1).to_broadcast([P, TB, E]), ALU.add)
                    dve.drain()
                    for t in range(TB):
                        top2(nc, dve, t, logits, iota8, best, index, index_f, chosen)
                    nc.vector.tensor_tensor(gap[:], best[:, :, 1], best[:, :, 0], ALU.subtract)\
                        .then_inc(gap_ready.sem, 1)
                    dve.wait_ge(exp_ready.sem, exp_ready.now(b, 1))
                    nc.vector.tensor_scalar(mix[:, :, 1], exp_gap[:], 1.0, None, ALU.add)
                    dve.drain()
                    nc.vector.reciprocal(mix[:, :, 0], mix[:, :, 1])
                    dve.drain()
                    nc.vector.tensor_tensor(mix[:, :, 1], mix[:, :, 0], exp_gap[:], ALU.mult)
                    dve.drain()
                    nc.vector.tensor_tensor(chosen[:], chosen[:], spread(mix[:], E), ALU.mult)
                    dve.drain()
                    nc.vector.tensor_tensor(weight[:], chosen[:, :, 0, :], chosen[:, :, 1, :], ALU.add)\
                        .then_inc(weight_ready.sem, 1)
                    dve.wait_ge(bias_done.sem, bias_done.now(b, 1))
                    nc.vector.tensor_copy(total[:], tiles(PS[:, 6, :])).then_inc(total_started.sem, 1)
                    for e in range(E):
                        dve.drain()
                        dve.wait_ge(down_half.sem, down_half.now(b, 2 * e + 2))
                        for t in range(TB):
                            nc.vector.scalar_tensor_tensor(total[:, t, :], tiles(PS[:, 4 + e % 2, :])[:, t, :],
                                                           weight[:, t, e:e + 1], total[:, t, :], ALU.mult, ALU.add)
                        dve.drain()
                        dve.sem_inc(added.sem, 1)
                    dve.wait_ge(norm.residual_in.sem, norm.residual_in.now(norm.turn(b), 1))
                    nc.vector.tensor_tensor(total[:], total[:], norm.x_in[:], ALU.add)
                    dve.drain()
                    for t in range(TB):
                        nc.vector.bn_stats(inner_stats[:, t, :], total[:, t, :])
                    dve.drain()
                    for t in range(TB):
                        nc.vector.bn_aggr(inner_mv[:, t, :], inner_stats[:, t, :])
                    dve.drain()
                    dve.sem_inc(inner_var_ready.sem, 1)
                    dve.wait_ge(inner_rstd_step.sem, inner_rstd_step.now(b, 2))
                    for t in range(TB):
                        nc.vector.tensor_scalar(total[:, t, :], total[:, t, :], inner_mv[:, t, 0:1],
                                                inner_rstd[:, t:t + 1], ALU.subtract, ALU.mult)
                    dve.drain()
                    for w, op in ((gamma, ALU.mult), (beta, ALU.add)):
                        nc.vector.tensor_tensor(total[:], total[:], w[:, :].unsqueeze(1).to_broadcast([P, TB, D]), op)
                        dve.drain()
                    norm.vector(dve, b, (down_half.sem, down_half.now(b, 2 * E)), source=total[:])

            @block.tensor
            def _(pe):
                pe.wait_ge(weights_in, 128)
                for s in (router_done, weight_turned, bias_done, up_done, down_half):
                    s.start(pe)
                norm.start_tensor(pe)
                mm = nc.tensor.matmul
                with pe.Fori(0, B) as b:
                    pe.wait_ge(xt_in.sem, xt_in.now(b, 1))
                    pe.wait_ge(total_started.sem, total_started.prev(b, 1))
                    for t in range(TB):
                        for c in range(KC):
                            last = mm(PS[:, 6, t * E:(t + 1) * E], xt[:, c, t * P:(t + 1) * P], router[:, c, :],
                                      start=c == 0, stop=c == KC - 1)
                    last.then_inc(router_done.sem, 1)

                    def up_half(h):
                        e = h // 2
                        if h >= 2:
                            pe.wait_ge(hidden_ready.sem, hidden_ready.now(b, h - 1))
                        else:
                            pe.wait_ge(hidden_ready.sem, hidden_ready.prev(b, 2 * E - 1 + h))
                        for m in range(HB // 2):
                            for c in range(KC):
                                last = mm(half_banks(h)[:, m, :], up[:, c, e, (h % 2) * (HB // 2) + m, :],
                                          xt[:, c, :], start=c == 0, stop=c == KC - 1)
                        last.then_inc(up_done.sem, 1)

                    up_half(0)
                    pe.wait_ge(weight_ready.sem, weight_ready.now(b, 1))
                    for t in range(TB):
                        last = nc.tensor.transpose(PS[0:E, 6, t * P:(t + 1) * P], weight[:, t, :], core.ident[:])
                    last.then_inc(weight_turned.sem, 1)
                    up_half(1)
                    pe.wait_ge(weight_t_ready.sem, weight_t_ready.now(b, 1))
                    for t in range(TB):
                        last = mm(PS[:, 6, t * D:(t + 1) * D], weight_t[0:E, t * P:(t + 1) * P], down_bias[0:E, :],
                                  start=True, stop=True)
                    last.then_inc(bias_done.sem, 1)
                    for h in range(2 * E):
                        e = h // 2
                        pe.wait_ge(hidden_ready.sem, hidden_ready.now(b, h + 1))
                        if h % 2 == 0:
                            if e >= 2:
                                pe.wait_ge(added.sem, added.now(b, e - 1))
                            else:
                                pe.wait_ge(added.sem, added.prev(b, E - 1 + e))
                        for t in range(TB):
                            for m in range(HB // 2):
                                last = mm(PS[:, 4 + e % 2, t * D:(t + 1) * D], hidden[:, h % 2, m, t * P:(t + 1) * P],
                                          down[:, e, (h % 2) * (HB // 2) + m, :],
                                          start=h % 2 == 0 and m == 0 and t == 0,
                                          stop=h % 2 == 1 and m == HB // 2 - 1, skip_group_check=True)
                        last.then_inc(down_half.sem, 1)
                        if h + 2 < 2 * E:
                            up_half(h + 2)


def program(nc, dram, out):
    core = Core(nc, dram, out)
    constants(core)
    core.end_block()
    for layer in BLOCKS:
        for build in layer:
            build(core)
            core.end_block()


BLOCKS = [
    [block_self_attention], [block_cross_attention_0], [block_experts_0],
    [block_mixer_project, block_mixer_solve, block_mixer_scan, block_mixer_mix],
    [block_cross_attention_1], [block_experts_1],
]


def layouts(a):
    f = {}
    x = a["x"].reshape(B * SEQ, D)
    f["x"], f["x_t"] = x, x.T

    def chunks(w, n=P):
        return w.reshape(w.shape[0] // n, n, -1).transpose(1, 0, 2)

    hd = 1024
    wkv, bkv = a["L0_attn_Wkv"], a["L0_attn_bkv"]
    wqk = np.stack([a["L0_attn_Wq"].reshape(KC, P, 8, P), wkv[:, :hd].reshape(KC, P, 8, P)], axis=3)
    f["sa_wqk"] = wqk.transpose(1, 0, 2, 3, 4)
    f["sa_bqk"] = np.stack([a["L0_attn_bq"].reshape(8, P), bkv[:hd].reshape(8, P)], axis=1).transpose(2, 0, 1)
    f["sa_wv"] = chunks(wkv[:, hd:])
    f["sa_bv"] = bkv[hd:]
    f["sa_wo"] = chunks(a["L0_attn_Wo"])
    f["sa_bo"] = a["L0_attn_bo"]
    dim = 64
    inv_freq = 1.0 / np.float32(10000.0) ** (np.arange(0, dim, 2, dtype=np.float32) / np.float32(dim))
    angle = np.tile(inv_freq.astype(np.float32), 4)[:, None] * np.arange(SEQ, dtype=np.float32)[None]
    angle = angle.astype(np.float32)
    scale = np.array([dim ** -0.5, 1.0], np.float32)[None, :, None]
    sign = np.tile(np.repeat(np.array([1.0, -1.0], np.float32), 32), 2)[:, None, None]
    f["cos"] = np.cos(angle)[:, None, :] * scale
    f["sin"] = np.sin(angle)[:, None, :] * scale * sign

    def padded(w):
        w = w.reshape(-1, 4, 4, 16)
        return np.concatenate([w, np.zeros_like(w)], axis=3).reshape(-1, 4, P)

    f["ctx_t"] = chunks(a["ctx_1024"].reshape(-1, D).T)
    f["key_mask"] = a["mask_BxS2_if1"]
    for to, src, turn in (("ca", "L0_xattn", True), ("cb", "L1_xattn", False)):
        w = {n: a[f"{src}_W{n}"].T if turn else a[f"{src}_W{n}"] for n in "qkvo"}
        for n in "qk":
            f[f"{to}_w{n}"] = padded(w[n]).reshape(KC, P, 4, P).transpose(1, 0, 2, 3)
            f[f"{to}_b{n}"] = padded(a[f"{src}_b{n}"][None])[0].T
        for n in "vo":
            f[f"{to}_w{n}"] = chunks(w[n])
            f[f"{to}_b{n}"] = a[f"{src}_b{n}"]

    def pad(w, axis):
        widths = [(0, 0)] * w.ndim
        widths[axis] = (0, -w.shape[axis] % P)
        return np.pad(w, widths)

    f["ea_up"] = pad(a["L0_ffn_w_up"], 1).reshape(8, 3, P, KC, P).transpose(4, 3, 0, 1, 2)
    f["ea_down"] = pad(a["L0_ffn_w_down"], 2).reshape(8, D, 3, P).transpose(3, 0, 2, 1)
    f["ea_shared_up"] = pad(a["L0_ffn_shared_w_up"], 0).reshape(3, P, KC, P).transpose(3, 2, 0, 1)
    f["ea_shared_down"] = pad(a["L0_ffn_shared_w_down"], 1).reshape(D, 3, P).transpose(2, 1, 0)
    f["ea_gate"] = chunks(a["L0_ffn_gate_w"].T)
    f["ea_gate_bias"] = a["L0_ffn_expert_bias"]
    f["eb_up"] = a["L1_ffn_W1"].reshape(8, 8, P, KC, P).transpose(4, 3, 0, 1, 2)
    f["eb_up_bias"] = a["L1_ffn_b1"].reshape(8, 8, P).transpose(2, 0, 1)
    f["eb_down"] = a["L1_ffn_W2"].reshape(8, D, 8, P).transpose(3, 0, 2, 1)
    f["eb_down_bias"] = a["L1_ffn_b2"]
    f["eb_router"] = chunks(a["L1_ffn_Wr"].T)
    f["eb_router_bias"] = a["L1_ffn_br"]
    qkv = np.stack([a[f"L1_attn_W{n}"] for n in "qkv"], axis=1)
    f["mp_w"] = qkv.reshape(KC, P, 3, KC, P).transpose(1, 0, 2, 3, 4)
    f["mp_w_beta"] = chunks(a["L1_attn_Wb"])
    conv = np.stack([a[f"L1_attn_conv_{n}_w"] for n in "qkv"])
    f["mp_conv_w"] = conv.reshape(3, KC, P, CONV).transpose(2, 0, 1, 3)
    f["mp_local_w"], f["mp_mid_w"] = chunks(a["L1_attn_local_w"]), chunks(a["L1_attn_mid_w"])
    f["mm_w1"] = pad(pad(a["L1_attn_r_w1"], 0), 1).reshape(KC + 1, P, 5, P).transpose(1, 0, 2, 3)
    f["mm_b1"] = pad(a["L1_attn_r_b1"], 0).reshape(5, P).T
    f["mm_w2"] = chunks(pad(a["L1_attn_r_w2"], 0))
    f["mm_b2"] = a["L1_attn_r_b2"]
    f["mm_mix_w"], f["mm_onorm_w"] = a["L1_attn_mix_w"].reshape(-1), a["L1_attn_onorm_w"]
    f["mm_wo"] = chunks(a["L1_attn_Wo"])
    f["eb_gamma"], f["eb_beta"] = a["L1_ffn_gamma"], a["L1_ffn_beta"]
    return f


def kernel(**inputs):
    import concourse.bacc as bacc
    from concourse.bass_utils import run_bass_kernel_spmd

    f = layouts({k: np.asarray(v) for k, v in inputs.items()})
    nc = bacc.Bacc("TRN2", target_bir_lowering=False, num_devices=1)
    arrays, dram = {}, {}
    for name, v in f.items():
        v = np.ascontiguousarray(v)
        arrays["in_" + name] = v
        dram[name] = nc.dram_tensor("in_" + name, v.shape, mybir.dt.from_np(v.dtype), kind="ExternalInput").ap()
    out = nc.dram_tensor("out", (B * SEQ, D), F32, kind="ExternalOutput").ap()
    program(nc, dram, out)
    r = run_bass_kernel_spmd(nc, [arrays], core_ids=[0])
    return r.results[0]["out"].reshape(B, SEQ, D)
```

```python
from contextlib import ExitStack

import numpy as np

import concourse.bass as bass
from concourse import mybir

F32 = mybir.dt.float32
BF16 = mybir.dt.bfloat16
I32 = mybir.dt.int32
ALU = mybir.AluOpType
ACT = mybir.ActivationFunctionType
AX = mybir.AxisListType

P = 128
B = 8
SEQ = 256
D = 256
KC = D // P
TB = SEQ // P
LN_EPS = 1e-5
NEG = -1e30


class Signal:

    def __init__(self, core, name, per, unit=1):
        self.sem = core.semaphore(name)
        self.per, self.unit = per, unit

    def start(self, eng):
        eng.sem_inc(self.sem, self.per * self.unit)

    def now(self, i, k):
        return (i + 1) * (self.per * self.unit) + k * self.unit

    def prev(self, i, k):
        return i * (self.per * self.unit) + k * self.unit


def spread(ap, n):
    return ap.unsqueeze(len(ap.shape)).to_broadcast(list(ap.shape) + [n])


class Core:

    def __init__(self, nc, dram, out):
        self.nc, self.dram, self.out = nc, dram, out
        self.block_semaphores = []
        self.PS = nc.alloc_psum_tensor("PS", [P, 8, 512], F32)
        self.ident = nc.alloc_sbuf_tensor("ident", [P, P], F32)
        self.ident16 = nc.alloc_sbuf_tensor("ident16", [P, P], BF16)
        self.minus_half = nc.alloc_sbuf_tensor("minus_half", [P, 16], F32)
        self.eps = nc.alloc_sbuf_tensor("eps", [P, 16], F32)
        self.X = nc.alloc_sbuf_tensor("X", [P, B * TB, D], F32)
        self.XT = nc.alloc_sbuf_tensor("XT", [P, KC, B * SEQ], F32)

        self.norm_signals = {
            name: Signal(self, name, per, unit) for name, per, unit in (
                ("residual_in", 1, 16), ("residual_used", 1, 1), ("var_ready", 1, 1), ("rstd_step", 2, 1),
                ("x_ready", 1, 1), ("transposed", 1, 1), ("xt_ready", 1, 1), ("stored", 2, 16), ("left", 1, 1))}
        self.block_semaphores = []

    def semaphore(self, name):
        self.block_semaphores.append(self.nc.alloc_semaphore(name))
        return self.block_semaphores[-1]

    def end_block(self):
        self.nc.clear_and_free_semaphores(self.block_semaphores)
        self.nc.all_engine_barrier()
        self.block_semaphores = []

    def x_of(self, b):
        return self.X[:, bass.ds(b * TB, TB), :]

    def xt_of(self, b):
        return self.XT[:, :, bass.ds(b * SEQ, SEQ)]


def constants(core):
    nc = core.nc
    zeroed = core.semaphore("identities_zeroed")
    with nc.Block() as block:
        @block.gpsimd
        def _(pool):
            nc.gpsimd.memset(core.minus_half[:], -0.5)
            nc.gpsimd.memset(core.eps[:], LN_EPS)
            nc.gpsimd.memset(core.ident[:], 0.0).then_inc(zeroed, 1)
            nc.gpsimd.memset(core.ident16[:], 0.0).then_inc(zeroed, 1)
            pool.wait_ge(zeroed, 2)
            for eye in (core.ident, core.ident16):
                nc.gpsimd.affine_select(out=eye[:], in_=eye[:], compare_op=ALU.not_equal, fill=1.0,
                                        base=0, pattern=[[-1, P]], channel_multiplier=1)


class Norm:

    def __init__(self, core, ctx, name, layer, bank, bias=None):
        nc = core.nc
        self.core, self.bank, self.bias = core, bank, bias

        def sb(n, shape, dt=F32):
            return ctx.enter_context(nc.sbuf_tensor(f"{name}_norm_{n}", shape, dt))

        self.x_in = sb("x_in", [P, TB, D])
        self.y = sb("y", [P, TB, D])
        self.x_new = sb("x_new", [P, TB, D])
        self.xt_new = sb("xt_new", [P, KC, SEQ])
        self.stats = sb("stats", [P, TB, 6])
        self.mean_var = sb("mean_var", [P, TB, 2])
        self.rstd = sb("rstd", [P, TB])
        self.layer = layer
        s = core.norm_signals
        self.residual_in, self.residual_used, self.var_ready = s["residual_in"], s["residual_used"], s["var_ready"]
        self.rstd_step, self.x_ready, self.transposed = s["rstd_step"], s["x_ready"], s["transposed"]
        self.xt_ready, self.stored, self.left = s["xt_ready"], s["stored"], s["left"]

    def turn(self, b):
        return b + self.layer * B

    def start(self, eng, *signals):
        if self.layer == 0:
            for s in signals:
                s.start(eng)

    def start_sync(self, sp):
        self.start(sp, self.residual_in, self.stored, self.left)

    def load(self, sp, b):
        sp.wait_ge(self.residual_used.sem, self.residual_used.prev(self.turn(b), 1))
        sp.dma_start(self.x_in[:], self.core.x_of(b)).then_inc(self.residual_in.sem, 16)

    def store(self, sp, b, last=False):
        sp.wait_ge(self.x_ready.sem, self.x_ready.now(self.turn(b), 1))
        if last:
            for t in range(TB):
                sp.dma_start(self.core.out[bass.ds(b * SEQ + t * P, P), :],
                             self.x_new[:, t, :]).then_inc(self.stored.sem, 16)
        else:
            sp.dma_start(self.core.x_of(b), self.x_new[:]).then_inc(self.stored.sem, 16)
            sp.wait_ge(self.xt_ready.sem, self.xt_ready.now(self.turn(b), 1))
            sp.dma_start(self.core.xt_of(b), self.xt_new[:]).then_inc(self.stored.sem, 16)
        sp.wait_ge(self.stored.sem, self.stored.now(self.turn(b), 2))
        sp.sem_inc(self.left.sem, 1)

    def start_vector(self, dve):
        self.start(dve, self.residual_used, self.var_ready, self.x_ready)

    def vector(self, dve, b, out_ready, source=None, between=None):
        nc = self.core.nc
        if source is None:
            source = self.core.PS[:, self.bank, :].rearrange("p (t d) -> p t d", t=TB)
        dve.wait_ge(self.residual_in.sem, self.residual_in.now(self.turn(b), 1))
        dve.wait_ge(*out_ready)
        nc.vector.tensor_tensor(self.y[:], source, self.x_in[:], ALU.add).then_inc(self.residual_used.sem, 1)
        dve.drain()
        if self.bias is not None:
            nc.vector.tensor_tensor(self.y[:], self.y[:], self.bias[:, :].unsqueeze(1).to_broadcast([P, TB, D]),
                                    ALU.add)
            dve.drain()
        for t in range(TB):
            nc.vector.bn_stats(self.stats[:, t, :], self.y[:, t, :])
        dve.drain()
        for t in range(TB):
            nc.vector.bn_aggr(self.mean_var[:, t, :], self.stats[:, t, :])
        dve.drain()
        dve.sem_inc(self.var_ready.sem, 1)
        if between is not None:
            between()
        dve.wait_ge(self.rstd_step.sem, self.rstd_step.now(self.turn(b), 2))
        dve.wait_ge(self.left.sem, self.left.prev(self.turn(b), 1))
        for t in range(TB):
            nc.vector.tensor_scalar(self.x_new[:, t, :], self.y[:, t, :], self.mean_var[:, t, 0:1],
                                    self.rstd[:, t:t + 1], ALU.subtract, ALU.mult)
        dve.drain()
        dve.sem_inc(self.x_ready.sem, 1)

    def start_gpsimd(self, pool):
        self.start(pool, self.rstd_step)

    def gpsimd(self, pool, b):
        nc = self.core.nc
        pool.wait_ge(self.var_ready.sem, self.var_ready.now(self.turn(b), 1))
        nc.gpsimd.tensor_tensor(self.rstd[:], self.mean_var[:, :, 1], self.core.eps[:, 0:TB],
                                ALU.add).then_inc(self.rstd_step.sem, 1)
        pool.wait_ge(self.rstd_step.sem, self.rstd_step.now(self.turn(b), 1))
        nc.gpsimd.tensor_tensor(self.rstd[:], self.rstd[:], self.core.minus_half[:, 0:TB],
                                ALU.pow).then_inc(self.rstd_step.sem, 1)
        pool.drain()

    def start_tensor(self, pe):
        self.start(pe, self.transposed)

    def tensor(self, pe, b):
        nc = self.core.nc
        pe.wait_ge(self.x_ready.sem, self.x_ready.now(self.turn(b), 1))
        for c in range(KC):
            for t in range(TB):
                last = nc.tensor.transpose(self.core.PS[:, self.bank, (c * TB + t) * P:(c * TB + t + 1) * P],
                                           self.x_new[:, t, c * P:(c + 1) * P], self.core.ident[:])
        last.then_inc(self.transposed.sem, 1)

    def start_scalar(self, act):
        self.start(act, self.xt_ready)

    def scalar(self, act, b):
        nc = self.core.nc
        act.wait_ge(self.transposed.sem, self.transposed.now(self.turn(b), 1))
        act.wait_ge(self.left.sem, self.left.prev(self.turn(b), 1))
        nc.scalar.activation(self.xt_new[:].rearrange("p c n -> p (c n)"), self.core.PS[:, self.bank, :],
                             ACT.Copy).then_inc(self.xt_ready.sem, 1)


def block_self_attention(core):
    H, DH = 16, 64
    NP, HD = H // 2, H * DH
    WIDE = DH + 1
    PARTS = 3
    DEEP = 4
    AHEAD = 3
    nc, PS, dram = core.nc, core.PS, core.dram
    with ExitStack() as ctx:
        def sb(n, shape, dt=F32):
            return ctx.enter_context(nc.sbuf_tensor(f"sa_{n}", shape, dt))

        wqk = sb("wqk", [P, KC, NP, 2, P])
        wv = sb("wv", [P, KC, HD])
        wo = sb("wo", [P, NP, D])
        bqk = sb("bqk", [P, NP, 2])
        bv = sb("bv", [P, HD])
        bo = sb("bo", [P, D])
        cos = sb("cos", [P, 2, SEQ])
        sin = sb("sin", [P, 2, SEQ])
        mask_qk = sb("mask_qk", [P, P], BF16)
        mask_kq = sb("mask_kq", [P, P], BF16)
        sel32 = sb("sel32", [P, PARTS, 2, P])
        sel = sb("sel", [P, 2, P], BF16)
        xt = sb("xt", [P, KC, SEQ])
        v = sb("v", [P, TB, H, WIDE])
        raw = sb("raw", [P, DEEP, 2, SEQ])
        swapped = sb("swapped", [P, DEEP, 2, SEQ])
        rot1 = sb("rot1", [P, 2, SEQ])
        q = sb("q", [P, DEEP, SEQ])
        k = sb("k", [P, DEEP, 2, SEQ])
        neg_max = sb("neg_max", [P, TB, 2])
        rest = sb("rest", [P, 2, TB, 2])
        max_parts = sb("max_parts", [P, TB, PARTS, 2], BF16)
        max_t = sb("max_t", [P, SEQ], BF16)
        probs = sb("probs", [P, 2, 2, 384])
        rden = sb("rden", [P, TB, 2])
        o = sb("o", [P, TB, 2, DH])
        ot = sb("ot", [P, NP, SEQ])
        norm = Norm(core, ctx, "sa", 0, 4, bias=bo)

        v_weights_in = core.semaphore("sa_v_weights_in")
        qk_weights_in = core.semaphore("sa_qk_weights_in")
        out_weights_in = core.semaphore("sa_out_weights_in")
        activations_in = core.semaphore("sa_activations_in")
        consts = core.semaphore("sa_constants_ready")
        sel_ready = core.semaphore("sa_selector_ready")
        xt_in = Signal(core, "sa_xt_in", 1, 16)
        v_done = Signal(core, "sa_v_projected", 1)
        v_ready = Signal(core, "sa_v_ready", 1)
        qk_done = Signal(core, "sa_qk_projected", NP)
        raw_ready = Signal(core, "sa_raw_ready", NP)
        swap_ready = Signal(core, "sa_swapped_ready", NP)
        raw_used = Signal(core, "sa_raw_used", NP)
        qk_ready = Signal(core, "sa_qk_rotated", NP)
        s_done = Signal(core, "sa_scores_for_max", NP)
        max_ready = Signal(core, "sa_max_ready", NP)
        maxt_done = Signal(core, "sa_max_transposed", NP)
        maxt_ready = Signal(core, "sa_max_row_ready", NP)
        st_done = Signal(core, "sa_scores_ready", NP)
        probs_ready = Signal(core, "sa_probs_ready", NP)
        o_done = Signal(core, "sa_o_done", NP)
        o_ready = Signal(core, "sa_o_ready", NP)
        ot_done = Signal(core, "sa_o_transposed", NP)
        ot_ready = Signal(core, "sa_ot_ready", NP)
        out_done = Signal(core, "sa_out_done", 1)

        def ago(signal, b, p, n):
            return signal.now(b, p + 1 - n) if p >= n else signal.prev(b, NP + p + 1 - n)

        def turned_max():
            return PS[:, 5, :].bitcast(BF16)

        with nc.Block() as block:
            @block.sync
            def _(sp):
                xt_in.start(sp)
                x_t = dram["x_t"].rearrange("(c p) n -> p c n", p=P)
                sp.dma_start(xt[:], x_t[:, :, 0:SEQ]).then_inc(xt_in.sem, 16)
                sp.dma_start(wv[:], dram["sa_wv"]).then_inc(v_weights_in, 16)
                sp.dma_start(bv[:], dram["sa_bv"].partition_broadcast(P)).then_inc(v_weights_in, 16)
                for dst, name in ((bqk, "sa_bqk"), (cos, "cos"), (sin, "sin"), (wqk, "sa_wqk")):
                    sp.dma_start(dst[:], dram[name]).then_inc(qk_weights_in, 16)
                sp.dma_start(wo[:], dram["sa_wo"]).then_inc(out_weights_in, 16)
                sp.dma_start(bo[:], dram["sa_bo"].partition_broadcast(P)).then_inc(out_weights_in, 16)
                sp.dma_start(core.XT[:], x_t).then_inc(activations_in, 16)
                sp.dma_start(core.X[:], dram["x"].rearrange("(n p) d -> p n d", p=P)).then_inc(activations_in, 16)
                sp.wait_ge(activations_in, 32)
                norm.start_sync(sp)

                def load(b):
                    sp.wait_ge(v_done.sem, v_done.prev(b, 1))
                    sp.wait_ge(qk_done.sem, qk_done.prev(b, NP))
                    sp.dma_start(xt[:], core.xt_of(b)).then_inc(xt_in.sem, 16)

                def rest_of(b, following):
                    norm.load(sp, b)
                    if following:
                        load(b + 1)
                    norm.store(sp, b)

                with sp.Fori(0, B - 1) as b:
                    rest_of(b, True)
                rest_of(B - 1, False)

            @block.gpsimd
            def _(pool):
                nc.gpsimd.memset(mask_qk[:], 0.0).then_inc(consts, 1)
                nc.gpsimd.memset(mask_kq[:], 0.0).then_inc(consts, 1)
                nc.gpsimd.memset(sel32[:], 0.0).then_inc(consts, 1)
                nc.gpsimd.memset(max_t[:], 0.0).then_inc(consts, 1)
                nc.gpsimd.memset(k[:], 0.0).then_inc(consts, 1)
                nc.gpsimd.memset(v[:, :, :, DH:WIDE], 1.0).then_inc(consts, 1)
                pool.wait_ge(consts, 6)
                nc.gpsimd.affine_select(out=mask_qk[:], in_=mask_qk[:], compare_op=ALU.is_ge, fill=NEG,
                                        base=0, pattern=[[-1, P]], channel_multiplier=1).then_inc(consts, 1)
                nc.gpsimd.affine_select(out=mask_kq[:], in_=mask_kq[:], compare_op=ALU.is_ge, fill=NEG,
                                        base=0, pattern=[[1, P]], channel_multiplier=-1).then_inc(consts, 1)
                nc.gpsimd.affine_select(out=sel32[:], in_=sel32[:], compare_op=ALU.not_equal, fill=1.0, base=0,
                                        pattern=[[-2, PARTS], [-1, 2], [0, P]], channel_multiplier=1)\
                    .then_inc(consts, 1)
                pool.wait_ge(qk_weights_in, 64)
                swap_ready.start(pool)
                norm.start_gpsimd(pool)

                def turn_halves(b, p):
                    pool.wait_ge(raw_ready.sem, raw_ready.now(b, p + 1))
                    pool.wait_ge(raw_used.sem, ago(raw_used, b, p, DEEP))
                    for to in range(4):
                        source = to ^ 1
                        nc.gpsimd.tensor_tensor(swapped[32 * to:32 * to + 32, p % DEEP, :, :],
                                                raw[32 * source:32 * source + 32, p % DEEP, :, :],
                                                sin[32 * source:32 * source + 32, :, :], ALU.mult)
                    pool.drain()
                    pool.sem_inc(swap_ready.sem, 1)

                def rest_of(b, following):
                    for p in range(1, NP):
                        turn_halves(b, p)
                    if following:
                        turn_halves(b + 1, 0)
                    norm.gpsimd(pool, b)

                turn_halves(0, 0)
                with pool.Fori(0, B - 1) as b:
                    rest_of(b, True)
                rest_of(B - 1, False)

            @block.scalar
            def _(act):
                act.wait_ge(qk_weights_in, 64)
                act.wait_ge(consts, 9)
                for s in (raw_ready, maxt_ready, probs_ready, ot_ready):
                    s.start(act)
                norm.start_scalar(act)

                def evacuate_qk(b, p):
                    act.wait_ge(qk_done.sem, qk_done.now(b, p + 1))
                    act.wait_ge(raw_used.sem, ago(raw_used, b, p, DEEP))
                    for n in range(2):
                        nc.scalar.activation(raw[:, p % DEEP, n, :], PS[:, 6 + p % 2, n * SEQ:(n + 1) * SEQ],
                                             ACT.Identity, bias=bqk[:, p, n:n + 1])
                    act.drain()
                    act.sem_inc(raw_ready.sem, 1)

                def evacuate_ot(b, p):
                    act.wait_ge(ot_done.sem, ot_done.now(b, p + 1))
                    if p == 0:
                        act.wait_ge(out_done.sem, out_done.prev(b, 1))
                    nc.scalar.activation(ot[:, p, :], PS[:, 5, 0:SEQ], ACT.Identity).then_inc(ot_ready.sem, 1)

                def rest_of(b, following):
                    for p in range(NP):
                        if p >= 2:
                            evacuate_ot(b, p - 2)
                        if p + AHEAD < NP:
                            evacuate_qk(b, p + AHEAD)
                        act.wait_ge(maxt_done.sem, maxt_done.now(b, p + 1))
                        nc.scalar.activation(max_t[0:2 * PARTS, :], turned_max()[0:2 * PARTS, 0:SEQ], ACT.Identity)\
                            .then_inc(maxt_ready.sem, 1)
                        act.wait_ge(st_done.sem, st_done.now(b, p + 1))
                        act.wait_ge(o_done.sem, ago(o_done, b, p, 2))
                        nc.scalar.activation(probs[:, p % 2, :, :], PS[:, 2:4, 0:384], ACT.Exp)\
                            .then_inc(probs_ready.sem, 1)
                    evacuate_ot(b, NP - 2)
                    evacuate_ot(b, NP - 1)
                    if following:
                        for p in range(AHEAD):
                            evacuate_qk(b + 1, p)
                    norm.scalar(act, b)

                for p in range(AHEAD):
                    evacuate_qk(0, p)
                with act.Fori(0, B - 1) as b:
                    rest_of(b, True)
                rest_of(B - 1, False)

            @block.vector
            def _(dve):
                dve.wait_ge(v_weights_in, 32)
                dve.wait_ge(consts, 9)
                nc.vector.tensor_tensor(sel[:], sel32[:, 0, :, :], sel32[:, 1, :, :], ALU.add)
                dve.drain()
                nc.vector.tensor_tensor(sel[:], sel[:], sel32[:, 2, :, :], ALU.add).then_inc(sel_ready, 1)
                for s in (v_ready, raw_used, qk_ready, max_ready, o_ready):
                    s.start(dve)
                norm.start_vector(dve)

                def take_v(b):
                    dve.wait_ge(o_done.sem, o_done.prev(b, NP))
                    dve.wait_ge(v_done.sem, v_done.now(b, 1))
                    for t in range(TB):
                        for h8 in (0, 8):
                            nc.vector.tensor_tensor(v[:, t, h8:h8 + 8, 0:DH],
                                                    PS[:, 2 * t + h8 // 8, :].rearrange("p (h d) -> p h d", d=DH),
                                                    bv[:, h8 * DH:(h8 + 8) * DH].rearrange("p (h d) -> p h d", d=DH),
                                                    ALU.add)
                    dve.drain()
                    dve.sem_inc(v_ready.sem, 1)

                def rotate(b, p):
                    dve.wait_ge(raw_ready.sem, raw_ready.now(b, p + 1))
                    nc.vector.tensor_tensor(rot1[:], raw[:, p % DEEP, :, :], cos[:], ALU.mult)
                    dve.drain()
                    dve.wait_ge(swap_ready.sem, swap_ready.now(b, p + 1))
                    dve.wait_ge(st_done.sem, ago(st_done, b, p, DEEP))
                    nc.vector.tensor_tensor(q[:, p % DEEP, :], rot1[:, 0, :], swapped[:, p % DEEP, 0, :], ALU.add)
                    for h in range(2):
                        rows = slice(DH * h, DH * h + DH)
                        nc.vector.tensor_tensor(k[rows, p % DEEP, h, :], rot1[rows, 1, :],
                                                swapped[rows, p % DEEP, 1, :], ALU.add)
                    dve.drain()
                    dve.sem_inc(raw_used.sem, 1)
                    dve.sem_inc(qk_ready.sem, 1)

                def maxima(b, p):
                    dve.wait_ge(s_done.sem, s_done.now(b, p + 1))
                    dve.wait_ge(maxt_done.sem, ago(maxt_done, b, p, 1))
                    for t in range(TB):
                        nc.vector.tensor_reduce(neg_max[:, t, :], PS[:, t, 0:(t + 1) * SEQ]
                                                .rearrange("p (h n) -> p h n", h=2), AX.X, ALU.max, negate=True)
                    dve.drain()
                    nc.vector.tensor_copy(max_parts[:, :, 0, :], neg_max[:])
                    dve.drain()
                    nc.vector.tensor_tensor(rest[:, 0, :, :], neg_max[:], max_parts[:, :, 0, :], ALU.subtract)
                    dve.drain()
                    nc.vector.tensor_copy(max_parts[:, :, 1, :], rest[:, 0, :, :])
                    dve.drain()
                    nc.vector.tensor_tensor(max_parts[:, :, 2, :], rest[:, 0, :, :], max_parts[:, :, 1, :],
                                            ALU.subtract).then_inc(max_ready.sem, 1)

                def normalize(b, p):
                    dve.wait_ge(o_done.sem, o_done.now(b, p + 1))
                    wide = PS[:, 4, 0:4 * WIDE].rearrange("p (t h d) -> p t h d", t=TB, h=2)
                    nc.vector.reciprocal(rden[:], wide[:, :, :, DH])
                    dve.drain()
                    dve.wait_ge(ot_done.sem, ago(ot_done, b, p, 1))
                    nc.vector.tensor_tensor(o[:], wide[:, :, :, 0:DH], spread(rden[:], DH), ALU.mult)\
                        .then_inc(o_ready.sem, 1)

                def rest_of(b, following):
                    for p in range(NP):
                        if p + 2 < NP:
                            rotate(b, p + 2)
                        if p + 1 < NP:
                            maxima(b, p + 1)
                        if p:
                            normalize(b, p - 1)
                    normalize(b, NP - 1)
                    if following:
                        take_v(b + 1)
                        rotate(b + 1, 0)
                    dve.wait_ge(out_weights_in, 32)
                    norm.vector(dve, b, (out_done.sem, out_done.now(b, 1)))
                    if following:
                        maxima(b + 1, 0)
                        rotate(b + 1, 1)

                take_v(0)
                dve.wait_ge(qk_weights_in, 64)
                rotate(0, 0)
                rotate(0, 1)
                maxima(0, 0)
                with dve.Fori(0, B - 1) as b:
                    rest_of(b, True)
                rest_of(B - 1, False)

            @block.tensor
            def _(pe):
                pe.wait_ge(v_weights_in, 32)
                pe.wait_ge(consts, 9)
                pe.wait_ge(sel_ready, 1)
                for s in (v_done, qk_done, s_done, maxt_done, st_done, o_done, ot_done, out_done):
                    s.start(pe)
                norm.start_tensor(pe)
                mm = nc.tensor.matmul

                def project_v(b):
                    pe.wait_ge(xt_in.sem, xt_in.now(b, 1))
                    pe.wait_ge(max_ready.sem, max_ready.prev(b, NP))
                    pe.wait_ge(probs_ready.sem, probs_ready.prev(b, NP))
                    for t in range(TB):
                        for half in range(2):
                            for c in range(KC):
                                last = mm(PS[:, 2 * t + half, :], xt[:, c, t * P:(t + 1) * P],
                                          wv[:, c, half * 512:(half + 1) * 512], start=c == 0, stop=c == KC - 1)
                    last.then_inc(v_done.sem, 1)

                def project(b, p):
                    pe.wait_ge(raw_ready.sem, ago(raw_ready, b, p, 2))
                    for n in range(2):
                        for c in range(KC):
                            last = mm(PS[:, 6 + p % 2, n * SEQ:(n + 1) * SEQ], wqk[:, c, p, n, :],
                                      xt[:, c, :], start=c == 0, stop=c == KC - 1)
                    last.then_inc(qk_done.sem, 1)

                def scores_for_max(b, p):
                    pe.wait_ge(qk_ready.sem, qk_ready.now(b, p + 1))
                    if p == 0:
                        pe.wait_ge(v_ready.sem, v_ready.now(b, 1))
                    else:
                        pe.wait_ge(max_ready.sem, max_ready.now(b, p))
                    for t in range(TB):
                        keys = (t + 1) * P
                        mm(PS[:, t, 0:2 * keys], q[:, p % DEEP, t * P:(t + 1) * P], k[:, p % DEEP, :, 0:keys],
                           start=True, stop=False, skip_group_check=True)
                        diagonal = PS[:, t, 0:2 * keys].rearrange("p (h n) -> p h n", h=2)[:, :, t * P:keys]
                        last = mm(diagonal, core.ident16[:], mask_qk[:, :].unsqueeze(1).to_broadcast([P, 2, P]),
                                  start=False, stop=True, skip_group_check=True)
                    last.then_inc(s_done.sem, 1)

                def turn_max(b, p):
                    pe.wait_ge(max_ready.sem, max_ready.now(b, p + 1))
                    pe.wait_ge(ot_ready.sem, ot_ready.now(b, p - 1) if p >= 2 else ot_ready.prev(b, NP))
                    for t in range(TB):
                        last = nc.tensor.transpose(turned_max()[0:2 * PARTS, t * P:(t + 1) * P],
                                                   max_parts[:, t, :, :].rearrange("p a h -> p (a h)"),
                                                   core.ident16[:])
                    last.then_inc(maxt_done.sem, 1)

                def scores(b, p):
                    if p == 0:
                        pe.wait_ge(v_ready.sem, v_ready.now(b, 1))
                    else:
                        pe.wait_ge(probs_ready.sem, probs_ready.now(b, p))
                    for h in range(2):
                        mm(PS[:, 2 + h, 0:SEQ], k[:, p % DEEP, h, 0:P], q[:, p % DEEP, :], start=True, stop=False,
                           skip_group_check=True)
                        mm(PS[:, 2 + h, SEQ:384], k[:, p % DEEP, h, P:SEQ], q[:, p % DEEP, P:SEQ], start=False,
                           stop=False, skip_group_check=True)
                        mm(PS[:, 2 + h, 0:512].rearrange("p (a n) -> p a n", a=2)[:, :, 0:P], core.ident16[:],
                           mask_kq[:, :].unsqueeze(1).to_broadcast([P, 2, P]), start=False, stop=False,
                           skip_group_check=True)
                    pe.wait_ge(maxt_ready.sem, maxt_ready.now(b, p + 1))
                    for h in range(2):
                        mm(PS[:, 2 + h, 0:SEQ], sel[:, h, :], max_t[:, :], start=False, stop=True,
                           skip_group_check=True)
                        last = mm(PS[:, 2 + h, SEQ:384], sel[:, h, :], max_t[:, P:SEQ], start=False, stop=True,
                                  skip_group_check=True)
                    last.then_inc(st_done.sem, 1)

                def outputs(b, p):
                    pe.wait_ge(probs_ready.sem, probs_ready.now(b, p + 1))
                    pe.wait_ge(o_ready.sem, ago(o_ready, b, p, 1))
                    if p == 0:
                        pe.wait_ge(norm.xt_ready.sem, norm.xt_ready.prev(norm.turn(b), 1))
                    for t in range(TB):
                        parts = [(0, 0)] if t == 0 else [(P, 0), (SEQ, 1)]
                        for h in range(2):
                            at = (t * 2 + h) * WIDE
                            for m, (col, kt) in enumerate(parts):
                                last = mm(PS[:, 4, at:at + WIDE], probs[:, p % 2, h, col:col + P],
                                          v[:, kt, 2 * p + h, :], start=m == 0, stop=m == len(parts) - 1)
                    last.then_inc(o_done.sem, 1)

                def turn_outputs(b, p):
                    pe.wait_ge(o_ready.sem, o_ready.now(b, p + 1))
                    pe.wait_ge(maxt_ready.sem, maxt_ready.now(b, min(p + 2, NP)))
                    pe.wait_ge(ot_ready.sem, ago(ot_ready, b, p, 1))
                    for t in range(TB):
                        last = nc.tensor.transpose(PS[:, 5, t * P:(t + 1) * P],
                                                   o[:, t, :, :].rearrange("p h d -> p (h d)"), core.ident[:])
                    last.then_inc(ot_done.sem, 1)

                def project_output(b):
                    pe.wait_ge(out_weights_in, 32)
                    pe.wait_ge(ot_ready.sem, ot_ready.now(b, NP))
                    for t in range(TB):
                        for c in range(NP):
                            last = mm(PS[:, 4, t * D:(t + 1) * D], ot[:, c, t * P:(t + 1) * P], wo[:, c, :],
                                      start=c == 0, stop=c == NP - 1)
                    last.then_inc(out_done.sem, 1)

                def rest_of(b, following):
                    for p in range(NP):
                        if p + 1 < NP:
                            scores_for_max(b, p + 1)
                        if p >= 2:
                            turn_outputs(b, p - 2)
                        if p + AHEAD < NP:
                            project(b, p + AHEAD)
                        turn_max(b, p)
                        scores(b, p)
                        if p:
                            outputs(b, p - 1)
                    outputs(b, NP - 1)
                    turn_outputs(b, NP - 2)
                    if following:
                        project_v(b + 1)
                    turn_outputs(b, NP - 1)
                    if following:
                        project(b + 1, 0)
                    project_output(b)
                    if following:
                        for p in range(1, AHEAD):
                            project(b + 1, p)
                        scores_for_max(b + 1, 0)
                    norm.tensor(pe, b)

                project_v(0)
                pe.wait_ge(qk_weights_in, 64)
                for p in range(AHEAD):
                    project(0, p)
                scores_for_max(0, 0)
                with pe.Fori(0, B - 1) as b:
                    rest_of(b, True)
                rest_of(B - 1, False)


def cross_attention(core, name, half, dram_name):
    H, DH, CTX, PARTS = 16, 16, 77, 3
    HC = H // KC
    UNITS, HU = 4, 4
    WIDE = 32
    nc, PS, dram = core.nc, core.PS, core.dram
    PD = BF16 if half else F32
    with ExitStack() as ctx:
        def sb(n, shape, dt=F32):
            return ctx.enter_context(nc.sbuf_tensor(f"{name}_{n}", shape, dt))

        def sig(n, per, unit=1):
            return Signal(core, f"{name}_{n}", per, unit)

        w32 = {n: sb(n, [P, KC, D]) for n in ("wq", "wk", "wv", "wo")}
        w = {n: sb(n + "16", [P, KC, D], BF16) for n in w32} if half else w32
        bias_shapes = {"bq": [P, KC], "bk": [P, KC], "bv": [P, D], "bo": [P, D]}
        b32 = {n: sb(n, s) for n, s in bias_shapes.items()}
        b16 = {n: sb(n + "16", s, BF16) for n, s in bias_shapes.items()} if half else None
        head_of_row = sb("head_of_row", [P, HC])
        sel_parts = sb("sel_parts", [P, PARTS, H])
        sel = sb("sel", [P, H, CTX], BF16)
        xt_in_tile = sb("xt", [P, KC, SEQ])
        ct_in_tile = sb("ct", [P, KC, CTX])
        xt = sb("xt16", [P, KC, SEQ], BF16) if half else xt_in_tile
        ct = sb("ct16", [P, KC, CTX], BF16) if half else ct_in_tile
        q = sb("q", [P, KC, SEQ], PD)
        k = sb("k", [P, H, CTX], PD)
        v = sb("v", [P, H, WIDE])
        neg_max = sb("neg_max", [P, TB, H])
        rest = sb("rest", [P, TB, H])
        max_parts = sb("max_parts", [P, TB, P // H, H], BF16)
        max_t = sb("max_t", [P, SEQ], BF16)
        probs = sb("probs", [P, H, SEQ])
        raw = sb("raw", [P, UNITS, SEQ])
        rden = sb("rden", [P, TB, H])
        o = sb("o", [P, TB, D])
        ot = sb("ot", [P, KC, SEQ], PD)
        if half:
            q_round = sb("q_round", [P, KC, SEQ], BF16)
            k_round = sb("k_round", [P, KC, CTX], BF16)
            v_round = sb("v_round", [P, D], BF16)
            v16 = sb("v16", [P, D], BF16)
            out_round = sb("out_round", [P, TB, D], BF16)
            out16 = sb("out16", [P, TB, D], BF16)
            causal_qk = sb("causal_qk", [P, CTX])
            causal_kq = sb("causal_kq", [P, SEQ])
            keys_row = sb("keys_row", [P, CTX], I32)
            keys_col = sb("keys_col", [P, 1], I32)
            keymask_row = sb("keymask_row", [P, CTX])
            keymask_col = sb("keymask_col", [P, 1])
            mask_qk = sb("mask_qk", [P, TB, CTX], BF16)
            mask_kq = sb("mask_kq", [P, SEQ], BF16)
        norm = Norm(core, ctx, name, 4 if half else 1, 5, bias=None if half else b32["bo"])

        weights_in = core.semaphore(f"{name}_weights_in")
        n_weights = len(w32) + len(b32)
        consts = core.semaphore(f"{name}_constants_ready")
        n_filled = 9 if half else 5
        n_consts = n_filled + (5 if half else 3)
        sel_ready = core.semaphore(f"{name}_selector_ready")
        inputs_in = sig("inputs_in", 4 if half else 2, 16)
        qkv_done = sig("qkv_projected", 1)
        qk_ready = sig("qk_ready", 1)
        v_ready = sig("v_ready", 1)
        s_done = sig("scores_for_max", UNITS)
        s_used = sig("scores_for_max_used", UNITS)
        max_ready = sig("max_ready", 1)
        maxt_done = sig("max_transposed", 1)
        maxt_ready = sig("max_rows_ready", 1)
        st_done = sig("scores_ready", UNITS)
        probs_ready = sig("probs_ready", UNITS)
        raw_done = sig("raw_outputs_done", 1)
        raw_ready = sig("raw_outputs_ready", 1)
        o_done = sig("o_done", 1)
        o_ready = sig("o_ready", 1)
        ot_done = sig("o_transposed", 1)
        ot_ready = sig("ot_ready", 1)
        out_done = sig("out_done", 1)
        if half:
            cast = sig("inputs_cast", 1)
            rounded = sig("projections_rounded", 1)
            out_rounded = sig("out_rounded", 1)

        def q_bank():
            return PS[:, 6, :].rearrange("p (c n) -> p c n", n=SEQ)

        def k_bank():
            return PS[:, 7, D:D + KC * CTX].rearrange("p (c n) -> p c n", n=CTX)

        def v_bank():
            return PS[0:CTX, 7, 0:D]

        def turned_max():
            return PS[:, 6, :].bitcast(BF16)

        def heads(ap):
            return ap.rearrange("p (h d) -> p h d", d=DH)

        with nc.Block() as block:
            @block.sync
            def _(sp):
                for n in ("wq", "wk", "wv", "wo", "bq", "bk"):
                    sp.dma_start({**w32, **b32}[n][:], dram[f"{dram_name}_{n}"]).then_inc(weights_in, 16)
                for n in ("bv", "bo"):
                    sp.dma_start(b32[n][:], dram[f"{dram_name}_{n}"].partition_broadcast(P)).then_inc(weights_in, 16)
                inputs_in.start(sp)
                norm.start_sync(sp)

                def load(b):
                    if half:
                        sp.wait_ge(qk_ready.sem, qk_ready.prev(b, 1))
                        sp.wait_ge(cast.sem, cast.prev(b, 1))
                        sp.dma_start(keys_row[:], dram["key_mask"][bass.ds(b, 1), :]
                                     .rearrange("a n -> (a n)").partition_broadcast(P)).then_inc(inputs_in.sem, 16)
                        sp.dma_start(keys_col[0:CTX, :], dram["key_mask"][bass.ds(b, 1), :]
                                     .rearrange("a n -> n a")).then_inc(inputs_in.sem, 16)
                    else:
                        sp.wait_ge(qkv_done.sem, qkv_done.prev(b, 1))
                    sp.dma_start(xt_in_tile[:], core.xt_of(b)).then_inc(inputs_in.sem, 16)
                    sp.dma_start(ct_in_tile[:], dram["ctx_t"][:, :, bass.ds(b * CTX, CTX)]).then_inc(inputs_in.sem, 16)

                load(0)
                load(1)
                with sp.Fori(0, B - 2) as b:
                    norm.load(sp, b)
                    load(b + 2)
                    norm.store(sp, b)
                for b in range(B - 2, B):
                    norm.load(sp, b)
                    norm.store(sp, b)

            @block.gpsimd
            def _(pool):
                nc.gpsimd.memset(sel_parts[:], 0.0).then_inc(consts, 1)
                nc.gpsimd.memset(max_parts[:], 0.0).then_inc(consts, 1)
                nc.gpsimd.memset(v[:, :, DH:DH + 1], 1.0).then_inc(consts, 1)
                nc.gpsimd.memset(v[:, :, DH + 1:WIDE], 0.0).then_inc(consts, 1)
                nc.gpsimd.memset(head_of_row[:], 1.0).then_inc(consts, 1)
                if half:
                    nc.gpsimd.memset(causal_qk[:], 0.0).then_inc(consts, 1)
                    nc.gpsimd.memset(causal_kq[:], 0.0).then_inc(consts, 1)
                    nc.gpsimd.memset(keymask_col[:], 0.0).then_inc(consts, 1)
                    nc.gpsimd.memset(keys_col[:], 1).then_inc(consts, 1)
                pool.wait_ge(consts, n_filled)
                nc.gpsimd.affine_select(out=sel_parts[:], in_=sel_parts[:], compare_op=ALU.not_equal, fill=1.0,
                                        base=0, pattern=[[-H, PARTS], [-1, H]], channel_multiplier=1)\
                    .then_inc(consts, 1)
                nc.gpsimd.affine_select(out=head_of_row[:], in_=head_of_row[:], compare_op=ALU.is_ge, fill=0.0,
                                        base=0, pattern=[[-DH, HC]], channel_multiplier=1).then_inc(consts, 1)
                if half:
                    nc.gpsimd.affine_select(out=causal_qk[:], in_=causal_qk[:], compare_op=ALU.is_ge, fill=NEG,
                                            base=0, pattern=[[-1, CTX]], channel_multiplier=1).then_inc(consts, 1)
                    nc.gpsimd.affine_select(out=causal_kq[:], in_=causal_kq[:], compare_op=ALU.is_ge, fill=NEG,
                                            base=0, pattern=[[1, SEQ]], channel_multiplier=-1).then_inc(consts, 1)
                pool.wait_ge(consts, n_consts - 1)
                nc.gpsimd.affine_select(out=head_of_row[:], in_=head_of_row[:], compare_op=ALU.is_ge, fill=0.0,
                                        base=DH - 1, pattern=[[DH, HC]], channel_multiplier=-1).then_inc(consts, 1)
                norm.start_gpsimd(pool)
                with pool.Fori(0, B) as b:
                    norm.gpsimd(pool, b)

            @block.scalar
            def _(act):
                act.wait_ge(weights_in, 16 * n_weights)
                act.wait_ge(consts, n_consts)
                for s in (maxt_ready, probs_ready, raw_ready, ot_ready) + ((rounded, out_rounded) if half else ()):
                    s.start(act)
                norm.start_scalar(act)

                def round_projections(b):
                    act.wait_ge(qkv_done.sem, qkv_done.now(b, 1))
                    act.wait_ge(v_ready.sem, v_ready.prev(b, 1))
                    nc.scalar.activation(q_round[:], q_bank(), ACT.Copy)
                    nc.scalar.activation(k_round[:], k_bank(), ACT.Copy)
                    nc.scalar.activation(v_round[0:CTX, :], v_bank(), ACT.Copy)
                    act.drain()
                    act.sem_inc(rounded.sem, 1)

                def take_max_rows(b):
                    act.wait_ge(maxt_done.sem, maxt_done.now(b, 1))
                    nc.scalar.activation(max_t[:], turned_max()[:, 0:SEQ], ACT.Copy)\
                        .then_inc(maxt_ready.sem, 1)

                def exponentials(b, unit):
                    act.wait_ge(st_done.sem, st_done.now(b, unit + 1))
                    bank = 2 * (unit % 2)
                    nc.scalar.activation(probs[0:CTX, HU * unit:HU * (unit + 1), :],
                                         PS[0:CTX, bank:bank + 2, :].rearrange("p a (h n) -> p (a h) n", n=SEQ),
                                         ACT.Exp).then_inc(probs_ready.sem, 1)

                def rest_of(b, following):
                    exponentials(b, 2)
                    exponentials(b, 3)
                    if following and half:
                        round_projections(b + 1)
                    act.wait_ge(raw_done.sem, raw_done.now(b, 1))
                    nc.scalar.activation(raw[:], PS[:, 4:6, :].rearrange("p a (g n) -> p (a g) n", n=SEQ),
                                         ACT.Copy).then_inc(raw_ready.sem, 1)
                    act.wait_ge(ot_done.sem, ot_done.now(b, 1))
                    nc.scalar.activation(ot[:].rearrange("p c n -> p (c n)"), PS[:, 4, :],
                                         ACT.Copy).then_inc(ot_ready.sem, 1)
                    if half:
                        act.wait_ge(out_done.sem, out_done.now(b, 1))
                        nc.scalar.activation(out_round[:].rearrange("p t d -> p (t d)"), PS[:, 5, :],
                                             ACT.Copy).then_inc(out_rounded.sem, 1)
                    if following:
                        take_max_rows(b + 1)
                        exponentials(b + 1, 0)
                        exponentials(b + 1, 1)
                    norm.scalar(act, b)

                if half:
                    round_projections(0)
                take_max_rows(0)
                exponentials(0, 0)
                exponentials(0, 1)
                with act.Fori(0, B - 1) as b:
                    rest_of(b, True)
                rest_of(B - 1, False)

            @block.vector
            def _(dve):
                dve.wait_ge(weights_in, 16 * n_weights)
                dve.wait_ge(consts, n_consts)
                if half:
                    for n in w32:
                        nc.vector.tensor_copy(w[n][:], w32[n][:])
                    for n in b32:
                        nc.vector.tensor_copy(b16[n][:], b32[n][:])
                    dve.drain()
                    for n in b32:
                        nc.vector.tensor_copy(b32[n][:], b16[n][:])
                for part in range(1, PARTS):
                    nc.vector.tensor_tensor(sel_parts[:, 0, :], sel_parts[:, 0, :], sel_parts[:, part, :], ALU.add)
                    dve.drain()
                nc.vector.tensor_copy(sel[:], spread(sel_parts[:, 0, :], CTX)).then_inc(sel_ready, 1)
                for s in (qk_ready, v_ready, s_used, max_ready, o_ready) + ((cast,) if half else ()):
                    s.start(dve)
                norm.start_vector(dve)

                def cast_inputs(b):
                    dve.wait_ge(inputs_in.sem, inputs_in.now(b, inputs_in.per))
                    dve.wait_ge(qkv_done.sem, qkv_done.prev(b, 1))
                    nc.vector.tensor_copy(xt[:], xt_in_tile[:])
                    nc.vector.tensor_copy(ct[:], ct_in_tile[:])
                    nc.vector.tensor_scalar(keymask_row[:], keys_row[:], 0.0, NEG, ALU.is_le, ALU.mult)
                    nc.vector.tensor_scalar(keymask_col[0:CTX, :], keys_col[0:CTX, :], 0.0, NEG, ALU.is_le, ALU.mult)
                    dve.drain()
                    dve.sem_inc(cast.sem, 1)

                def take_qk(b):
                    if half:
                        dve.wait_ge(rounded.sem, rounded.now(b, 1))
                        nc.vector.tensor_tensor(mask_qk[:, 0, :], causal_qk[:], keymask_row[:], ALU.add)
                        nc.vector.tensor_copy(mask_qk[:, 1, :], keymask_row[:])
                        nc.vector.tensor_scalar(mask_kq[:], causal_kq[:], keymask_col[:, 0:1], None, ALU.add)
                        q_from, k_from = q_round[:], k_round[:]
                    else:
                        dve.wait_ge(qkv_done.sem, qkv_done.now(b, 1))
                        q_from, k_from = q_bank(), k_bank()
                    for c in range(KC):
                        nc.vector.tensor_scalar(q[:, c, :], q_from[:, c, :], b32["bq"][:, c:c + 1], DH ** -0.5,
                                                ALU.add, ALU.mult)
                        nc.vector.scalar_tensor_tensor(k[:, HC * c:HC * (c + 1), :],
                                                       k_from[:, c, :].unsqueeze(1).to_broadcast([P, HC, CTX]),
                                                       b32["bk"][:, c:c + 1], spread(head_of_row[:], CTX),
                                                       ALU.add, ALU.mult)
                    dve.drain()
                    dve.sem_inc(qk_ready.sem, 1)

                def take_v(b):
                    if half:
                        nc.vector.tensor_tensor(v16[0:CTX, :], v_round[0:CTX, :], b16["bv"][0:CTX, :], ALU.add)
                        dve.drain()
                        nc.vector.tensor_copy(v[0:CTX, :, 0:DH], heads(v16[0:CTX, :]))
                    else:
                        nc.vector.tensor_tensor(v[0:CTX, :, 0:DH], heads(v_bank()), heads(b32["bv"][0:CTX, :]), ALU.add)
                    dve.drain()
                    dve.sem_inc(v_ready.sem, 1)

                def maxima(b):
                    for unit in range(UNITS):
                        dve.wait_ge(s_done.sem, s_done.now(b, unit + 1))
                        t, c, bank = unit // KC, unit % KC, 2 * (unit % 2)
                        nc.vector.tensor_reduce(
                            neg_max[:, t, HC * c:HC * (c + 1)].rearrange("p (a h) -> p a h", a=2),
                            PS[:, bank:bank + 2, 0:HU * CTX].rearrange("p a (h n) -> p a h n", n=CTX),
                            AX.X, ALU.max, negate=True).then_inc(s_used.sem, 1)
                    dve.drain()
                    nc.vector.tensor_copy(max_parts[:, :, 0, :], neg_max[:])
                    dve.drain()
                    nc.vector.tensor_tensor(rest[:], neg_max[:], max_parts[:, :, 0, :], ALU.subtract)
                    dve.drain()
                    nc.vector.tensor_copy(max_parts[:, :, 1, :], rest[:])
                    dve.drain()
                    nc.vector.tensor_tensor(max_parts[:, :, 2, :], rest[:], max_parts[:, :, 1, :],
                                            ALU.subtract).then_inc(max_ready.sem, 1)

                def normalize(b):
                    dve.wait_ge(o_done.sem, o_done.now(b, 1))
                    both = PS[:, 4:6, :].rearrange("p t (h d) -> p t h d", d=WIDE)
                    nc.vector.reciprocal(rden[:], both[:, :, :, DH])
                    dve.drain()
                    for t in range(TB):
                        nc.vector.tensor_tensor(heads(o[:, t, :]), both[:, t, :, 0:DH], spread(rden[:, t, :], DH),
                                                ALU.mult)
                    dve.drain()
                    dve.sem_inc(o_ready.sem, 1)

                def rest_of(b, following):
                    if following:
                        if half:
                            cast_inputs(b + 1)
                        take_qk(b + 1)
                    normalize(b)
                    if following:
                        take_v(b + 1)
                        maxima(b + 1)
                    if half:
                        dve.wait_ge(out_rounded.sem, out_rounded.now(b, 1))
                        nc.vector.tensor_tensor(out16[:], out_round[:],
                                                b16["bo"][:, :].unsqueeze(1).to_broadcast([P, TB, D]), ALU.add)
                        dve.drain()
                        norm.vector(dve, b, (out_rounded.sem, out_rounded.now(b, 1)), source=out16[:])
                    else:
                        norm.vector(dve, b, (out_done.sem, out_done.now(b, 1)))

                if half:
                    cast_inputs(0)
                take_qk(0)
                take_v(0)
                maxima(0)
                with dve.Fori(0, B - 1) as b:
                    rest_of(b, True)
                rest_of(B - 1, False)

            @block.tensor
            def _(pe):
                pe.wait_ge(weights_in, 16 * n_weights)
                pe.wait_ge(consts, n_consts)
                pe.wait_ge(sel_ready, 1)
                for s in (qkv_done, s_done, maxt_done, st_done, raw_done, o_done, ot_done, out_done):
                    s.start(pe)
                norm.start_tensor(pe)
                mm = nc.tensor.matmul

                def project(b):
                    if half:
                        pe.wait_ge(cast.sem, cast.now(b, 1))
                    else:
                        pe.wait_ge(inputs_in.sem, inputs_in.now(b, inputs_in.per))
                    pe.wait_ge(maxt_ready.sem, maxt_ready.prev(b, 1))
                    pe.wait_ge(v_ready.sem, v_ready.prev(b, 1))
                    for to in range(KC):
                        for c in range(KC):
                            mm(q_bank()[:, to, :], w["wq"][:, c, to * P:(to + 1) * P], xt[:, c, :],
                               start=c == 0, stop=c == KC - 1)
                    for to in range(KC):
                        for c in range(KC):
                            mm(k_bank()[:, to, :], w["wk"][:, c, to * P:(to + 1) * P], ct[:, c, :],
                               start=c == 0, stop=c == KC - 1)
                    for c in range(KC):
                        last = mm(v_bank(), ct[:, c, :], w["wv"][:, c, :], start=c == 0, stop=c == KC - 1)
                    last.then_inc(qkv_done.sem, 1)

                def scores_for_max(b, unit):
                    t, c, bank = unit // KC, unit % KC, 2 * (unit % 2)
                    if unit == 0:
                        pe.wait_ge(qk_ready.sem, qk_ready.now(b, 1))
                    if unit < 2:
                        pe.wait_ge(probs_ready.sem, probs_ready.prev(b, unit + 3))
                    else:
                        pe.wait_ge(s_used.sem, s_used.now(b, unit - 1))
                    for a in range(2):
                        h = HC * c + HU * a
                        last = mm(PS[:, bank + a, 0:HU * CTX], q[:, c, t * P:(t + 1) * P], k[:, h:h + HU, :],
                                  start=True, stop=not half, skip_group_check=True)
                    if half:
                        for a in range(2):
                            last = mm(PS[:, bank + a, 0:HU * CTX], core.ident16[:],
                                      mask_qk[:, t, :].unsqueeze(1).to_broadcast([P, HU, CTX]),
                                      start=False, stop=True, skip_group_check=True)
                    last.then_inc(s_done.sem, 1)

                def turn_max(b):
                    pe.wait_ge(max_ready.sem, max_ready.now(b, 1))
                    for t in range(TB):
                        last = nc.tensor.transpose(turned_max()[:, t * P:(t + 1) * P],
                                                   max_parts[:, t, :, :].rearrange("p a h -> p (a h)"),
                                                   core.ident16[:])
                    last.then_inc(maxt_done.sem, 1)

                def scores(b, unit):
                    if unit < 2:
                        pe.wait_ge(s_used.sem, s_used.now(b, unit + 3))
                    else:
                        pe.wait_ge(probs_ready.sem, probs_ready.now(b, unit - 1))
                    if unit == 0:
                        pe.wait_ge(maxt_ready.sem, maxt_ready.now(b, 1))
                    bank = 2 * (unit % 2)
                    for i in range(HU):
                        h = HU * unit + i
                        to = PS[0:CTX, bank + i // 2, (i % 2) * SEQ:(i % 2 + 1) * SEQ]
                        mm(to, k[:, h, :], q[:, h // HC, :], start=i % 2 == 0, stop=False, skip_group_check=True)
                        last = mm(to, sel[:, h, :], max_t[:], start=False, stop=not half, skip_group_check=True)
                    if half:
                        for a in range(2):
                            last = mm(PS[0:CTX, bank + a, :].rearrange("p (h n) -> p h n", n=SEQ),
                                      core.ident16[:, 0:CTX], mask_kq[:].unsqueeze(1).to_broadcast([P, 2, SEQ]),
                                      start=False, stop=True, skip_group_check=True)
                    last.then_inc(st_done.sem, 1)

                def outputs(b):
                    pe.wait_ge(probs_ready.sem, probs_ready.now(b, UNITS))
                    pe.wait_ge(v_ready.sem, v_ready.now(b, 1))
                    pe.wait_ge(ot_ready.sem, ot_ready.prev(b, 1))
                    pe.wait_ge(norm.xt_ready.sem, norm.xt_ready.prev(norm.turn(b), 1))
                    for unit in range(UNITS):
                        for j in range(HU):
                            h = HU * unit + j
                            last = mm(PS[WIDE * j:WIDE * (j + 1), 4 + unit // 2, (unit % 2) * SEQ:(unit % 2 + 1) * SEQ],
                                      v[0:CTX, h, :], probs[0:CTX, h, :], start=True, stop=True)
                    last.then_inc(raw_done.sem, 1)

                def to_queries(b):
                    pe.wait_ge(raw_ready.sem, raw_ready.now(b, 1))
                    for t in range(TB):
                        for unit in range(UNITS):
                            last = nc.tensor.transpose(PS[:, 4 + t, unit * P:(unit + 1) * P],
                                                       raw[:, unit, t * P:(t + 1) * P], core.ident[:])
                    last.then_inc(o_done.sem, 1)

                def turn_outputs(b):
                    pe.wait_ge(o_ready.sem, o_ready.now(b, 1))
                    for c in range(KC):
                        for t in range(TB):
                            last = nc.tensor.transpose(PS[:, 4, (c * TB + t) * P:(c * TB + t + 1) * P],
                                                       o[:, t, c * P:(c + 1) * P], core.ident[:])
                    last.then_inc(ot_done.sem, 1)

                def project_output(b):
                    pe.wait_ge(ot_ready.sem, ot_ready.now(b, 1))
                    for t in range(TB):
                        for c in range(KC):
                            last = mm(PS[:, 5, t * D:(t + 1) * D], ot[:, c, t * P:(t + 1) * P], w["wo"][:, c, :],
                                      start=c == 0, stop=c == KC - 1)
                    last.then_inc(out_done.sem, 1)

                def rest_of(b, following):
                    scores(b, 2)
                    scores(b, 3)
                    if following:
                        project(b + 1)
                    outputs(b)
                    if following:
                        scores_for_max(b + 1, 0)
                    to_queries(b)
                    if following:
                        scores_for_max(b + 1, 1)
                    turn_outputs(b)
                    if following:
                        scores_for_max(b + 1, 2)
                    project_output(b)
                    if following:
                        scores_for_max(b + 1, 3)
                        turn_max(b + 1)
                        scores(b + 1, 0)
                        scores(b + 1, 1)
                    norm.tensor(pe, b)

                project(0)
                for unit in range(UNITS):
                    scores_for_max(0, unit)
                turn_max(0)
                scores(0, 0)
                scores(0, 1)
                with pe.Fori(0, B - 1) as b:
                    rest_of(b, True)
                rest_of(B - 1, False)


def block_cross_attention_0(core):
    cross_attention(core, "ca", False, "ca")


def block_cross_attention_1(core):
    cross_attention(core, "cb", True, "cb")


def top2(nc, dve, t, scores, iota8, best, index, index_f, chosen):
    nc.vector.max(best[:, t, :], scores[:, t, :])
    dve.drain()
    nc.vector.max_index(index[:, t, :], best[:, t, :], scores[:, t, :])
    dve.drain()
    nc.vector.tensor_copy(index_f[:, t, :], index[:, t, :])
    dve.drain()
    for r in range(2):
        nc.vector.tensor_scalar(chosen[:, t, r, :], iota8[:], index_f[:, t, r:r + 1], None, ALU.is_equal)
    dve.drain()


def block_experts_0(core):
    E, HB = 8, 3
    nc, PS, dram = core.nc, core.PS, core.dram
    with ExitStack() as ctx:
        def sb(n, shape, dt=F32):
            return ctx.enter_context(nc.sbuf_tensor(f"ea_{n}", shape, dt))

        def sig(n, per, unit=1):
            return Signal(core, f"ea_{n}", per, unit)

        up32 = sb("up32", [P, KC, E, HB, P])
        down32 = sb("down32", [P, E, HB, D])
        up = sb("up", [P, KC, E, HB, P], BF16)
        down = sb("down", [P, E, HB, D], BF16)
        shared_up = sb("shared_up", [P, KC, HB, P])
        shared_down = sb("shared_down", [P, HB, D])
        gate = sb("gate", [P, KC, E])
        gate_bias = sb("gate_bias", [P, E])
        iota8 = sb("iota8", [P, E])
        sel = sb("sel", [P, E, P])
        xt = sb("xt", [P, 2, KC, SEQ])
        tanh = sb("tanh", [P, TB, E])
        scores = sb("scores", [P, TB, E])
        biased = sb("biased", [P, TB, E])
        best = sb("best", [P, TB, 8])
        index = sb("index", [P, TB, 8], mybir.dt.uint32)
        index_f = sb("index_f", [P, TB, 8])
        chosen = sb("chosen", [P, TB, 2, E])
        both = sb("both", [P, TB, E])
        weight = sb("weight", [P, TB, E])
        weight_t = sb("weight_t", [P, SEQ])
        scaled = sb("scaled", [P, 2, KC, SEQ], BF16)
        relu = sb("relu", [P, 2, HB, SEQ], BF16)
        hidden = sb("hidden", [P, 2, HB, SEQ], BF16)
        shared_relu = sb("shared_relu", [P, HB, SEQ])
        shared_hidden = sb("shared_hidden", [P, HB, SEQ])
        routed = sb("routed", [P, 2, TB, D], BF16)
        total = sb("total", [P, TB, D])
        summed = sb("summed", [P, TB, D])
        norm = Norm(core, ctx, "ea", 2, 7)

        gate_in = core.semaphore("ea_gate_in")
        expert_in = [core.semaphore(f"ea_expert_{e}_in") for e in range(E)]
        shared_in = core.semaphore("ea_shared_in")
        cast = core.semaphore("ea_experts_cast")
        consts = core.semaphore("ea_constants_ready")
        xt_in = sig("xt_in", 1, 16)
        gate_done = sig("gate_done", 1)
        tanh_ready = sig("tanh_ready", 1)
        weight_ready = sig("weight_ready", 1)
        weight_turned = sig("weight_turned", 1)
        weight_t_ready = sig("weight_t_ready", 1)
        spread_done = sig("scores_spread", E)
        scaled_ready = sig("scaled_ready", E)
        up_done = sig("up_done", E + 1)
        relu_ready = sig("relu_ready", E + 1)
        hidden_ready = sig("hidden_ready", E + 1)
        down_done = sig("down_done", E)
        routed_ready = sig("routed_ready", E)
        summed_step = sig("summed_step", E - 1)
        shared_done = sig("shared_done", 1)
        total_ready = sig("total_ready", 1)

        def up_banks(e):
            return PS[:, 2 + 2 * (e % 2):4 + 2 * (e % 2), :].rearrange("p a n -> p (a n)")[:, 0:HB * SEQ]\
                .rearrange("p (h n) -> p h n", n=SEQ)

        def tiles(ap):
            return ap.rearrange("p (t d) -> p t d", t=TB)

        with nc.Block() as block:
            @block.sync
            def _(sp):
                sp.dma_start(gate[:], dram["ea_gate"]).then_inc(gate_in, 16)
                sp.dma_start(gate_bias[:], dram["ea_gate_bias"].partition_broadcast(P)).then_inc(gate_in, 16)
                xt_in.start(sp)
                norm.start_sync(sp)

                def load(b, par):
                    sp.dma_start(xt[:, par, :, :], core.xt_of(b)).then_inc(xt_in.sem, 16)

                load(0, 0)
                for e in range(E):
                    sp.dma_start(up32[:, :, e, :, :], dram["ea_up"][:, :, e, :, :]).then_inc(expert_in[e], 16)
                    sp.dma_start(down32[:, e, :, :], dram["ea_down"][:, e, :, :]).then_inc(expert_in[e], 16)
                sp.dma_start(shared_up[:], dram["ea_shared_up"]).then_inc(shared_in, 16)
                sp.dma_start(shared_down[:], dram["ea_shared_down"]).then_inc(shared_in, 16)
                sp.wait_ge(gate_done.sem, gate_done.now(0, 1))
                load(1, 1)
                with sp.Fori(0, B // 2 - 1) as m:
                    for par in range(2):
                        b = m * 2 + par
                        norm.load(sp, b)
                        sp.wait_ge(up_done.sem, up_done.now(b, E + 1))
                        sp.wait_ge(scaled_ready.sem, scaled_ready.now(b, E))
                        load(b + 2, par)
                        norm.store(sp, b)
                for b in range(B - 2, B):
                    norm.load(sp, b)
                    norm.store(sp, b)

            @block.gpsimd
            def _(pool):
                nc.gpsimd.iota(iota8[:], pattern=[[1, E]], base=0, channel_multiplier=0,
                               allow_small_or_imprecise_dtypes=True).then_inc(consts, 1)
                nc.gpsimd.memset(sel[:], 0.0).then_inc(consts, 1)
                nc.gpsimd.memset(weight_t[:], 0.0).then_inc(consts, 1)
                pool.wait_ge(consts, 3)
                nc.gpsimd.affine_select(out=sel[:], in_=sel[:], compare_op=ALU.not_equal, fill=1.0,
                                        base=0, pattern=[[-1, E], [0, P]], channel_multiplier=1).then_inc(consts, 1)
                summed_step.start(pool)
                norm.start_gpsimd(pool)
                with pool.Fori(0, B) as b:
                    pool.wait_ge(total_ready.sem, total_ready.prev(b, 1))
                    for e in range(1, E):
                        pool.wait_ge(routed_ready.sem, routed_ready.now(b, e + 1))
                        if e > 1:
                            pool.wait_ge(summed_step.sem, summed_step.now(b, e - 1))
                        nc.gpsimd.tensor_tensor(summed[:], summed[:] if e > 1 else routed[:, 0, :, :],
                                                routed[:, e % 2, :, :], ALU.add).then_inc(summed_step.sem, 1)
                    norm.gpsimd(pool, b)

            @block.scalar
            def _(act):
                for s in (tanh_ready, weight_t_ready, relu_ready, routed_ready):
                    s.start(act)
                norm.start_scalar(act)

                def tanh_of_gate(b):
                    act.wait_ge(gate_done.sem, gate_done.now(b, 1))
                    act.wait_ge(weight_ready.sem, weight_ready.prev(b, 1))
                    nc.scalar.activation(tanh[:], PS[:, 7, 0:TB * E].rearrange("p (t e) -> p t e", t=TB), ACT.Tanh,
                                         scale=0.5).then_inc(tanh_ready.sem, 1)

                def take_weight_t(b):
                    act.wait_ge(weight_turned.sem, weight_turned.now(b, 1))
                    nc.scalar.activation(weight_t[0:E, :], PS[0:E, 7, 0:SEQ], ACT.Copy).then_inc(weight_t_ready.sem, 1)

                def relu_of(b, e):
                    act.wait_ge(up_done.sem, up_done.now(b, e + 1))
                    if e == E:
                        act.wait_ge(hidden_ready.sem, hidden_ready.prev(b, E + 1))
                        to = shared_relu[:]
                    else:
                        k = e - 1 if e >= 2 else E - 1 + e
                        act.wait_ge(hidden_ready.sem, hidden_ready.now(b, k) if e >= 2 else hidden_ready.prev(b, k))
                        to = relu[:, e % 2, :, :]
                    nc.scalar.activation(to, up_banks(e), ACT.Relu).then_inc(relu_ready.sem, 1)

                def rest_of(b, following):
                    for e in range(E):
                        if following and e == 6:
                            take_weight_t(b + 1)
                        relu_of(b, e + 1)
                        if following and e == 1:
                            tanh_of_gate(b + 1)
                        act.wait_ge(down_done.sem, down_done.now(b, e + 1))
                        if e >= 2:
                            act.wait_ge(summed_step.sem, summed_step.now(b, max(e - 2, 1)))
                        else:
                            act.wait_ge(summed_step.sem, summed_step.prev(b, E - 2 + e))
                        nc.scalar.activation(routed[:, e % 2, :, :], tiles(PS[:, 6, :]),
                                             ACT.Copy).then_inc(routed_ready.sem, 1)
                    if following:
                        relu_of(b + 1, 0)
                    norm.scalar(act, b)

                tanh_of_gate(0)
                act.wait_ge(consts, 4)
                take_weight_t(0)
                relu_of(0, 0)
                with act.Fori(0, B - 1) as b:
                    rest_of(b, True)
                rest_of(B - 1, False)

            @block.vector
            def _(dve):
                dve.wait_ge(gate_in, 32)
                dve.wait_ge(consts, 4)
                for s in (weight_ready, scaled_ready, hidden_ready, total_ready):
                    s.start(dve)
                norm.start_vector(dve)

                def route(b):
                    dve.wait_ge(tanh_ready.sem, tanh_ready.now(b, 1))
                    nc.vector.tensor_scalar(scores[:], tanh[:], 0.5, 0.5, ALU.mult, ALU.add)
                    dve.drain()
                    nc.vector.tensor_tensor(biased[:], scores[:],
                                            gate_bias[:, :].unsqueeze(1).to_broadcast([P, TB, E]), ALU.add)
                    dve.drain()
                    for t in range(TB):
                        top2(nc, dve, t, biased, iota8, best, index, index_f, chosen)
                    nc.vector.tensor_tensor(both[:], chosen[:, :, 0, :], chosen[:, :, 1, :], ALU.add)
                    dve.drain()
                    nc.vector.tensor_tensor(weight[:], both[:], scores[:], ALU.mult).then_inc(weight_ready.sem, 1)

                def scale(b, par, e):
                    dve.wait_ge(spread_done.sem, spread_done.now(b, e + 1))
                    if e >= 2:
                        dve.wait_ge(up_done.sem, up_done.now(b, e - 1))
                    else:
                        dve.wait_ge(up_done.sem, up_done.prev(b, E - 1 + e))
                    nc.vector.tensor_tensor(scaled[:, e % 2, :, :], xt[:, par, :, :],
                                            PS[:, e % 2, 0:SEQ].unsqueeze(1).to_broadcast([P, KC, SEQ]),
                                            ALU.mult).then_inc(scaled_ready.sem, 1)

                def square(b, e):
                    dve.wait_ge(relu_ready.sem, relu_ready.now(b, e + 1))
                    if e == E:
                        dve.wait_ge(shared_done.sem, shared_done.prev(b, 1))
                        nc.vector.tensor_tensor(shared_hidden[:], shared_relu[:], shared_relu[:],
                                                ALU.mult).then_inc(hidden_ready.sem, 1)
                    else:
                        if e >= 2:
                            dve.wait_ge(down_done.sem, down_done.now(b, e - 1))
                        else:
                            dve.wait_ge(down_done.sem, down_done.prev(b, E - 1 + e))
                        nc.vector.tensor_tensor(hidden[:, e % 2, :, :], relu[:, e % 2, :, :],
                                                relu[:, e % 2, :, :], ALU.mult).then_inc(hidden_ready.sem, 1)

                def cast_expert(e):
                    dve.wait_ge(expert_in[e], 32)
                    nc.vector.tensor_copy(up[:, :, e, :, :], up32[:, :, e, :, :])
                    nc.vector.tensor_copy(down[:, e, :, :], down32[:, e, :, :])
                    dve.drain()
                    dve.sem_inc(cast, 1)

                def rest_of(b, par, following, first=False):
                    for e in range(E + 1):
                        if first and e + 1 < E:
                            cast_expert(e + 1)
                        if e + 1 < E:
                            scale(b, par, e + 1)
                        square(b, e)
                        if following and e == 2:
                            route(b + 1)
                    if following:
                        dve.wait_ge(xt_in.sem, xt_in.now(b + 1, 1))
                        scale(b + 1, 1 - par, 0)
                    dve.wait_ge(summed_step.sem, summed_step.now(b, E - 1))
                    dve.wait_ge(shared_done.sem, shared_done.now(b, 1))
                    nc.vector.tensor_tensor(total[:], tiles(PS[:, 7, :]), summed[:], ALU.add)\
                        .then_inc(total_ready.sem, 1)
                    dve.drain()
                    norm.vector(dve, b, (shared_done.sem, shared_done.now(b, 1)), source=total[:])

                route(0)
                dve.wait_ge(xt_in.sem, xt_in.now(0, 1))
                cast_expert(0)
                scale(0, 0, 0)
                rest_of(0, 0, True, first=True)
                rest_of(1, 1, True)
                with dve.Fori(1, B // 2 - 1) as m:
                    for par in range(2):
                        rest_of(m * 2 + par, par, True)
                rest_of(B - 2, 0, True)
                rest_of(B - 1, 1, False)

            @block.tensor
            def _(pe):
                pe.wait_ge(gate_in, 32)
                pe.wait_ge(consts, 4)
                for s in (gate_done, weight_turned, spread_done, up_done, down_done, shared_done):
                    s.start(pe)
                norm.start_tensor(pe)
                mm = nc.tensor.matmul

                def gate_of(b, par):
                    pe.wait_ge(xt_in.sem, xt_in.now(b, 1))
                    for t in range(TB):
                        for c in range(KC):
                            last = mm(PS[:, 7, t * E:(t + 1) * E], xt[:, par, c, t * P:(t + 1) * P], gate[:, c, :],
                                      start=c == 0, stop=c == KC - 1)
                    last.then_inc(gate_done.sem, 1)

                def turn_weight(b):
                    pe.wait_ge(weight_ready.sem, weight_ready.now(b, 1))
                    for t in range(TB):
                        last = nc.tensor.transpose(PS[0:E, 7, t * P:(t + 1) * P], weight[:, t, :], core.ident[:])
                    last.then_inc(weight_turned.sem, 1)

                def spread_of(b, e):
                    if e == 0:
                        pe.wait_ge(weight_t_ready.sem, weight_t_ready.now(b, 1))
                    if e >= 2:
                        pe.wait_ge(scaled_ready.sem, scaled_ready.now(b, e - 1))
                    else:
                        pe.wait_ge(scaled_ready.sem, scaled_ready.prev(b, E - 1 + e))
                    mm(PS[:, e % 2, 0:SEQ], sel[:, e, :], weight_t[:], start=True, stop=True)\
                        .then_inc(spread_done.sem, 1)

                def up_of(b, par, e, first=False):
                    if first and e < E:
                        pe.wait_ge(cast, e + 1)
                    elif first:
                        pe.wait_ge(shared_in, 32)
                    if e < E:
                        pe.wait_ge(scaled_ready.sem, scaled_ready.now(b, e + 1))
                    if e >= 2:
                        pe.wait_ge(relu_ready.sem, relu_ready.now(b, e - 1))
                    else:
                        pe.wait_ge(relu_ready.sem, relu_ready.prev(b, E + 1 - e))
                    for h in range(HB):
                        for c in range(KC):
                            if e < E:
                                last = mm(up_banks(e)[:, h, :], up[:, c, e, h, :], scaled[:, e % 2, c, :],
                                          start=c == 0, stop=c == KC - 1)
                            else:
                                last = mm(up_banks(e)[:, h, :], shared_up[:, c, h, :], xt[:, par, c, :],
                                          start=c == 0, stop=c == KC - 1)
                    last.then_inc(up_done.sem, 1)

                def down_of(b, e):
                    pe.wait_ge(hidden_ready.sem, hidden_ready.now(b, e + 1))
                    pe.wait_ge(routed_ready.sem, routed_ready.now(b, e) if e else routed_ready.prev(b, E))
                    for t in range(TB):
                        for h in range(HB):
                            last = mm(PS[:, 6, t * D:(t + 1) * D], hidden[:, e % 2, h, t * P:(t + 1) * P],
                                      down[:, e, h, :], start=h == 0, stop=h == HB - 1)
                    last.then_inc(down_done.sem, 1)

                def shared_down_of(b, following):
                    pe.wait_ge(hidden_ready.sem, hidden_ready.now(b, E + 1))
                    if following:
                        pe.wait_ge(weight_t_ready.sem, weight_t_ready.now(b + 1, 1))
                    else:
                        pe.wait_ge(norm.xt_ready.sem, norm.xt_ready.prev(norm.turn(b), 1))
                    for t in range(TB):
                        for h in range(HB):
                            last = mm(PS[:, 7, t * D:(t + 1) * D], shared_hidden[:, h, t * P:(t + 1) * P],
                                      shared_down[:, h, :], start=h == 0, stop=h == HB - 1)
                    last.then_inc(shared_done.sem, 1)

                def rest_of(b, par, following, first=False):
                    for e in range(E):
                        if following and e == 1:
                            pe.wait_ge(norm.xt_ready.sem, norm.xt_ready.prev(norm.turn(b), 1))
                            gate_of(b + 1, 1 - par)
                        if following and e == 6:
                            turn_weight(b + 1)
                        if e + 2 < E:
                            spread_of(b, e + 2)
                        up_of(b, par, e + 1, first)
                        down_of(b, e)
                    if following:
                        spread_of(b + 1, 0)
                        spread_of(b + 1, 1)
                    shared_down_of(b, following)
                    if following:
                        up_of(b + 1, 1 - par, 0)
                    norm.tensor(pe, b)

                gate_of(0, 0)
                turn_weight(0)
                spread_of(0, 0)
                spread_of(0, 1)
                up_of(0, 0, 0, first=True)
                rest_of(0, 0, True, first=True)
                rest_of(1, 1, True)
                with pe.Fori(1, B // 2 - 1) as m:
                    for par in range(2):
                        rest_of(m * 2 + par, par, True)
                rest_of(B - 2, 0, True)
                rest_of(B - 1, 1, False)



MH, MD = 4, 64
CHUNK = 32
NCH = SEQ // CHUNK
LOCAL, MID = 7, 25
CONV = 4
OUTS = ("local", "mid", "delta", "v")


class MixerScratch:

    def __init__(self, nc):
        def dram(name, shape):
            return nc.dram_tensor(name, shape, F32, kind="Internal").ap()

        self.outs = dram("mixer_outs", (len(OUTS), B * SEQ, D))
        self.k = dram("mixer_k", (B, NCH, CHUNK, MH, MD))
        self.qk_t = dram("mixer_qk_t", (2, P, KC, B, NCH, CHUNK))
        self.gram = dram("mixer_gram", (B, TB, P // CHUNK, CHUNK, MH, CHUNK))
        self.beta = dram("mixer_beta", (B, MH, NCH, CHUNK))
        self.solved = dram("mixer_solved", (NCH, MH, CHUNK, B, CHUNK))


def block_mixer_project(core):
    nc, PS, dram = core.nc, core.PS, core.dram
    core.mixer = scratch = MixerScratch(nc)
    PAD = MID - 1
    BY_VECTOR = 5
    with ExitStack() as ctx:
        def sb(n, shape, dt=F32):
            return ctx.enter_context(nc.sbuf_tensor(f"mp_{n}", shape, dt))

        def sig(n, per, unit=1):
            return Signal(core, f"mp_{n}", per, unit)

        w = sb("w", [P, KC, 3, KC, P])
        w_beta = sb("w_beta", [P, KC, MH])
        conv_w = sb("conv_w", [P, 3, KC, CONV])
        conv_half = sb("conv_half", [P, 3, KC, CONV])
        local_w = sb("local_w", [P, KC, LOCAL])
        mid_w = sb("mid_w", [P, KC, MID])
        mid_diag = sb("mid_diag", [P, KC, MID, P])
        eps12 = sb("eps12", [P, 16])
        xt = sb("xt", [P, KC, SEQ])
        padded = sb("padded", [P, 3, KC, CONV - 1 + SEQ])
        y = sb("y", [P, 3, KC, SEQ])
        tanh = sb("tanh", [P, 3, KC, SEQ])
        tanh_beta = sb("tanh_beta", [MH, SEQ])
        beta_next = sb("beta_next", [MH, SEQ])
        beta = sb("beta", [MH, SEQ])
        qk = sb("qk", [P, 2, KC, SEQ])
        v_pad = sb("v_pad", [P, KC, PAD + SEQ])
        local_t = sb("local_t", [P, KC, SEQ])
        mid_part = sb("mid_part", [P, KC, SEQ])
        mid_t = sb("mid_t", [P, KC, SEQ])
        squares = sb("squares", [P, 2 * TB * MH, MD])
        sums = sb("sums", [P, 2 * TB * MH])
        rnorm = sb("rnorm", [P, 2 * TB * MH])
        v_tok = sb("v_tok", [P, TB, D])
        lm_tok = sb("lm_tok", [P, 2, TB, D])
        qk_tok = sb("qk_tok", [P, 2, TB, D])
        qk_t = sb("qk_t", [P, 2, KC, SEQ])
        gram = sb("gram", [P, TB, MH, CHUNK])

        weights_in = core.semaphore("mp_weights_in")
        consts = core.semaphore("mp_constants_ready")
        seen = core.semaphore("mp_qk_t_seen")
        xt_in = sig("xt_in", 1, 16)
        projected = sig("projected", 1)
        padded_ready = sig("padded_ready", 1)
        conv_ready = sig("conv_ready", 1)
        tanh_ready = sig("tanh_ready", 1)
        silu_ready = sig("silu_ready", 1)
        local_ready = sig("local_ready", 1)
        mid_done = sig("mid_done", 1)
        mid_ready = sig("mid_ready", 1)
        qkv_turned = sig("qkv_turned", 1)
        squares_ready = sig("squares_ready", 1)
        v_tok_ready = sig("v_tok_ready", 1)
        sums_ready = sig("sums_ready", 1)
        rnorm_step = sig("rnorm_step", 2)
        lm_turned = sig("lm_turned", 1)
        lm_ready = sig("lm_ready", 1)
        qk_tok_ready = sig("qk_normed", 1)
        qk_turned = sig("qk_turned", 1)
        qk_t_ready = sig("qk_t_ready", 1)
        gram_done = sig("gram_done", 1)
        gram_ready = sig("gram_ready", 1)
        N_STORES = 3 * TB + TB + 2 + TB + 1
        stored = sig("stored", N_STORES, 16)
        left = sig("results_left", 1)

        with nc.Block() as block:
            @block.sync
            def _(sp):
                for dst, n in ((w, "mp_w"), (w_beta, "mp_w_beta"), (conv_w, "mp_conv_w"), (local_w, "mp_local_w"),
                               (mid_w, "mp_mid_w")):
                    sp.dma_start(dst[:], dram[n]).then_inc(weights_in, 16)
                for s in (xt_in, stored, left):
                    s.start(sp)

                def load(b, ahead):
                    sp.wait_ge(projected.sem, projected.prev(b + ahead, 1))
                    sp.dma_start(xt[:], core.XT[:, :, bass.ds(b * SEQ + ahead * SEQ, SEQ)]).then_inc(xt_in.sem, 16)

                def store(b):
                    sp.wait_ge(lm_ready.sem, lm_ready.now(b, 1))
                    for t in range(TB):
                        rows = bass.ds(b * SEQ + t * P, P)
                        sp.dma_start(scratch.outs[0, rows, :], lm_tok[:, 0, t, :]).then_inc(stored.sem, 16)
                        sp.dma_start(scratch.outs[1, rows, :], lm_tok[:, 1, t, :]).then_inc(stored.sem, 16)
                        sp.dma_start(scratch.outs[3, rows, :], v_tok[:, t, :]).then_inc(stored.sem, 16)
                    sp.wait_ge(qk_tok_ready.sem, qk_tok_ready.now(b, 1))
                    k_rows = scratch.k.rearrange("b n t h d -> (b n t) (h d)")
                    for t in range(TB):
                        sp.dma_start(k_rows[bass.ds(b * SEQ + t * P, P), :], qk_tok[:, 1, t, :])\
                            .then_inc(stored.sem, 16)
                    sp.dma_start(scratch.beta.rearrange("b h n t -> b h (n t)")[bass.ds(b, 1), :, :]
                                 .rearrange("a h n -> h (a n)"), beta[:]).then_inc(stored.sem, 16)
                    sp.wait_ge(qk_t_ready.sem, qk_t_ready.now(b, 1))
                    sp.sem_inc(seen, 1)
                    for i in range(2):
                        sp.dma_start(scratch.qk_t[i].rearrange("p c b n t -> p c (b n t)")
                                     [:, :, bass.ds(b * SEQ, SEQ)], qk_t[:, i, :, :]).then_inc(stored.sem, 16)
                    sp.wait_ge(gram_ready.sem, gram_ready.now(b, 1))
                    gram_rows = scratch.gram.rearrange("b u c i h j -> (b u c i) (h j)")
                    for t in range(TB):
                        sp.dma_start(gram_rows[bass.ds(b * SEQ + t * P, P), :],
                                     gram[:, t, :, :].rearrange("p h j -> p (h j)")).then_inc(stored.sem, 16)
                    sp.wait_ge(stored.sem, stored.now(b, N_STORES))
                    sp.sem_inc(left.sem, 1)

                load(0, 0)
                load(0, 1)
                with sp.Fori(0, B - 2) as b:
                    load(b, 2)
                    store(b)
                for b in range(B - 2, B):
                    store(b)

            @block.gpsimd
            def _(pool):
                nc.gpsimd.memset(eps12[:], 1e-12).then_inc(consts, 1)
                nc.gpsimd.memset(padded[:], 0.0).then_inc(consts, 1)
                nc.gpsimd.memset(v_pad[:], 0.0).then_inc(consts, 1)
                pool.wait_ge(weights_in, 80)
                for c in range(KC):
                    nc.gpsimd.tensor_tensor(mid_diag[:, c, :, :],
                                            core.ident[:, :].unsqueeze(1).to_broadcast([P, MID, P]),
                                            spread(mid_w[:, c, :], P), ALU.mult).then_inc(consts, 1)
                rnorm_step.start(pool)
                with pool.Fori(0, B) as b:
                    pool.wait_ge(sums_ready.sem, sums_ready.now(b, 1))
                    nc.gpsimd.tensor_tensor(rnorm[:], sums[:], eps12[:], ALU.add).then_inc(rnorm_step.sem, 1)
                    pool.wait_ge(rnorm_step.sem, rnorm_step.now(b, 1))
                    nc.gpsimd.tensor_tensor(rnorm[:], rnorm[:], core.minus_half[:], ALU.pow)\
                        .then_inc(rnorm_step.sem, 1)

            @block.scalar
            def _(act):
                act.wait_ge(consts, 5)
                for s in (padded_ready, tanh_ready, squares_ready, v_tok_ready, lm_ready, qk_t_ready,
                          gram_ready):
                    s.start(act)

                def take_projections(b):
                    act.wait_ge(projected.sem, projected.now(b, 1))
                    act.wait_ge(conv_ready.sem, conv_ready.prev(b, 1))
                    act.wait_ge(silu_ready.sem, silu_ready.prev(b, 1))
                    nc.scalar.activation(padded[:].rearrange("p a c n -> p (a c) n")[:, :, CONV - 1:],
                                         PS[:, 5:8, :].rearrange("p a (c n) -> p (a c) n", c=KC), ACT.Copy)
                    nc.scalar.activation(tanh_beta[:], PS[0:MH, 3, 0:SEQ], ACT.Tanh, scale=0.5)
                    act.drain()
                    act.sem_inc(padded_ready.sem, 1)

                def tanh_of_convolved(b):
                    act.wait_ge(conv_ready.sem, conv_ready.now(b, 1))
                    nc.scalar.activation(tanh[:], y[:], ACT.Tanh).then_inc(tanh_ready.sem, 1)

                def square(b):
                    act.wait_ge(qkv_turned.sem, qkv_turned.now(b, 1))
                    nc.scalar.activation(squares[:].rearrange("p (a m) d -> p a (m d)", a=2), PS[:, 0:2, :],
                                         ACT.Square).then_inc(squares_ready.sem, 1)

                def take_v(b):
                    act.wait_ge(left.sem, left.prev(b, 1))
                    nc.scalar.activation(v_tok[:].rearrange("p t d -> p (t d)"), PS[:, 2, :],
                                         ACT.Copy).then_inc(v_tok_ready.sem, 1)

                def take_results(b):
                    act.wait_ge(lm_turned.sem, lm_turned.now(b, 1))
                    nc.scalar.activation(lm_tok[:].rearrange("p a t d -> p a (t d)"), PS[:, 5:7, :],
                                         ACT.Copy).then_inc(lm_ready.sem, 1)
                    act.wait_ge(qk_turned.sem, qk_turned.now(b, 1))
                    for i, bank in enumerate((3, 7)):
                        nc.scalar.activation(qk_t[:, i, :, :].rearrange("p c n -> p (c n)"), PS[:, bank, :], ACT.Copy)
                    act.drain()
                    act.sem_inc(qk_t_ready.sem, 1)
                    act.wait_ge(gram_done.sem, gram_done.now(b, 1))
                    for i in range(2):
                        for c4 in range(P // CHUNK):
                            at = slice(c4 * CHUNK, (c4 + 1) * CHUNK)
                            nc.scalar.activation(
                                gram[at, :, :, :].rearrange("p t (g i) j -> p t g i j", i=2)[:, :, :, i, :],
                                PS[at, i, :].rearrange("p (t g j) -> p t g j", t=TB, g=2)[:, :, :, at], ACT.Copy)
                    act.drain()
                    act.sem_inc(gram_ready.sem, 1)

                def rest_of(b, following):
                    square(b)
                    if following:
                        take_projections(b + 1)
                    take_v(b)
                    if following:
                        tanh_of_convolved(b + 1)
                    take_results(b)

                take_projections(0)
                tanh_of_convolved(0)
                with act.Fori(0, B - 1) as b:
                    rest_of(b, True)
                rest_of(B - 1, False)

            @block.vector
            def _(dve):
                dve.wait_ge(weights_in, 80)
                dve.wait_ge(consts, 5)
                nc.vector.tensor_scalar(conv_half[:], conv_w[:], 0.5, None, ALU.mult)
                dve.drain()
                for s in (conv_ready, silu_ready, local_ready, sums_ready, qk_tok_ready, mid_ready):
                    s.start(dve)

                def convolve(to, source, weight, taps, parts):
                    for tap in range(taps):
                        for part in parts:
                            shifted = source(part, tap)
                            scalar = weight(part, tap)
                            if tap == 0:
                                nc.vector.tensor_scalar(to(part), shifted, scalar, None, ALU.mult)
                            else:
                                nc.vector.scalar_tensor_tensor(to(part), shifted, scalar, to(part), ALU.mult, ALU.add)
                        dve.drain()


                def convolve_projections(b):
                    dve.wait_ge(padded_ready.sem, padded_ready.now(b, 1))
                    convolve(lambda p: y[:, p[0], p[1], :],
                             lambda p, tap: padded[:, p[0], p[1], tap:tap + SEQ],
                             lambda p, tap: conv_half[:, p[0], p[1], tap:tap + 1],
                             CONV, [(a, c) for a in range(3) for c in range(KC)])
                    dve.sem_inc(conv_ready.sem, 1)

                def silu(b):
                    dve.wait_ge(tanh_ready.sem, tanh_ready.now(b, 1))
                    dve.wait_ge(mid_done.sem, mid_done.prev(b, 1))
                    nc.vector.scalar_tensor_tensor(qk[:], tanh[:, 0:2, :, :], 1.0, y[:, 0:2, :, :], ALU.add, ALU.mult)
                    nc.vector.scalar_tensor_tensor(v_pad[:, :, PAD:], tanh[:, 2, :, :], 1.0, y[:, 2, :, :], ALU.add,
                                                   ALU.mult)
                    nc.vector.tensor_scalar(beta_next[:], tanh_beta[:], 0.5, 0.5, ALU.mult, ALU.add)
                    dve.drain()
                    dve.sem_inc(silu_ready.sem, 1)

                def convolve_local(b):
                    dve.wait_ge(lm_turned.sem, lm_turned.prev(b, 1))
                    convolve(lambda c: local_t[:, c, :],
                             lambda c, tap: v_pad[:, c, PAD - LOCAL + 1 + tap:PAD - LOCAL + 1 + tap + SEQ],
                             lambda c, tap: local_w[:, c, tap:tap + 1], LOCAL, range(KC))
                    dve.sem_inc(local_ready.sem, 1)

                def sum_squares(b):
                    dve.wait_ge(squares_ready.sem, squares_ready.now(b, 1))
                    nc.vector.tensor_reduce(sums[:], squares[:], AX.X, ALU.add).then_inc(sums_ready.sem, 1)

                def normalize(b):
                    dve.wait_ge(rnorm_step.sem, rnorm_step.now(b, 2))
                    dve.wait_ge(left.sem, left.prev(b, 1))
                    nc.vector.tensor_copy(beta[:], beta_next[:])
                    nc.vector.tensor_tensor(qk_tok[:].rearrange("p a t (h d) -> p (a t h) d", d=MD),
                                            PS[:, 0:2, :].rearrange("p a (m d) -> p (a m) d", d=MD),
                                            spread(rnorm[:], MD), ALU.mult)
                    dve.drain()
                    dve.sem_inc(qk_tok_ready.sem, 1)

                def rest_of(b, following):
                    convolve_local(b)
                    sum_squares(b)
                    if following:
                        convolve_projections(b + 1)
                    normalize(b)
                    convolve(lambda c: mid_part[:, c, :],
                             lambda c, tap: v_pad[:, c, tap:tap + SEQ],
                             lambda c, tap: mid_w[:, c, tap:tap + 1], BY_VECTOR, range(KC))
                    dve.wait_ge(mid_done.sem, mid_done.now(b, 1))
                    nc.vector.tensor_tensor(mid_t[:].rearrange("p c n -> p (c n)"), PS[:, 4, :],
                                            mid_part[:].rearrange("p c n -> p (c n)"), ALU.add)\
                        .then_inc(mid_ready.sem, 1)
                    if following:
                        silu(b + 1)

                convolve_projections(0)
                silu(0)
                with dve.Fori(0, B - 1) as b:
                    rest_of(b, True)
                rest_of(B - 1, False)

            @block.tensor
            def _(pe):
                pe.wait_ge(weights_in, 80)
                pe.wait_ge(consts, 5)
                for s in (projected, mid_done, qkv_turned, lm_turned, qk_turned, gram_done):
                    s.start(pe)
                mm = nc.tensor.matmul

                def turn(bank, source):
                    for t in range(TB):
                        for c in range(KC):
                            last = nc.tensor.transpose(PS[:, bank, t * D + c * P:t * D + (c + 1) * P],
                                                       source(c, t), core.ident[:])
                    return last


                def project(b):
                    pe.wait_ge(xt_in.sem, xt_in.now(b, 1))
                    for a in range(3):
                        for oc in range(KC):
                            for c in range(KC):
                                mm(PS[:, 5 + a, oc * SEQ:(oc + 1) * SEQ], w[:, c, a, oc, :], xt[:, c, :],
                                   start=c == 0, stop=c == KC - 1)
                    for c in range(KC):
                        last = mm(PS[0:MH, 3, 0:SEQ], w_beta[:, c, :], xt[:, c, :], start=c == 0, stop=c == KC - 1)
                    last.then_inc(projected.sem, 1)

                def turn_qkv(b):
                    pe.wait_ge(silu_ready.sem, silu_ready.now(b, 1))
                    pe.wait_ge(gram_ready.sem, gram_ready.prev(b, 1))
                    pe.wait_ge(v_tok_ready.sem, v_tok_ready.prev(b, 1))
                    pe.wait_ge(lm_ready.sem, lm_ready.prev(b, 1))
                    pe.wait_ge(qk_t_ready.sem, qk_t_ready.prev(b, 1))
                    turn(0, lambda c, t: qk[:, 0, c, t * P:(t + 1) * P])
                    turn(1, lambda c, t: qk[:, 1, c, t * P:(t + 1) * P])
                    turn(2, lambda c, t: v_pad[:, c, PAD + t * P:PAD + (t + 1) * P]).then_inc(qkv_turned.sem, 1)

                def convolve_mid(b):
                    pe.wait_ge(mid_ready.sem, mid_ready.prev(b, 1))
                    for c in range(KC):
                        for tap in range(BY_VECTOR, MID):
                            last = mm(PS[:, 4, c * SEQ:(c + 1) * SEQ], mid_diag[:, c, tap, :],
                                      v_pad[:, c, tap:tap + SEQ], start=tap == BY_VECTOR, stop=tap == MID - 1)
                    last.then_inc(mid_done.sem, 1)

                def finish(b, following):
                    if following:
                        pe.wait_ge(padded_ready.sem, padded_ready.now(b + 1, 1))
                    pe.wait_ge(local_ready.sem, local_ready.now(b, 1))
                    turn(5, lambda c, t: local_t[:, c, t * P:(t + 1) * P])
                    pe.wait_ge(mid_ready.sem, mid_ready.now(b, 1))
                    turn(6, lambda c, t: mid_t[:, c, t * P:(t + 1) * P]).then_inc(lm_turned.sem, 1)
                    pe.wait_ge(qk_tok_ready.sem, qk_tok_ready.now(b, 1))
                    for i, bank in enumerate((3, 7)):
                        for c in range(KC):
                            for t in range(TB):
                                last = nc.tensor.transpose(PS[:, bank, (c * TB + t) * P:(c * TB + t + 1) * P],
                                                           qk_tok[:, i, t, c * P:(c + 1) * P], core.ident[:])
                    last.then_inc(qk_turned.sem, 1)
                    pe.wait_ge(qk_t_ready.sem, qk_t_ready.now(b, 1))
                    for t in range(TB):
                        for g in range(KC):
                            for i in range(2):
                                keys = qk_t[MD * i:MD * (i + 1), 1, g, t * P:(t + 1) * P]
                                last = mm(PS[:, i, (t * 2 + g) * P:(t * 2 + g + 1) * P], keys, keys,
                                          start=True, stop=True)
                    last.then_inc(gram_done.sem, 1)

                def rest_of(b, following):
                    turn_qkv(b)
                    if following:
                        project(b + 1)
                    convolve_mid(b)
                    finish(b, following)

                project(0)
                with pe.Fori(0, B - 1) as b:
                    rest_of(b, True)
                rest_of(B - 1, False)


def block_mixer_solve(core):
    nc, scratch = core.nc, core.mixer
    NG = B * NCH * MH // P
    BG = B // NG
    C = CHUNK
    with ExitStack() as ctx:
        def sb(n, shape, dt=F32):
            return ctx.enter_context(nc.sbuf_tensor(f"ms_{n}", shape, dt))

        gram = sb("gram", [P, NG, C, C])
        beta = sb("beta", [P, NG, C])
        strict = sb("strict", [P, C, C])
        eye = sb("eye", [P, C, C])
        T = sb("T", [P, NG, C, C])
        product = sb("product", [P, NG * C * C])
        row = sb("row", [P, NG, C])
        out = sb("out", [P, NG, C, C])
        loaded = core.semaphore("ms_loaded")
        consts = core.semaphore("ms_constants_ready")
        solved = core.semaphore("ms_solved")
        stored = core.semaphore("ms_stored")
        with nc.Block() as block:
            @block.sync
            def _(sp):
                for g in range(NG):
                    for h in range(MH):
                        rows = slice(h, P, MH)
                        src = scratch.gram[g * BG:(g + 1) * BG, :, :, :, h, :]
                        sp.dma_start(gram[rows, g, :, :], src.rearrange("b u c i j -> (b u c) i j"))\
                            .then_inc(loaded, 16)
                        sp.dma_start(beta[rows, g, :], scratch.beta[g * BG:(g + 1) * BG, h, :, :])\
                            .then_inc(loaded, 16)
                sp.wait_ge(solved, 1)
                for b in range(B):
                    rows = slice((b % BG) * NCH * MH, (b % BG + 1) * NCH * MH)
                    sp.dma_start(scratch.solved.rearrange("n h j b i -> (n h) j b i")[:, :, b, :],
                                 out[rows, b // BG, :, :]).then_inc(stored, 16)
                sp.wait_ge(stored, 16 * B)

            @block.gpsimd
            def _(pool):
                nc.gpsimd.memset(strict[:], -1.0).then_inc(consts, 1)
                nc.gpsimd.memset(eye[:], 0.0).then_inc(consts, 1)
                pool.wait_ge(consts, 2)
                nc.gpsimd.affine_select(out=strict[:], in_=strict[:], compare_op=ALU.is_gt, fill=0.0, base=0,
                                        pattern=[[1, C], [-1, C]], channel_multiplier=0).then_inc(consts, 1)
                nc.gpsimd.affine_select(out=eye[:], in_=eye[:], compare_op=ALU.not_equal, fill=1.0, base=0,
                                        pattern=[[1, C], [-1, C]], channel_multiplier=0).then_inc(consts, 1)

            @block.vector
            def _(dve):
                dve.wait_ge(loaded, 16 * 2 * NG * MH)
                dve.wait_ge(consts, 4)
                for g in range(NG):
                    nc.vector.tensor_tensor(T[:, g, :, :], gram[:, g, :, :], strict[:], ALU.mult)
                dve.drain()
                nc.vector.tensor_tensor(T[:], T[:], spread(beta[:], C), ALU.mult)
                dve.drain()
                for i in range(1, C):
                    prod = product[:, 0:NG * i * i].rearrange("p (g c j) -> p g c j", g=NG, c=i)
                    nc.vector.tensor_tensor(prod, T[:, :, i, 0:i].unsqueeze(2).to_broadcast([P, NG, i, i]),
                                            T[:, :, 0:i, 0:i].rearrange("p g j c -> p g c j"), ALU.mult)
                    dve.drain()
                    nc.vector.tensor_reduce(row[:, :, 0:i], prod, AX.X, ALU.add)
                    dve.drain()
                    nc.vector.tensor_tensor(T[:, :, i, 0:i], T[:, :, i, 0:i], row[:, :, 0:i], ALU.add)
                    dve.drain()
                for g in range(NG):
                    nc.vector.tensor_tensor(out[:, g, :, :], T[:, g, :, :].rearrange("p i j -> p j i"), eye[:], ALU.add)
                dve.drain()
                nc.vector.tensor_tensor(out[:], out[:], spread(beta[:], C), ALU.mult).then_inc(solved, 1)


def block_mixer_scan(core):
    nc, PS, scratch = core.nc, core.PS, core.mixer
    C = CHUNK
    with ExitStack() as ctx:
        def sb(n, shape, dt=F32):
            return ctx.enter_context(nc.sbuf_tensor(f"mc_{n}", shape, dt))

        qk_bd = sb("qk_bd", [P, 2, 2, KC, B, P])
        k_bd = sb("k_bd", [P, 2, KC, B, P])
        t_bd = sb("t_bd", [P, 2, B, P])
        v = sb("v", [P, 2, B, MD])
        causal = sb("causal", [P, P])
        attn = sb("attn", [P, B, P])
        rest = sb("rest", [P, B, MD])
        u = sb("u", [P, B, MD])
        S = sb("S", [P, KC, B, MD])
        o = sb("o", [P, 2, B, MD])
        zeroed = core.semaphore("mc_zeroed")
        N_LOADS = 4 * MH + MH
        loaded = [core.semaphore(f"mc_loaded_{i}") for i in range(2)]

        def sig(n, per, unit=1):
            return Signal(core, f"mc_{n}", per, unit)

        attn_done = sig("attn_done", 2)
        attn_ready = sig("attn_ready", 2)
        ks_done = sig("ks_done", 2)
        rest_ready = sig("rest_ready", 2)
        u_done = sig("u_done", 2)
        u_ready = sig("u_ready", 2)
        o_done = sig("o_done", 2)
        o_ready = sig("o_ready", 2)
        s_done = sig("state_update_done", 2)
        s_ready = sig("state_ready", 2)
        o_stored = sig("o_stored", 2 * MH, 16)

        def by_head(bank):
            return PS[:, bank, :].rearrange("p (b d) -> p b d", d=MD)

        with nc.Block() as block:
            @block.sync
            def _(sp):
                sp.wait_ge(zeroed, 6)
                o_stored.start(sp)
                def load(m, par):
                    n = bass.ds(2 * m + par, 1)
                    for h in range(MH):
                        c, i = h // 2, h % 2
                        at = slice(h * C, (h + 1) * C)
                        rows = slice(i * MD, (i + 1) * MD)
                        for a in range(2):
                            sp.dma_start(qk_bd[rows, par, a, c, :, at],
                                         scratch.qk_t[a, rows, c, :, n, :].rearrange("p b a t -> p b (a t)"))\
                                .then_inc(loaded[par], 16)
                        sp.dma_start(k_bd[at, par, c, :, rows],
                                     scratch.k[:, n, :, h, :].rearrange("b a t d -> (a t) b d"))\
                            .then_inc(loaded[par], 16)
                        sp.dma_start(v[at, par, :, :],
                                     scratch.outs[3].rearrange("(b n t) f -> b n t f", n=NCH, t=C)
                                     [:, n, :, h * MD:(h + 1) * MD].rearrange("b a t d -> (a t) b d"))\
                            .then_inc(loaded[par], 16)
                        sp.dma_start(t_bd[at, par, :, at],
                                     scratch.solved[n, h, :, :, :].rearrange("a j b i -> (a j) b i"))\
                            .then_inc(loaded[par], 16)

                def store(m, par):
                    n = bass.ds(2 * m + par, 1)
                    sp.wait_ge(o_ready.sem, o_ready.now(m, par + 1))
                    for h in range(MH):
                        sp.dma_start(scratch.outs[2].rearrange("(b n t) f -> b n t f", n=NCH, t=C)
                                     [:, n, :, h * MD:(h + 1) * MD].rearrange("b a t d -> (a t) b d"),
                                     o[h * C:(h + 1) * C, par, :, :]).then_inc(o_stored.sem, 16)

                load(0, 0)
                load(0, 1)
                with sp.Fori(0, NCH // 2 - 1) as m:
                    for par in range(2):
                        store(m, par)
                        sp.wait_ge(o_done.sem, o_done.now(m, par + 1))
                        load(m + 1, par)
                for par in range(2):
                    store(NCH // 2 - 1, par)
                sp.wait_ge(o_stored.sem, o_stored.now(NCH // 2 - 1, 2 * MH))

            @block.gpsimd
            def _(pool):
                nc.gpsimd.memset(qk_bd[:], 0.0).then_inc(zeroed, 1)
                nc.gpsimd.memset(causal[:], 1.0).then_inc(zeroed, 1)
                pool.wait_ge(zeroed, 5)
                nc.gpsimd.affine_select(out=causal[:], in_=causal[:], compare_op=ALU.is_ge, fill=0.0, base=0,
                                        pattern=[[1, P]], channel_multiplier=-1).then_inc(zeroed, 1)

            @block.scalar
            def _(act):
                for s in (u_ready, o_ready):
                    s.start(act)
                with act.Fori(0, NCH // 2) as m:
                    act.wait_ge(o_stored.sem, o_stored.prev(m, 2 * MH))
                    for par in range(2):
                        act.wait_ge(u_done.sem, u_done.now(m, par + 1))
                        nc.scalar.activation(u[:], by_head(3), ACT.Copy).then_inc(u_ready.sem, 1)
                        act.wait_ge(o_done.sem, o_done.now(m, par + 1))
                        nc.scalar.activation(o[:, par, :, :], by_head(4), ACT.Copy).then_inc(o_ready.sem, 1)

            @block.vector
            def _(dve):
                nc.vector.memset(k_bd[:], 0.0).then_inc(zeroed, 1)
                nc.vector.memset(t_bd[:], 0.0).then_inc(zeroed, 1)
                nc.vector.memset(S[:], 0.0).then_inc(zeroed, 1)
                dve.wait_ge(zeroed, 6)
                for s in (attn_ready, rest_ready, s_ready):
                    s.start(dve)
                with dve.Fori(0, NCH // 2) as m:
                    for par in range(2):
                        dve.wait_ge(attn_done.sem, attn_done.now(m, par + 1))
                        dve.wait_ge(o_done.sem, o_done.now(m, 1) if par else o_done.prev(m, 2))
                        for half in range(2):
                            nc.vector.tensor_tensor(attn[:, 4 * half:4 * half + 4, :],
                                                    PS[:, half, :].rearrange("p (b i) -> p b i", i=P),
                                                    causal[:, :].unsqueeze(1).to_broadcast([P, 4, P]), ALU.mult)
                        dve.drain()
                        dve.sem_inc(attn_ready.sem, 1)
                        dve.wait_ge(ks_done.sem, ks_done.now(m, par + 1))
                        nc.vector.tensor_tensor(rest[:], v[:, par, :, :], by_head(2), ALU.subtract)\
                            .then_inc(rest_ready.sem, 1)
                        dve.wait_ge(s_done.sem, s_done.now(m, par + 1))
                        for c in range(KC):
                            nc.vector.tensor_tensor(S[:, c, :, :], by_head(5 + c), S[:, c, :, :], ALU.add)
                        dve.drain()
                        dve.sem_inc(s_ready.sem, 1)

            @block.tensor
            def _(pe):
                pe.wait_ge(zeroed, 6)
                for s in (attn_done, ks_done, u_done, o_done, s_done):
                    s.start(pe)
                mm = nc.tensor.matmul
                with pe.Fori(0, NCH // 2) as m:
                    for par in range(2):
                        pe.wait_ge(loaded[par], (m + 1) * (16 * N_LOADS))
                        before = (lambda s: s.now(m, 1)) if par else (lambda s: s.prev(m, 2))
                        pe.wait_ge(attn_ready.sem, before(attn_ready))
                        for b in range(B):
                            for c in range(KC):
                                last = mm(PS[:, b // 4, (b % 4) * P:(b % 4 + 1) * P], qk_bd[:, par, 1, c, b, :],
                                          qk_bd[:, par, 0, c, b, :], start=c == 0, stop=c == KC - 1)
                        last.then_inc(attn_done.sem, 1)
                        pe.wait_ge(s_ready.sem, before(s_ready))
                        pe.wait_ge(rest_ready.sem, before(rest_ready))
                        for b in range(B):
                            for c in range(KC):
                                last = mm(by_head(2)[:, b, :], qk_bd[:, par, 1, c, b, :], S[:, c, b, :],
                                          start=c == 0, stop=c == KC - 1)
                        last.then_inc(ks_done.sem, 1)
                        pe.wait_ge(o_ready.sem, before(o_ready))
                        for b in range(B):
                            for c in range(KC):
                                mm(by_head(4)[:, b, :], qk_bd[:, par, 0, c, b, :], S[:, c, b, :],
                                   start=b == 0 and c == 0, stop=False, skip_group_check=True)
                        pe.wait_ge(rest_ready.sem, rest_ready.now(m, par + 1))
                        pe.wait_ge(u_ready.sem, before(u_ready))
                        for b in range(B):
                            last = mm(by_head(3)[:, b, :], t_bd[:, par, b, :], rest[:, b, :], start=True, stop=True)
                        last.then_inc(u_done.sem, 1)
                        pe.wait_ge(u_ready.sem, u_ready.now(m, par + 1))
                        for b in range(B):
                            for c in range(KC):
                                last = mm(by_head(5 + c)[:, b, :], k_bd[:, par, c, b, :], u[:, b, :],
                                          start=True, stop=True)
                        last.then_inc(s_done.sem, 1)
                        pe.wait_ge(attn_ready.sem, attn_ready.now(m, par + 1))
                        for b in range(B):
                            last = mm(by_head(4)[:, b, :], attn[:, b, :], u[:, b, :], start=False, stop=True,
                                      skip_group_check=True)
                        last.then_inc(o_done.sem, 1)


def block_mixer_mix(core):
    nc, PS, dram, scratch = core.nc, core.PS, core.dram, core.mixer
    O = len(OUTS)
    HB = 5
    NF = 14 * MH
    FLOOR = 0.01
    PAIRS = [(0, 1, 3), (1, 2, 2), (2, 3, 1)]
    with ExitStack() as ctx:
        def sb(n, shape, dt=F32):
            return ctx.enter_context(nc.sbuf_tensor(f"mm_{n}", shape, dt))

        def sig(n, per, unit=1):
            return Signal(core, f"mm_{n}", per, unit)

        w1 = sb("w1", [P, KC + 1, HB, P])
        b1 = sb("b1", [P, HB])
        w2 = sb("w2", [P, HB, O * MH])
        b2 = sb("b2", [P, O * MH])
        mix_w = sb("mix_w", [P, D])
        onorm_w = sb("onorm_w", [P, MD])
        wo = sb("wo", [P, KC, D])
        eps5 = sb("eps5", [P, 16])
        inv_md = sb("inv_md", [P, 16])
        xt = sb("xt", [P, KC, SEQ])
        outs = sb("outs", [P, 2, TB, O, D])
        squares = sb("squares", [P, TB, O, D])
        pairs = sb("pairs", [P, TB, 6, D])
        sums = sb("sums", [P, TB, O, MH])
        sumsq = sb("sumsq", [P, TB, O, MH])
        stats = sb("stats", [P, TB, P])
        stats_t = sb("stats_t", [NF, SEQ])
        hid = sb("hid", [P, HB, SEQ])
        tanh = sb("tanh", [P, HB, SEQ])
        act2 = sb("act2", [P, HB, SEQ])
        logits = sb("logits", [P, TB, MH, O])
        top = sb("top", [P, TB, MH])
        expd = sb("expd", [P, TB, MH, O])
        den = sb("den", [P, TB, MH])
        prob = sb("prob", [P, TB, MH, O])
        weighted = sb("weighted", [P, TB, O, D])
        mixed = sb("mixed", [P, TB, D])
        mixed2 = sb("mixed2", [P, TB, D])
        ms = sb("ms", [P, 2, TB, MH])
        rms = sb("rms", [P, 2, TB, MH])
        mixed_t = sb("mixed_t", [P, KC, SEQ])
        norm = Norm(core, ctx, "mm", 3, 7)

        weights_in = core.semaphore("mm_weights_in")
        consts = core.semaphore("mm_constants_ready")
        w2_halved = core.semaphore("mm_w2_halved")
        outs_in = [sig(f"branches_{par}_in", TB, 16) for par in range(2)]
        xt_in = sig("xt_in", 1, 16)
        outs_used = sig("branches_mixed", 1)
        pairs_ready = sig("pairs_ready", 1)
        squares_ready = sig("squares_ready", 1)
        stats_ready = sig("stats_ready", 1)
        stats_turned = sig("stats_turned", 1)
        stats_t_ready = sig("stats_t_ready", 1)
        hid_done = sig("hid_done", 1)
        tanh_ready = sig("tanh_ready", 1)
        act_ready = sig("hidden_ready", 1)
        logits_done = sig("logits_done", 1)
        shifted_ready = sig("shifted_ready", 1)
        exp_ready = sig("exp_ready", 1)
        ms_ready = sig("ms_ready", 2)
        rms_step = sig("rms_step", 6)
        mixed_ready = sig("mixed_ready", 1)
        mixed_turned = sig("mixed_turned", 1)
        mixed_t_ready = sig("mixed_t_ready", 1)
        out_done = sig("out_done", 1)

        def loaded(b, par):
            return outs_in[par].now(0, TB) + (b - par) * (TB * 16 // 2)

        def heads(ap):
            return ap.rearrange("p t (h d) -> p (t h) d", d=MD)

        with nc.Block() as block:
            @block.sync
            def _(sp):
                for dst, n in ((w1, "mm_w1"), (b1, "mm_b1"), (w2, "mm_w2"), (wo, "mm_wo")):
                    sp.dma_start(dst[:], dram[n]).then_inc(weights_in, 16)
                for dst, n in ((b2, "mm_b2"), (mix_w, "mm_mix_w"), (onorm_w, "mm_onorm_w")):
                    sp.dma_start(dst[:], dram[n].partition_broadcast(P)).then_inc(weights_in, 16)
                for s in outs_in:
                    s.start(sp)
                xt_in.start(sp)
                norm.start_sync(sp)

                def load(b, par, waits=True):
                    if waits:
                        sp.wait_ge(outs_used.sem, outs_used.prev(b - 1, 1))
                    for t in range(TB):
                        sp.dma_start(outs[:, par, t, :, :], scratch.outs[:, bass.ds(b * SEQ + t * P, P), :]
                                     .rearrange("o p f -> p o f")).then_inc(outs_in[par].sem, 16)
                    sp.wait_ge(hid_done.sem, hid_done.prev(b, 1))
                    sp.dma_start(xt[:], core.xt_of(b)).then_inc(xt_in.sem, 16)

                load(0, 0, waits=False)
                load(1, 1, waits=False)
                with sp.Fori(0, B // 2 - 1) as m:
                    for par in range(2):
                        b = m * 2 + par
                        norm.load(sp, b)
                        load(b + 2, par)
                        norm.store(sp, b)
                for b in range(B - 2, B):
                    norm.load(sp, b)
                    norm.store(sp, b)

            @block.gpsimd
            def _(pool):
                nc.gpsimd.memset(eps5[:], 1e-5).then_inc(consts, 1)
                nc.gpsimd.memset(inv_md[:], 1.0 / MD).then_inc(consts, 1)
                nc.gpsimd.memset(stats[:], 0.0).then_inc(consts, 1)
                pool.wait_ge(consts, 3)
                pairs_ready.start(pool)
                rms_step.start(pool)
                norm.start_gpsimd(pool)

                def multiply_pairs(b, par):
                    pool.wait_ge(outs_in[par].sem, loaded(b, par))
                    pool.wait_ge(stats_ready.sem, stats_ready.prev(b, 1))
                    for t in range(TB):
                        at = 0
                        for first, second, n in PAIRS:
                            nc.gpsimd.tensor_tensor(pairs[:, t, at:at + n, :], outs[:, par, t, second:second + n, :],
                                                    outs[:, par, t, first, :].unsqueeze(1).to_broadcast([P, n, D]),
                                                    ALU.mult)
                            at += n
                    pool.drain()
                    pool.sem_inc(pairs_ready.sem, 1)

                def rest_of(b, par, following):
                    for k in range(2):
                        pool.wait_ge(ms_ready.sem, ms_ready.now(b, k + 1))
                        flat = rms[:, k, :, :].rearrange("p t h -> p (t h)")
                        steps = ((ms[:, k, :, :].rearrange("p t h -> p (t h)"), inv_md, ALU.mult),
                                 (flat, eps5, ALU.add), (flat, core.minus_half, ALU.pow))
                        for i, (src, const, op) in enumerate(steps):
                            if i:
                                pool.wait_ge(rms_step.sem, rms_step.now(b, 3 * k + i))
                            nc.gpsimd.tensor_tensor(flat, src, const[:, 0:TB * MH], op).then_inc(rms_step.sem, 1)
                    if following == 2:
                        multiply_pairs(b + 2, par)
                    norm.gpsimd(pool, b)

                multiply_pairs(0, 0)
                multiply_pairs(1, 1)
                with pool.Fori(0, B // 2 - 1) as m:
                    for par in range(2):
                        rest_of(m * 2 + par, par, 2)
                rest_of(B - 2, 0, 1)
                rest_of(B - 1, 1, 0)

            @block.scalar
            def _(act):
                act.wait_ge(weights_in, 112)
                for s in (squares_ready, stats_t_ready, tanh_ready, exp_ready, mixed_t_ready):
                    s.start(act)
                norm.start_scalar(act)

                def square(b, par):
                    act.wait_ge(outs_in[par].sem, loaded(b, par))
                    act.wait_ge(stats_ready.sem, stats_ready.prev(b, 1))
                    nc.scalar.activation(squares[:], outs[:, par, :, :, :], ACT.Square).then_inc(squares_ready.sem, 1)

                def take_stats_t(b):
                    act.wait_ge(stats_turned.sem, stats_turned.now(b, 1))
                    nc.scalar.activation(stats_t[:], PS[0:NF, 3, 0:SEQ], ACT.Copy).then_inc(stats_t_ready.sem, 1)

                def take_hidden(b):
                    act.wait_ge(hid_done.sem, hid_done.now(b, 1))
                    act.wait_ge(act_ready.sem, act_ready.prev(b, 1))
                    for h in range(HB):
                        nc.scalar.activation(hid[:, h, :], PS[:, h // 2, (h % 2) * SEQ:(h % 2 + 1) * SEQ],
                                             ACT.Identity, bias=b1[:, h:h + 1])
                    act.drain()
                    nc.scalar.activation(tanh[:], hid[:], ACT.Tanh, scale=0.5).then_inc(tanh_ready.sem, 1)

                def exponentials(b):
                    act.wait_ge(shifted_ready.sem, shifted_ready.now(b, 1))
                    nc.scalar.activation(expd[:], logits[:], ACT.Exp).then_inc(exp_ready.sem, 1)

                def rest_of(b, par, following):
                    if following:
                        take_stats_t(b + 1)
                    if following == 2:
                        square(b + 2, par)
                    if following:
                        take_hidden(b + 1)
                    act.wait_ge(mixed_turned.sem, mixed_turned.now(b, 1))
                    nc.scalar.activation(mixed_t[:].rearrange("p c n -> p (c n)"), PS[:, 5, :],
                                         ACT.Copy).then_inc(mixed_t_ready.sem, 1)
                    if following:
                        exponentials(b + 1)
                    norm.scalar(act, b)

                square(0, 0)
                take_stats_t(0)
                square(1, 1)
                take_hidden(0)
                exponentials(0)
                with act.Fori(0, B // 2 - 1) as m:
                    for par in range(2):
                        rest_of(m * 2 + par, par, 2)
                rest_of(B - 2, 0, 1)
                rest_of(B - 1, 1, 0)

            @block.vector
            def _(dve):
                dve.wait_ge(weights_in, 112)
                nc.vector.tensor_scalar(w2[:], w2[:], 0.5, None, ALU.mult).then_inc(w2_halved, 1)
                dve.wait_ge(consts, 3)
                for s in (stats_ready, act_ready, shifted_ready, ms_ready, mixed_ready, outs_used):
                    s.start(dve)
                norm.start_vector(dve)

                def sum_branches(b, par):
                    dve.wait_ge(outs_in[par].sem, loaded(b, par))
                    nc.vector.tensor_reduce(sums[:], outs[:, par, :, :, :].rearrange("p t o (h d) -> p (t o) h d", d=MD), AX.X,
                                            ALU.add)
                    dve.wait_ge(squares_ready.sem, squares_ready.now(b, 1))
                    nc.vector.tensor_reduce(sumsq[:], squares[:].rearrange("p t o (h d) -> p (t o) h d", d=MD), AX.X,
                                            ALU.add)

                def statistics(b):
                    dve.wait_ge(stats_turned.sem, stats_turned.prev(b, 1))
                    by_kind = stats[:, :, 0:NF].rearrange("p t (k h) -> p t k h", h=MH)
                    dve.wait_ge(pairs_ready.sem, pairs_ready.now(b, 1))
                    for t in range(TB):
                        nc.vector.tensor_reduce(by_kind[:, t, 8:14, :], pairs[:, t, :, :]
                                                .rearrange("p k (h d) -> p k h d", d=MD), AX.X, ALU.add)
                    dve.drain()
                    nc.vector.tensor_scalar(by_kind[:, :, 8:14, :], by_kind[:, :, 8:14, :], 1.0 / MD, None, ALU.mult)
                    for t in range(TB):
                        nc.vector.tensor_scalar(by_kind[:, t, 0:8:2, :], sums[:, t, :, :], 1.0 / MD, None, ALU.mult)
                    dve.drain()
                    for t in range(TB):
                        nc.vector.tensor_tensor(sums[:, t, :, :], sums[:, t, :, :], by_kind[:, t, 0:8:2, :], ALU.mult)
                    dve.drain()
                    nc.vector.tensor_tensor(sumsq[:], sumsq[:], sums[:], ALU.subtract)
                    dve.drain()
                    for t in range(TB):
                        nc.vector.tensor_scalar(by_kind[:, t, 1:8:2, :], sumsq[:, t, :, :], 1.0 / (MD - 1), None,
                                                ALU.mult)
                    dve.drain()
                    dve.sem_inc(stats_ready.sem, 1)

                def finish_hidden(b):
                    dve.wait_ge(tanh_ready.sem, tanh_ready.now(b, 1))
                    dve.wait_ge(logits_done.sem, logits_done.prev(b, 1))
                    nc.vector.scalar_tensor_tensor(act2[:], tanh[:], 1.0, hid[:], ALU.add, ALU.mult)\
                        .then_inc(act_ready.sem, 1)

                def shift_logits(b):
                    dve.wait_ge(logits_done.sem, logits_done.now(b, 1))
                    flat = logits[:].rearrange("p t h o -> p t (h o)")
                    nc.vector.tensor_tensor(flat, PS[:, 4, 0:TB * O * MH].rearrange("p (t n) -> p t n", t=TB),
                                            b2[:, :].unsqueeze(1).to_broadcast([P, TB, O * MH]), ALU.add)
                    dve.drain()
                    nc.vector.tensor_reduce(top[:], logits[:], AX.X, ALU.max)
                    dve.drain()
                    nc.vector.tensor_tensor(logits[:], logits[:], spread(top[:], O), ALU.subtract)\
                        .then_inc(shifted_ready.sem, 1)

                def mix(b, par):
                    dve.wait_ge(exp_ready.sem, exp_ready.now(b, 1))
                    nc.vector.tensor_reduce(den[:], expd[:], AX.X, ALU.add)
                    dve.drain()
                    nc.vector.reciprocal(den[:], den[:])
                    dve.drain()
                    nc.vector.tensor_tensor(prob[:], expd[:], spread(den[:], O), ALU.mult)
                    dve.drain()
                    nc.vector.tensor_scalar(prob[:], prob[:], 1.0 - 4.0 * FLOOR, FLOOR, ALU.mult, ALU.add)
                    dve.drain()
                    for t in range(TB):
                        nc.vector.tensor_tensor(weighted[:, t, :, :].rearrange("p o (h d) -> p o h d", d=MD),
                                                outs[:, par, t, :, :].rearrange("p o (h d) -> p o h d", d=MD),
                                                spread(prob[:, t, :, :].rearrange("p h o -> p o h"), MD), ALU.mult)
                    dve.drain()
                    dve.sem_inc(outs_used.sem, 1)
                    for t in range(TB):
                        nc.vector.tensor_reduce(mixed[:, t, :], weighted[:, t, :, :].rearrange("p o f -> p f o"), AX.X,
                                                ALU.add)
                    dve.drain()

                def square_sums(b, k, src):
                    nc.vector.tensor_tensor(weighted[:, :, 0, :], src[:], src[:], ALU.mult)
                    dve.drain()
                    nc.vector.tensor_reduce(ms[:, k, :, :], weighted[:, :, 0, :]
                                            .rearrange("p t (h d) -> p t h d", d=MD), AX.X, ALU.add)\
                        .then_inc(ms_ready.sem, 1)

                def scale_by_rms(b, k, to, src):
                    dve.wait_ge(rms_step.sem, rms_step.now(b, 3 * k + 3))
                    nc.vector.tensor_tensor(heads(to[:]), heads(src[:]),
                                            spread(rms[:, k, :, :].rearrange("p t h -> p (t h)"), MD), ALU.mult)
                    dve.drain()

                def rest_of(b, par, following):
                    mix(b, par)
                    square_sums(b, 0, mixed)
                    if following:
                        statistics(b + 1)
                    scale_by_rms(b, 0, mixed2, mixed)
                    nc.vector.tensor_tensor(mixed2[:], mixed2[:], mix_w[:, :].unsqueeze(1).to_broadcast([P, TB, D]),
                                            ALU.mult)
                    dve.drain()
                    square_sums(b, 1, mixed2)
                    scale_by_rms(b, 1, mixed, mixed2)
                    nc.vector.tensor_tensor(heads(mixed[:]), heads(mixed[:]),
                                            onorm_w[:, :].unsqueeze(1).to_broadcast([P, TB * MH, MD]), ALU.mult)\
                        .then_inc(mixed_ready.sem, 1)
                    if following == 2:
                        sum_branches(b + 2, par)
                    if following:
                        finish_hidden(b + 1)
                    norm.vector(dve, b, (out_done.sem, out_done.now(b, 1)))
                    if following:
                        shift_logits(b + 1)

                sum_branches(0, 0)
                statistics(0)
                sum_branches(1, 1)
                finish_hidden(0)
                shift_logits(0)
                with dve.Fori(0, B // 2 - 1) as m:
                    for par in range(2):
                        rest_of(m * 2 + par, par, 2)
                rest_of(B - 2, 0, 1)
                rest_of(B - 1, 1, 0)

            @block.tensor
            def _(pe):
                pe.wait_ge(weights_in, 112)
                pe.wait_ge(consts, 3)
                pe.wait_ge(w2_halved, 1)
                for s in (stats_turned, hid_done, logits_done, mixed_turned, out_done):
                    s.start(pe)
                norm.start_tensor(pe)
                mm = nc.tensor.matmul

                def turn_stats(b):
                    pe.wait_ge(stats_ready.sem, stats_ready.now(b, 1))
                    pe.wait_ge(stats_t_ready.sem, stats_t_ready.prev(b, 1))
                    for t in range(TB):
                        last = nc.tensor.transpose(PS[:, 3, t * P:(t + 1) * P], stats[:, t, :], core.ident[:])
                    last.then_inc(stats_turned.sem, 1)

                def hidden(b):
                    pe.wait_ge(stats_t_ready.sem, stats_t_ready.now(b, 1))
                    pe.wait_ge(xt_in.sem, xt_in.now(b, 1))
                    pe.wait_ge(tanh_ready.sem, tanh_ready.prev(b, 1))
                    for h in range(HB):
                        to = PS[:, h // 2, (h % 2) * SEQ:(h % 2 + 1) * SEQ]
                        for c in range(KC):
                            mm(to, w1[:, c, h, :], xt[:, c, :], start=c == 0, stop=False)
                        last = mm(to, w1[0:NF, KC, h, :], stats_t[:], start=False, stop=True)
                    last.then_inc(hid_done.sem, 1)

                def router_logits(b):
                    pe.wait_ge(act_ready.sem, act_ready.now(b, 1))
                    pe.wait_ge(shifted_ready.sem, shifted_ready.prev(b, 1))
                    for t in range(TB):
                        for h in range(HB):
                            last = mm(PS[:, 4, t * O * MH:(t + 1) * O * MH], act2[:, h, t * P:(t + 1) * P], w2[:, h, :],
                                      start=h == 0, stop=h == HB - 1)
                    last.then_inc(logits_done.sem, 1)

                def turn_mixed(b):
                    pe.wait_ge(mixed_ready.sem, mixed_ready.now(b, 1))
                    pe.wait_ge(mixed_t_ready.sem, mixed_t_ready.prev(b, 1))
                    for c in range(KC):
                        for t in range(TB):
                            last = nc.tensor.transpose(PS[:, 5, (c * TB + t) * P:(c * TB + t + 1) * P],
                                                       mixed[:, t, c * P:(c + 1) * P], core.ident[:])
                    last.then_inc(mixed_turned.sem, 1)

                def project_output(b):
                    pe.wait_ge(mixed_t_ready.sem, mixed_t_ready.now(b, 1))
                    pe.wait_ge(norm.xt_ready.sem, norm.xt_ready.prev(norm.turn(b), 1))
                    for t in range(TB):
                        for c in range(KC):
                            last = mm(PS[:, 7, t * D:(t + 1) * D], mixed_t[:, c, t * P:(t + 1) * P], wo[:, c, :],
                                      start=c == 0, stop=c == KC - 1)
                    last.then_inc(out_done.sem, 1)

                def rest_of(b, par, following):
                    if following:
                        turn_stats(b + 1)
                        hidden(b + 1)
                    turn_mixed(b)
                    project_output(b)
                    if following:
                        router_logits(b + 1)
                    norm.tensor(pe, b)

                turn_stats(0)
                hidden(0)
                router_logits(0)
                with pe.Fori(0, B // 2 - 1) as m:
                    for par in range(2):
                        rest_of(m * 2 + par, par, 2)
                rest_of(B - 2, 0, 1)
                rest_of(B - 1, 1, 0)


def block_experts_1(core):
    E, HB = 8, 8
    nc, PS, dram = core.nc, core.PS, core.dram
    with ExitStack() as ctx:
        def sb(n, shape, dt=F32):
            return ctx.enter_context(nc.sbuf_tensor(f"eb_{n}", shape, dt))

        def sig(n, per, unit=1):
            return Signal(core, f"eb_{n}", per, unit)

        up = sb("up", [P, KC, E, HB, P])
        down = sb("down", [P, E, HB, D])
        up_bias = sb("up_bias", [P, E, HB])
        down_bias = sb("down_bias", [P, D])
        router = sb("router", [P, KC, E])
        router_bias = sb("router_bias", [P, E])
        gamma = sb("gamma", [P, D])
        beta = sb("beta", [P, D])
        iota8 = sb("iota8", [P, E])
        xt_route = sb("xt_route", [P, KC, SEQ])
        xt = sb("xt", [P, KC, SEQ])
        logits = sb("logits", [P, TB, E])
        best = sb("best", [P, TB, 8])
        index = sb("index", [P, TB, 8], mybir.dt.uint32)
        index_f = sb("index_f", [P, TB, 8])
        chosen = sb("chosen", [P, TB, 2, E])
        gap = sb("gap", [P, TB])
        mix = sb("mix", [P, TB, 2])
        exp_gap = sb("exp_gap", [P, TB])
        weight_next = sb("weight_next", [P, TB, E])
        weight = sb("weight", [P, TB, E])
        weight_t = sb("weight_t", [P, SEQ])
        hidden = sb("hidden", [P, 2, HB // 2, SEQ])
        total = sb("total", [P, TB, D])
        inner_stats = sb("inner_stats", [P, TB, 6])
        inner_mv = sb("inner_mean_var", [P, TB, 2])
        inner_rstd = sb("inner_rstd", [P, TB])
        norm = Norm(core, ctx, "eb", 5, 7)

        weights_in = core.semaphore("eb_weights_in")
        consts = core.semaphore("eb_constants_ready")
        expert_in = [core.semaphore(f"eb_expert_{e}_in") for e in range(E)]
        route_in = sig("xt_route_in", 1, 16)
        xt_in = sig("xt_in", 1, 16)
        router_done = sig("router_done", 1)
        gap_ready = sig("gap_ready", 1)
        exp_ready = sig("exp_ready", 1)
        weight_ready = sig("weight_ready", 1)
        weight_turned = sig("weight_turned", 1)
        weight_t_ready = sig("weight_t_ready", 1)
        bias_done = sig("mixed_bias_done", 1)
        total_started = sig("total_started", 1)
        up_done = sig("up_done", 2 * E)
        hidden_ready = sig("hidden_ready", 2 * E)
        down_half = sig("down_half", 2 * E)
        added = sig("expert_added", E)
        inner_var_ready = sig("inner_variance_ready", 1)
        inner_rstd_step = sig("inner_rstd_step", 2)

        def tiles(ap):
            return ap.rearrange("p (t d) -> p t d", t=TB)

        def half_banks(h):
            return PS[:, 2 * (h % 2):2 * (h % 2) + 2, :].rearrange("p a (m n) -> p (a m) n", n=SEQ)

        with nc.Block() as block:
            @block.sync
            def _(sp):
                for dst, n in ((up_bias, "eb_up_bias"), (router, "eb_router")):
                    sp.dma_start(dst[:], dram[n]).then_inc(weights_in, 16)
                sp.dma_start(down_bias[0:E, :], dram["eb_down_bias"]).then_inc(weights_in, 16)
                for dst, n in ((router_bias, "eb_router_bias"), (gamma, "eb_gamma"), (beta, "eb_beta")):
                    sp.dma_start(dst[:], dram[n].partition_broadcast(P)).then_inc(weights_in, 16)
                route_in.start(sp)
                xt_in.start(sp)
                norm.start_sync(sp)

                def load_for_router(b):
                    sp.wait_ge(router_done.sem, router_done.prev(b, 1))
                    sp.dma_start(xt_route[:], core.xt_of(b)).then_inc(route_in.sem, 16)

                def load_for_experts(b):
                    sp.wait_ge(up_done.sem, up_done.prev(b, 2 * E))
                    sp.dma_start(xt[:], core.xt_of(b)).then_inc(xt_in.sem, 16)

                load_for_router(0)
                load_for_experts(0)
                for e in range(E):
                    sp.dma_start(up[:, :, e, :, :], dram["eb_up"][:, :, e, :, :]).then_inc(expert_in[e], 16)
                    sp.dma_start(down[:, e, :, :], dram["eb_down"][:, e, :, :]).then_inc(expert_in[e], 16)
                with sp.Fori(0, B - 1) as b:
                    norm.load(sp, b)
                    load_for_router(b + 1)
                    load_for_experts(b + 1)
                    norm.store(sp, b, last=True)
                norm.load(sp, B - 1)
                norm.store(sp, B - 1, last=True)

            @block.gpsimd
            def _(pool):
                nc.gpsimd.iota(iota8[:], pattern=[[1, E]], base=0, channel_multiplier=0,
                               allow_small_or_imprecise_dtypes=True).then_inc(consts, 1)
                inner_rstd_step.start(pool)
                norm.start_gpsimd(pool)
                with pool.Fori(0, B) as b:
                    pool.wait_ge(inner_var_ready.sem, inner_var_ready.now(b, 1))
                    nc.gpsimd.tensor_tensor(inner_rstd[:], inner_mv[:, :, 1], core.eps[:, 0:TB],
                                            ALU.add).then_inc(inner_rstd_step.sem, 1)
                    pool.wait_ge(inner_rstd_step.sem, inner_rstd_step.now(b, 1))
                    nc.gpsimd.tensor_tensor(inner_rstd[:], inner_rstd[:], core.minus_half[:, 0:TB],
                                            ALU.pow).then_inc(inner_rstd_step.sem, 1)
                    norm.gpsimd(pool, b)

            @block.scalar
            def _(act):
                act.wait_ge(weights_in, 96)
                for s in (exp_ready, weight_t_ready, hidden_ready):
                    s.start(act)
                norm.start_scalar(act)

                def exp_of_gap(b):
                    act.wait_ge(gap_ready.sem, gap_ready.now(b, 1))
                    nc.scalar.activation(exp_gap[:], gap[:], ACT.Exp).then_inc(exp_ready.sem, 1)

                def take_weight_t(b):
                    act.wait_ge(weight_turned.sem, weight_turned.now(b, 1))
                    nc.scalar.activation(weight_t[0:E, :], PS[0:E, 6, 0:SEQ], ACT.Copy).then_inc(weight_t_ready.sem, 1)

                def rest_of(b, following):
                    for h in range(2 * E):
                        act.wait_ge(up_done.sem, up_done.now(b, h + 1))
                        if h >= 2:
                            act.wait_ge(down_half.sem, down_half.now(b, h - 1))
                        else:
                            act.wait_ge(down_half.sem, down_half.prev(b, 2 * E - 1 + h))
                        for m in range(HB // 2):
                            n = (h % 2) * (HB // 2) + m
                            nc.scalar.activation(hidden[:, h % 2, m, :], half_banks(h)[:, m, :], ACT.Relu,
                                                 bias=up_bias[:, h // 2, n:n + 1])
                        act.drain()
                        act.sem_inc(hidden_ready.sem, 1)
                        if following and h == 7:
                            exp_of_gap(b + 1)
                        if following and h == 10:
                            take_weight_t(b + 1)

                exp_of_gap(0)
                take_weight_t(0)
                with act.Fori(0, B - 1) as b:
                    rest_of(b, True)
                rest_of(B - 1, False)

            @block.vector
            def _(dve):
                dve.wait_ge(weights_in, 96)
                dve.wait_ge(consts, 1)
                for s in (gap_ready, weight_ready, total_started, added, inner_var_ready):
                    s.start(dve)
                norm.start_vector(dve)

                def route(b):
                    dve.wait_ge(router_done.sem, router_done.now(b, 1))
                    nc.vector.tensor_tensor(logits[:], PS[:, 6, 0:TB * E].rearrange("p (t e) -> p t e", t=TB),
                                            router_bias[:, :].unsqueeze(1).to_broadcast([P, TB, E]), ALU.add)
                    dve.drain()
                    for t in range(TB):
                        top2(nc, dve, t, logits, iota8, best, index, index_f, chosen)
                    nc.vector.tensor_tensor(gap[:], best[:, :, 1], best[:, :, 0], ALU.subtract)\
                        .then_inc(gap_ready.sem, 1)
                    dve.wait_ge(exp_ready.sem, exp_ready.now(b, 1))
                    nc.vector.tensor_scalar(mix[:, :, 1], exp_gap[:], 1.0, None, ALU.add)
                    dve.drain()
                    nc.vector.reciprocal(mix[:, :, 0], mix[:, :, 1])
                    dve.drain()
                    nc.vector.tensor_tensor(mix[:, :, 1], mix[:, :, 0], exp_gap[:], ALU.mult)
                    dve.drain()
                    nc.vector.tensor_tensor(chosen[:], chosen[:], spread(mix[:], E), ALU.mult)
                    dve.drain()
                    nc.vector.tensor_tensor(weight_next[:], chosen[:, :, 0, :], chosen[:, :, 1, :], ALU.add)\
                        .then_inc(weight_ready.sem, 1)

                def rest_of(b, following):
                    dve.wait_ge(bias_done.sem, bias_done.now(b, 1))
                    nc.vector.tensor_copy(weight[:], weight_next[:])
                    nc.vector.tensor_copy(total[:], tiles(PS[:, 6, :]))
                    dve.drain()
                    dve.sem_inc(total_started.sem, 1)
                    for e in range(E):
                        dve.wait_ge(down_half.sem, down_half.now(b, 2 * e + 2))
                        for t in range(TB):
                            nc.vector.scalar_tensor_tensor(total[:, t, :], tiles(PS[:, 4 + e % 2, :])[:, t, :],
                                                           weight[:, t, e:e + 1], total[:, t, :], ALU.mult, ALU.add)
                        dve.drain()
                        dve.sem_inc(added.sem, 1)
                        if following and e == 2:
                            route(b + 1)
                    dve.wait_ge(norm.residual_in.sem, norm.residual_in.now(norm.turn(b), 1))
                    nc.vector.tensor_tensor(total[:], total[:], norm.x_in[:], ALU.add)
                    dve.drain()
                    for t in range(TB):
                        nc.vector.bn_stats(inner_stats[:, t, :], total[:, t, :])
                    dve.drain()
                    for t in range(TB):
                        nc.vector.bn_aggr(inner_mv[:, t, :], inner_stats[:, t, :])
                    dve.drain()
                    dve.sem_inc(inner_var_ready.sem, 1)
                    dve.wait_ge(inner_rstd_step.sem, inner_rstd_step.now(b, 2))
                    for t in range(TB):
                        nc.vector.tensor_scalar(total[:, t, :], total[:, t, :], inner_mv[:, t, 0:1],
                                                inner_rstd[:, t:t + 1], ALU.subtract, ALU.mult)
                    dve.drain()
                    for w, op in ((gamma, ALU.mult), (beta, ALU.add)):
                        nc.vector.tensor_tensor(total[:], total[:], w[:, :].unsqueeze(1).to_broadcast([P, TB, D]), op)
                        dve.drain()
                    norm.vector(dve, b, (down_half.sem, down_half.now(b, 2 * E)), source=total[:])

                route(0)
                with dve.Fori(0, B - 1) as b:
                    rest_of(b, True)
                rest_of(B - 1, False)

            @block.tensor
            def _(pe):
                pe.wait_ge(weights_in, 96)
                for s in (router_done, weight_turned, bias_done, up_done, down_half):
                    s.start(pe)
                norm.start_tensor(pe)
                mm = nc.tensor.matmul

                def route(b):
                    pe.wait_ge(route_in.sem, route_in.now(b, 1))
                    pe.wait_ge(total_started.sem, total_started.prev(b, 1))
                    for t in range(TB):
                        for c in range(KC):
                            last = mm(PS[:, 6, t * E:(t + 1) * E], xt_route[:, c, t * P:(t + 1) * P],
                                      router[:, c, :], start=c == 0, stop=c == KC - 1)
                    last.then_inc(router_done.sem, 1)

                def turn_weight(b):
                    pe.wait_ge(weight_ready.sem, weight_ready.now(b, 1))
                    for t in range(TB):
                        last = nc.tensor.transpose(PS[0:E, 6, t * P:(t + 1) * P], weight_next[:, t, :], core.ident[:])
                    last.then_inc(weight_turned.sem, 1)

                def mix_bias(b):
                    pe.wait_ge(weight_t_ready.sem, weight_t_ready.now(b, 1))
                    for t in range(TB):
                        last = mm(PS[:, 6, t * D:(t + 1) * D], weight_t[0:E, t * P:(t + 1) * P], down_bias[0:E, :],
                                  start=True, stop=True)
                    last.then_inc(bias_done.sem, 1)

                def up_half(b, h, first):
                    e = h // 2
                    if first:
                        pe.wait_ge(expert_in[e], 32)
                    if h == 0:
                        pe.wait_ge(xt_in.sem, xt_in.now(b, 1))
                    if h >= 2:
                        pe.wait_ge(hidden_ready.sem, hidden_ready.now(b, h - 1))
                    else:
                        pe.wait_ge(hidden_ready.sem, hidden_ready.prev(b, 2 * E - 1 + h))
                    for m in range(HB // 2):
                        for c in range(KC):
                            last = mm(half_banks(h)[:, m, :], up[:, c, e, (h % 2) * (HB // 2) + m, :],
                                      xt[:, c, :], start=c == 0, stop=c == KC - 1)
                    last.then_inc(up_done.sem, 1)

                def down_of(b, h):
                    e = h // 2
                    pe.wait_ge(hidden_ready.sem, hidden_ready.now(b, h + 1))
                    if h % 2 == 0:
                        if e >= 2:
                            pe.wait_ge(added.sem, added.now(b, e - 1))
                        else:
                            pe.wait_ge(added.sem, added.prev(b, E - 1 + e))
                    for t in range(TB):
                        for m in range(HB // 2):
                            last = mm(PS[:, 4 + e % 2, t * D:(t + 1) * D], hidden[:, h % 2, m, t * P:(t + 1) * P],
                                      down[:, e, (h % 2) * (HB // 2) + m, :],
                                      start=h % 2 == 0 and m == 0 and t == 0,
                                      stop=h % 2 == 1 and m == HB // 2 - 1, skip_group_check=True)
                    last.then_inc(down_half.sem, 1)

                def rest_of(b, following, first=False):
                    for h in range(2 * E):
                        down_of(b, h)
                        if following and h == 3:
                            route(b + 1)
                        if following and h == 9:
                            turn_weight(b + 1)
                        if following and h == 11:
                            mix_bias(b + 1)
                        if h + 2 < 2 * E:
                            up_half(b, h + 2, first)
                        elif following:
                            up_half(b + 1, h + 2 - 2 * E, False)

                route(0)
                up_half(0, 0, True)
                turn_weight(0)
                up_half(0, 1, True)
                mix_bias(0)
                rest_of(0, True, first=True)
                with pe.Fori(1, B - 1) as b:
                    rest_of(b, True)
                rest_of(B - 1, False)


def program(nc, dram, out):
    core = Core(nc, dram, out)
    constants(core)
    core.end_block()
    for layer in BLOCKS:
        for build in layer:
            build(core)
            core.end_block()


BLOCKS = [
    [block_self_attention], [block_cross_attention_0], [block_experts_0],
    [block_mixer_project, block_mixer_solve, block_mixer_scan, block_mixer_mix],
    [block_cross_attention_1], [block_experts_1],
]


def layouts(a):
    f = {}
    x = a["x"].reshape(B * SEQ, D)
    f["x"], f["x_t"] = x, x.T

    def chunks(w, n=P):
        return w.reshape(w.shape[0] // n, n, -1).transpose(1, 0, 2)

    hd = 1024
    wkv, bkv = a["L0_attn_Wkv"], a["L0_attn_bkv"]
    wqk = np.stack([a["L0_attn_Wq"].reshape(KC, P, 8, P), wkv[:, :hd].reshape(KC, P, 8, P)], axis=3)
    f["sa_wqk"] = wqk.transpose(1, 0, 2, 3, 4)
    f["sa_bqk"] = np.stack([a["L0_attn_bq"].reshape(8, P), bkv[:hd].reshape(8, P)], axis=1).transpose(2, 0, 1)
    f["sa_wv"] = chunks(wkv[:, hd:])
    f["sa_bv"] = bkv[hd:]
    f["sa_wo"] = chunks(a["L0_attn_Wo"])
    f["sa_bo"] = a["L0_attn_bo"]
    dim = 64
    inv_freq = 1.0 / np.float32(10000.0) ** (np.arange(0, dim, 2, dtype=np.float32) / np.float32(dim))
    angle = np.tile(inv_freq.astype(np.float32), 4)[:, None] * np.arange(SEQ, dtype=np.float32)[None]
    angle = angle.astype(np.float32)
    scale = np.array([dim ** -0.5, 1.0], np.float32)[None, :, None]
    sign = np.tile(np.repeat(np.array([1.0, -1.0], np.float32), 32), 2)[:, None, None]
    f["cos"] = np.cos(angle)[:, None, :] * scale
    f["sin"] = np.sin(angle)[:, None, :] * scale * sign

    f["ctx_t"] = chunks(a["ctx_1024"].reshape(-1, D).T)
    f["key_mask"] = a["mask_BxS2_if1"]
    for to, src, turn in (("ca", "L0_xattn", True), ("cb", "L1_xattn", False)):
        w = {n: a[f"{src}_W{n}"].T if turn else a[f"{src}_W{n}"] for n in "qkvo"}
        for n in "qkvo":
            f[f"{to}_w{n}"] = chunks(w[n])
            bias = a[f"{src}_b{n}"]
            f[f"{to}_b{n}"] = bias.reshape(KC, P).T if n in "qk" else bias

    def pad(w, axis):
        widths = [(0, 0)] * w.ndim
        widths[axis] = (0, -w.shape[axis] % P)
        return np.pad(w, widths)

    f["ea_up"] = pad(a["L0_ffn_w_up"], 1).reshape(8, 3, P, KC, P).transpose(4, 3, 0, 1, 2)
    f["ea_down"] = pad(a["L0_ffn_w_down"], 2).reshape(8, D, 3, P).transpose(3, 0, 2, 1)
    f["ea_shared_up"] = pad(a["L0_ffn_shared_w_up"], 0).reshape(3, P, KC, P).transpose(3, 2, 0, 1)
    f["ea_shared_down"] = pad(a["L0_ffn_shared_w_down"], 1).reshape(D, 3, P).transpose(2, 1, 0)
    f["ea_gate"] = chunks(a["L0_ffn_gate_w"].T)
    f["ea_gate_bias"] = a["L0_ffn_expert_bias"]
    f["eb_up"] = a["L1_ffn_W1"].reshape(8, 8, P, KC, P).transpose(4, 3, 0, 1, 2)
    f["eb_up_bias"] = a["L1_ffn_b1"].reshape(8, 8, P).transpose(2, 0, 1)
    f["eb_down"] = a["L1_ffn_W2"].reshape(8, D, 8, P).transpose(3, 0, 2, 1)
    f["eb_down_bias"] = a["L1_ffn_b2"]
    f["eb_router"] = chunks(a["L1_ffn_Wr"].T)
    f["eb_router_bias"] = a["L1_ffn_br"]
    qkv = np.stack([a[f"L1_attn_W{n}"] for n in "qkv"], axis=1)
    f["mp_w"] = qkv.reshape(KC, P, 3, KC, P).transpose(1, 0, 2, 3, 4)
    f["mp_w_beta"] = chunks(a["L1_attn_Wb"])
    conv = np.stack([a[f"L1_attn_conv_{n}_w"] for n in "qkv"])
    f["mp_conv_w"] = conv.reshape(3, KC, P, CONV).transpose(2, 0, 1, 3)
    f["mp_local_w"], f["mp_mid_w"] = chunks(a["L1_attn_local_w"]), chunks(a["L1_attn_mid_w"])
    f["mm_w1"] = pad(pad(a["L1_attn_r_w1"], 0), 1).reshape(KC + 1, P, 5, P).transpose(1, 0, 2, 3)
    f["mm_b1"] = pad(a["L1_attn_r_b1"], 0).reshape(5, P).T
    f["mm_w2"] = chunks(pad(a["L1_attn_r_w2"], 0))
    f["mm_b2"] = a["L1_attn_r_b2"]
    f["mm_mix_w"], f["mm_onorm_w"] = a["L1_attn_mix_w"].reshape(-1), a["L1_attn_onorm_w"]
    f["mm_wo"] = chunks(a["L1_attn_Wo"])
    f["eb_gamma"], f["eb_beta"] = a["L1_ffn_gamma"], a["L1_ffn_beta"]
    return f


def kernel(**inputs):
    import concourse.bacc as bacc
    from concourse.bass_utils import run_bass_kernel_spmd

    f = layouts({k: np.asarray(v) for k, v in inputs.items()})
    nc = bacc.Bacc("TRN2", target_bir_lowering=False, num_devices=1)
    arrays, dram = {}, {}
    for name, v in f.items():
        v = np.ascontiguousarray(v)
        arrays["in_" + name] = v
        dram[name] = nc.dram_tensor("in_" + name, v.shape, mybir.dt.from_np(v.dtype), kind="ExternalInput").ap()
    out = nc.dram_tensor("out", (B * SEQ, D), F32, kind="ExternalOutput").ap()
    program(nc, dram, out)
    r = run_bass_kernel_spmd(nc, [arrays], core_ids=[0])
    return r.results[0]["out"].reshape(B, SEQ, D)
```
